# Optimizing a Trainium2 kernel written in Bass

```python
import numpy as np
import jax
import jax.numpy as jnp

def _softmax(x, axis=-1):
    return jax.nn.softmax(x, axis=axis)

def _gelu(x):
    return jax.nn.gelu(x, approximate=True)

def _silu(x):
    return jax.nn.silu(x)

def _sigmoid(x):
    return jax.nn.sigmoid(x)

def _layernorm(x, axis=-1, eps=1e-05):
    m = jnp.mean(x, axis=axis, keepdims=True)
    v = jnp.var(x, axis=axis, keepdims=True)
    return (x - m) / jnp.sqrt(v + eps)

def _scatter_add(tgt, idx, src, axis=0):
    return tgt.at[idx].add(src)

def _segment_sum(src, seg, n):
    return jax.ops.segment_sum(src, seg, n)
kernel_name = 'mk_decoder_preln_d4_seqx_r8_14550b'

def setup_inputs(seed: int=0):
    np.random.seed(seed)
    _w = jnp.asarray

    def _rec_inputs():
        import jax
        import jax.numpy as jnp
        _rk = jax.random.key(seed)
        x = -0.000929 + 1 * jax.random.normal(jax.random.fold_in(_rk, 1), (64, 64, 128), jnp.float32)
        _lenS = 64 - jax.random.randint(jax.random.fold_in(_rk, 7), (64,), 0, max(1, 64 // 4) + 1, jnp.int32)
        _lenS2 = 64 - jax.random.randint(jax.random.fold_in(_rk, 8), (64,), 0, max(1, 64 // 4) + 1, jnp.int32)
        _ctx_1024P = jax.random.normal(jax.random.fold_in(_rk, 11), (64, 16, 128), jnp.float32)
        _ctx_1024c = jax.random.dirichlet(jax.random.fold_in(_rk, 511), 0.3 * jnp.ones((16,), jnp.float32), (64, 64))
        _ctx_1024t = jnp.einsum('bsk,bkd->bsd', _ctx_1024c, _ctx_1024P)
        _ctx_1024t = _ctx_1024t * jax.lax.rsqrt(jnp.mean(jnp.square(_ctx_1024t)) + 1e-12) * 0.953939
        ctx_1024 = -1.52775e-05 + 0.999936 * (_ctx_1024t + 0.3 * jax.random.normal(jax.random.fold_in(_rk, 611), (64, 64, 128), jnp.float32))
        _validS = jnp.arange(64)[None, :] < _lenS[:, None]
        _validS2 = jnp.arange(64)[None, :] < _lenS2[:, None]
        _causal = jnp.tril(jnp.ones((64, 64), dtype=bool))
        mask_BxS2_ik0 = jnp.where(jnp.broadcast_to(_validS2[:, :], (64, 64)), 0, 1).astype(jnp.int32)
        mask_BxS2_ik1 = jnp.where(jnp.broadcast_to(_validS2[:, :], (64, 64)), 1, 0).astype(jnp.int32)
        return (x, ctx_1024, mask_BxS2_ik0, mask_BxS2_ik1)
    x, ctx_1024, mask_BxS2_ik0, mask_BxS2_ik1 = _rec_inputs()

    def _L0_attn_setup():
        import jax, jax.numpy as jnp
        import numpy as np
        EPS = 1e-12
        key = jax.random.key(seed)
        k1, k2 = jax.random.split(key)
        b, n, d = (4, 512, 128)
        x = jax.random.normal(k1, (b, n, d), dtype=jnp.float32)
        W_qkva = jax.random.normal(k2, (3 * d, d), dtype=jnp.float32) * 0.02
        gamma = jnp.ones((d,), dtype=jnp.float32)
        return {'x': x, 'W_qkva': W_qkva, 'gamma': gamma}
    _L0_attn_all = _L0_attn_setup()
    _L0_attn_in = {k: v for k, v in _L0_attn_all.items() if k in ('W_qkva', 'gamma')}
    del _L0_attn_all

    def _L0_xattn_setup():
        import jax, jax.numpy as jnp
        import numpy as np
        DIM = 128
        H = 16
        D = 64
        INNER = H * D
        EPS = 1e-05

        def layernorm(x, w, b):
            mu = jnp.mean(x, axis=-1, keepdims=True)
            var = jnp.var(x, axis=-1, keepdims=True)
            return (x - mu) * jax.lax.rsqrt(var + EPS) * w + b
        key = jax.random.key(seed)
        ks = jax.random.split(key, 8)
        B, N, S = (4, 32, 1024)
        s = 1.0 / np.sqrt(DIM)
        return {'latents': jax.random.normal(ks[0], (B, N, DIM), jnp.float32), 'context': jax.random.normal(ks[1], (B, S, DIM), jnp.float32), 'ln_l_w': jnp.ones((DIM,), jnp.float32), 'ln_l_b': jnp.zeros((DIM,), jnp.float32), 'ln_c_w': jnp.ones((DIM,), jnp.float32), 'ln_c_b': jnp.zeros((DIM,), jnp.float32), 'Wq': jax.random.normal(ks[2], (DIM, INNER), jnp.float32) * s, 'Wkv': jax.random.normal(ks[3], (DIM, 2 * INNER), jnp.float32) * s, 'Wo': jax.random.normal(ks[4], (INNER, DIM), jnp.float32) * (1.0 / np.sqrt(INNER)), 'bo': jnp.zeros((DIM,), jnp.float32)}
    _L0_xattn_all = _L0_xattn_setup()
    _L0_xattn_in = {k: v for k, v in _L0_xattn_all.items() if k in ('ln_l_w', 'ln_l_b', 'ln_c_w', 'ln_c_b', 'Wq', 'Wkv', 'Wo', 'bo')}
    del _L0_xattn_all

    def _L0_ffn_setup():
        import jax, jax.numpy as jnp
        import numpy as np
        K = 2
        CAP_FACTOR = 1.25
        key = jax.random.key(seed)
        ks = jax.random.split(key, 6)
        B, T, C, H, E = (8, 256, 128, 512, 8)
        return {'x': jax.random.normal(ks[0], (B, T, C), dtype=jnp.float32), 'Wr': jax.random.normal(ks[1], (C, E), dtype=jnp.float32) * 0.02, 'W1': jax.random.normal(ks[2], (E, C, H), dtype=jnp.float32) * 0.02, 'b1': jax.random.normal(ks[3], (E, H), dtype=jnp.float32) * 0.02, 'W2': jax.random.normal(ks[4], (E, H, C), dtype=jnp.float32) * 0.02, 'b2': jax.random.normal(ks[5], (E, C), dtype=jnp.float32) * 0.02}
    _L0_ffn_all = _L0_ffn_setup()
    _L0_ffn_in = {k: v for k, v in _L0_ffn_all.items() if k in ('Wr', 'W1', 'b1', 'W2', 'b2')}
    del _L0_ffn_all

    def _L1_attn_setup():
        import jax, jax.numpy as jnp
        import numpy as np
        from jax import lax
        B, T, H = (4, 128, 128)
        NH, KD, VD = (4, 64, 128)
        DK, DV = (KD // NH, VD // NH)
        R, R5, G = (32, 160, 64)
        EPS = 1e-05

        def _forward(h, x_proj_mu, xl_w1, xl_w2, xl_b2, x_out_w, x_bias, r_w, w_w1, w_w2, w_b, k_w, v_w, g_w, bonus, gn_weight, gn_bias, o_w):
            B_, T_, H_ = h.shape
            shifted = jnp.pad(h, ((0, 0), (1, 0), (0, 0)))[:, :T_]
            delta = shifted - h
            x_lerp = h + delta * x_proj_mu
            x0 = jnp.tanh(x_lerp @ xl_w1.T) @ xl_w2.T + xl_b2
            x1 = jnp.tanh(x0).reshape(B_, T_, 5, R)
            x2 = jnp.einsum('btnr,hnr->btnh', x1, x_out_w.reshape(H_, 5, R))
            mus = x2 + x_bias
            r_mu, w_mu, k_mu, v_mu, g_mu = (mus[:, :, i] for i in range(5))
            r = (h + delta * r_mu) @ r_w.T
            w_in = h + delta * w_mu
            w = jnp.tanh(w_in @ w_w1.T) @ w_w2.T + w_b
            k = (h + delta * k_mu) @ k_w.T
            v = (h + delta * v_mu) @ v_w.T
            g = (h + delta * g_mu) @ g_w.T
            r = r.reshape(B_, T_, NH, DK)
            k = k.reshape(B_, T_, NH, DK)
            v = v.reshape(B_, T_, NH, DV)
            wd = jnp.exp(-jnp.exp(w.reshape(B_, T_, NH, DK)))

            def step(S, xs):
                r_t, k_t, v_t, w_t = xs
                o_t = jnp.einsum('bhk,bhkv->bhv', r_t, S) + jnp.sum(r_t * bonus * k_t, -1, keepdims=True) * v_t
                S = S * w_t[..., None] + k_t[..., None] * v_t[..., None, :]
                return (S, o_t)
            xs = tuple((jnp.swapaxes(a, 0, 1) for a in (r, k, v, wd)))
            S0 = jnp.zeros((B_, NH, DK, DV), jnp.float32)
            _, oT = lax.scan(step, S0, xs)
            o = jnp.swapaxes(oT, 0, 1)
            mean = o.mean(-1, keepdims=True)
            var = o.var(-1, keepdims=True)
            o = ((o - mean) * lax.rsqrt(var + EPS)).reshape(B_, T_, VD)
            o = (o * gn_weight + gn_bias) * jax.nn.silu(g)
            return o @ o_w.T
        key = jax.random.key(seed)
        ks = jax.random.split(key, 20)
        n = lambda k, s, sc=0.02: jax.random.normal(k, s, dtype=jnp.float32) * sc
        return {'hidden_states': jax.random.normal(ks[0], (B, T, H), dtype=jnp.float32), 'x_proj_mu': n(ks[1], (H,), 0.1), 'xl_w1': n(ks[2], (R, H)), 'xl_w2': n(ks[3], (R5, R)), 'xl_b2': jnp.zeros((R5,), jnp.float32), 'x_out_w': n(ks[4], (H, R5)), 'x_bias': n(ks[5], (5, H), 0.1), 'r_w': n(ks[6], (KD, H)), 'w_w1': n(ks[7], (G, H)), 'w_w2': n(ks[8], (KD, G)), 'w_b': n(ks[9], (KD,), 0.1), 'k_w': n(ks[10], (KD, H)), 'v_w': n(ks[11], (VD, H)), 'g_w': n(ks[12], (VD, H)), 'bonus': n(ks[13], (NH, DK), 0.1), 'gn_weight': jnp.ones((VD,), jnp.float32), 'gn_bias': jnp.zeros((VD,), jnp.float32), 'o_w': n(ks[14], (H, VD))}
    _L1_attn_all = _L1_attn_setup()
    _L1_attn_in = {k: v for k, v in _L1_attn_all.items() if k in ('x_proj_mu', 'xl_w1', 'xl_w2', 'xl_b2', 'x_out_w', 'x_bias', 'r_w', 'w_w1', 'w_w2', 'w_b', 'k_w', 'v_w', 'g_w', 'bonus', 'gn_weight', 'gn_bias', 'o_w')}
    del _L1_attn_all

    def _L1_xattn_setup():
        import jax, jax.numpy as jnp
        import numpy as np
        import math
        EPS = 1e-08
        LN_EPS = 1e-05
        B, S, E, NH = (2, 256, 128, 4)
        DH = E // NH

        def _mlstm_cell(q, k, v, igate_w, igate_b, fgate_w, fgate_b, out_w):
            Bq, Sq, Eq = q.shape
            if_in = jnp.concatenate([q, k, v], axis=-1)
            ig = jnp.einsum('bsf,hf->bsh', if_in, igate_w) + igate_b
            fg = jnp.einsum('bsf,hf->bsh', if_in, fgate_w) + fgate_b
            ig = jnp.transpose(ig, (0, 2, 1))[..., None]
            fg = jnp.transpose(fg, (0, 2, 1))[..., None]
            qh = q.reshape(Bq, Sq, NH, DH).transpose(0, 2, 1, 3)
            kh = k.reshape(Bq, Sq, NH, DH).transpose(0, 2, 1, 3)
            vh = v.reshape(Bq, Sq, NH, DH).transpose(0, 2, 1, 3)
            log_fg = jax.nn.log_sigmoid(fg)
            cs = jnp.cumsum(log_fg, axis=2)
            cs_shift = jnp.concatenate([jnp.zeros_like(cs[:, :, :1]), cs[:, :, :-1]], axis=2)
            logfg_mat = cs - jnp.swapaxes(cs_shift, -2, -1)
            ltr = jnp.tril(jnp.ones((Sq, Sq), dtype=bool))
            logfg_mat = jnp.where(ltr, logfg_mat, -jnp.inf)
            log_D = logfg_mat + jnp.swapaxes(ig, -2, -1)
            max_log_D = jnp.max(log_D, axis=-1, keepdims=True)
            D = jnp.exp(log_D - max_log_D)
            qk = jnp.einsum('bhsd,bhtd->bhst', qh, kh / math.sqrt(DH))
            C = qk * D
            sum_C_abs = jnp.abs(jnp.sum(C, axis=-1, keepdims=True))
            normaliser = jnp.maximum(sum_C_abs, jnp.exp(-max_log_D))
            C_norm = C / (normaliser + EPS)
            h = jnp.einsum('bhst,bhtd->bhsd', C_norm, vh)
            mean = jnp.mean(h, axis=-1, keepdims=True)
            var = jnp.mean((h - mean) ** 2, axis=-1, keepdims=True)
            h_norm = (h - mean) / jnp.sqrt(var + LN_EPS)
            scale = (1.0 + out_w).reshape(1, NH, 1, DH)
            h_norm = h_norm * scale
            return h_norm.transpose(0, 2, 1, 3).reshape(Bq, Sq, Eq)
        key = jax.random.key(seed)
        ks = jax.random.split(key, 7)
        std_g = math.sqrt(2.0 / (5.0 * 3 * E))
        return {'q': jax.random.normal(ks[0], (B, S, E), dtype=jnp.float32), 'k': jax.random.normal(ks[1], (B, S, E), dtype=jnp.float32), 'v': jax.random.normal(ks[2], (B, S, E), dtype=jnp.float32), 'igate_w': jax.random.normal(ks[3], (NH, 3 * E), dtype=jnp.float32) * std_g, 'igate_b': jax.random.normal(ks[4], (NH,), dtype=jnp.float32) * 0.1, 'fgate_w': jax.random.normal(ks[5], (NH, 3 * E), dtype=jnp.float32) * std_g, 'fgate_b': jnp.linspace(3.4, 6.0, NH, dtype=jnp.float32), 'out_w': jnp.zeros((E,), dtype=jnp.float32)}
    _L1_xattn_all = _L1_xattn_setup()
    _L1_xattn_in = {k: v for k, v in _L1_xattn_all.items() if k in ('igate_w', 'igate_b', 'fgate_w', 'fgate_b', 'out_w')}
    del _L1_xattn_all

    def _L1_ffn_setup():
        import jax, jax.numpy as jnp
        import numpy as np
        EPS = 1e-05

        @jax.custom_vjp
        def ste_quantize(w):
            scale = jnp.maximum(jnp.mean(jnp.abs(w)), EPS)
            return jnp.clip(jnp.round(w / scale), -1.0, 1.0)

        def _ste_fwd(w):
            return (ste_quantize(w), None)

        def _ste_bwd(_, g):
            return (g,)
        ste_quantize.defvjp(_ste_fwd, _ste_bwd)
        key = jax.random.key(seed)
        k1, k2 = jax.random.split(key)
        x = jax.random.normal(k1, (8, 1024, 128), dtype=jnp.float32)
        weight = jax.random.normal(k2, (128, 128), dtype=jnp.float32) * 0.02
        return {'x': x, 'weight': weight}
    _L1_ffn_all = _L1_ffn_setup()
    _L1_ffn_in = {k: v for k, v in _L1_ffn_all.items() if k in ('weight',)}
    del _L1_ffn_all

    def _L2_attn_setup():
        import jax, jax.numpy as jnp
        import numpy as np
        B, L = (2, 128)
        D_MODEL, D_CKV, D_CQ = (128, 32, 64)
        N_HEAD, D_HEAD, D_ROPE = (8, 64, 32)
        N_IDX_HEAD = 4
        K_TS, LW = (96, 64)
        ROPE_BASE = 10000.0

        def _pope(x, angles):
            cos, sin = (jnp.cos(angles), jnp.sin(angles))
            mu1, mu2 = jnp.split(jax.nn.softplus(x), 2, axis=-1)
            return jnp.concatenate([mu1 * cos - mu2 * sin, mu1 * sin + mu2 * cos], axis=-1)

        def _forward(x, W_dkv, W_uk, W_uv, W_dq, W_uq, W_qr, W_kr, W_out, idx_wq, idx_wk, idx_w, raw_delta):
            B_, L_, _ = x.shape
            c_kv = x @ W_dkv
            q_i = (x @ idx_wq).reshape(B_, L_, N_IDX_HEAD, D_HEAD)
            k_i = x @ idx_wk
            s_i = jax.nn.relu(jnp.einsum('bthd,bsd->bths', q_i, k_i))
            I = jnp.einsum('bths,h->bts', s_i, idx_w)
            qpos = jnp.arange(L_)[:, None]
            kpos = jnp.arange(L_)[None, :]
            local = (kpos >= qpos - LW + 1) & (kpos <= qpos)
            causal = kpos > qpos
            I = jnp.where(local[None], jnp.inf, I)
            I = jnp.where(causal[None], -jnp.inf, I)
            kk = min(K_TS, L_)
            _, idx = jax.lax.top_k(I, kk)
            bi = jnp.arange(B_)[:, None, None]
            key_c = (c_kv @ W_uk)[bi, idx].reshape(B_, L_, kk, N_HEAD, D_HEAD)
            value = (c_kv @ W_uv)[bi, idx].reshape(B_, L_, kk, N_HEAD, D_HEAD)
            c_q = x @ W_dq
            query_c = (c_q @ W_uq).reshape(B_, L_, N_HEAD, D_HEAD)
            half = D_ROPE // 2
            theta = 1.0 / ROPE_BASE ** (2.0 * jnp.arange(half, dtype=jnp.float32) / D_ROPE)
            delta = -2.0 * jnp.pi * jax.nn.sigmoid(raw_delta)
            angles_q = jnp.arange(L_, dtype=jnp.float32)[:, None] * theta[None, :] + delta
            query_r = _pope((c_q @ W_qr).reshape(B_, L_, N_HEAD, D_ROPE), angles_q[None, :, None, :])
            kr_sel = (x @ W_kr)[bi, idx]
            angles_k = jnp.arange(kk, dtype=jnp.float32)[:, None] * theta[None, :] + delta
            key_r = _pope(kr_sel, angles_k[None, None, :, :])
            scale = (D_HEAD + D_ROPE) ** (-0.5)
            q_c = query_c.transpose(0, 2, 1, 3)
            q_r = query_r.transpose(0, 2, 1, 3)
            k_c = key_c.transpose(0, 3, 1, 2, 4)
            v = value.transpose(0, 3, 1, 2, 4)
            scores = (jnp.einsum('bhld,bhlkd->bhlk', q_c, k_c) + jnp.einsum('bhld,blkd->bhlk', q_r, key_r)) * scale
            attn = jax.nn.softmax(scores.astype(jnp.float32), axis=-1).astype(v.dtype)
            out = jnp.einsum('bhlk,bhlkd->bhld', attn, v)
            out = out.transpose(0, 2, 1, 3).reshape(B_, L_, N_HEAD * D_HEAD)
            return out @ W_out
        key = jax.random.key(seed)
        ks = jax.random.split(key, 14)

        def w(k, shape, fan_in):
            return jax.random.normal(k, shape, dtype=jnp.float32) * fan_in ** (-0.5)
        return {'x': jax.random.normal(ks[0], (B, L, D_MODEL), dtype=jnp.float32), 'W_dkv': w(ks[1], (D_MODEL, D_CKV), D_MODEL), 'W_uk': w(ks[2], (D_CKV, N_HEAD * D_HEAD), D_CKV), 'W_uv': w(ks[3], (D_CKV, N_HEAD * D_HEAD), D_CKV), 'W_dq': w(ks[4], (D_MODEL, D_CQ), D_MODEL), 'W_uq': w(ks[5], (D_CQ, N_HEAD * D_HEAD), D_CQ), 'W_qr': w(ks[6], (D_CQ, N_HEAD * D_ROPE), D_CQ), 'W_kr': w(ks[7], (D_MODEL, D_ROPE), D_MODEL), 'W_out': w(ks[8], (N_HEAD * D_HEAD, D_MODEL), N_HEAD * D_HEAD), 'idx_wq': w(ks[9], (D_MODEL, N_IDX_HEAD * D_HEAD), D_MODEL), 'idx_wk': w(ks[10], (D_MODEL, D_HEAD), D_MODEL), 'idx_w': jnp.ones((N_IDX_HEAD,), dtype=jnp.float32), 'raw_delta': jax.random.normal(ks[11], (D_ROPE // 2,), dtype=jnp.float32) * 0.1}
    _L2_attn_all = _L2_attn_setup()
    _L2_attn_in = {k: v for k, v in _L2_attn_all.items() if k in ('W_dkv', 'W_uk', 'W_uv', 'W_dq', 'W_uq', 'W_qr', 'W_kr', 'W_out', 'idx_wq', 'idx_wk', 'idx_w', 'raw_delta')}
    del _L2_attn_all

    def _L2_xattn_setup():
        import jax, jax.numpy as jnp
        import numpy as np
        DIM = 128
        HEADS = 16
        HEAD_DIM = DIM // HEADS
        SCALE = HEAD_DIM ** (-0.5)
        MASK_FILL = -1000000000.0

        def layer_norm(x, gamma, beta, eps=1e-05):
            mu = jnp.mean(x, axis=-1, keepdims=True)
            var = jnp.var(x, axis=-1, keepdims=True)
            return (x - mu) * jax.lax.rsqrt(var + eps) * gamma + beta
        key = jax.random.key(seed)
        ks = jax.random.split(key, 10)
        B, N1, N2, C = (8, 32, 512, DIM)
        s = C ** (-0.5)
        return {'x': jax.random.normal(ks[0], (B, N1, C), jnp.float32), 'kv': jax.random.normal(ks[1], (B, N2, C), jnp.float32), 'padding_mask': jax.random.randint(ks[2], (B, N2), 0, 2, jnp.int32), 'w_q': jax.random.normal(ks[3], (C, C), jnp.float32) * s, 'w_kv': jax.random.normal(ks[4], (C, 2 * C), jnp.float32) * s, 'w_proj': jax.random.normal(ks[5], (C, C), jnp.float32) * s, 'b_proj': jnp.zeros((C,), jnp.float32), 'g_x': jnp.ones((C,), jnp.float32), 'b_x': jnp.zeros((C,), jnp.float32), 'g_kv': jnp.ones((C,), jnp.float32), 'b_kv': jnp.zeros((C,), jnp.float32)}
    _L2_xattn_all = _L2_xattn_setup()
    _L2_xattn_in = {k: v for k, v in _L2_xattn_all.items() if k in ('w_q', 'w_kv', 'w_proj', 'b_proj', 'g_x', 'b_x', 'g_kv', 'b_kv')}
    del _L2_xattn_all

    def _L2_ffn_setup():
        import jax, jax.numpy as jnp
        import numpy as np
        DIM = 128
        HIDDEN = 352
        NUM_EXPERTS = 8
        TOP_K = 2
        BATCH, SEQ = (4, 256)
        key = jax.random.key(seed)
        ks = jax.random.split(key, 5)
        x = jax.random.normal(ks[0], (BATCH, SEQ, DIM), dtype=jnp.float32)
        gate_w = jax.random.normal(ks[1], (NUM_EXPERTS, DIM), dtype=jnp.float32) * 0.02
        w1 = jax.random.normal(ks[2], (NUM_EXPERTS, HIDDEN, DIM), dtype=jnp.float32) * 0.02
        w3 = jax.random.normal(ks[3], (NUM_EXPERTS, HIDDEN, DIM), dtype=jnp.float32) * 0.02
        w2 = jax.random.normal(ks[4], (NUM_EXPERTS, DIM, HIDDEN), dtype=jnp.float32) * 0.02
        return {'x': x, 'gate_w': gate_w, 'w1': w1, 'w3': w3, 'w2': w2}
    _L2_ffn_all = _L2_ffn_setup()
    _L2_ffn_in = {k: v for k, v in _L2_ffn_all.items() if k in ('gate_w', 'w1', 'w3', 'w2')}
    del _L2_ffn_all

    def _L3_attn_setup():
        import jax, jax.numpy as jnp
        import numpy as np
        from math import sqrt
        EMBED_DIM = 128
        NUM_HEADS = 16
        HEAD_DIM = EMBED_DIM // NUM_HEADS
        SCALE = sqrt(HEAD_DIM)

        def _rotate_half(x):
            x1 = x[..., 0::2]
            x2 = x[..., 1::2]
            return jnp.stack((-x2, x1), axis=-1).reshape(x.shape)

        def _apply_rope(x, seq_len):
            inv_freq = 1.0 / 10000.0 ** (jnp.arange(0, HEAD_DIM, 2, dtype=jnp.float32) / HEAD_DIM)
            pos = jnp.arange(seq_len, dtype=jnp.float32)
            freqs = jnp.outer(pos, inv_freq)
            emb = jnp.concatenate([freqs, freqs], -1)
            cos = jnp.cos(emb)[None, None].astype(x.dtype)
            sin = jnp.sin(emb)[None, None].astype(x.dtype)
            return x * cos + _rotate_half(x) * sin
        key = jax.random.key(seed)
        ks = jax.random.split(key, 9)
        B, S, E = (2, 256, EMBED_DIM)
        s = 1.0 / np.sqrt(E)
        return {'x': jax.random.normal(ks[0], (B, S, E), jnp.float32), 'Wq': jax.random.uniform(ks[1], (E, E), jnp.float32, -s, s), 'bq': jnp.zeros((E,), jnp.float32), 'Wk': jax.random.uniform(ks[2], (E, E), jnp.float32, -s, s), 'bk': jnp.zeros((E,), jnp.float32), 'Wv': jax.random.uniform(ks[3], (E, E), jnp.float32, -s, s), 'bv': jnp.zeros((E,), jnp.float32), 'Wo': jax.random.uniform(ks[4], (E, E), jnp.float32, -s, s), 'bo': jnp.zeros((E,), jnp.float32)}
    _L3_attn_all = _L3_attn_setup()
    _L3_attn_in = {k: v for k, v in _L3_attn_all.items() if k in ('Wq', 'bq', 'Wk', 'bk', 'Wv', 'bv', 'Wo', 'bo')}
    del _L3_attn_all

    def _L3_xattn_setup():
        import jax, jax.numpy as jnp
        import numpy as np
        B, S, D = (8, 256, 128)
        key = jax.random.key(seed)
        ks = jax.random.split(key, 10)
        scale = 1.0 / np.sqrt(D)
        return {'query': jax.random.normal(ks[0], (B, S, D), jnp.float32), 'key': jax.random.normal(ks[1], (B, S, D), jnp.float32), 'value': jax.random.normal(ks[2], (B, S, D), jnp.float32), 'mask': jax.random.randint(ks[3], (B, S), 0, 2, jnp.int32), 'Wq': jax.random.uniform(ks[4], (D, D), jnp.float32, -scale, scale), 'bq': jax.random.uniform(ks[5], (D,), jnp.float32, -scale, scale), 'Wk': jax.random.uniform(ks[6], (D, D), jnp.float32, -scale, scale), 'bk': jax.random.uniform(ks[7], (D,), jnp.float32, -scale, scale), 'Wv': jax.random.uniform(ks[8], (D, D), jnp.float32, -scale, scale), 'bv': jax.random.uniform(ks[9], (D,), jnp.float32, -scale, scale)}
    _L3_xattn_all = _L3_xattn_setup()
    _L3_xattn_in = {k: v for k, v in _L3_xattn_all.items() if k in ('Wq', 'bq', 'Wk', 'bk', 'Wv', 'bv')}
    del _L3_xattn_all

    def _L3_ffn_setup():
        import jax, jax.numpy as jnp
        import numpy as np
        IN_F = 128
        OUT_F = 128
        N_EXPERTS = 8
        TOP_K = 2
        key = jax.random.key(seed)
        ks = jax.random.split(key, 5)
        scale_in = 1.0 / np.sqrt(IN_F)
        x = jax.random.normal(ks[0], (4, 256, IN_F), dtype=jnp.float32)
        W_experts = jax.random.uniform(ks[1], (N_EXPERTS, OUT_F, IN_F), jnp.float32, -scale_in, scale_in)
        b_experts = jax.random.uniform(ks[2], (N_EXPERTS, OUT_F), jnp.float32, -scale_in, scale_in)
        W_router = jax.random.uniform(ks[3], (N_EXPERTS, IN_F), jnp.float32, -scale_in, scale_in)
        b_router = jax.random.uniform(ks[4], (N_EXPERTS,), jnp.float32, -scale_in, scale_in)
        return {'x': x, 'W_experts': W_experts, 'b_experts': b_experts, 'W_router': W_router, 'b_router': b_router}
    _L3_ffn_all = _L3_ffn_setup()
    _L3_ffn_in = {k: v for k, v in _L3_ffn_all.items() if k in ('W_experts', 'b_experts', 'W_router', 'b_router')}
    del _L3_ffn_all
    return {'x': x, 'ctx_1024': ctx_1024, 'mask_BxS2_ik0': mask_BxS2_ik0, 'mask_BxS2_ik1': mask_BxS2_ik1, 'L0_attn_W_qkva': _L0_attn_in['W_qkva'], 'L0_attn_gamma': _L0_attn_in['gamma'], 'L0_xattn_ln_l_w': _L0_xattn_in['ln_l_w'], 'L0_xattn_ln_l_b': _L0_xattn_in['ln_l_b'], 'L0_xattn_ln_c_w': _L0_xattn_in['ln_c_w'], 'L0_xattn_ln_c_b': _L0_xattn_in['ln_c_b'], 'L0_xattn_Wq': _L0_xattn_in['Wq'], 'L0_xattn_Wkv': _L0_xattn_in['Wkv'], 'L0_xattn_Wo': _L0_xattn_in['Wo'], 'L0_xattn_bo': _L0_xattn_in['bo'], 'L0_ffn_Wr': _L0_ffn_in['Wr'], 'L0_ffn_W1': _L0_ffn_in['W1'], 'L0_ffn_b1': _L0_ffn_in['b1'], 'L0_ffn_W2': _L0_ffn_in['W2'], 'L0_ffn_b2': _L0_ffn_in['b2'], 'L1_attn_x_proj_mu': _L1_attn_in['x_proj_mu'], 'L1_attn_xl_w1': _L1_attn_in['xl_w1'], 'L1_attn_xl_w2': _L1_attn_in['xl_w2'], 'L1_attn_xl_b2': _L1_attn_in['xl_b2'], 'L1_attn_x_out_w': _L1_attn_in['x_out_w'], 'L1_attn_x_bias': _L1_attn_in['x_bias'], 'L1_attn_r_w': _L1_attn_in['r_w'], 'L1_attn_w_w1': _L1_attn_in['w_w1'], 'L1_attn_w_w2': _L1_attn_in['w_w2'], 'L1_attn_w_b': _L1_attn_in['w_b'], 'L1_attn_k_w': _L1_attn_in['k_w'], 'L1_attn_v_w': _L1_attn_in['v_w'], 'L1_attn_g_w': _L1_attn_in['g_w'], 'L1_attn_bonus': _L1_attn_in['bonus'], 'L1_attn_gn_weight': _L1_attn_in['gn_weight'], 'L1_attn_gn_bias': _L1_attn_in['gn_bias'], 'L1_attn_o_w': _L1_attn_in['o_w'], 'L1_xattn_igate_w': _L1_xattn_in['igate_w'], 'L1_xattn_igate_b': _L1_xattn_in['igate_b'], 'L1_xattn_fgate_w': _L1_xattn_in['fgate_w'], 'L1_xattn_fgate_b': _L1_xattn_in['fgate_b'], 'L1_xattn_out_w': _L1_xattn_in['out_w'], 'L1_ffn_weight': _L1_ffn_in['weight'], 'L2_attn_W_dkv': _L2_attn_in['W_dkv'], 'L2_attn_W_uk': _L2_attn_in['W_uk'], 'L2_attn_W_uv': _L2_attn_in['W_uv'], 'L2_attn_W_dq': _L2_attn_in['W_dq'], 'L2_attn_W_uq': _L2_attn_in['W_uq'], 'L2_attn_W_qr': _L2_attn_in['W_qr'], 'L2_attn_W_kr': _L2_attn_in['W_kr'], 'L2_attn_W_out': _L2_attn_in['W_out'], 'L2_attn_idx_wq': _L2_attn_in['idx_wq'], 'L2_attn_idx_wk': _L2_attn_in['idx_wk'], 'L2_attn_idx_w': _L2_attn_in['idx_w'], 'L2_attn_raw_delta': _L2_attn_in['raw_delta'], 'L2_xattn_w_q': _L2_xattn_in['w_q'], 'L2_xattn_w_kv': _L2_xattn_in['w_kv'], 'L2_xattn_w_proj': _L2_xattn_in['w_proj'], 'L2_xattn_b_proj': _L2_xattn_in['b_proj'], 'L2_xattn_g_x': _L2_xattn_in['g_x'], 'L2_xattn_b_x': _L2_xattn_in['b_x'], 'L2_xattn_g_kv': _L2_xattn_in['g_kv'], 'L2_xattn_b_kv': _L2_xattn_in['b_kv'], 'L2_ffn_gate_w': _L2_ffn_in['gate_w'], 'L2_ffn_w1': _L2_ffn_in['w1'], 'L2_ffn_w3': _L2_ffn_in['w3'], 'L2_ffn_w2': _L2_ffn_in['w2'], 'L3_attn_Wq': _L3_attn_in['Wq'], 'L3_attn_bq': _L3_attn_in['bq'], 'L3_attn_Wk': _L3_attn_in['Wk'], 'L3_attn_bk': _L3_attn_in['bk'], 'L3_attn_Wv': _L3_attn_in['Wv'], 'L3_attn_bv': _L3_attn_in['bv'], 'L3_attn_Wo': _L3_attn_in['Wo'], 'L3_attn_bo': _L3_attn_in['bo'], 'L3_xattn_Wq': _L3_xattn_in['Wq'], 'L3_xattn_bq': _L3_xattn_in['bq'], 'L3_xattn_Wk': _L3_xattn_in['Wk'], 'L3_xattn_bk': _L3_xattn_in['bk'], 'L3_xattn_Wv': _L3_xattn_in['Wv'], 'L3_xattn_bv': _L3_xattn_in['bv'], 'L3_ffn_W_experts': _L3_ffn_in['W_experts'], 'L3_ffn_b_experts': _L3_ffn_in['b_experts'], 'L3_ffn_W_router': _L3_ffn_in['W_router'], 'L3_ffn_b_router': _L3_ffn_in['b_router']}

def reference(x, ctx_1024, mask_BxS2_ik0, mask_BxS2_ik1, L0_attn_W_qkva, L0_attn_gamma, L0_xattn_ln_l_w, L0_xattn_ln_l_b, L0_xattn_ln_c_w, L0_xattn_ln_c_b, L0_xattn_Wq, L0_xattn_Wkv, L0_xattn_Wo, L0_xattn_bo, L0_ffn_Wr, L0_ffn_W1, L0_ffn_b1, L0_ffn_W2, L0_ffn_b2, L1_attn_x_proj_mu, L1_attn_xl_w1, L1_attn_xl_w2, L1_attn_xl_b2, L1_attn_x_out_w, L1_attn_x_bias, L1_attn_r_w, L1_attn_w_w1, L1_attn_w_w2, L1_attn_w_b, L1_attn_k_w, L1_attn_v_w, L1_attn_g_w, L1_attn_bonus, L1_attn_gn_weight, L1_attn_gn_bias, L1_attn_o_w, L1_xattn_igate_w, L1_xattn_igate_b, L1_xattn_fgate_w, L1_xattn_fgate_b, L1_xattn_out_w, L1_ffn_weight, L2_attn_W_dkv, L2_attn_W_uk, L2_attn_W_uv, L2_attn_W_dq, L2_attn_W_uq, L2_attn_W_qr, L2_attn_W_kr, L2_attn_W_out, L2_attn_idx_wq, L2_attn_idx_wk, L2_attn_idx_w, L2_attn_raw_delta, L2_xattn_w_q, L2_xattn_w_kv, L2_xattn_w_proj, L2_xattn_b_proj, L2_xattn_g_x, L2_xattn_b_x, L2_xattn_g_kv, L2_xattn_b_kv, L2_ffn_gate_w, L2_ffn_w1, L2_ffn_w3, L2_ffn_w2, L3_attn_Wq, L3_attn_bq, L3_attn_Wk, L3_attn_bk, L3_attn_Wv, L3_attn_bv, L3_attn_Wo, L3_attn_bo, L3_xattn_Wq, L3_xattn_bq, L3_xattn_Wk, L3_xattn_bk, L3_xattn_Wv, L3_xattn_bv, L3_ffn_W_experts, L3_ffn_b_experts, L3_ffn_W_router, L3_ffn_b_router):
    import jax
    import jax.numpy as jnp

    def _L0_attn_ref(x, W_qkva, gamma):
        import jax, jax.numpy as jnp
        import numpy as np
        EPS = 1e-12
        d = gamma.shape[0]
        scale = d ** 0.5
        norm = jnp.maximum(jnp.linalg.norm(x, axis=-1, keepdims=True), EPS)
        xn = x / norm * scale * gamma
        h = jnp.einsum('bnd,ed->bne', xn, W_qkva)
        q, kv, a = jnp.split(h, 3, axis=-1)
        a = jax.nn.sigmoid(a)

        def binop(e_i, e_j):
            a_i, kv_i = e_i
            a_j, kv_j = e_j
            return (a_j * a_i, a_j * kv_i + kv_j)
        _, y = jax.lax.associative_scan(binop, (a, kv), axis=1)
        return q * y

    def _L0_xattn_ref(latents, context, ln_l_w, ln_l_b, ln_c_w, ln_c_b, Wq, Wkv, Wo, bo):
        import jax, jax.numpy as jnp
        import numpy as np
        DIM = 128
        H = 16
        D = 64
        INNER = H * D
        EPS = 1e-05

        def layernorm(x, w, b):
            mu = jnp.mean(x, axis=-1, keepdims=True)
            var = jnp.var(x, axis=-1, keepdims=True)
            return (x - mu) * jax.lax.rsqrt(var + EPS) * w + b
        b, n, _ = latents.shape
        s = context.shape[1]
        lat = layernorm(latents, ln_l_w, ln_l_b)
        ctx = layernorm(context, ln_c_w, ln_c_b)
        q = (lat @ Wq).reshape(b, n, H, D).transpose(0, 2, 1, 3)
        kv = ctx @ Wkv
        k, v = jnp.split(kv, 2, axis=-1)
        k = k.reshape(b, s, H, D).transpose(0, 2, 1, 3)
        v = v.reshape(b, s, H, D).transpose(0, 2, 1, 3)
        scale = D ** (-0.5)
        attn = jnp.einsum('bhnd,bhsd->bhns', q, k) * scale
        attn = jnp.clip(attn, -11.0, 11.0)
        attn = jax.nn.softmax(attn, axis=-1)
        out = jnp.einsum('bhns,bhsd->bhnd', attn, v)
        out = out.transpose(0, 2, 1, 3).reshape(b, n, INNER)
        return out @ Wo + bo

    def _L0_ffn_ref(x, Wr, W1, b1, W2, b2):
        import jax, jax.numpy as jnp
        import numpy as np
        K = 2
        CAP_FACTOR = 1.25
        B, T, C = x.shape
        E = Wr.shape[1]
        capacity = int(T / E * CAP_FACTOR)
        probs = jax.nn.softmax(x @ Wr, axis=-1)
        topk_probs, topk_experts = jax.lax.top_k(probs, K)
        S = T * K
        e_flat = topk_experts.reshape(B, S)
        p_flat = topk_probs.reshape(B, S)
        x_rep = jnp.repeat(x, K, axis=1)
        onehot = jax.nn.one_hot(e_flat, E, dtype=jnp.int32)
        pos_all = jnp.cumsum(onehot, axis=1) - onehot
        pos = jnp.take_along_axis(pos_all, e_flat[..., None], axis=-1)[..., 0]
        keep = pos < capacity
        pos_c = jnp.minimum(pos, capacity - 1)
        b_idx = jnp.broadcast_to(jnp.arange(B)[:, None], (B, S))
        buf = jnp.zeros((E, B, capacity, C), dtype=x.dtype)
        buf = buf.at[e_flat, b_idx, pos_c].add(x_rep * keep[..., None].astype(x.dtype))
        h = jax.nn.relu(jnp.einsum('ebnc,ech->ebnh', buf, W1) + b1[:, None, None, :])
        y = jnp.einsum('ebnh,ehc->ebnc', h, W2) + b2[:, None, None, :]
        y_tok = y[e_flat, b_idx, pos_c]
        y_tok = y_tok * keep[..., None].astype(x.dtype) * p_flat[..., None]
        out = y_tok.reshape(B, T, K, C).sum(axis=2)
        return out

    def _L1_attn_ref(hidden_states, x_proj_mu, xl_w1, xl_w2, xl_b2, x_out_w, x_bias, r_w, w_w1, w_w2, w_b, k_w, v_w, g_w, bonus, gn_weight, gn_bias, o_w):
        import jax, jax.numpy as jnp
        import numpy as np
        from jax import lax
        B, T, H = (4, 128, 128)
        NH, KD, VD = (4, 64, 128)
        DK, DV = (KD // NH, VD // NH)
        R, R5, G = (32, 160, 64)
        EPS = 1e-05

        def _forward(h, x_proj_mu, xl_w1, xl_w2, xl_b2, x_out_w, x_bias, r_w, w_w1, w_w2, w_b, k_w, v_w, g_w, bonus, gn_weight, gn_bias, o_w):
            B_, T_, H_ = h.shape
            shifted = jnp.pad(h, ((0, 0), (1, 0), (0, 0)))[:, :T_]
            delta = shifted - h
            x_lerp = h + delta * x_proj_mu
            x0 = jnp.tanh(x_lerp @ xl_w1.T) @ xl_w2.T + xl_b2
            x1 = jnp.tanh(x0).reshape(B_, T_, 5, R)
            x2 = jnp.einsum('btnr,hnr->btnh', x1, x_out_w.reshape(H_, 5, R))
            mus = x2 + x_bias
            r_mu, w_mu, k_mu, v_mu, g_mu = (mus[:, :, i] for i in range(5))
            r = (h + delta * r_mu) @ r_w.T
            w_in = h + delta * w_mu
            w = jnp.tanh(w_in @ w_w1.T) @ w_w2.T + w_b
            k = (h + delta * k_mu) @ k_w.T
            v = (h + delta * v_mu) @ v_w.T
            g = (h + delta * g_mu) @ g_w.T
            r = r.reshape(B_, T_, NH, DK)
            k = k.reshape(B_, T_, NH, DK)
            v = v.reshape(B_, T_, NH, DV)
            wd = jnp.exp(-jnp.exp(w.reshape(B_, T_, NH, DK)))

            def step(S, xs):
                r_t, k_t, v_t, w_t = xs
                o_t = jnp.einsum('bhk,bhkv->bhv', r_t, S) + jnp.sum(r_t * bonus * k_t, -1, keepdims=True) * v_t
                S = S * w_t[..., None] + k_t[..., None] * v_t[..., None, :]
                return (S, o_t)
            xs = tuple((jnp.swapaxes(a, 0, 1) for a in (r, k, v, wd)))
            S0 = jnp.zeros((B_, NH, DK, DV), jnp.float32)
            _, oT = lax.scan(step, S0, xs)
            o = jnp.swapaxes(oT, 0, 1)
            mean = o.mean(-1, keepdims=True)
            var = o.var(-1, keepdims=True)
            o = ((o - mean) * lax.rsqrt(var + EPS)).reshape(B_, T_, VD)
            o = (o * gn_weight + gn_bias) * jax.nn.silu(g)
            return o @ o_w.T
        return _forward(hidden_states, x_proj_mu, xl_w1, xl_w2, xl_b2, x_out_w, x_bias, r_w, w_w1, w_w2, w_b, k_w, v_w, g_w, bonus, gn_weight, gn_bias, o_w)

    def _L1_xattn_ref(q, k, v, igate_w, igate_b, fgate_w, fgate_b, out_w):
        import jax, jax.numpy as jnp
        import numpy as np
        import math
        EPS = 1e-08
        LN_EPS = 1e-05
        B, S, E, NH = (2, 256, 128, 4)
        DH = E // NH

        def _mlstm_cell(q, k, v, igate_w, igate_b, fgate_w, fgate_b, out_w):
            Bq, Sq, Eq = q.shape
            if_in = jnp.concatenate([q, k, v], axis=-1)
            ig = jnp.einsum('bsf,hf->bsh', if_in, igate_w) + igate_b
            fg = jnp.einsum('bsf,hf->bsh', if_in, fgate_w) + fgate_b
            ig = jnp.transpose(ig, (0, 2, 1))[..., None]
            fg = jnp.transpose(fg, (0, 2, 1))[..., None]
            qh = q.reshape(Bq, Sq, NH, DH).transpose(0, 2, 1, 3)
            kh = k.reshape(Bq, Sq, NH, DH).transpose(0, 2, 1, 3)
            vh = v.reshape(Bq, Sq, NH, DH).transpose(0, 2, 1, 3)
            log_fg = jax.nn.log_sigmoid(fg)
            cs = jnp.cumsum(log_fg, axis=2)
            cs_shift = jnp.concatenate([jnp.zeros_like(cs[:, :, :1]), cs[:, :, :-1]], axis=2)
            logfg_mat = cs - jnp.swapaxes(cs_shift, -2, -1)
            ltr = jnp.tril(jnp.ones((Sq, Sq), dtype=bool))
            logfg_mat = jnp.where(ltr, logfg_mat, -jnp.inf)
            log_D = logfg_mat + jnp.swapaxes(ig, -2, -1)
            max_log_D = jnp.max(log_D, axis=-1, keepdims=True)
            D = jnp.exp(log_D - max_log_D)
            qk = jnp.einsum('bhsd,bhtd->bhst', qh, kh / math.sqrt(DH))
            C = qk * D
            sum_C_abs = jnp.abs(jnp.sum(C, axis=-1, keepdims=True))
            normaliser = jnp.maximum(sum_C_abs, jnp.exp(-max_log_D))
            C_norm = C / (normaliser + EPS)
            h = jnp.einsum('bhst,bhtd->bhsd', C_norm, vh)
            mean = jnp.mean(h, axis=-1, keepdims=True)
            var = jnp.mean((h - mean) ** 2, axis=-1, keepdims=True)
            h_norm = (h - mean) / jnp.sqrt(var + LN_EPS)
            scale = (1.0 + out_w).reshape(1, NH, 1, DH)
            h_norm = h_norm * scale
            return h_norm.transpose(0, 2, 1, 3).reshape(Bq, Sq, Eq)
        return _mlstm_cell(q, k, v, igate_w, igate_b, fgate_w, fgate_b, out_w)

    def _L1_ffn_ref(x, weight):
        import jax, jax.numpy as jnp
        import numpy as np
        EPS = 1e-05

        @jax.custom_vjp
        def ste_quantize(w):
            scale = jnp.maximum(jnp.mean(jnp.abs(w)), EPS)
            return jnp.clip(jnp.round(w / scale), -1.0, 1.0)

        def _ste_fwd(w):
            return (ste_quantize(w), None)

        def _ste_bwd(_, g):
            return (g,)
        ste_quantize.defvjp(_ste_fwd, _ste_bwd)
        w_ternary = ste_quantize(weight)
        scale = jnp.maximum(jnp.mean(jnp.abs(weight)), EPS)
        return jnp.einsum('bsi,oi->bso', x, w_ternary * scale)

    def _L2_attn_ref(x, W_dkv, W_uk, W_uv, W_dq, W_uq, W_qr, W_kr, W_out, idx_wq, idx_wk, idx_w, raw_delta):
        import jax, jax.numpy as jnp
        import numpy as np
        B, L = (2, 128)
        D_MODEL, D_CKV, D_CQ = (128, 32, 64)
        N_HEAD, D_HEAD, D_ROPE = (8, 64, 32)
        N_IDX_HEAD = 4
        K_TS, LW = (96, 64)
        ROPE_BASE = 10000.0

        def _pope(x, angles):
            cos, sin = (jnp.cos(angles), jnp.sin(angles))
            mu1, mu2 = jnp.split(jax.nn.softplus(x), 2, axis=-1)
            return jnp.concatenate([mu1 * cos - mu2 * sin, mu1 * sin + mu2 * cos], axis=-1)

        def _forward(x, W_dkv, W_uk, W_uv, W_dq, W_uq, W_qr, W_kr, W_out, idx_wq, idx_wk, idx_w, raw_delta):
            B_, L_, _ = x.shape
            c_kv = x @ W_dkv
            q_i = (x @ idx_wq).reshape(B_, L_, N_IDX_HEAD, D_HEAD)
            k_i = x @ idx_wk
            s_i = jax.nn.relu(jnp.einsum('bthd,bsd->bths', q_i, k_i))
            I = jnp.einsum('bths,h->bts', s_i, idx_w)
            qpos = jnp.arange(L_)[:, None]
            kpos = jnp.arange(L_)[None, :]
            local = (kpos >= qpos - LW + 1) & (kpos <= qpos)
            causal = kpos > qpos
            I = jnp.where(local[None], jnp.inf, I)
            I = jnp.where(causal[None], -jnp.inf, I)
            kk = min(K_TS, L_)
            _, idx = jax.lax.top_k(I, kk)
            bi = jnp.arange(B_)[:, None, None]
            key_c = (c_kv @ W_uk)[bi, idx].reshape(B_, L_, kk, N_HEAD, D_HEAD)
            value = (c_kv @ W_uv)[bi, idx].reshape(B_, L_, kk, N_HEAD, D_HEAD)
            c_q = x @ W_dq
            query_c = (c_q @ W_uq).reshape(B_, L_, N_HEAD, D_HEAD)
            half = D_ROPE // 2
            theta = 1.0 / ROPE_BASE ** (2.0 * jnp.arange(half, dtype=jnp.float32) / D_ROPE)
            delta = -2.0 * jnp.pi * jax.nn.sigmoid(raw_delta)
            angles_q = jnp.arange(L_, dtype=jnp.float32)[:, None] * theta[None, :] + delta
            query_r = _pope((c_q @ W_qr).reshape(B_, L_, N_HEAD, D_ROPE), angles_q[None, :, None, :])
            kr_sel = (x @ W_kr)[bi, idx]
            angles_k = jnp.arange(kk, dtype=jnp.float32)[:, None] * theta[None, :] + delta
            key_r = _pope(kr_sel, angles_k[None, None, :, :])
            scale = (D_HEAD + D_ROPE) ** (-0.5)
            q_c = query_c.transpose(0, 2, 1, 3)
            q_r = query_r.transpose(0, 2, 1, 3)
            k_c = key_c.transpose(0, 3, 1, 2, 4)
            v = value.transpose(0, 3, 1, 2, 4)
            scores = (jnp.einsum('bhld,bhlkd->bhlk', q_c, k_c) + jnp.einsum('bhld,blkd->bhlk', q_r, key_r)) * scale
            attn = jax.nn.softmax(scores.astype(jnp.float32), axis=-1).astype(v.dtype)
            out = jnp.einsum('bhlk,bhlkd->bhld', attn, v)
            out = out.transpose(0, 2, 1, 3).reshape(B_, L_, N_HEAD * D_HEAD)
            return out @ W_out
        return _forward(x, W_dkv, W_uk, W_uv, W_dq, W_uq, W_qr, W_kr, W_out, idx_wq, idx_wk, idx_w, raw_delta)

    def _L2_xattn_ref(x, kv, padding_mask, w_q, w_kv, w_proj, b_proj, g_x, b_x, g_kv, b_kv):
        import jax, jax.numpy as jnp
        import numpy as np
        DIM = 128
        HEADS = 16
        HEAD_DIM = DIM // HEADS
        SCALE = HEAD_DIM ** (-0.5)
        MASK_FILL = -1000000000.0

        def layer_norm(x, gamma, beta, eps=1e-05):
            mu = jnp.mean(x, axis=-1, keepdims=True)
            var = jnp.var(x, axis=-1, keepdims=True)
            return (x - mu) * jax.lax.rsqrt(var + eps) * gamma + beta
        B, N1, C = x.shape
        N2 = kv.shape[1]
        xn = layer_norm(x, g_x, b_x)
        kvn = layer_norm(kv, g_kv, b_kv)
        q = (xn @ w_q).reshape(B, N1, HEADS, HEAD_DIM).transpose(0, 2, 1, 3)
        kv_proj = (kvn @ w_kv).reshape(B, N2, 2, HEADS, HEAD_DIM).transpose(2, 0, 3, 1, 4)
        k, v = (kv_proj[0], kv_proj[1])
        attn = jnp.einsum('bhqd,bhkd->bhqk', q, k) * SCALE
        mask = padding_mask[:, None, None, :]
        attn = jnp.where(mask == 0, MASK_FILL, attn)
        attn = jax.nn.softmax(attn, axis=-1)
        out = jnp.einsum('bhqk,bhkd->bhqd', attn, v)
        out = out.transpose(0, 2, 1, 3).reshape(B, N1, C)
        return out @ w_proj + b_proj

    def _L2_ffn_ref(x, gate_w, w1, w3, w2):
        import jax, jax.numpy as jnp
        import numpy as np
        DIM = 128
        HIDDEN = 352
        NUM_EXPERTS = 8
        TOP_K = 2
        BATCH, SEQ = (4, 256)
        orig_shape = x.shape
        xf = x.reshape(-1, x.shape[-1])
        T = xf.shape[0]
        E, K = (gate_w.shape[0], TOP_K)
        scores = jax.nn.softmax(xf @ gate_w.T, axis=-1)
        expert_weights, expert_indices = jax.lax.top_k(scores, K)
        expert_weights = expert_weights / jnp.sum(expert_weights, axis=-1, keepdims=True)
        x_rep = jnp.repeat(xf, K, axis=0)
        flat_idx = expert_indices.reshape(-1)
        y = jnp.zeros_like(x_rep)
        for e in range(E):
            m = (flat_idx == e)[:, None]
            xe = jnp.where(m, x_rep, 0.0)
            h = jax.nn.silu(xe @ w1[e].T) * (xe @ w3[e].T)
            out = h @ w2[e].T
            y = y + jnp.where(m, out, 0.0)
        y = jnp.sum(y.reshape(T, K, -1) * expert_weights[..., None], axis=1)
        return y.reshape(orig_shape)

    def _L3_attn_ref(x, Wq, bq, Wk, bk, Wv, bv, Wo, bo):
        import jax, jax.numpy as jnp
        import numpy as np
        from math import sqrt
        EMBED_DIM = 128
        NUM_HEADS = 16
        HEAD_DIM = EMBED_DIM // NUM_HEADS
        SCALE = sqrt(HEAD_DIM)

        def _rotate_half(x):
            x1 = x[..., 0::2]
            x2 = x[..., 1::2]
            return jnp.stack((-x2, x1), axis=-1).reshape(x.shape)

        def _apply_rope(x, seq_len):
            inv_freq = 1.0 / 10000.0 ** (jnp.arange(0, HEAD_DIM, 2, dtype=jnp.float32) / HEAD_DIM)
            pos = jnp.arange(seq_len, dtype=jnp.float32)
            freqs = jnp.outer(pos, inv_freq)
            emb = jnp.concatenate([freqs, freqs], -1)
            cos = jnp.cos(emb)[None, None].astype(x.dtype)
            sin = jnp.sin(emb)[None, None].astype(x.dtype)
            return x * cos + _rotate_half(x) * sin
        B, S, E = x.shape
        H, D = (NUM_HEADS, HEAD_DIM)
        q = (x @ Wq.T + bq).reshape(B, S, H, D).transpose(0, 2, 1, 3)
        k = (x @ Wk.T + bk).reshape(B, S, H, D).transpose(0, 2, 1, 3)
        v = (x @ Wv.T + bv).reshape(B, S, H, D).transpose(0, 2, 1, 3)
        q = _apply_rope(q, S)
        k = _apply_rope(k, S)
        attn = jnp.einsum('bhqd,bhkd->bhqk', q, k) / SCALE
        attn = jax.nn.softmax(attn, axis=-1)
        out = jnp.einsum('bhqk,bhkd->bhqd', attn, v)
        out = out.transpose(0, 2, 1, 3).reshape(B, S, E)
        return out @ Wo.T + bo

    def _L3_xattn_ref(query, key, value, mask, Wq, bq, Wk, bk, Wv, bv):
        import jax, jax.numpy as jnp
        import numpy as np
        B, S, D = (8, 256, 128)
        Q = jnp.einsum('bsd,od->bso', query, Wq) + bq
        K = jnp.einsum('bsd,od->bso', key, Wk) + bk
        V = jnp.einsum('bsd,od->bso', value, Wv) + bv
        d_k = K.shape[-1]
        scores = jnp.einsum('bqd,bkd->bqk', Q, K) / jnp.sqrt(jnp.float32(d_k))
        m = (mask != 0)[:, None, :]
        scores = jnp.where(m, scores, -jnp.inf)
        weights = jax.nn.softmax(scores, axis=-1)
        out = jnp.einsum('bqk,bkv->bqv', weights, V)
        return out

    def _L3_ffn_ref(x, W_experts, b_experts, W_router, b_router):
        import jax, jax.numpy as jnp
        import numpy as np
        IN_F = 128
        OUT_F = 128
        N_EXPERTS = 8
        TOP_K = 2
        router_logits = jnp.einsum('bsd,ed->bse', x, W_router) + b_router
        router_weights = jax.nn.softmax(router_logits, axis=-1)
        if TOP_K < N_EXPERTS:
            topk_w, topk_idx = jax.lax.top_k(router_weights, TOP_K)
            sparse = jnp.zeros_like(router_weights)
            router_weights = jnp.take_along_axis(sparse, topk_idx, axis=-1)
            router_weights = sparse.at[..., :].set(0.0)
            b_idx = jnp.arange(sparse.shape[0])[:, None, None]
            s_idx = jnp.arange(sparse.shape[1])[None, :, None]
            router_weights = sparse.at[b_idx, s_idx, topk_idx].set(topk_w)
        expert_out = jnp.einsum('bsd,eod->bseo', x, W_experts) + b_experts
        return jnp.einsum('bseo,bse->bso', expert_out, router_weights)
    x = x + _L0_attn_ref(_layernorm(x, axis=-1), L0_attn_W_qkva, L0_attn_gamma)
    x = x + _L0_xattn_ref(_layernorm(x, axis=-1), ctx_1024, L0_xattn_ln_l_w, L0_xattn_ln_l_b, L0_xattn_ln_c_w, L0_xattn_ln_c_b, L0_xattn_Wq, L0_xattn_Wkv, L0_xattn_Wo, L0_xattn_bo)
    x = x + _L0_ffn_ref(_layernorm(x, axis=-1), L0_ffn_Wr, L0_ffn_W1, L0_ffn_b1, L0_ffn_W2, L0_ffn_b2)
    x = x + _L1_attn_ref(_layernorm(x, axis=-1), L1_attn_x_proj_mu, L1_attn_xl_w1, L1_attn_xl_w2, L1_attn_xl_b2, L1_attn_x_out_w, L1_attn_x_bias, L1_attn_r_w, L1_attn_w_w1, L1_attn_w_w2, L1_attn_w_b, L1_attn_k_w, L1_attn_v_w, L1_attn_g_w, L1_attn_bonus, L1_attn_gn_weight, L1_attn_gn_bias, L1_attn_o_w)
    x = x + _L1_xattn_ref(_layernorm(x, axis=-1), ctx_1024, ctx_1024, L1_xattn_igate_w, L1_xattn_igate_b, L1_xattn_fgate_w, L1_xattn_fgate_b, L1_xattn_out_w)
    x = x + _L1_ffn_ref(_layernorm(x, axis=-1), L1_ffn_weight)
    x = x + _L2_attn_ref(_layernorm(x, axis=-1), L2_attn_W_dkv, L2_attn_W_uk, L2_attn_W_uv, L2_attn_W_dq, L2_attn_W_uq, L2_attn_W_qr, L2_attn_W_kr, L2_attn_W_out, L2_attn_idx_wq, L2_attn_idx_wk, L2_attn_idx_w, L2_attn_raw_delta)
    x = x + _L2_xattn_ref(_layernorm(x, axis=-1), ctx_1024, mask_BxS2_ik0, L2_xattn_w_q, L2_xattn_w_kv, L2_xattn_w_proj, L2_xattn_b_proj, L2_xattn_g_x, L2_xattn_b_x, L2_xattn_g_kv, L2_xattn_b_kv)
    x = x + _L2_ffn_ref(_layernorm(x, axis=-1), L2_ffn_gate_w, L2_ffn_w1, L2_ffn_w3, L2_ffn_w2)
    x = x + _L3_attn_ref(_layernorm(x, axis=-1), L3_attn_Wq, L3_attn_bq, L3_attn_Wk, L3_attn_bk, L3_attn_Wv, L3_attn_bv, L3_attn_Wo, L3_attn_bo)
    x = x + _L3_xattn_ref(_layernorm(x, axis=-1), ctx_1024, ctx_1024, mask_BxS2_ik1, L3_xattn_Wq, L3_xattn_bq, L3_xattn_Wk, L3_xattn_bk, L3_xattn_Wv, L3_xattn_bv)
    x = x + _L3_ffn_ref(_layernorm(x, axis=-1), L3_ffn_W_experts, L3_ffn_b_experts, L3_ffn_W_router, L3_ffn_b_router)
    return x

_drawn_inputs = setup_inputs


def setup_inputs(seed=0):
    import zlib

    import numpy as np

    out = dict(_drawn_inputs(seed))
    spreads = {'L0_attn_gamma': (1.0, 0.6),
     'L0_xattn_ln_l_w': (1.0, 0.2),
     'L0_xattn_ln_l_b': (0.0, 0.312),
     'L0_xattn_ln_c_w': (1.0, 0.2),
     'L0_xattn_ln_c_b': (0.0, 0.1),
     'L0_xattn_bo': (0.0, 0.1),
     'L1_attn_xl_b2': (0.0, 0.8),
     'L1_attn_gn_weight': (1.0, 0.6),
     'L1_attn_gn_bias': (0.0, 0.8),
     'L1_xattn_out_w': (0.0, 0.1),
     'L2_attn_idx_w': (1.0, 0.2),
     'L2_xattn_b_proj': (0.0, 0.1),
     'L2_xattn_g_x': (1.0, 0.552),
     'L2_xattn_b_x': (0.0, 0.531),
     'L2_xattn_g_kv': (1.0, 0.2),
     'L2_xattn_b_kv': (0.0, 0.1),
     'L3_attn_bq': (0.0, 2.0),
     'L3_attn_bk': (0.0, 2.0),
     'L3_attn_bv': (0.0, 0.867),
     'L3_attn_bo': (0.0, 0.446)}
    factors = {'L0_ffn_Wr': 4.273,
     'L0_ffn_W1': 4.136,
     'L0_ffn_b1': 8.0,
     'L0_ffn_W2': 4.09,
     'L0_ffn_b2': 8.0,
     'L1_attn_x_proj_mu': 8.0,
     'L1_attn_xl_w1': 8.0,
     'L1_attn_xl_w2': 8.0,
     'L1_attn_x_out_w': 8.0,
     'L1_attn_x_bias': 6.108,
     'L1_attn_w_w1': 8.0,
     'L1_attn_w_w2': 8.0,
     'L1_attn_w_b': 8.0,
     'L1_attn_bonus': 6.147,
     'L1_xattn_igate_b': 64.0,
     'L1_xattn_fgate_w': 2.724,
     'L2_attn_W_qr': 2.972,
     'L2_attn_raw_delta': 64.0,
     'L2_ffn_gate_w': 8.0,
     'L2_ffn_w1': 8.0,
     'L2_ffn_w3': 8.0,
     'L2_ffn_w2': 8.0,
     'L3_attn_Wq': 6.716,
     'L3_attn_Wk': 7.122,
     'L3_xattn_Wq': 2.715,
     'L3_xattn_bq': 64.0,
     'L3_xattn_bk': 64.0,
     'L3_ffn_b_experts': 7.159,
     'L3_xattn_bv': 5.355,
     'L3_ffn_b_router': 5.628}
    for name, (base, spread) in spreads.items():
        noise = np.random.default_rng([zlib.crc32(name.encode()), seed]).standard_normal(out[name].shape)
        drawn = base * np.exp(spread * noise) if base else spread * noise
        out[name] = jnp.asarray(drawn.astype(out[name].dtype))
    for name, factor in factors.items():
        out[name] = (out[name] * factor).astype(out[name].dtype)
    return out
```

```python
from contextlib import ExitStack

import numpy as np

import concourse.bass as bass
from concourse import mybir

F32 = mybir.dt.float32
I32 = mybir.dt.int32
ALU = mybir.AluOpType
ACT = mybir.ActivationFunctionType
AX = mybir.AxisListType

B, T, D = 64, 64, 128
G = 512
NB = G // T
NT = G // 128
TURNS = B * T // (2 * G)
S = (0, 1)
LN_EPS = 1e-5


class Steps:

    def __init__(self, sem, names):
        self.sem, self.names, self.done = sem, list(names), 0
        self.number = {n: k for k, n in enumerate(self.names)}
        assert len(self.number) == len(self.names)

    def at(self, name, s):
        return 2 * self.number[name] + s + 1

    def one(self, name, s):
        assert self.done == 2 * self.number[name] + s, (name, s, self.names[self.done // 2], self.done % 2)
        self.done += 1
        return 1


def many(*parts):
    out = []
    for p in parts:
        if isinstance(p, tuple):
            out += [f"{n}{j}" for j in range(p[-1]) for n in p[:-1]]
        else:
            out.append(p)
    return out


def columns(table):
    at, n = {}, 0
    for name, w in table:
        at[name] = (n, w)
        n += w
    return at, n


CONSTS = [("ident", 128), ("mean", 128), ("mean32", 128), ("earlier", 128), ("slot", 10), ("rev", 8),
          ("keep", 512), ("start", 512), ("row32", 64), ("negrow32", 64), ("causal", 64), ("ones", 128),
          ("pcos", 64), ("psin", 64), ("psign", 1), ("rcos", 64), ("rsin", 64), ("head4", 4), ("rot", 128),
          ("ksum", 158), ("bonus_sum", 128)]
CONST_AT, CONST_N = columns(CONSTS)


def constants():
    c = {n: np.zeros((128, w), np.float32) for n, w in CONSTS}
    p = np.arange(128)
    c["ident"][p, p] = 1
    c["mean"][:] = 1 / 128
    c["mean32"][:] = np.where(p[:, None] // 32 == p[None] // 32, 1 / 32, 0)
    same = p[:, None] // T == p[None] // T
    c["earlier"][:] = same & (p[:, None] < p[None])
    c["slot"][:] = np.arange(10)
    c["rev"][:] = 8 - np.arange(8)
    c["keep"][:] = np.arange(G) % T != 0
    c["start"][:] = np.where(np.arange(G) % T == 0, -1e30, 0)
    c["row32"][p % 32 == 0] = 1
    c["negrow32"][p % 32 == 0] = -1
    c["causal"][:] = (p[:, None] % T) <= np.arange(T)[None]
    c["ones"][:] = 1
    pos = np.arange(T, dtype=np.float32)
    theta = (1.0 / np.float32(10000.0) ** (2.0 * np.arange(16, dtype=np.float32) / 32)).astype(np.float32)
    ang = (pos[None] * theta[p % 16][:, None]).astype(np.float32)
    c["pcos"][:], c["psin"][:] = np.cos(ang), np.sin(ang)
    c["psign"][:, 0] = np.where(p % 32 < 16, -1, 1)
    freq = (1.0 / np.float32(10000.0) ** (np.arange(0, 8, 2, dtype=np.float32) / 8)).astype(np.float32)
    ang = (pos[None] * freq[(p % 8) % 4][:, None]).astype(np.float32)
    c["rcos"][:], c["rsin"][:] = np.cos(ang), np.sin(ang)
    c["head4"][:] = (p[:, None] % 32) // 8 == np.arange(4)[None]
    even = p[p % 2 == 0]
    c["rot"][even + 1, even] = -1
    c["rot"][even, even + 1] = 1
    c["ksum"][p, ((p % 64) // 16) * 32 + p // 64 + 30] = 1
    q = p[:64]
    c["bonus_sum"][:64] = q[:, None] // 16 == p[None] // 32
    return np.concatenate([c[n] for n, _ in CONSTS], axis=1)


class Core:

    def __init__(self, nc, ctx, weights_at, weights_n, moe_at, moe_n):
        self.nc, self.ctx = nc, ctx
        self.moe_at = moe_at[0] | moe_at[1]
        self.moe = ctx.enter_context(nc.sbuf_tensor("moe_weights", [128, moe_n], F32))
        self.w_at = weights_at
        self.w = ctx.enter_context(nc.sbuf_tensor("weights", [128, weights_n], F32))
        self.c = ctx.enter_context(nc.sbuf_tensor("consts", [128, CONST_N], F32))
        self.psum = [[ctx.enter_context(nc.psum_tensor(f"psum{s}{k}", [128, G], F32)) for k in range(4)] for s in S]
        self.buf = {}
        self.sems = []

    def sbuf(self, name, cols, dt=F32):
        self.buf[name] = [self.ctx.enter_context(self.nc.sbuf_tensor(f"{name}{s}", [128, cols], dt)) for s in S]

    def const(self, name, rows=slice(0, 128)):
        o, w = CONST_AT[name]
        return self.c[rows, o:o + w]

    def weight(self, name, rows=slice(0, 128)):
        if name in self.moe_at:
            o, w = self.moe_at[name]
            return self.moe[rows, o:o + w]
        o, w = self.w_at[name]
        return self.w[rows, o:o + w]

    def steps(self, name, parts):
        sem = self.ctx.enter_context(self.nc.semaphore(name))
        self.sems.append(sem)
        return Steps(sem, many(*parts))

    def b(self, name, s, rows=slice(0, 128)):
        if name[0] == "t":
            return self.wide(s, int(name[1:]), 1, rows)
        return self.buf[name][s][rows, :]

    def wide(self, s, j, n, rows=slice(0, 128)):
        return self.buf["tmp"][s][rows, j * G:(j + n) * G]


def per_batch(ap):
    return ap.rearrange("p (b t) -> p b t", t=T)


class Norm:

    PE, DVE, ACT = ("mean", "var"), ("xc", "h"), ("sq", "ln", "rstd")

    def __init__(self, core, sub, src="x", out="h"):
        self.k, self.sub, self.src, self.out = core, sub, src, out

    def pe(self, eng):
        k, u = self.k, self.sub
        for s in S:
            u.input_ready(eng, s)
            eng.matmul(k.psum[s][0][:], k.const("mean"), k.b(self.src, s), start=True, stop=True)\
               .then_inc(u.pe.sem, u.pe.one("mean", s))
        for s in S:
            eng.wait_ge(u.act.sem, u.act.at("sq", s))
            eng.matmul(k.psum[s][1][:], k.const("mean"), k.b("t1", s), start=True, stop=True)\
               .then_inc(u.pe.sem, u.pe.one("var", s))

    def dve(self, eng):
        k, u = self.k, self.sub
        for s in S:
            eng.wait_ge(u.pe.sem, u.pe.at("mean", s))
            eng.tensor_tensor(k.b("t0", s), k.b(self.src, s), k.psum[s][0][:], ALU.subtract)\
               .then_inc(u.dve.sem, u.dve.one("xc", s))
        for s in S:
            eng.wait_ge(u.act.sem, u.act.at("rstd", s))
            eng.wait_ge(u.dve.sem, u.dve.at("xc", s))
            eng.tensor_tensor(k.b(self.out, s), k.b("t0", s), k.b("t1", s), ALU.mult)\
               .then_inc(u.dve.sem, u.dve.one("h", s))

    def act(self, eng):
        k, u = self.k, self.sub
        for s in S:
            eng.wait_ge(u.dve.sem, u.dve.at("xc", s))
            eng.activation(k.b("t1", s), k.b("t0", s), ACT.Square).then_inc(u.act.sem, u.act.one("sq", s))
        for s in S:
            eng.wait_ge(u.pe.sem, u.pe.at("var", s))
            eng.activation(k.b("t1", s), k.psum[s][1][:], ACT.Ln, bias=k.eps5[:, 0:1])\
               .then_inc(u.act.sem, u.act.one("ln", s))
        for s in S:
            eng.wait_ge(u.act.sem, u.act.at("ln", s))
            eng.activation(k.b("t1", s), k.b("t1", s), ACT.Exp, scale=-0.5)\
               .then_inc(u.act.sem, u.act.one("rstd", s))


class Sub:

    def __init__(self, core, prev):
        self.k, self.prev = core, prev

    def output_ready(self, eng, s):
        eng.wait_ge(self.dve.sem, self.dve.at("x", s))

    def input_ready(self, eng, s):
        self.prev.output_ready(eng, s)

    def pool(self, eng):
        pass


class Load:

    def __init__(self, core, x_in):
        self.x_in = x_in

    def output_ready(self, eng, s):
        eng.wait_ge(self.x_in[s], 16)


class L0Attn(Sub):

    def __init__(self, core, prev):
        super().__init__(core, prev)
        self.pe = core.steps("l0a_pe", [*Norm.PE, "q", "kv", "a"])
        self.act = core.steps("l0a_act", ["sq", "ln", "rstd", "r2", "lnn", "rnorm", "sig"])
        self.dve = core.steps("l0a_dve", ["xc", "h", "n2", "n2max", "xn", "gate0", "scan", "qy", "x"])
        self.norm = Norm(core, self)

    def pe_program(self, eng):
        k, u = self.k, self
        self.norm.pe(eng)
        for j, name in enumerate(("q", "kv", "a")):
            for s in S:
                if j == 0:
                    eng.wait_ge(u.dve.sem, u.dve.at("xn", s))
                bank = (0, 2, 3)[j]
                eng.matmul(k.psum[s][bank][:], k.weight("l0a_w")[:, j * D:(j + 1) * D], k.b("t3", s),
                           start=True, stop=True).then_inc(u.pe.sem, u.pe.one(name, s))

    def act_program(self, eng):
        k, u = self.k, self
        self.norm.act(eng)
        for s in S:
            eng.wait_ge(u.act.sem, u.act.at("rstd", s))
            eng.activation(k.b("t2", s), k.b("t1", s), ACT.Square).then_inc(u.act.sem, u.act.one("r2", s))
        for s in S:
            eng.wait_ge(u.dve.sem, u.dve.at("n2max", s))
            eng.activation(k.b("t2", s), k.b("t2", s), ACT.Ln, scale=float(2.0 ** 40))\
               .then_inc(u.act.sem, u.act.one("lnn", s))
        for s in S:
            eng.wait_ge(u.act.sem, u.act.at("lnn", s))
            eng.activation(k.b("t2", s), k.b("t2", s), ACT.Exp, scale=-0.5, bias=k.l0a_bias[:, 0:1])\
               .then_inc(u.act.sem, u.act.one("rnorm", s))
        for s in S:
            eng.wait_ge(u.pe.sem, u.pe.at("a", s))
            eng.activation(k.b("t4", s), k.psum[s][3][:], ACT.Sigmoid).then_inc(u.act.sem, u.act.one("sig", s))

    def dve_program(self, eng):
        k, u = self.k, self
        self.norm.dve(eng)
        for s in S:
            eng.wait_ge(u.act.sem, u.act.at("r2", s))
            eng.scalar_tensor_tensor(k.b("t2", s), k.psum[s][1][:], float(D), k.b("t2", s), ALU.mult, ALU.mult)\
               .then_inc(u.dve.sem, u.dve.one("n2", s))
        for s in S:
            eng.wait_ge(u.dve.sem, u.dve.at("n2", s))
            eng.tensor_scalar(k.b("t2", s), k.b("t2", s), 1e-24, None, ALU.max)\
               .then_inc(u.dve.sem, u.dve.one("n2max", s))
        for s in S:
            eng.wait_ge(u.act.sem, u.act.at("rnorm", s))
            eng.wait_ge(u.dve.sem, u.dve.at("h", s))
            eng.scalar_tensor_tensor(k.b("t3", s), k.b("h", s), k.weight("l0a_gamma"), k.b("t2", s),
                                     ALU.mult, ALU.mult).then_inc(u.dve.sem, u.dve.one("xn", s))
        for s in S:
            eng.wait_ge(u.act.sem, u.act.at("sig", s))
            eng.memset(per_batch(k.b("t4", s))[:, :, 0:1], 0.0).then_inc(u.dve.sem, u.dve.one("gate0", s))
        for s in S:
            eng.wait_ge(u.dve.sem, u.dve.at("gate0", s))
            eng.wait_ge(u.pe.sem, u.pe.at("kv", s))
            eng.tensor_tensor_scan(k.b("t5", s), k.b("t4", s), k.psum[s][2][:], 0.0, ALU.mult, ALU.add)\
               .then_inc(u.dve.sem, u.dve.one("scan", s))
        for s in S:
            eng.wait_ge(u.dve.sem, u.dve.at("scan", s))
            eng.tensor_tensor(k.b("t5", s), k.b("t5", s), k.psum[s][0][:], ALU.mult)\
               .then_inc(u.dve.sem, u.dve.one("qy", s))
        for s in S:
            eng.wait_ge(u.dve.sem, u.dve.at("qy", s))
            eng.tensor_tensor(k.b("x", s), k.b("x", s), k.b("t5", s), ALU.add)\
               .then_inc(u.dve.sem, u.dve.one("x", s))


class CtxNorm(Sub):

    def __init__(self, core, prev):
        super().__init__(core, prev)
        self.pe = core.steps("ctx_pe", Norm.PE)
        self.act = core.steps("ctx_act", Norm.ACT)
        self.dve = core.steps("ctx_dve", Norm.DVE)
        self.norm = Norm(core, self, src="c", out="cn")

    def input_ready(self, eng, s):
        eng.wait_ge(self.k.c_in[s], 16)

    def output_ready(self, eng, s):
        eng.wait_ge(self.dve.sem, self.dve.at("h", s))
        self.prev.output_ready(eng, s)

    def pe_program(self, eng):
        self.norm.pe(eng)

    def act_program(self, eng):
        self.norm.act(eng)

    def dve_program(self, eng):
        self.norm.dve(eng)


class TwiceNorm(Norm):

    PE = Norm.PE
    ACT = (*Norm.ACT, "r2", "ln2", "rstd2")
    DVE = (*Norm.DVE, "var2", "lat", "latb")

    def __init__(self, core, sub, w, b):
        super().__init__(core, sub)
        self.w, self.bias = w, b

    def act(self, eng):
        super().act(eng)
        k, u = self.k, self.sub
        for s in S:
            eng.wait_ge(u.act.sem, u.act.at("rstd", s))
            eng.activation(k.b("t2", s), k.b("t1", s), ACT.Square).then_inc(u.act.sem, u.act.one("r2", s))
        for s in S:
            eng.wait_ge(u.dve.sem, u.dve.at("var2", s))
            eng.activation(k.b("t2", s), k.b("t2", s), ACT.Ln, bias=k.eps5[:, 0:1])\
               .then_inc(u.act.sem, u.act.one("ln2", s))
        for s in S:
            eng.wait_ge(u.act.sem, u.act.at("ln2", s))
            eng.activation(k.b("t2", s), k.b("t2", s), ACT.Exp, scale=-0.5)\
               .then_inc(u.act.sem, u.act.one("rstd2", s))

    def dve(self, eng):
        super().dve(eng)
        k, u = self.k, self.sub
        for s in S:
            eng.wait_ge(u.act.sem, u.act.at("r2", s))
            eng.tensor_tensor(k.b("t2", s), k.psum[s][1][:], k.b("t2", s), ALU.mult)\
               .then_inc(u.dve.sem, u.dve.one("var2", s))
        for s in S:
            eng.wait_ge(u.act.sem, u.act.at("rstd2", s))
            eng.wait_ge(u.dve.sem, u.dve.at("h", s))
            eng.scalar_tensor_tensor(k.b("t3", s), k.b("h", s), k.weight(self.w), k.b("t2", s), ALU.mult, ALU.mult)\
               .then_inc(u.dve.sem, u.dve.one("lat", s))
        for s in S:
            eng.wait_ge(u.dve.sem, u.dve.at("lat", s))
            eng.tensor_scalar(k.b("t3", s), k.b("t3", s), k.weight(self.bias), None, ALU.add)\
               .then_inc(u.dve.sem, u.dve.one("latb", s))


class L0Xattn(Sub):

    HEADS, DH = 8, 64

    def __init__(self, core, prev):
        super().__init__(core, prev)
        pe, act, dve = list(TwiceNorm.PE), list(TwiceNorm.ACT), [*TwiceNorm.DVE, "ctxa"]
        for hh in range(2):
            for p in range(4 * hh, 4 * hh + 4):
                pe += [f"q{p}", f"k{p}"]
                act += [f"qs{p}"]
                dve += [f"ks{p}"]
            for j in range(4 * hh, 4 * hh + 4):
                pe += [f"v{j}", f"score{j}", f"pv{j}", f"turn{j}"]
                act += [f"vs{j}", f"exp{j}", f"outs{j}"]
                dve += [f"clip{j}", f"recip{j}", f"lo{j}", f"hi{j}"]
            pe += [f"wo{hh}"]
            dve += ["x_half" if hh == 0 else "x"]
        self.pe, self.act, self.dve = core.steps("l0x_pe", pe), core.steps("l0x_act", act), core.steps("l0x_dve", dve)
        self.norm = TwiceNorm(core, self, "l0x_ln_l_w", "l0x_ln_l_b")

    def pe_program(self, eng):
        k, u = self.k, self
        self.norm.pe(eng)
        for hh in range(2):
            for p in range(4 * hh, 4 * hh + 4):
                for s in S:
                    if p == 0:
                        eng.wait_ge(u.dve.sem, u.dve.at("latb", s))
                    if p % 4 >= 2:
                        eng.wait_ge(u.act.sem, u.act.at(f"qs{p - 2}", s))
                    if p == 4:
                        eng.wait_ge(u.dve.sem, u.dve.at("x_half", s))
                        eng.wait_ge(u.act.sem, u.act.at("outs3", s))
                    eng.matmul(k.psum[s][p % 2][:], k.weight("l0x_wq")[:, p * 128:(p + 1) * 128], k.b("t3", s),
                               start=True, stop=True).then_inc(u.pe.sem, u.pe.one(f"q{p}", s))
                for s in S:
                    if p == 0:
                        eng.wait_ge(u.dve.sem, u.dve.at("ctxa", s))
                    if p % 4 >= 2:
                        eng.wait_ge(u.dve.sem, u.dve.at(f"ks{p - 2}", s))
                    if p == 4:
                        eng.wait_ge(u.dve.sem, u.dve.at("hi3", s))
                    eng.matmul(k.psum[s][2 + p % 2][:], k.weight("l0x_wkv")[:, p * 128:(p + 1) * 128], k.b("t4", s),
                               start=True, stop=True).then_inc(u.pe.sem, u.pe.one(f"k{p}", s))
            for j in range(4 * hh, 4 * hh + 4):
                t = j % 4
                for s in S:
                    if t == 0:
                        eng.wait_ge(u.act.sem, u.act.at(f"qs{4 * hh + 3}", s))
                    else:
                        eng.wait_ge(u.act.sem, u.act.at(f"outs{j - 1}", s))
                    eng.matmul(k.psum[s][1][:], k.b("t4", s)[:, t * 128:(t + 1) * 128],
                               k.weight("l0x_wkv")[:, 1024 + hh * G:1024 + (hh + 1) * G],
                               start=True, stop=True).then_inc(u.pe.sem, u.pe.one(f"v{j}", s))
                for s in S:
                    if t == 0:
                        eng.wait_ge(u.dve.sem, u.dve.at(f"ks{4 * hh + 3}", s))
                    else:
                        eng.wait_ge(u.dve.sem, u.dve.at(f"hi{j - 1}", s))
                    for h in range(8):
                        half = slice(64 * (h % 2), 64 * (h % 2) + 64)
                        for b in range(2):
                            at = t * 128 + b * T
                            mm = eng.matmul(k.psum[s][2 * (h % 2)][b * T:(b + 1) * T, h // 2 * T:(h // 2 + 1) * T],
                                            k.b(f"t{9 + h // 2}", s, half)[:, at:at + T],
                                            k.b(f"t{5 + h // 2}", s, half)[:, at:at + T], start=True, stop=True)
                    mm.then_inc(u.pe.sem, u.pe.one(f"score{j}", s))
                for s in S:
                    eng.wait_ge(u.act.sem, u.act.at(f"exp{j}", s))
                    vb = k.vb[s].ap().rearrange("p (h c) -> p h c", c=65)
                    for h in range(8):
                        for b in range(2):
                            rows = slice(b * T, (b + 1) * T)
                            mm = eng.matmul(k.psum[s][2 + h // 4][rows, (h % 4) * 65:(h % 4 + 1) * 65],
                                            k.b("t13", s, rows)[:, h * T:(h + 1) * T], vb[rows, h, :],
                                            start=True, stop=True)
                    mm.then_inc(u.pe.sem, u.pe.one(f"pv{j}", s))
                for s in S:
                    eng.wait_ge(u.dve.sem, u.dve.at(f"hi{j}", s))
                    for p in range(4):
                        mm = eng.transpose(k.psum[s][1][:, p * 128:(p + 1) * 128],
                                           k.b("t14", s)[:, p * 128:(p + 1) * 128], k.const("ident"))
                    mm.then_inc(u.pe.sem, u.pe.one(f"turn{j}", s))
            for s in S:
                eng.wait_ge(u.act.sem, u.act.at(f"outs{4 * hh + 3}", s))
                for p in range(4):
                    at = (4 * hh + p) * 128
                    mm = eng.matmul(k.psum[s][0][:], k.weight("l0x_wo")[:, at:at + 128], k.b(f"t{5 + p}", s),
                                    start=p == 0, stop=p == 3)
                mm.then_inc(u.pe.sem, u.pe.one(f"wo{hh}", s))

    def act_program(self, eng):
        k, u = self.k, self
        self.norm.act(eng)
        for hh in range(2):
            for p in range(4 * hh, 4 * hh + 4):
                for s in S:
                    eng.wait_ge(u.pe.sem, u.pe.at(f"q{p}", s))
                    eng.copy(k.b(f"t{5 + p % 4}", s), k.psum[s][p % 2][:]).then_inc(u.act.sem, u.act.one(f"qs{p}", s))
            for j in range(4 * hh, 4 * hh + 4):
                for s in S:
                    eng.wait_ge(u.pe.sem, u.pe.at(f"v{j}", s))
                    eng.copy(k.vb[s].ap().rearrange("p (h c) -> p h c", c=65)[:, 0:8, 0:64],
                             k.psum[s][1][:].rearrange("p (h c) -> p h c", c=64))\
                       .then_inc(u.act.sem, u.act.one(f"vs{j}", s))
                for s in S:
                    eng.wait_ge(u.dve.sem, u.dve.at(f"clip{j}", s))
                    eng.activation(k.b("t13", s), k.b("t13", s), ACT.Exp, scale=0.125)\
                       .then_inc(u.act.sem, u.act.one(f"exp{j}", s))
                for s in S:
                    eng.wait_ge(u.pe.sem, u.pe.at(f"turn{j}", s))
                    t = j % 4
                    eng.copy(k.wide(s, 5, 4).rearrange("p (q n) -> p q n", n=G)[:, :, t * 128:(t + 1) * 128],
                             k.psum[s][1][:].rearrange("p (q n) -> p q n", n=128))\
                       .then_inc(u.act.sem, u.act.one(f"outs{j}", s))

    def dve_program(self, eng):
        k, u = self.k, self
        self.norm.dve(eng)
        for s in S:
            eng.tensor_scalar(k.b("t4", s), k.b("cn", s), k.weight("l0x_ln_c_w"), k.weight("l0x_ln_c_b"),
                              ALU.mult, ALU.add).then_inc(u.dve.sem, u.dve.one("ctxa", s))
        for hh in range(2):
            for p in range(4 * hh, 4 * hh + 4):
                for s in S:
                    eng.wait_ge(u.pe.sem, u.pe.at(f"k{p}", s))
                    eng.tensor_copy(k.b(f"t{9 + p % 4}", s), k.psum[s][2 + p % 2][:])\
                       .then_inc(u.dve.sem, u.dve.one(f"ks{p}", s))
            for j in range(4 * hh, 4 * hh + 4):
                for s in S:
                    eng.wait_ge(u.pe.sem, u.pe.at(f"score{j}", s))
                    for odd in range(2):
                        ins = eng.tensor_scalar(
                            k.b("t13", s).rearrange("p (q o t) -> p q o t", o=2, t=T)[:, :, odd, :],
                            k.psum[s][2 * odd][:, 0:256].rearrange("p (q t) -> p q t", t=T),
                            -88.0, 88.0, ALU.max, ALU.min)
                    ins.then_inc(u.dve.sem, u.dve.one(f"clip{j}", s))
                outs = lambda s, c: k.psum[s][2 + c][:, 0:260].rearrange("p (h c) -> p h c", c=65)
                for s in S:
                    eng.wait_ge(u.pe.sem, u.pe.at(f"pv{j}", s))
                    eng.reciprocal(k.small[s][:, 0:4], outs(s, 0)[:, :, 64])
                    eng.reciprocal(k.small[s][:, 4:8], outs(s, 1)[:, :, 64])\
                       .then_inc(u.dve.sem, u.dve.one(f"recip{j}", s))
                for c, name in enumerate(("lo", "hi")):
                    for s in S:
                        eng.wait_ge(u.dve.sem, u.dve.at(f"recip{j}", s))
                        eng.tensor_tensor(k.b("t14", s)[:, c * 256:(c + 1) * 256].rearrange("p (h c) -> p h c", c=64),
                                          outs(s, c)[:, :, 0:64],
                                          k.small[s][:, 4 * c:4 * c + 4].unsqueeze(2).broadcast_to([128, 4, 64]),
                                          ALU.mult).then_inc(u.dve.sem, u.dve.one(f"{name}{j}", s))
            for s in S:
                eng.wait_ge(u.pe.sem, u.pe.at(f"wo{hh}", s))
                if hh == 0:
                    eng.tensor_tensor(k.b("x", s), k.b("x", s), k.psum[s][0][:], ALU.add)\
                       .then_inc(u.dve.sem, u.dve.one("x_half", s))
                else:
                    eng.wait_ge(u.dve.sem, u.dve.at("x_half", s))
                    eng.scalar_tensor_tensor(k.b("x", s), k.psum[s][0][:], k.weight("l0x_bo"), k.b("x", s),
                                             ALU.add, ALU.add).then_inc(u.dve.sem, u.dve.one("x", s))


class Gate:

    PE, ACT = ("logit",), ("gexp",)
    DVE = ("glogit", "gmax", "gsub", "gsum", "grecip", "gprob", "gm0", "ge0", "gkey0", "gmk0", "gsel0", "grest",
           "gm1", "ge1", "gkey1", "gmk1", "gsel1", "gboth", "gate")

    def __init__(self, core, sub, weight, bias=None):
        self.k, self.sub, self.weight, self.bias = core, sub, weight, bias

    def g(self, s, n):
        return self.k.gate[s][:, 32 * n:32 * n + 32]

    def pe(self, eng):
        k, u = self.k, self.sub
        for s in S:
            eng.wait_ge(u.dve.sem, u.dve.at("h", s))
            for t in range(NT):
                mm = eng.matmul(k.psum[s][2][:, t * 8:t * 8 + 8], k.b("h", s)[:, t * 128:(t + 1) * 128],
                                k.weight(self.weight), start=True, stop=True)
            mm.then_inc(u.pe.sem, u.pe.one("logit", s))

    def act(self, eng):
        k, u = self.k, self.sub
        for s in S:
            eng.wait_ge(u.dve.sem, u.dve.at("gsub", s))
            eng.activation(self.g(s, 0), self.g(s, 0), ACT.Exp).then_inc(u.act.sem, u.act.one("gexp", s))

    def dve(self, eng):
        k, u = self.k, self.sub
        g = self.g
        t8 = lambda ap: ap.rearrange("p (t e) -> p t e", e=8)
        sm = lambda s, j: k.small[s][:, 16 + 4 * j:20 + 4 * j]
        over = lambda ap: ap.unsqueeze(2).broadcast_to([128, NT, 8])
        rev = k.const("rev").unsqueeze(1).broadcast_to([128, NT, 8])
        for s in S:
            eng.wait_ge(u.pe.sem, u.pe.at("logit", s))
            if self.bias:
                ins = eng.tensor_tensor(t8(g(s, 0)), t8(k.psum[s][2][:, 0:32]),
                                        k.weight(self.bias).unsqueeze(1).broadcast_to([128, NT, 8]), ALU.add)
            else:
                ins = eng.tensor_copy(g(s, 0), k.psum[s][2][:, 0:32])
            ins.then_inc(u.dve.sem, u.dve.one("glogit", s))
        for s in S:
            eng.wait_ge(u.dve.sem, u.dve.at("glogit", s))
            eng.tensor_reduce(sm(s, 0), t8(g(s, 0)), AX.X, ALU.max).then_inc(u.dve.sem, u.dve.one("gmax", s))
        for s in S:
            eng.wait_ge(u.dve.sem, u.dve.at("gmax", s))
            eng.tensor_tensor(t8(g(s, 0)), t8(g(s, 0)), over(sm(s, 0)), ALU.subtract)\
               .then_inc(u.dve.sem, u.dve.one("gsub", s))
        for s in S:
            eng.wait_ge(u.act.sem, u.act.at("gexp", s))
            eng.tensor_reduce(sm(s, 1), t8(g(s, 0)), AX.X, ALU.add).then_inc(u.dve.sem, u.dve.one("gsum", s))
        for s in S:
            eng.wait_ge(u.dve.sem, u.dve.at("gsum", s))
            eng.reciprocal(sm(s, 2), sm(s, 1)).then_inc(u.dve.sem, u.dve.one("grecip", s))
        for s in S:
            eng.wait_ge(u.dve.sem, u.dve.at("grecip", s))
            eng.tensor_tensor(t8(g(s, 1)), t8(g(s, 0)), over(sm(s, 2)), ALU.mult).then_inc(u.dve.sem, u.dve.one("gprob", s))
        for n, src, cand, sel in ((0, 1, 2, 3), (1, 4, 5, 6)):
            for s in S:
                eng.wait_ge(u.dve.sem, u.dve.at("gprob" if n == 0 else "grest", s))
                eng.tensor_reduce(sm(s, 3 + n), t8(g(s, src)), AX.X, ALU.max).then_inc(u.dve.sem, u.dve.one(f"gm{n}", s))
            for s in S:
                eng.wait_ge(u.dve.sem, u.dve.at(f"gm{n}", s))
                eng.tensor_tensor(t8(g(s, cand)), t8(g(s, src)), over(sm(s, 3 + n)), ALU.is_equal)\
                   .then_inc(u.dve.sem, u.dve.one(f"ge{n}", s))
            for s in S:
                eng.wait_ge(u.dve.sem, u.dve.at(f"ge{n}", s))
                eng.tensor_tensor(t8(g(s, cand)), t8(g(s, cand)), rev, ALU.mult).then_inc(u.dve.sem, u.dve.one(f"gkey{n}", s))
            for s in S:
                eng.wait_ge(u.dve.sem, u.dve.at(f"gkey{n}", s))
                eng.tensor_reduce(sm(s, 5 + n), t8(g(s, cand)), AX.X, ALU.max).then_inc(u.dve.sem, u.dve.one(f"gmk{n}", s))
            for s in S:
                eng.wait_ge(u.dve.sem, u.dve.at(f"gmk{n}", s))
                eng.tensor_tensor(t8(g(s, sel)), t8(g(s, cand)), over(sm(s, 5 + n)), ALU.is_equal)\
                   .then_inc(u.dve.sem, u.dve.one(f"gsel{n}", s))
            if n == 0:
                for s in S:
                    eng.wait_ge(u.dve.sem, u.dve.at("gsel0", s))
                    eng.scalar_tensor_tensor(g(s, 4), g(s, 3), -2.0, g(s, 1), ALU.mult, ALU.add)\
                       .then_inc(u.dve.sem, u.dve.one("grest", s))
        for s in S:
            eng.wait_ge(u.dve.sem, u.dve.at("gsel1", s))
            eng.tensor_tensor(g(s, 7), g(s, 3), g(s, 6), ALU.add).then_inc(u.dve.sem, u.dve.one("gboth", s))
        for s in S:
            eng.wait_ge(u.dve.sem, u.dve.at("gboth", s))
            eng.tensor_tensor(g(s, 8), g(s, 1), g(s, 7), ALU.mult).then_inc(u.dve.sem, u.dve.one("gate", s))


class L0Ffn(Sub):

    E, CAP, HID = 8, 10, 4
    SLOTS = E * CAP

    def __init__(self, core, prev):
        super().__init__(core, prev)
        n = range(self.E // 2)
        self.pe = core.steps("l0f_pe", [*Norm.PE, *Gate.PE, "htok", "rank", "gt", "fill"]
                             + [f"{a}{j}" for j in n for a in ("up", "down")] + ["yt", "comb"])
        self.act = core.steps("l0f_act", [*Norm.ACT, *Gate.ACT, "htok", "gt", "fill"] + [f"relu{j}" for j in n] + ["yt"])
        self.dve = core.steps("l0f_dve", [*Norm.DVE, *Gate.DVE, "hot", "disp", "gated"] + [f"y{j}" for j in n] + ["x"])
        self.norm = Norm(core, self)
        self.gate = Gate(core, self, "l0f_wr")

    def places(self):
        return self.k.wide(0, 10, 3)[:, 0:1280]

    def results(self):
        return self.k.wide(1, 10, 3)[:, 0:1280]

    def hidden(self, odd):
        return self.k.wide(odd, 13, 2)[:, 0:640]

    def pe_program(self, eng):
        k, u = self.k, self
        self.norm.pe(eng)
        eng.wait_ge(k.moe_in[0], 16)
        self.gate.pe(eng)
        for s in S:
            for t in range(NT):
                mm = eng.transpose(k.psum[s][0][:, t * 128:(t + 1) * 128], k.b("h", s)[:, t * 128:(t + 1) * 128],
                                   k.const("ident"))
            mm.then_inc(u.pe.sem, u.pe.one("htok", s))
        for s in S:
            eng.wait_ge(u.dve.sem, u.dve.at("gboth", s))
            eng.matmul(k.psum[s][3][:, 0:32], k.const("earlier"), self.gate.g(s, 7), start=True, stop=True)\
               .then_inc(u.pe.sem, u.pe.one("rank", s))
        for s in S:
            eng.wait_ge(u.dve.sem, u.dve.at("gated", s))
            for t in range(NT):
                mm = eng.transpose(k.psum[s][1][0:80, t * 128:(t + 1) * 128], k.b("t5", s)[:, t * 80:(t + 1) * 80],
                                   k.const("ident"))
            mm.then_inc(u.pe.sem, u.pe.one("gt", s))
        for s in S:
            eng.wait_ge(u.act.sem, u.act.at("htok", s))
            for t in range(NT):
                for b in range(2):
                    rows = slice(b * T, (b + 1) * T)
                    mm = eng.matmul(k.psum[s][2 + b][:, t * 80:(t + 1) * 80], k.b("t6", s, rows)[:, t * 128:(t + 1) * 128],
                                    k.b("t4", s, rows)[:, t * 80:(t + 1) * 80], start=True, stop=True)
            mm.then_inc(u.pe.sem, u.pe.one("fill", s))
        for j in range(self.E // 2):
            for odd in range(2):
                e = 2 * j + odd
                if j == 0:
                    for s in S:
                        eng.wait_ge(u.act.sem, u.act.at("fill", s))
                        eng.wait_ge(u.act.sem, u.act.at("gt", s))
                else:
                    eng.wait_ge(u.act.sem, u.act.at(f"relu{j - 1}", odd))
                for c in range(self.HID):
                    mm = eng.matmul(k.psum[odd][c // 3][:, c % 3 * 160:(c % 3 + 1) * 160],
                                    k.weight("l0f_w1")[:, e * 512 + c * 128:e * 512 + (c + 1) * 128],
                                    self.places()[:, e * 160:(e + 1) * 160], start=True, stop=True)
                mm.then_inc(u.pe.sem, u.pe.one(f"up{j}", odd))
            for odd in range(2):
                e = 2 * j + odd
                eng.wait_ge(u.act.sem, u.act.at(f"relu{j}", odd))
                if j:
                    eng.wait_ge(u.dve.sem, u.dve.at(f"y{j - 1}", odd))
                for c in range(self.HID):
                    mm = eng.matmul(k.psum[odd][2][:, 0:160],
                                    k.weight("l0f_w2")[:, (e * 4 + c) * 128:(e * 4 + c + 1) * 128],
                                    self.hidden(odd)[:, c * 160:(c + 1) * 160], start=c == 0, stop=c == self.HID - 1)
                mm.then_inc(u.pe.sem, u.pe.one(f"down{j}", odd))
        for s in S:
            eng.wait_ge(u.dve.sem, u.dve.at("y3", 0))
            eng.wait_ge(u.dve.sem, u.dve.at("y3", 1))
            for b in range(NB):
                at = (s * NB + b) * 80
                mm = eng.transpose(k.psum[s][b // 4][0:80, b % 4 * 128:(b % 4 + 1) * 128], self.results()[:, at:at + 80],
                                   k.const("ident"))
            mm.then_inc(u.pe.sem, u.pe.one("yt", s))
        for s in S:
            eng.wait_ge(u.act.sem, u.act.at("yt", s))
            for b in range(NB):
                mm = eng.matmul(k.psum[s][2][:, b * T:(b + 1) * T],
                                k.wide(s, 8, 2, slice(0, 80))[:, b * 128:(b + 1) * 128],
                                k.b("t7", s, slice(0, 80))[:, b * T:(b + 1) * T], start=True, stop=True)
            mm.then_inc(u.pe.sem, u.pe.one("comb", s))

    def act_program(self, eng):
        k, u = self.k, self
        self.norm.act(eng)
        self.gate.act(eng)
        for s in S:
            eng.wait_ge(u.pe.sem, u.pe.at("htok", s))
            eng.copy(k.b("t6", s), k.psum[s][0][:]).then_inc(u.act.sem, u.act.one("htok", s))
        for s in S:
            eng.wait_ge(u.pe.sem, u.pe.at("gt", s))
            eng.copy(k.b("t7", s, slice(0, 80)), k.psum[s][1][0:80, :]).then_inc(u.act.sem, u.act.one("gt", s))
        for s in S:
            eng.wait_ge(u.pe.sem, u.pe.at("fill", s))
            for b in range(2):
                to = self.places().rearrange("p (e s t b c) -> p e s t b c", e=8, s=2, t=NT, b=2)[:, :, s, :, b, :]
                ins = eng.copy(to, k.psum[s][2 + b][:, 0:320].rearrange("p (t e c) -> p e t c", t=NT, e=8))
            ins.then_inc(u.act.sem, u.act.one("fill", s))
        for j in range(self.E // 2):
            for odd in range(2):
                e = 2 * j + odd
                eng.wait_ge(u.pe.sem, u.pe.at(f"up{j}", odd))
                for c in range(self.HID):
                    ins = eng.activation(self.hidden(odd)[:, c * 160:(c + 1) * 160],
                                         k.psum[odd][c // 3][:, c % 3 * 160:(c % 3 + 1) * 160], ACT.Relu,
                                         bias=k.weight("l0f_b1")[:, e * 4 + c:e * 4 + c + 1])
                ins.then_inc(u.act.sem, u.act.one(f"relu{j}", odd))
        for s in S:
            eng.wait_ge(u.pe.sem, u.pe.at("yt", s))
            for c in range(2):
                ins = eng.copy(k.wide(s, 8, 2, slice(0, 80))[:, c * G:(c + 1) * G], k.psum[s][c][0:80, :])
            ins.then_inc(u.act.sem, u.act.one("yt", s))

    def dve_program(self, eng):
        k, u = self.k, self
        self.norm.dve(eng)
        self.gate.dve(eng)
        hot = lambda name, s: k.b(name, s)[:, 0:320].rearrange("p (e c) -> p e c", c=self.CAP)
        over = lambda ap: ap.unsqueeze(2).broadcast_to([128, 32, self.CAP])
        for s in S:
            eng.wait_ge(u.pe.sem, u.pe.at("rank", s))
            eng.tensor_tensor(hot("t4", s), over(k.psum[s][3][:, 0:32]),
                              k.const("slot").unsqueeze(1).broadcast_to([128, 32, self.CAP]), ALU.is_equal)\
               .then_inc(u.dve.sem, u.dve.one("hot", s))
        for s in S:
            eng.wait_ge(u.dve.sem, u.dve.at("hot", s))
            eng.tensor_tensor(hot("t4", s), hot("t4", s), over(self.gate.g(s, 7)), ALU.mult)\
               .then_inc(u.dve.sem, u.dve.one("disp", s))
        for s in S:
            eng.wait_ge(u.dve.sem, u.dve.at("disp", s))
            eng.tensor_tensor(hot("t5", s), hot("t4", s), over(self.gate.g(s, 1)), ALU.mult)\
               .then_inc(u.dve.sem, u.dve.one("gated", s))
        for j in range(self.E // 2):
            for odd in range(2):
                e = 2 * j + odd
                eng.wait_ge(u.pe.sem, u.pe.at(f"down{j}", odd))
                eng.tensor_scalar(self.results().rearrange("p (b e c) -> p b e c", e=8, c=10)[:, :, e, :],
                                  k.psum[odd][2][:, 0:160].rearrange("p (b c) -> p b c", c=10),
                                  k.weight("l0f_b2")[:, e:e + 1], None, ALU.add).then_inc(u.dve.sem, u.dve.one(f"y{j}", odd))
        for s in S:
            eng.wait_ge(u.pe.sem, u.pe.at("comb", s))
            eng.tensor_tensor(k.b("x", s), k.b("x", s), k.psum[s][2][:], ALU.add).then_inc(u.dve.sem, u.dve.one("x", s))


class GroupNorm:

    PE, ACT, DVE = ("gmean", "gvar"), ("gsq", "gln", "grstd"), ("gxc", "gn")

    def __init__(self, core, sub, src, ready):
        self.k, self.sub, self.src, self.ready = core, sub, src, ready

    def pe(self, eng):
        k, u = self.k, self.sub
        for s in S:
            self.ready(eng, s)
            eng.matmul(k.psum[s][2][:], k.const("mean32"), k.b(self.src, s), start=True, stop=True)\
               .then_inc(u.pe.sem, u.pe.one("gmean", s))
        for s in S:
            eng.wait_ge(u.act.sem, u.act.at("gsq", s))
            eng.matmul(k.psum[s][3][:], k.const("mean32"), k.b("t13", s), start=True, stop=True)\
               .then_inc(u.pe.sem, u.pe.one("gvar", s))

    def act(self, eng):
        k, u = self.k, self.sub
        for s in S:
            eng.wait_ge(u.dve.sem, u.dve.at("gxc", s))
            eng.activation(k.b("t13", s), k.b("t12", s), ACT.Square).then_inc(u.act.sem, u.act.one("gsq", s))
        for s in S:
            eng.wait_ge(u.pe.sem, u.pe.at("gvar", s))
            eng.activation(k.b("t13", s), k.psum[s][3][:], ACT.Ln, bias=k.eps5[:, 0:1])\
               .then_inc(u.act.sem, u.act.one("gln", s))
        for s in S:
            eng.wait_ge(u.act.sem, u.act.at("gln", s))
            eng.activation(k.b("t13", s), k.b("t13", s), ACT.Exp, scale=-0.5).then_inc(u.act.sem, u.act.one("grstd", s))

    def dve(self, eng):
        k, u = self.k, self.sub
        for s in S:
            eng.wait_ge(u.pe.sem, u.pe.at("gmean", s))
            eng.tensor_tensor(k.b("t12", s), k.b(self.src, s), k.psum[s][2][:], ALU.subtract)\
               .then_inc(u.dve.sem, u.dve.one("gxc", s))
        for s in S:
            eng.wait_ge(u.act.sem, u.act.at("grstd", s))
            eng.wait_ge(u.dve.sem, u.dve.at("gxc", s))
            eng.tensor_tensor(k.b("t12", s), k.b("t12", s), k.b("t13", s), ALU.mult)\
               .then_inc(u.dve.sem, u.dve.one("gn", s))


class L1Xattn(Sub):

    def __init__(self, core, prev):
        super().__init__(core, prev)
        self.pe = core.steps("l1x_pe", [*Norm.PE, "ig", "fg", "logd", "qk", "num", *GroupNorm.PE])
        self.act = core.steps("l1x_act", [*Norm.ACT, "fabs", "fexp", "fln", "expnm", "dexp", "absd", *GroupNorm.ACT])
        self.dve = core.steps("l1x_dve", [*Norm.DVE, "f", "lf", "cs", "g", "gs", "m", "csm", "dmin", "dmask", "c",
                                          "norm", "norme", "nrec", "out", *GroupNorm.DVE, "x"])
        self.norm = Norm(core, self)
        self.gn = GroupNorm(core, self, "t11", lambda eng, s: eng.wait_ge(self.dve.sem, self.dve.at("out", s)))

    def pe_program(self, eng):
        k, u = self.k, self
        self.norm.pe(eng)
        for bank, name in ((0, "ig"), (1, "fg")):
            w = k.weight("l1x_" + name)
            for s in S:
                eng.wait_ge(u.dve.sem, u.dve.at("h", s))
                eng.wait_ge(k.c_in[s], 16)
                for j, part in enumerate(("h", "c", "c")):
                    mm = eng.matmul(k.psum[s][bank][:], w[:, j * 128:(j + 1) * 128], k.b(part, s), start=j == 0, stop=j == 2)
                mm.then_inc(u.pe.sem, u.pe.one(name, s))
        place = [(h, t, b) for h in range(4) for t in range(NT) for b in range(2)]
        for s in S:
            eng.wait_ge(u.dve.sem, u.dve.at("m", s))
            for h, t, b in place:
                rows, at = slice(32 * h, 32 * h + 32), t * 128 + b * T
                out = k.psum[s][h][b * T:(b + 1) * T, t * T:(t + 1) * T]
                pos = (32 * h, 64 * b)
                eng.matmul(out, k.b("t5", s, rows)[:, at:at + T], k.const("row32", rows), start=True, stop=False,
                           tile_position=pos)
                mm = eng.matmul(out, k.const("negrow32", rows), k.b("t6", s, rows)[:, at:at + T], start=False, stop=True,
                                tile_position=pos)
            mm.then_inc(u.pe.sem, u.pe.one("logd", s))
        for s in S:
            for h, t, b in place:
                rows, at = slice(32 * h, 32 * h + 32), t * 128 + b * T
                mm = eng.matmul(k.psum[s][h][b * T:(b + 1) * T, 256 + t * T:256 + (t + 1) * T],
                                k.b("c", s, rows)[:, at:at + T], k.b("h", s, rows)[:, at:at + T], start=True, stop=True,
                                tile_position=(32 * h, 64 * b))
            mm.then_inc(u.pe.sem, u.pe.one("qk", s))
        for s in S:
            eng.wait_ge(u.dve.sem, u.dve.at("c", s))
            eng.wait_ge(k.ctok_in[s], 16)
            for h, t, b in place:
                rows, cols = slice(64 * b, 64 * b + 64), slice((h * NT + t) * T, (h * NT + t + 1) * T)
                weights = k.wide(s, 8, 2, rows)[:, cols]
                heads = slice(32 * h, 32 * h + 32)
                eng.matmul(k.psum[s][b][heads, t * T:(t + 1) * T], k.b("ctok", s, rows)[:, t * 128 + 32 * h:t * 128 + 32 * h + 32],
                           weights, start=True, stop=True, tile_position=(64 * b, 32 * h))
                mm = eng.matmul(k.psum[s][b][heads, 256 + t * T:256 + (t + 1) * T], k.const("ones", rows)[:, 0:32],
                                weights, start=True, stop=True, tile_position=(64 * b, 32 * h))
            mm.then_inc(u.pe.sem, u.pe.one("num", s))
        self.gn.pe(eng)

    def act_program(self, eng):
        k, u = self.k, self
        self.norm.act(eng)
        for s in S:
            eng.wait_ge(u.dve.sem, u.dve.at("f", s))
            eng.activation(k.b("t3", s), k.b("t2", s), ACT.Abs).then_inc(u.act.sem, u.act.one("fabs", s))
        for s in S:
            eng.wait_ge(u.act.sem, u.act.at("fabs", s))
            eng.activation(k.b("t3", s), k.b("t3", s), ACT.Exp, scale=-1.0).then_inc(u.act.sem, u.act.one("fexp", s))
        for s in S:
            eng.wait_ge(u.act.sem, u.act.at("fexp", s))
            eng.activation(k.b("t3", s), k.b("t3", s), ACT.Ln, bias=1.0).then_inc(u.act.sem, u.act.one("fln", s))
        for s in S:
            eng.wait_ge(u.dve.sem, u.dve.at("csm", s))
            eng.activation(k.b("t7", s), k.b("t7", s), ACT.Exp, scale=-1.0).then_inc(u.act.sem, u.act.one("expnm", s))
        for s in S:
            eng.wait_ge(u.dve.sem, u.dve.at("dmin", s))
            eng.activation(k.wide(s, 8, 2), k.wide(s, 8, 2), ACT.Exp).then_inc(u.act.sem, u.act.one("dexp", s))
        for s in S:
            eng.wait_ge(u.pe.sem, u.pe.at("num", s))
            for b in range(2):
                ins = eng.activation(k.b("t10", s).rearrange("p (t b q) -> p t b q", b=2, q=T)[:, :, b, :],
                                     k.psum[s][b][:, 256:512].rearrange("p (t q) -> p t q", q=T), ACT.Abs)
            ins.then_inc(u.act.sem, u.act.one("absd", s))
        self.gn.act(eng)

    def dve_program(self, eng):
        k, u = self.k, self
        self.norm.dve(eng)
        for s in S:
            eng.wait_ge(u.pe.sem, u.pe.at("fg", s))
            eng.tensor_scalar(k.b("t2", s), k.psum[s][1][:], k.weight("l1x_fgb"), None, ALU.add)\
               .then_inc(u.dve.sem, u.dve.one("f", s))
        for s in S:
            eng.wait_ge(u.act.sem, u.act.at("fln", s))
            eng.scalar_tensor_tensor(k.b("t2", s), k.b("t2", s), 0.0, k.b("t3", s), ALU.min, ALU.subtract)\
               .then_inc(u.dve.sem, u.dve.one("lf", s))
        for s in S:
            eng.wait_ge(u.dve.sem, u.dve.at("lf", s))
            eng.tensor_tensor_scan(k.b("t4", s), k.const("keep"), k.b("t2", s), 0.0, ALU.mult, ALU.add)\
               .then_inc(u.dve.sem, u.dve.one("cs", s))
        for s in S:
            eng.tensor_scalar(k.b("t5", s), k.psum[s][0][:], k.weight("l1x_igb"), None, ALU.add)\
               .then_inc(u.dve.sem, u.dve.one("g", s))
        for s in S:
            eng.wait_ge(u.dve.sem, u.dve.at("g", s))
            late = per_batch(k.b("t5", s))[:, :, 1:T]
            eng.tensor_tensor(late, late, per_batch(k.b("t4", s))[:, :, 0:T - 1], ALU.subtract)\
               .then_inc(u.dve.sem, u.dve.one("gs", s))
        for s in S:
            eng.wait_ge(u.dve.sem, u.dve.at("gs", s))
            eng.tensor_tensor_scan(k.b("t6", s), k.const("start"), k.b("t5", s), 0.0, ALU.add, ALU.max)\
               .then_inc(u.dve.sem, u.dve.one("m", s))
        for s in S:
            eng.wait_ge(u.dve.sem, u.dve.at("m", s))
            eng.tensor_tensor(k.b("t7", s), k.b("t4", s), k.b("t6", s), ALU.add).then_inc(u.dve.sem, u.dve.one("csm", s))
        for s in S:
            eng.wait_ge(u.pe.sem, u.pe.at("qk", s))
            for h in range(4):
                ins = eng.tensor_scalar(k.wide(s, 8, 2)[:, h * 256:(h + 1) * 256], k.psum[s][h][:, 0:256], 0.0, None, ALU.min)
            ins.then_inc(u.dve.sem, u.dve.one("dmin", s))
        for s in S:
            eng.wait_ge(u.act.sem, u.act.at("dexp", s))
            w = k.wide(s, 8, 2).rearrange("p (h q) -> p h q", q=T)
            eng.tensor_tensor(w, w, k.const("causal").unsqueeze(1).broadcast_to([128, 16, T]), ALU.mult)\
               .then_inc(u.dve.sem, u.dve.one("dmask", s))
        for s in S:
            eng.wait_ge(u.dve.sem, u.dve.at("dmask", s))
            for h in range(4):
                w = k.wide(s, 8, 2)[:, h * 256:(h + 1) * 256]
                ins = eng.scalar_tensor_tensor(w, k.psum[s][h][:, 256:512], 32 ** -0.5, w, ALU.mult, ALU.mult)
            ins.then_inc(u.dve.sem, u.dve.one("c", s))
        for s in S:
            eng.wait_ge(u.act.sem, u.act.at("absd", s))
            eng.tensor_tensor(k.b("t10", s), k.b("t10", s), k.b("t7", s), ALU.max).then_inc(u.dve.sem, u.dve.one("norm", s))
        for s in S:
            eng.wait_ge(u.dve.sem, u.dve.at("norm", s))
            eng.tensor_scalar(k.b("t10", s), k.b("t10", s), 1e-8, None, ALU.add).then_inc(u.dve.sem, u.dve.one("norme", s))
        for s in S:
            eng.wait_ge(u.dve.sem, u.dve.at("norme", s))
            eng.reciprocal(k.b("t10", s), k.b("t10", s)).then_inc(u.dve.sem, u.dve.one("nrec", s))
        for s in S:
            eng.wait_ge(u.dve.sem, u.dve.at("nrec", s))
            tile = lambda name, b: k.b(name, s).rearrange("p (t b q) -> p t b q", b=2, q=T)[:, :, b, :]
            for b in range(2):
                ins = eng.tensor_tensor(tile("t11", b), k.psum[s][b][:, 0:256].rearrange("p (t q) -> p t q", q=T),
                                        tile("t10", b), ALU.mult)
            ins.then_inc(u.dve.sem, u.dve.one("out", s))
        self.gn.dve(eng)
        for s in S:
            eng.wait_ge(u.dve.sem, u.dve.at("gn", s))
            eng.scalar_tensor_tensor(k.b("x", s), k.b("t12", s), k.out_scale[:, 0:1], k.b("x", s), ALU.mult, ALU.add)\
               .then_inc(u.dve.sem, u.dve.one("x", s))


class L3Xattn(Sub):

    def __init__(self, core, prev):
        super().__init__(core, prev)
        self.pe = core.steps("l3x_pe", [*Norm.PE, "k", "v", "q", "score", "turn", "pv"])
        self.act = core.steps("l3x_act", [*Norm.ACT, "ks", "vs", "exp", "probs"])
        self.dve = core.steps("l3x_dve", ["fill", "fillneg", *Norm.DVE, "qs", "masked", "max", "sub", "sum", "recip", "scaled", "x"])
        self.norm = Norm(core, self)

    def pe_program(self, eng):
        k, u = self.k, self
        self.norm.pe(eng)
        for s in S:
            eng.wait_ge(k.c_in[s], 16)
            eng.matmul(k.psum[s][2][:], k.weight("l3x_wk"), k.b("c", s), start=True, stop=True)\
               .then_inc(u.pe.sem, u.pe.one("k", s))
        for s in S:
            for tp in range(2):
                for b in range(2):
                    for t2 in range(2):
                        at = (2 * tp + t2) * 128 + b * T
                        mm = eng.matmul(k.psum[s][3][64 * t2:64 * t2 + 64, (2 * tp + b) * 128:(2 * tp + b + 1) * 128],
                                        k.b("c", s)[:, at:at + T], k.weight("l3x_wv"), start=True, stop=True)
            mm.then_inc(u.pe.sem, u.pe.one("v", s))
        for s in S:
            eng.wait_ge(u.dve.sem, u.dve.at("h", s))
            eng.matmul(k.psum[s][0][:], k.weight("l3x_wq"), k.b("h", s), start=True, stop=True)\
               .then_inc(u.pe.sem, u.pe.one("q", s))
        for s in S:
            eng.wait_ge(u.act.sem, u.act.at("ks", s))
            eng.wait_ge(u.dve.sem, u.dve.at("qs", s))
            for t in range(NT):
                for b in range(2):
                    at = t * 128 + b * T
                    mm = eng.matmul(k.psum[s][2][b * T:(b + 1) * T, t * T:(t + 1) * T], k.b("t5", s)[:, at:at + T],
                                    k.b("t6", s)[:, at:at + T], start=True, stop=True)
            mm.then_inc(u.pe.sem, u.pe.one("score", s))
        for s in S:
            eng.wait_ge(u.dve.sem, u.dve.at("scaled", s))
            for tp in range(2):
                mm = eng.transpose(k.psum[s][0][:, tp * 128:(tp + 1) * 128], k.b("t11", s)[:, tp * 128:(tp + 1) * 128],
                                   k.const("ident"))
            mm.then_inc(u.pe.sem, u.pe.one("turn", s))
        for s in S:
            eng.wait_ge(u.act.sem, u.act.at("probs", s))
            eng.wait_ge(u.act.sem, u.act.at("vs", s))
            for tp in range(2):
                for b in range(2):
                    for t2 in range(2):
                        rows = slice(64 * t2, 64 * t2 + 64)
                        mm = eng.matmul(k.psum[s][1 + t2][:, (2 * tp + b) * T:(2 * tp + b + 1) * T],
                                        k.b("t7", s, rows)[:, (2 * tp + b) * 128:(2 * tp + b + 1) * 128],
                                        k.b("t12", s, rows)[:, tp * 128 + b * T:tp * 128 + (b + 1) * T], start=True, stop=True)
            mm.then_inc(u.pe.sem, u.pe.one("pv", s))

    def act_program(self, eng):
        k, u = self.k, self
        self.norm.act(eng)
        for s in S:
            eng.wait_ge(u.pe.sem, u.pe.at("k", s))
            eng.activation(k.b("t6", s), k.psum[s][2][:], ACT.Identity, bias=k.weight("l3x_bk"))\
               .then_inc(u.act.sem, u.act.one("ks", s))
        for s in S:
            eng.wait_ge(u.pe.sem, u.pe.at("v", s))
            eng.copy(k.b("t7", s), k.psum[s][3][:]).then_inc(u.act.sem, u.act.one("vs", s))
        for s in S:
            eng.wait_ge(u.dve.sem, u.dve.at("sub", s))
            eng.activation(k.b("t11", s)[:, 0:256], k.b("t11", s)[:, 0:256], ACT.Exp).then_inc(u.act.sem, u.act.one("exp", s))
        for s in S:
            eng.wait_ge(u.pe.sem, u.pe.at("turn", s))
            eng.copy(k.b("t12", s)[:, 0:256], k.psum[s][0][:, 0:256]).then_inc(u.act.sem, u.act.one("probs", s))

    def dve_program(self, eng):
        k, u = self.k, self
        for s in S:
            eng.wait_ge(k.mask_in[s], 80)
            eng.tensor_scalar(k.fill1[s][:], k.fill1[s][:].bitcast(I32), 0.0, 1.0, ALU.not_equal, ALU.subtract)\
               .then_inc(u.dve.sem, u.dve.one("fill", s))
        for s in S:
            eng.wait_ge(u.dve.sem, u.dve.at("fill", s))
            eng.tensor_scalar(k.fill1[s][:], k.fill1[s][:], 3e38, None, ALU.mult).then_inc(u.dve.sem, u.dve.one("fillneg", s))
        self.norm.dve(eng)
        for s in S:
            eng.wait_ge(u.pe.sem, u.pe.at("q", s))
            eng.tensor_scalar(k.b("t5", s), k.psum[s][0][:], k.weight("l3x_bq"), None, ALU.add)\
               .then_inc(u.dve.sem, u.dve.one("qs", s))
        w = lambda s: k.b("t11", s)[:, 0:256]
        tiles = lambda s: w(s).rearrange("p (t j) -> p t j", j=T)
        for s in S:
            eng.wait_ge(u.pe.sem, u.pe.at("score", s))
            eng.wait_ge(u.dve.sem, u.dve.at("fillneg", s))
            eng.scalar_tensor_tensor(w(s), k.psum[s][2][:, 0:256], 128 ** -0.5, k.fill1[s][:], ALU.mult, ALU.add)\
               .then_inc(u.dve.sem, u.dve.one("masked", s))
        for s in S:
            eng.wait_ge(u.dve.sem, u.dve.at("masked", s))
            eng.tensor_reduce(k.small[s][:, 0:4], tiles(s), AX.X, ALU.max).then_inc(u.dve.sem, u.dve.one("max", s))
        for s in S:
            eng.wait_ge(u.dve.sem, u.dve.at("max", s))
            eng.tensor_tensor(tiles(s), tiles(s), k.small[s][:, 0:4].unsqueeze(2).broadcast_to([128, 4, T]), ALU.subtract)\
               .then_inc(u.dve.sem, u.dve.one("sub", s))
        for s in S:
            eng.wait_ge(u.act.sem, u.act.at("exp", s))
            eng.tensor_reduce(k.small[s][:, 4:8], tiles(s), AX.X, ALU.add).then_inc(u.dve.sem, u.dve.one("sum", s))
        for s in S:
            eng.wait_ge(u.dve.sem, u.dve.at("sum", s))
            eng.reciprocal(k.small[s][:, 8:12], k.small[s][:, 4:8]).then_inc(u.dve.sem, u.dve.one("recip", s))
        for s in S:
            eng.wait_ge(u.dve.sem, u.dve.at("recip", s))
            eng.tensor_tensor(tiles(s), tiles(s), k.small[s][:, 8:12].unsqueeze(2).broadcast_to([128, 4, T]), ALU.mult)\
               .then_inc(u.dve.sem, u.dve.one("scaled", s))
        for s in S:
            eng.wait_ge(u.pe.sem, u.pe.at("pv", s))
            for t2 in range(2):
                to = k.b("x", s).rearrange("p (a t n) -> p a t n", t=2, n=128)[:, :, t2, :]
                ins = eng.scalar_tensor_tensor(to, k.psum[s][1 + t2][:, 0:256].rearrange("p (a n) -> p a n", n=128),
                                               k.weight("l3x_bv"), to, ALU.add, ALU.add)
            ins.then_inc(u.dve.sem, u.dve.one("x", s))


class Attention16:

    def __init__(self, core, sub, masked, scale, values, value_w, value_bias, out_w, out_bias):
        self.k, self.sub, self.masked, self.scale = core, sub, masked, scale
        self.values, self.value_w, self.value_bias, self.out_w, self.out_bias = values, value_w, value_bias, out_w, out_bias

    PE = [n for j in range(8) for n in ([f"v{j}"] if j % 2 == 0 else []) + [f"score{j}", f"turn{j}", f"pv{j}"]
          + ([f"back{j}"] if j % 2 else [])] + ["wo"]
    ACT = [n for j in range(8) for n in ([f"vs{j}"] if j % 2 == 0 else []) + [f"exp{j}", f"probs{j}"]
           + ([f"outs{j}"] if j % 2 else [])]
    DVE = ["spread"] + [n for j in range(8) for n in (f"fill{j}", f"max{j}", f"sub{j}", f"recip{j}", f"out{j}")] + ["x"]

    def pe(self, eng):
        k, u = self.k, self.sub
        vw = k.weight(self.value_w[0])[:, self.value_w[1]:self.value_w[1] + D]
        for j in range(8):
            t, half = j // 2, j % 2
            if half == 0:
                for s in S:
                    if j >= 2:
                        eng.wait_ge(u.act.sem, u.act.at(f"probs{j - 1}", s))
                        eng.wait_ge(u.pe.sem, u.pe.at(f"pv{j - 1}", s))
                    else:
                        eng.wait_ge(u.dve.sem, u.dve.at("spread", s))
                    for b in range(2):
                        at = t * 128 + b * T
                        for h2 in range(2):
                            mm = eng.matmul(k.psum[s][1][64 * h2:64 * h2 + 64, b * 128:(b + 1) * 128],
                                            k.b(self.values, s)[:, at:at + T], vw, start=True, stop=True)
                    mm.then_inc(u.pe.sem, u.pe.one(f"v{j}", s))
            for s in S:
                eng.wait_ge(u.dve.sem, u.dve.at(f"sub{j - 1}" if j else "spread", s))
                if half == 0 and j:
                    eng.wait_ge(u.act.sem, u.act.at(f"outs{j - 1}", s))
                for g in (2 * half, 2 * half + 1):
                    rows = slice(32 * g, 32 * g + 32)
                    for b in range(2):
                        at = t * 128 + b * T
                        mm = eng.matmul(k.psum[s][2 * (g % 2)][b * T:(b + 1) * T, 0:256], k.b("t5", s, rows)[:, at:at + T],
                                        k.wide(s, 7, 4, rows)[:, (2 * t + b) * 256:(2 * t + b + 1) * 256],
                                        start=True, stop=True, tile_position=(32 * g, 64 * b))
                mm.then_inc(u.pe.sem, u.pe.one(f"score{j}", s))
            for s in S:
                eng.wait_ge(u.act.sem, u.act.at(f"exp{j}", s))
                for p in range(4):
                    mm = eng.transpose(k.psum[s][1][:, p * 128:(p + 1) * 128],
                                       k.b("t11", s)[:, p * 128:(p + 1) * 128], k.const("ident"))
                mm.then_inc(u.pe.sem, u.pe.one(f"turn{j}", s))
            for s in S:
                eng.wait_ge(u.act.sem, u.act.at(f"probs{j}", s))
                if half == 0 and j:
                    eng.wait_ge(u.dve.sem, u.dve.at(f"out{j - 1}", s))
                vbd = k.vbd[s].ap().rearrange("p (b q c) -> p b q c", b=2, c=18)
                for p in range(4):
                    for b in range(2):
                        mm = eng.matmul(k.psum[s][3][b * T:(b + 1) * T, half * 72 + p * 18:half * 72 + (p + 1) * 18],
                                        k.b("t12", s)[:, p * 128 + b * T:p * 128 + (b + 1) * T],
                                        vbd[:, b, 4 * half + p, :], start=True, stop=True)
                mm.then_inc(u.pe.sem, u.pe.one(f"pv{j}", s))
            if half:
                for s in S:
                    eng.wait_ge(u.dve.sem, u.dve.at(f"out{j}", s))
                    eng.transpose(k.psum[s][0][:, 0:128], k.b("t13", s)[:, 0:128], k.const("ident"))\
                       .then_inc(u.pe.sem, u.pe.one(f"back{j}", s))
        for s in S:
            eng.wait_ge(u.act.sem, u.act.at("outs7", s))
            eng.matmul(k.psum[s][1][:], k.weight(self.out_w), k.b("t14", s), start=True, stop=True)\
               .then_inc(u.pe.sem, u.pe.one("wo", s))

    def act(self, eng):
        k, u = self.k, self.sub
        for j in range(8):
            t, half = j // 2, j % 2
            if half == 0:
                for s in S:
                    eng.wait_ge(u.pe.sem, u.pe.at(f"v{j}", s))
                    for h2 in range(2):
                        rows = slice(64 * h2, 64 * h2 + 64)
                        ins = eng.copy(k.vbd[s][rows, :].rearrange("p (q c) -> p q c", c=18)[:, :, 9 * h2:9 * h2 + 8],
                                       k.psum[s][1][rows, 0:256].rearrange("p (q c) -> p q c", c=16)[:, :, 8 * h2:8 * h2 + 8])
                    ins.then_inc(u.act.sem, u.act.one(f"vs{j}", s))
            for s in S:
                eng.wait_ge(u.dve.sem, u.dve.at(f"sub{j}", s))
                eng.activation(k.b("t11", s), k.b("t11", s), ACT.Exp, scale=1.0 if self.masked else self.scale)\
                   .then_inc(u.act.sem, u.act.one(f"exp{j}", s))
            for s in S:
                eng.wait_ge(u.pe.sem, u.pe.at(f"turn{j}", s))
                eng.copy(k.b("t12", s), k.psum[s][1][:]).then_inc(u.act.sem, u.act.one(f"probs{j}", s))
            if half:
                for s in S:
                    eng.wait_ge(u.pe.sem, u.pe.at(f"back{j}", s))
                    to = k.b("t14", s)[:, t * 128:(t + 1) * 128]
                    if self.value_bias:
                        ins = eng.activation(to, k.psum[s][0][:, 0:128], ACT.Identity, bias=k.weight(self.value_bias))
                    else:
                        ins = eng.copy(to, k.psum[s][0][:, 0:128])
                    ins.then_inc(u.act.sem, u.act.one(f"outs{j}", s))

    def dve(self, eng, keys_ready):
        k, u = self.k, self.sub
        for s in S:
            keys_ready(eng, s)
            eng.tensor_tensor(k.wide(s, 7, 4).rearrange("p (b h j) -> p b h j", h=4, j=T),
                              per_batch(k.b("t6", s)).unsqueeze(2).broadcast_to([128, NB, 4, T]),
                              k.const("head4").unsqueeze(1).unsqueeze(3).broadcast_to([128, NB, 4, T]), ALU.mult)\
               .then_inc(u.dve.sem, u.dve.one("spread", s))
        heads = lambda ap: ap.rearrange("p (h j) -> p h j", j=T)
        for j in range(8):
            t, half = j // 2, j % 2
            for s in S:
                eng.wait_ge(u.pe.sem, u.pe.at(f"score{j}", s))
                if self.masked:
                    for c in range(2):
                        ins = eng.scalar_tensor_tensor(
                            heads(k.b("t11", s)[:, c * 256:(c + 1) * 256]), heads(k.psum[s][2 * c][:, 0:256]), self.scale,
                            k.fill0[s][:, t * T:(t + 1) * T].unsqueeze(1).broadcast_to([128, 4, T]), ALU.mult, ALU.add)
                else:
                    for c in range(2):
                        ins = eng.tensor_copy(k.b("t11", s)[:, c * 256:(c + 1) * 256], k.psum[s][2 * c][:, 0:256])
                ins.then_inc(u.dve.sem, u.dve.one(f"fill{j}", s))
            for s in S:
                eng.wait_ge(u.dve.sem, u.dve.at(f"fill{j}", s))
                eng.tensor_reduce(k.small[s][:, 0:8], heads(k.b("t11", s)), AX.X, ALU.max)\
                   .then_inc(u.dve.sem, u.dve.one(f"max{j}", s))
            for s in S:
                eng.wait_ge(u.dve.sem, u.dve.at(f"max{j}", s))
                eng.tensor_tensor(heads(k.b("t11", s)), heads(k.b("t11", s)),
                                  k.small[s][:, 0:8].unsqueeze(2).broadcast_to([128, 8, T]), ALU.subtract)\
                   .then_inc(u.dve.sem, u.dve.one(f"sub{j}", s))
            outs = lambda s: k.psum[s][3][:, half * 72:half * 72 + 72].rearrange("p (h c) -> p h c", c=9)
            for s in S:
                eng.wait_ge(u.pe.sem, u.pe.at(f"pv{j}", s))
                eng.reciprocal(k.small[s][:, 8:16], outs(s)[:, :, 8]).then_inc(u.dve.sem, u.dve.one(f"recip{j}", s))
            for s in S:
                eng.wait_ge(u.dve.sem, u.dve.at(f"recip{j}", s))
                eng.tensor_tensor(k.b("t13", s)[:, half * T:half * T + T].rearrange("p (h c) -> p h c", c=8),
                                  outs(s)[:, :, 0:8], k.small[s][:, 8:16].unsqueeze(2).broadcast_to([128, 8, 8]), ALU.mult)\
                   .then_inc(u.dve.sem, u.dve.one(f"out{j}", s))
        for s in S:
            eng.wait_ge(u.pe.sem, u.pe.at("wo", s))
            eng.scalar_tensor_tensor(k.b("x", s), k.psum[s][1][:], k.weight(self.out_bias), k.b("x", s), ALU.add, ALU.add)\
               .then_inc(u.dve.sem, u.dve.one("x", s))


class L2Xattn(Sub):

    def __init__(self, core, prev):
        super().__init__(core, prev)
        self.pe = core.steps("l2x_pe", [*TwiceNorm.PE, "q", "k", *Attention16.PE])
        self.act = core.steps("l2x_act", [*TwiceNorm.ACT, "qs", *Attention16.ACT])
        self.dve = core.steps("l2x_dve", ["fill", "fillneg", "keymask", *TwiceNorm.DVE, "kvn", "ks", *Attention16.DVE])
        self.norm = TwiceNorm(core, self, "l2x_gx", "l2x_bx")
        self.att = Attention16(core, self, True, 8 ** -0.5, "t4", ("l2x_wkv", D), None, "l2x_wo", "l2x_bo")

    def pe_program(self, eng):
        k, u = self.k, self
        self.norm.pe(eng)
        for s in S:
            eng.wait_ge(u.dve.sem, u.dve.at("latb", s))
            eng.matmul(k.psum[s][0][:], k.weight("l2x_wq"), k.b("t3", s), start=True, stop=True)\
               .then_inc(u.pe.sem, u.pe.one("q", s))
        for s in S:
            eng.wait_ge(u.dve.sem, u.dve.at("kvn", s))
            eng.matmul(k.psum[s][2][:], k.weight("l2x_wkv")[:, 0:D], k.b("t4", s), start=True, stop=True)\
               .then_inc(u.pe.sem, u.pe.one("k", s))
        for s in S:
            eng.wait_ge(u.act.sem, u.act.at("qs", s))
        self.att.pe(eng)

    def act_program(self, eng):
        k, u = self.k, self
        self.norm.act(eng)
        for s in S:
            eng.wait_ge(u.pe.sem, u.pe.at("q", s))
            eng.copy(k.b("t5", s), k.psum[s][0][:]).then_inc(u.act.sem, u.act.one("qs", s))
        self.att.act(eng)

    def dve_program(self, eng):
        k, u = self.k, self
        for s in S:
            eng.wait_ge(k.mask_in[s], 80)
            eng.tensor_scalar(k.fill0[s][:], k.fill0[s][:].bitcast(I32), 0.0, 1.0, ALU.not_equal, ALU.subtract)\
               .then_inc(u.dve.sem, u.dve.one("fill", s))
        for s in S:
            eng.wait_ge(u.dve.sem, u.dve.at("fill", s))
            eng.tensor_scalar(k.fill0[s][:], k.fill0[s][:], 1e9, None, ALU.mult)\
               .then_inc(u.dve.sem, u.dve.one("fillneg", s))
        for s in S:
            eng.tensor_scalar(k.keymask[s][:], k.keymask[s][:].bitcast(I32), 0.0, None, ALU.not_equal)\
               .then_inc(u.dve.sem, u.dve.one("keymask", s))
        self.norm.dve(eng)
        for s in S:
            eng.tensor_scalar(k.b("t4", s), k.b("cn", s), k.weight("l2x_gkv"), k.weight("l2x_bkv"),
                              ALU.mult, ALU.add).then_inc(u.dve.sem, u.dve.one("kvn", s))
        for s in S:
            eng.wait_ge(u.pe.sem, u.pe.at("k", s))
            eng.wait_ge(u.dve.sem, u.dve.at("keymask", s))
            eng.tensor_tensor(k.b("t6", s), k.psum[s][2][:], k.keymask[s][:], ALU.mult)\
               .then_inc(u.dve.sem, u.dve.one("ks", s))
        self.att.dve(eng, lambda eng, s: eng.wait_ge(u.dve.sem, u.dve.at("ks", s)))


class L3Attn(Sub):

    def __init__(self, core, prev):
        super().__init__(core, prev)
        self.pe = core.steps("l3a_pe", [*Norm.PE, "q", "qr", "k", "kr", *Attention16.PE])
        self.act = core.steps("l3a_act", [*Norm.ACT, *Attention16.ACT])
        self.dve = core.steps("l3a_dve", [*Norm.DVE, "qc", "qs", "qrope", "kc", "ks", "krope", *Attention16.DVE])
        self.norm = Norm(core, self)
        self.att = Attention16(core, self, False, 8 ** -0.5, "h", ("l3a_wv", 0), "l3a_bv", "l3a_wo", "l3a_bo")

    def pe_program(self, eng):
        k, u = self.k, self
        self.norm.pe(eng)
        for bank, name, w in ((0, "q", k.weight("l3a_wq")), (1, "qr", k.rotated[:, 0:D]), (2, "k", k.weight("l3a_wk")),
                              (3, "kr", k.rotated[:, D:2 * D])):
            for s in S:
                if name == "q":
                    eng.wait_ge(u.dve.sem, u.dve.at("h", s))
                eng.matmul(k.psum[s][bank][:], w, k.b("h", s), start=True, stop=True)\
                   .then_inc(u.pe.sem, u.pe.one(name, s))
        self.att.pe(eng)

    def act_program(self, eng):
        self.norm.act(eng)
        self.att.act(eng)

    def dve_program(self, eng):
        k, u = self.k, self
        self.norm.dve(eng)
        over = lambda table: k.const(table).unsqueeze(1).broadcast_to([128, NB, T])
        for bank, a, out, part, bias, rbias in ((0, "q", "t5", "t4", "l3a_bq", 0), (2, "k", "t6", "t7", "l3a_bk", 1)):
            for s in S:
                eng.wait_ge(u.pe.sem, u.pe.at(a, s))
                eng.scalar_tensor_tensor(per_batch(k.b(out, s)), per_batch(k.psum[s][bank][:]), k.weight(bias),
                                         over("rcos"), ALU.add, ALU.mult).then_inc(u.dve.sem, u.dve.one(a + "c", s))
            for s in S:
                eng.wait_ge(u.pe.sem, u.pe.at(a + "r", s))
                eng.scalar_tensor_tensor(per_batch(k.b(part, s)), per_batch(k.psum[s][bank + 1][:]),
                                         k.rot_bias[:, rbias:rbias + 1], over("rsin"), ALU.add, ALU.mult)\
                   .then_inc(u.dve.sem, u.dve.one(a + "s", s))
            for s in S:
                eng.wait_ge(u.dve.sem, u.dve.at(a + "s", s))
                eng.tensor_tensor(k.b(out, s), k.b(out, s), k.b(part, s), ALU.add)\
                   .then_inc(u.dve.sem, u.dve.one(a + "rope", s))
        self.att.dve(eng, lambda eng, s: eng.wait_ge(u.dve.sem, u.dve.at("krope", s)))


class L2Attn(Sub):

    ROPE = ["q0", "q1", "q2", "q3", "k", "ks"]

    def __init__(self, core, prev):
        super().__init__(core, prev)
        rope = self.ROPE
        pe = [*Norm.PE, "ckv", "cq"] + ["r_" + n for n in rope] + [f"{a}{p}" for p in range(4) for a in "qk"]
        act = [*Norm.ACT, "ckv", "cq"] + [f"{a}_{n}" for n in rope for a in ("abs", "exp", "ln")] + [f"q{p}" for p in range(4)]
        dve = [*Norm.DVE] + [n for r in rope for n in (f"mu_{r}", f"rot_{r}")] + ["kr"] + [f"k{p}" for p in range(4)]
        for t in range(4):
            pe += [f"v{t}_0", f"v{t}_1", f"score{t}", f"turn{t}", f"pv{t}", f"back{t}"]
            act += [f"v{t}_0", f"exp{t}", f"probs{t}", f"outs{t}"]
            dve += [f"v{t}_1", f"max{t}", f"sub{t}", f"recip{t}", f"out{t}"]
        self.pe = core.steps("l2a_pe", pe + ["wo"])
        self.act = core.steps("l2a_act", act)
        self.dve = core.steps("l2a_dve", dve + ["x"])
        self.norm = Norm(core, self)

    QR = ("t0", "t1", "t13", "t14")

    def pe_program(self, eng):
        k, u = self.k, self
        self.norm.pe(eng)
        ckv, cq = (lambda s: k.b("t2", s, slice(0, 32))), (lambda s: k.b("t3", s, slice(0, 64)))
        for s in S:
            eng.wait_ge(u.dve.sem, u.dve.at("h", s))
            eng.matmul(k.psum[s][2][0:32, :], k.weight("l2a_dkv"), k.b("h", s), start=True, stop=True)\
               .then_inc(u.pe.sem, u.pe.one("ckv", s))
        for s in S:
            eng.matmul(k.psum[s][3][0:64, :], k.weight("l2a_dq"), k.b("h", s), start=True, stop=True)\
               .then_inc(u.pe.sem, u.pe.one("cq", s))
        for j, n in enumerate(self.ROPE):
            for s in S:
                if j == 0:
                    eng.wait_ge(u.act.sem, u.act.at("cq", s))
                if j >= 2:
                    eng.wait_ge(u.dve.sem, u.dve.at("mu_" + self.ROPE[j - 2], s))
                if j < 4:
                    w = k.weight("l2a_qrq", slice(0, 64))[:, j * 128:(j + 1) * 128]
                    mm = eng.matmul(k.psum[s][j % 2][:], w, cq(s), start=True, stop=True)
                else:
                    mm = eng.matmul(k.psum[s][j % 2][:], k.weight(("l2a_kr", "l2a_krs")[j - 4]), k.b("h", s),
                                    start=True, stop=True)
                mm.then_inc(u.pe.sem, u.pe.one("r_" + n, s))
        for p in range(4):
            for s in S:
                if p < 2:
                    eng.wait_ge(u.dve.sem, u.dve.at("mu_ks", s))
                else:
                    eng.wait_ge(u.act.sem, u.act.at(f"q{p - 2}", s))
                eng.matmul(k.psum[s][p % 2][:], k.weight("l2a_uq", slice(0, 64))[:, p * 128:(p + 1) * 128], cq(s),
                           start=True, stop=True).then_inc(u.pe.sem, u.pe.one(f"q{p}", s))
            for s in S:
                if p >= 2:
                    eng.wait_ge(u.dve.sem, u.dve.at(f"k{p - 2}", s))
                eng.matmul(k.psum[s][2 + p % 2][:], k.weight("l2a_uk", slice(0, 32))[:, p * 128:(p + 1) * 128], ckv(s),
                           start=True, stop=True).then_inc(u.pe.sem, u.pe.one(f"k{p}", s))
        for t in range(4):
            for b in range(2):
                for s in S:
                    if t == 0:
                        eng.wait_ge(u.act.sem, u.act.at("q3", s))
                        eng.wait_ge(u.dve.sem, u.dve.at("k3", s))
                    elif b == 0:
                        eng.wait_ge(u.act.sem, u.act.at(f"outs{t - 1}", s))
                    else:
                        eng.wait_ge(u.dve.sem, u.dve.at(f"out{t - 1}", s))
                    at = t * 128 + b * T
                    for h2 in range(2):
                        mm = eng.matmul(k.psum[s][1 + 2 * b][64 * h2:64 * h2 + 64, :], ckv(s)[:, at:at + T],
                                        k.weight("l2a_uv", slice(0, 32)), start=True, stop=True)
                    mm.then_inc(u.pe.sem, u.pe.one(f"v{t}_{b}", s))
            for s in S:
                if t:
                    eng.wait_ge(u.dve.sem, u.dve.at(f"out{t - 1}", s))
                else:
                    eng.wait_ge(u.dve.sem, u.dve.at("k3", s))
                for h in range(8):
                    half = slice(64 * (h % 2), 64 * (h % 2) + 64)
                    for b in range(2):
                        at = t * 128 + b * T
                        out = k.psum[s][2 * (h % 2)][b * T:(b + 1) * T, h // 2 * T:(h // 2 + 1) * T]
                        eng.matmul(out, k.b(f"t{5 + h // 2}", s, half)[:, at:at + T],
                                   k.b(f"t{9 + h // 2}", s, half)[:, at:at + T], start=True, stop=False)
                        mm = eng.matmul(out, k.b(self.QR[h // 2], s, half)[:, at:at + T],
                                        k.b("t4", s, half)[:, at:at + T], start=False, stop=True)
                mm.then_inc(u.pe.sem, u.pe.one(f"score{t}", s))
            for s in S:
                eng.wait_ge(u.act.sem, u.act.at(f"exp{t}", s))
                for p in range(4):
                    mm = eng.transpose(k.psum[s][1][:, p * 128:(p + 1) * 128],
                                       k.b("t15", s)[:, p * 128:(p + 1) * 128], k.const("ident"))
                mm.then_inc(u.pe.sem, u.pe.one(f"turn{t}", s))
            for s in S:
                eng.wait_ge(u.act.sem, u.act.at(f"probs{t}", s))
                eng.wait_ge(u.dve.sem, u.dve.at(f"v{t}_1", s))
                for h in range(8):
                    half = slice(64 * (h % 2), 64 * (h % 2) + 64)
                    for b in range(2):
                        vb = k.vb[s][half, b * 520:(b + 1) * 520].rearrange("p (h c) -> p h c", c=65)
                        mm = eng.matmul(k.psum[s][2 + h % 2][b * T:(b + 1) * T, h // 2 * 65:(h // 2 + 1) * 65],
                                        k.b("t3", s, half)[:, h // 2 * 128 + b * T:h // 2 * 128 + (b + 1) * T],
                                        vb[:, h, :], start=True, stop=True)
                mm.then_inc(u.pe.sem, u.pe.one(f"pv{t}", s))
            for s in S:
                eng.wait_ge(u.dve.sem, u.dve.at(f"out{t}", s))
                for p in range(4):
                    mm = eng.transpose(k.psum[s][1][:, p * 128:(p + 1) * 128],
                                       k.b("t15", s)[:, p * 128:(p + 1) * 128], k.const("ident"))
                mm.then_inc(u.pe.sem, u.pe.one(f"back{t}", s))
        for s in S:
            eng.wait_ge(u.act.sem, u.act.at("outs3", s))
            for p in range(4):
                mm = eng.matmul(k.psum[s][0][:], k.weight("l2a_out")[:, p * 128:(p + 1) * 128], k.b(f"t{5 + p}", s),
                                start=p == 0, stop=p == 3)
            mm.then_inc(u.pe.sem, u.pe.one("wo", s))

    def act_program(self, eng):
        k, u = self.k, self
        self.norm.act(eng)
        for s in S:
            eng.wait_ge(u.pe.sem, u.pe.at("ckv", s))
            eng.copy(k.b("t2", s, slice(0, 32)), k.psum[s][2][0:32, :]).then_inc(u.act.sem, u.act.one("ckv", s))
        for s in S:
            eng.wait_ge(u.pe.sem, u.pe.at("cq", s))
            eng.copy(k.b("t3", s, slice(0, 64)), k.psum[s][3][0:64, :]).then_inc(u.act.sem, u.act.one("cq", s))
        for j, n in enumerate(self.ROPE):
            part = self.QR[j] if j < 4 else ("t15", "t5")[j - 4]
            for s in S:
                eng.wait_ge(u.pe.sem, u.pe.at("r_" + n, s))
                eng.wait_ge(u.dve.sem, u.dve.at("h", s))
                eng.activation(k.b(part, s), k.psum[s][j % 2][:], ACT.Abs).then_inc(u.act.sem, u.act.one("abs_" + n, s))
            for s in S:
                eng.wait_ge(u.act.sem, u.act.at("abs_" + n, s))
                eng.activation(k.b(part, s), k.b(part, s), ACT.Exp, scale=-1.0).then_inc(u.act.sem, u.act.one("exp_" + n, s))
            for s in S:
                eng.wait_ge(u.act.sem, u.act.at("exp_" + n, s))
                eng.activation(k.b(part, s), k.b(part, s), ACT.Ln, bias=1.0).then_inc(u.act.sem, u.act.one("ln_" + n, s))
        for p in range(4):
            for s in S:
                eng.wait_ge(u.pe.sem, u.pe.at(f"q{p}", s))
                eng.wait_ge(u.dve.sem, u.dve.at("kr", s))
                eng.copy(k.b(f"t{5 + p}", s), k.psum[s][p % 2][:]).then_inc(u.act.sem, u.act.one(f"q{p}", s))
        for t in range(4):
            for s in S:
                eng.wait_ge(u.pe.sem, u.pe.at(f"v{t}_0", s))
                eng.copy(k.vb[s][:, 0:520].rearrange("p (h c) -> p h c", c=65)[:, :, 0:64],
                         k.psum[s][1][:].rearrange("p (h c) -> p h c", c=64)).then_inc(u.act.sem, u.act.one(f"v{t}_0", s))
            for s in S:
                eng.wait_ge(u.dve.sem, u.dve.at(f"sub{t}", s))
                eng.activation(k.b("t15", s), k.b("t15", s), ACT.Exp, scale=96 ** -0.5)\
                   .then_inc(u.act.sem, u.act.one(f"exp{t}", s))
            for s in S:
                eng.wait_ge(u.pe.sem, u.pe.at(f"turn{t}", s))
                eng.copy(k.b("t3", s), k.psum[s][1][:]).then_inc(u.act.sem, u.act.one(f"probs{t}", s))
            for s in S:
                eng.wait_ge(u.pe.sem, u.pe.at(f"back{t}", s))
                eng.copy(k.wide(s, 5, 4).rearrange("p (q n) -> p q n", n=G)[:, :, t * 128:(t + 1) * 128],
                         k.psum[s][1][:].rearrange("p (q n) -> p q n", n=128)).then_inc(u.act.sem, u.act.one(f"outs{t}", s))

    def dve_program(self, eng):
        k, u = self.k, self
        self.norm.dve(eng)
        over = lambda table: table.unsqueeze(1).broadcast_to([128, NB, T])
        for j, n in enumerate(self.ROPE):
            part = self.QR[j] if j < 4 else ("t15", "t5")[j - 4]
            table = k.pope[:, 0:T] if j < 4 else k.pope[:, (j - 3) * T:(j - 2) * T]
            for s in S:
                eng.wait_ge(u.act.sem, u.act.at("ln_" + n, s))
                eng.scalar_tensor_tensor(k.b(part, s), k.psum[s][j % 2][:], 0.0, k.b(part, s), ALU.max, ALU.add)\
                   .then_inc(u.dve.sem, u.dve.one("mu_" + n, s))
            for s in S:
                eng.wait_ge(u.dve.sem, u.dve.at("mu_" + n, s))
                eng.tensor_tensor(per_batch(k.b(part, s)), per_batch(k.b(part, s)), over(table), ALU.mult)\
                   .then_inc(u.dve.sem, u.dve.one("rot_" + n, s))
        for s in S:
            eng.wait_ge(u.dve.sem, u.dve.at("rot_ks", s))
            eng.tensor_tensor(k.b("t4", s), k.b("t15", s), k.b("t5", s), ALU.add).then_inc(u.dve.sem, u.dve.one("kr", s))
        for p in range(4):
            for s in S:
                eng.wait_ge(u.pe.sem, u.pe.at(f"k{p}", s))
                eng.tensor_copy(k.b(f"t{9 + p}", s), k.psum[s][2 + p % 2][:]).then_inc(u.dve.sem, u.dve.one(f"k{p}", s))
        for t in range(4):
            for s in S:
                eng.wait_ge(u.pe.sem, u.pe.at(f"v{t}_1", s))
                eng.tensor_copy(k.vb[s][:, 520:1040].rearrange("p (h c) -> p h c", c=65)[:, :, 0:64],
                                k.psum[s][3][:].rearrange("p (h c) -> p h c", c=64))\
                   .then_inc(u.dve.sem, u.dve.one(f"v{t}_1", s))
            heads = lambda bank: bank[:, 0:256].rearrange("p (q j) -> p q j", j=T)
            sm = lambda s, c: k.small[s][:, 0:16].rearrange("p (a q o) -> p a q o", a=2, o=2)[:, :, :, c]
            mine = lambda s, c: k.b("t15", s).rearrange("p (q o j) -> p q o j", o=2, j=T)[:, :, c, :]
            for s in S:
                eng.wait_ge(u.pe.sem, u.pe.at(f"score{t}", s))
                for c in range(2):
                    ins = eng.tensor_reduce(sm(s, c)[:, 0], heads(k.psum[s][2 * c]), AX.X, ALU.max)
                ins.then_inc(u.dve.sem, u.dve.one(f"max{t}", s))
            for s in S:
                eng.wait_ge(u.dve.sem, u.dve.at(f"max{t}", s))
                if t:
                    eng.wait_ge(u.pe.sem, u.pe.at(f"back{t - 1}", s))
                for c in range(2):
                    ins = eng.tensor_tensor(mine(s, c), heads(k.psum[s][2 * c]),
                                            sm(s, c)[:, 0].unsqueeze(2).broadcast_to([128, 4, T]), ALU.subtract)
                ins.then_inc(u.dve.sem, u.dve.one(f"sub{t}", s))
            outs = lambda s, c: k.psum[s][2 + c][:, 0:260].rearrange("p (q c) -> p q c", c=65)
            for s in S:
                eng.wait_ge(u.pe.sem, u.pe.at(f"pv{t}", s))
                for c in range(2):
                    ins = eng.reciprocal(sm(s, c)[:, 1], outs(s, c)[:, :, 64])
                ins.then_inc(u.dve.sem, u.dve.one(f"recip{t}", s))
            for s in S:
                eng.wait_ge(u.dve.sem, u.dve.at(f"recip{t}", s))
                for c in range(2):
                    ins = eng.tensor_tensor(mine(s, c), outs(s, c)[:, :, 0:64],
                                            sm(s, c)[:, 1].unsqueeze(2).broadcast_to([128, 4, T]), ALU.mult)
                ins.then_inc(u.dve.sem, u.dve.one(f"out{t}", s))
        for s in S:
            eng.wait_ge(u.pe.sem, u.pe.at("wo", s))
            eng.tensor_tensor(k.b("x", s), k.psum[s][0][:], k.b("x", s), ALU.add).then_inc(u.dve.sem, u.dve.one("x", s))


class L1Attn(Sub):

    PAIRS = 16

    def __init__(self, core, prev):
        super().__init__(core, prev)
        five = range(5)
        n = range(self.PAIRS)
        self.pe = core.steps("l1a_pe", [*Norm.PE, "w1", "x0", "x0e"] + [f"mu{j}" for j in five]
                             + ["r", "ww1", "k", "ww2", "v", "g", "bonus"]
                             + [a for j in range(17) for a in ([f"vb{j}"] if j < 16 else []) + ([f"os{j - 1}"] if j else [])]
                             + [*GroupNorm.PE, "y"])
        self.act = core.steps("l1a_act", [*Norm.ACT, "w1", "x1", "x1e", "r", "ww1", "ks", "ew", "wd", "vs", "silu", *GroupNorm.ACT])
        self.dve = core.steps("l1a_dve", [*Norm.DVE, "delta", "delta0", "lerp"] + [f"{a}{j}" for j in five for a in ("m", "in")]
                              + ["zeros", "ksh", "rbk", "xv", "bv"] + [f"{a}{j}" for j in n for a in ("kv", "scan", "rt")]
                              + ["o", *GroupNorm.DVE, "gnw", "gated", "x"])
        self.norm = Norm(core, self)
        self.gn = GroupNorm(core, self, "t6", lambda eng, s: eng.wait_ge(self.dve.sem, self.dve.at("o", s)))

    def pe_program(self, eng):
        k, u = self.k, self
        self.norm.pe(eng)
        low = slice(0, 32)
        for s in S:
            eng.wait_ge(u.dve.sem, u.dve.at("lerp", s))
            eng.matmul(k.psum[s][2][0:32, :], k.weight("l1a_w1"), k.b("t3", s), start=True, stop=True)\
               .then_inc(u.pe.sem, u.pe.one("w1", s))
        for s in S:
            eng.wait_ge(u.act.sem, u.act.at("w1", s))
            eng.matmul(k.psum[s][0][:], k.weight("l1a_w2", low)[:, 0:128], k.b("t4", s, low), start=True, stop=True)\
               .then_inc(u.pe.sem, u.pe.one("x0", s))
        for s in S:
            eng.matmul(k.psum[s][1][0:32, :], k.weight("l1a_w2", low)[:, 128:160], k.b("t4", s, low), start=True, stop=True)\
               .then_inc(u.pe.sem, u.pe.one("x0e", s))
        for j in range(5):
            for s in S:
                if j == 0:
                    eng.wait_ge(u.act.sem, u.act.at("x1e", s))
                if j >= 2:
                    eng.wait_ge(u.dve.sem, u.dve.at(f"m{j - 2}", s))
                rows = slice(32 * j, 32 * j + 32) if j < 4 else low
                w, x1 = (k.weight("l1a_xo", rows), k.b("t5", s, rows)) if j < 4 else (k.weight("l1a_xoe", low), k.b("t6", s, low))
                eng.matmul(k.psum[s][j % 2][:], w, x1, start=True, stop=True).then_inc(u.pe.sem, u.pe.one(f"mu{j}", s))
        for name, bank, w, x, ready in (("r", 2, "l1a_r", "t7", "in0"), ("ww1", 3, "l1a_ww1", "t8", "in1"),
                                        ("k", 1, "l1a_k", "t9", "in2"), ("ww2", 0, None, None, None),
                                        ("v", 2, "l1a_v", "t10", "in3"), ("g", 3, "l1a_g", "t11", "in4")):
            for s in S:
                if name == "ww2":
                    eng.wait_ge(u.act.sem, u.act.at("ww1", s))
                    eng.wait_ge(u.dve.sem, u.dve.at("in4", s))
                    mm = eng.matmul(k.psum[s][0][:], k.weight("l1a_ww2", slice(0, 64)), k.b("t4", s, slice(0, 64)),
                                    start=True, stop=True)
                else:
                    eng.wait_ge(u.dve.sem, u.dve.at(ready, s))
                    if name == "k":
                        eng.wait_ge(u.dve.sem, u.dve.at("m3", s))
                    if name in "vg":
                        eng.wait_ge(u.act.sem, u.act.at("ww1", s))
                    out = k.psum[s][bank][0:64, :] if name == "ww1" else k.psum[s][bank][:]
                    mm = eng.matmul(out, k.weight(w), k.b(x, s), start=True, stop=True)
                mm.then_inc(u.pe.sem, u.pe.one(name, s))
        for s in S:
            eng.wait_ge(u.dve.sem, u.dve.at("rbk", s))
            eng.wait_ge(u.act.sem, u.act.at("wd", s))
            eng.matmul(k.psum[s][0][:], k.const("bonus_sum", slice(0, 64)), k.b("t14", s, slice(0, 64)),
                       start=True, stop=True).then_inc(u.pe.sem, u.pe.one("bonus", s))
        for j in range(self.PAIRS + 1):
            if j < self.PAIRS:
                for s in S:
                    if j < 2:
                        eng.wait_ge(u.dve.sem, u.dve.at("bv", s))
                    else:
                        eng.wait_ge(u.dve.sem, u.dve.at(f"kv{j - 2}", s))
                    eng.matmul(k.psum[s][j % 2][:], k.vexp[:, j * 128:(j + 1) * 128], k.b("t15", s), start=True, stop=True)\
                       .then_inc(u.pe.sem, u.pe.one(f"vb{j}", s))
            if j:
                n = j - 1
                for s in S:
                    eng.wait_ge(u.dve.sem, u.dve.at(f"rt{n}", s))
                    eng.matmul(k.psum[s][2][:], k.const("ksum")[:, 30 - 2 * n:158 - 2 * n], k.b(f"t{4 + n % 2}", s),
                               start=n == 0, stop=n == self.PAIRS - 1).then_inc(u.pe.sem, u.pe.one(f"os{n}", s))
        self.gn.pe(eng)
        for s in S:
            eng.wait_ge(u.dve.sem, u.dve.at("gated", s))
            eng.matmul(k.psum[s][0][:], k.weight("l1a_o"), k.b("t12", s), start=True, stop=True)\
               .then_inc(u.pe.sem, u.pe.one("y", s))

    def act_program(self, eng):
        k, u = self.k, self
        self.norm.act(eng)
        late = lambda name, s: per_batch(k.b(name, s))[:, :, 1:T]
        early = lambda name, s: per_batch(k.b(name, s))[:, :, 0:T - 1]
        for s in S:
            eng.wait_ge(u.pe.sem, u.pe.at("w1", s))
            eng.activation(k.b("t4", s, slice(0, 32)), k.psum[s][2][0:32, :], ACT.Tanh).then_inc(u.act.sem, u.act.one("w1", s))
        for s in S:
            eng.wait_ge(u.pe.sem, u.pe.at("x0", s))
            eng.activation(k.b("t5", s), k.psum[s][0][:], ACT.Tanh, bias=k.weight("l1a_b2")).then_inc(u.act.sem, u.act.one("x1", s))
        for s in S:
            eng.wait_ge(u.pe.sem, u.pe.at("x0e", s))
            eng.activation(k.b("t6", s, slice(0, 32)), k.psum[s][1][0:32, :], ACT.Tanh,
                           bias=k.weight("l1a_b2e", slice(0, 32))).then_inc(u.act.sem, u.act.one("x1e", s))
        for s in S:
            eng.wait_ge(u.pe.sem, u.pe.at("r", s))
            eng.copy(k.b("t3", s), k.psum[s][2][:]).then_inc(u.act.sem, u.act.one("r", s))
        for s in S:
            eng.wait_ge(u.pe.sem, u.pe.at("ww1", s))
            eng.activation(k.b("t4", s, slice(0, 64)), k.psum[s][3][0:64, :], ACT.Tanh).then_inc(u.act.sem, u.act.one("ww1", s))
        for s in S:
            eng.wait_ge(u.pe.sem, u.pe.at("k", s))
            eng.copy(k.b("t9", s), k.psum[s][1][:]).then_inc(u.act.sem, u.act.one("ks", s))
        for s in S:
            eng.wait_ge(u.pe.sem, u.pe.at("ww2", s))
            eng.activation(k.b("t8", s), k.psum[s][0][:], ACT.Exp, bias=k.weight("l1a_wb")).then_inc(u.act.sem, u.act.one("ew", s))
        for s in S:
            eng.wait_ge(u.act.sem, u.act.at("ew", s))
            eng.wait_ge(u.dve.sem, u.dve.at("zeros", s))
            eng.activation(late("t12", s), early("t8", s), ACT.Exp, scale=-1.0).then_inc(u.act.sem, u.act.one("wd", s))
        for s in S:
            eng.wait_ge(u.pe.sem, u.pe.at("v", s))
            eng.wait_ge(u.act.sem, u.act.at("wd", s))
            eng.copy(k.b("t8", s), k.psum[s][2][:]).then_inc(u.act.sem, u.act.one("vs", s))
        for s in S:
            eng.wait_ge(u.pe.sem, u.pe.at("g", s))
            eng.activation(k.b("t11", s), k.psum[s][3][:], ACT.Silu).then_inc(u.act.sem, u.act.one("silu", s))
        self.gn.act(eng)

    def dve_program(self, eng):
        k, u = self.k, self
        self.norm.dve(eng)
        late = lambda name, s: per_batch(k.b(name, s))[:, :, 1:T]
        early = lambda name, s: per_batch(k.b(name, s))[:, :, 0:T - 1]
        first = lambda name, s: per_batch(k.b(name, s))[:, :, 0:1]
        for s in S:
            eng.wait_ge(u.dve.sem, u.dve.at("h", s))
            eng.tensor_tensor(late("t2", s), early("h", s), late("h", s), ALU.subtract).then_inc(u.dve.sem, u.dve.one("delta", s))
        for s in S:
            eng.tensor_scalar(first("t2", s), first("h", s), -1.0, None, ALU.mult).then_inc(u.dve.sem, u.dve.one("delta0", s))
        for s in S:
            eng.wait_ge(u.dve.sem, u.dve.at("delta0", s))
            eng.scalar_tensor_tensor(k.b("t3", s), k.b("t2", s), k.weight("l1a_mu"), k.b("h", s), ALU.mult, ALU.add)\
               .then_inc(u.dve.sem, u.dve.one("lerp", s))
        for j in range(5):
            for s in S:
                eng.wait_ge(u.pe.sem, u.pe.at(f"mu{j}", s))
                eng.scalar_tensor_tensor(k.b(f"t{7 + j}", s), k.psum[s][j % 2][:], k.weight("l1a_xb")[:, j:j + 1],
                                         k.b("t2", s), ALU.add, ALU.mult).then_inc(u.dve.sem, u.dve.one(f"m{j}", s))
            for s in S:
                eng.wait_ge(u.dve.sem, u.dve.at(f"m{j}", s))
                eng.tensor_tensor(k.b(f"t{7 + j}", s), k.b(f"t{7 + j}", s), k.b("h", s), ALU.add)\
                   .then_inc(u.dve.sem, u.dve.one(f"in{j}", s))
        for s in S:
            for name in ("t12", "t13", "t15"):
                ins = eng.memset(first(name, s), 0.0)
            ins.then_inc(u.dve.sem, u.dve.one("zeros", s))
        for s in S:
            eng.wait_ge(u.act.sem, u.act.at("ks", s))
            eng.tensor_copy(late("t13", s), early("t9", s)).then_inc(u.dve.sem, u.dve.one("ksh", s))
        for s in S:
            eng.scalar_tensor_tensor(k.b("t14", s), k.b("t3", s), k.weight("l1a_bonus"), k.b("t9", s), ALU.mult, ALU.mult)\
               .then_inc(u.dve.sem, u.dve.one("rbk", s))
        for s in S:
            eng.wait_ge(u.dve.sem, u.dve.at("in3", s))
            eng.tensor_copy(late("t15", s), early("t10", s)).then_inc(u.dve.sem, u.dve.one("xv", s))
        for s in S:
            eng.wait_ge(u.pe.sem, u.pe.at("bonus", s))
            eng.wait_ge(u.act.sem, u.act.at("vs", s))
            eng.tensor_tensor(k.b("t14", s), k.b("t8", s), k.psum[s][0][:], ALU.mult).then_inc(u.dve.sem, u.dve.one("bv", s))
        for j in range(self.PAIRS):
            w = f"t{4 + j % 2}"
            for s in S:
                eng.wait_ge(u.pe.sem, u.pe.at(f"vb{j}", s))
                if j >= 2:
                    eng.wait_ge(u.pe.sem, u.pe.at(f"os{j - 2}", s))
                eng.tensor_tensor(k.b(w, s), k.b("t13", s), k.psum[s][j % 2][:], ALU.mult).then_inc(u.dve.sem, u.dve.one(f"kv{j}", s))
            for s in S:
                eng.wait_ge(u.dve.sem, u.dve.at(f"kv{j}", s))
                eng.tensor_tensor_scan(k.b(w, s), k.b("t12", s), k.b(w, s), 0.0, ALU.mult, ALU.add)\
                   .then_inc(u.dve.sem, u.dve.one(f"scan{j}", s))
            for s in S:
                eng.wait_ge(u.dve.sem, u.dve.at(f"scan{j}", s))
                eng.tensor_tensor(k.b(w, s), k.b(w, s), k.b("t3", s), ALU.mult).then_inc(u.dve.sem, u.dve.one(f"rt{j}", s))
        for s in S:
            eng.wait_ge(u.pe.sem, u.pe.at("os15", s))
            eng.tensor_tensor(k.b("t6", s), k.b("t14", s), k.psum[s][2][:], ALU.add).then_inc(u.dve.sem, u.dve.one("o", s))
        self.gn.dve(eng)
        for s in S:
            eng.wait_ge(u.dve.sem, u.dve.at("gn", s))
            eng.tensor_scalar(k.b("t12", s), k.b("t12", s), k.weight("l1a_gnw"), k.weight("l1a_gnb"), ALU.mult, ALU.add)\
               .then_inc(u.dve.sem, u.dve.one("gnw", s))
        for s in S:
            eng.wait_ge(u.dve.sem, u.dve.at("gnw", s))
            eng.tensor_tensor(k.b("t12", s), k.b("t12", s), k.b("t11", s), ALU.mult).then_inc(u.dve.sem, u.dve.one("gated", s))
        for s in S:
            eng.wait_ge(u.pe.sem, u.pe.at("y", s))
            eng.tensor_tensor(k.b("x", s), k.b("x", s), k.psum[s][0][:], ALU.add).then_inc(u.dve.sem, u.dve.one("x", s))


class L2Ffn(Sub):

    TILES = (128, 128, 96)

    def __init__(self, core, prev):
        super().__init__(core, prev)
        n = range(24)
        self.pe = core.steps("l2f_pe", [*Norm.PE, *Gate.PE, "gt"]
                             + [a for i in range(25) for a in ([f"gb{i // 3}"] if i % 3 == 0 and i < 24 else [])
                                + ([f"u{i}", f"v{i}"] if i < 24 else []) + ([f"d{i - 1}"] if i else [])])
        self.act = core.steps("l2f_act", [*Norm.ACT, *Gate.ACT, "gt"] + [f"silu{i}" for i in n])
        self.dve = core.steps("l2f_dve", [*Norm.DVE, *Gate.DVE, "wsum", "wrecip", "weights"]
                              + [a for i in n for a in ([f"xg{i // 3}"] if i % 3 == 0 else []) + [f"hid{i}"]] + ["x"])
        self.norm = Norm(core, self)
        self.gate = Gate(core, self, "l2f_gate")

    def pe_program(self, eng):
        k, u = self.k, self
        self.norm.pe(eng)
        eng.wait_ge(k.moe_in[1], 16)
        self.gate.pe(eng)
        for s in S:
            eng.wait_ge(u.dve.sem, u.dve.at("weights", s))
            for t in range(NT):
                mm = eng.transpose(k.psum[s][3][0:8, t * 128:(t + 1) * 128], self.gate.g(s, 8)[:, t * 8:t * 8 + 8],
                                   k.const("ident"))
            mm.then_inc(u.pe.sem, u.pe.one("gt", s))
        for i in range(25):
            e, c = divmod(i, 3)
            if c == 0 and i < 24:
                for s in S:
                    if e == 0:
                        eng.wait_ge(u.act.sem, u.act.at("gt", s))
                    else:
                        eng.wait_ge(u.dve.sem, u.dve.at(f"xg{e - 1}", s))
                    one = k.const("ident", slice(0, 8))[:, e:e + 1].broadcast_to([8, 128])
                    eng.matmul(k.psum[s][3][:], one, k.b("t4", s, slice(0, 8)), start=True, stop=True)\
                       .then_inc(u.pe.sem, u.pe.one(f"gb{e}", s))
            if i < 24:
                m = self.TILES[c]
                for s in S:
                    if i:
                        eng.wait_ge(u.act.sem, u.act.at(f"silu{i - 1}", s))
                    w = k.weight("l2f_w1")[:, e * 352 + c * 128:e * 352 + c * 128 + m]
                    eng.matmul(k.psum[s][0][0:m, :], w, k.b("h", s), start=True, stop=True)\
                       .then_inc(u.pe.sem, u.pe.one(f"u{i}", s))
                for s in S:
                    if i:
                        eng.wait_ge(u.dve.sem, u.dve.at(f"hid{i - 1}", s))
                    if c == 0:
                        eng.wait_ge(u.dve.sem, u.dve.at(f"xg{e}", s))
                    w = k.weight("l2f_w3")[:, e * 352 + c * 128:e * 352 + c * 128 + m]
                    eng.matmul(k.psum[s][1][0:m, :], w, k.b(f"t{5 + e % 2}", s), start=True, stop=True)\
                       .then_inc(u.pe.sem, u.pe.one(f"v{i}", s))
            if i:
                n = i - 1
                m = self.TILES[n % 3]
                for s in S:
                    eng.wait_ge(u.dve.sem, u.dve.at(f"hid{n}", s))
                    eng.matmul(k.psum[s][2][:], k.weight("l2f_w2", slice(0, m))[:, n * 128:(n + 1) * 128],
                               k.b(f"t{9 + n % 2}", s, slice(0, m)), start=n == 0, stop=n == 23)\
                       .then_inc(u.pe.sem, u.pe.one(f"d{n}", s))

    def act_program(self, eng):
        k, u = self.k, self
        self.norm.act(eng)
        self.gate.act(eng)
        for s in S:
            eng.wait_ge(u.pe.sem, u.pe.at("gt", s))
            eng.copy(k.b("t4", s, slice(0, 8)), k.psum[s][3][0:8, :]).then_inc(u.act.sem, u.act.one("gt", s))
        for i in range(24):
            rows = slice(0, self.TILES[i % 3])
            for s in S:
                eng.wait_ge(u.pe.sem, u.pe.at(f"u{i}", s))
                if i >= 2:
                    eng.wait_ge(u.dve.sem, u.dve.at(f"hid{i - 2}", s))
                eng.activation(k.b(f"t{7 + i % 2}", s, rows), k.psum[s][0][rows, :], ACT.Silu)\
                   .then_inc(u.act.sem, u.act.one(f"silu{i}", s))

    def dve_program(self, eng):
        k, u = self.k, self
        self.norm.dve(eng)
        self.gate.dve(eng)
        g8 = lambda s: self.gate.g(s, 8).rearrange("p (t e) -> p t e", e=8)
        for s in S:
            eng.wait_ge(u.dve.sem, u.dve.at("gate", s))
            eng.tensor_reduce(k.small[s][:, 44:48], g8(s), AX.X, ALU.add).then_inc(u.dve.sem, u.dve.one("wsum", s))
        for s in S:
            eng.wait_ge(u.dve.sem, u.dve.at("wsum", s))
            eng.reciprocal(k.small[s][:, 48:52], k.small[s][:, 44:48]).then_inc(u.dve.sem, u.dve.one("wrecip", s))
        for s in S:
            eng.wait_ge(u.dve.sem, u.dve.at("wrecip", s))
            eng.tensor_tensor(g8(s), g8(s), k.small[s][:, 48:52].unsqueeze(2).broadcast_to([128, NT, 8]), ALU.mult)\
               .then_inc(u.dve.sem, u.dve.one("weights", s))
        for i in range(24):
            e, rows = i // 3, slice(0, self.TILES[i % 3])
            if i % 3 == 0:
                for s in S:
                    eng.wait_ge(u.pe.sem, u.pe.at(f"gb{e}", s))
                    eng.tensor_tensor(k.b(f"t{5 + e % 2}", s), k.b("h", s), k.psum[s][3][:], ALU.mult)\
                       .then_inc(u.dve.sem, u.dve.one(f"xg{e}", s))
            for s in S:
                eng.wait_ge(u.pe.sem, u.pe.at(f"v{i}", s))
                eng.wait_ge(u.act.sem, u.act.at(f"silu{i}", s))
                eng.tensor_tensor(k.b(f"t{9 + i % 2}", s, rows), k.b(f"t{7 + i % 2}", s, rows), k.psum[s][1][rows, :],
                                  ALU.mult).then_inc(u.dve.sem, u.dve.one(f"hid{i}", s))
        for s in S:
            eng.wait_ge(u.pe.sem, u.pe.at("d23", s))
            eng.tensor_tensor(k.b("x", s), k.b("x", s), k.psum[s][2][:], ALU.add).then_inc(u.dve.sem, u.dve.one("x", s))


class L3Ffn(Sub):

    def __init__(self, core, prev):
        super().__init__(core, prev)
        self.pe = core.steps("l3f_pe", [*Norm.PE, *Gate.PE, "gt"]
                             + [a for i in range(9) for a in ([f"y{i}"] if i < 8 else []) + ([f"sum{i - 1}"] if i else [])])
        self.act = core.steps("l3f_act", [*Norm.ACT, *Gate.ACT, "gt"])
        self.dve = core.steps("l3f_dve", [*Norm.DVE, *Gate.DVE] + [f"z{i}" for i in range(8)] + ["x"])
        self.norm = Norm(core, self)
        self.gate = Gate(core, self, "l3f_wr", "l3f_br")

    def pe_program(self, eng):
        k, u = self.k, self
        self.norm.pe(eng)
        self.gate.pe(eng)
        for s in S:
            eng.wait_ge(u.dve.sem, u.dve.at("gate", s))
            for t in range(NT):
                mm = eng.transpose(k.psum[s][3][0:8, t * 128:(t + 1) * 128], self.gate.g(s, 8)[:, t * 8:t * 8 + 8],
                                   k.const("ident"))
            mm.then_inc(u.pe.sem, u.pe.one("gt", s))
        for i in range(9):
            if i < 8:
                t, c = divmod(i, 2)
                for s in S:
                    if i >= 2:
                        eng.wait_ge(u.dve.sem, u.dve.at(f"z{i - 2}", s))
                    eng.matmul(k.psum[s][c][:], k.b("h", s)[:, t * 128:(t + 1) * 128], k.weight("l3f_w")[:, c * G:(c + 1) * G],
                               start=True, stop=True).then_inc(u.pe.sem, u.pe.one(f"y{i}", s))
            if i:
                n = i - 1
                t, c = divmod(n, 2)
                for s in S:
                    out = k.psum[s][2][:, t * 128:(t + 1) * 128]
                    if n == 0:
                        eng.wait_ge(u.act.sem, u.act.at("gt", s))
                    if c == 0:
                        eng.matmul(out, k.weight("l3f_b", slice(0, 8)), k.b("t4", s, slice(0, 8))[:, t * 128:(t + 1) * 128],
                                   start=True, stop=False)
                    eng.wait_ge(u.dve.sem, u.dve.at(f"z{n}", s))
                    for e in range(4):
                        mm = eng.matmul(out, k.b(f"t{5 + n % 2}", s)[:, e * 128:(e + 1) * 128], k.const("ident"),
                                        start=False, stop=c == 1 and e == 3)
                    mm.then_inc(u.pe.sem, u.pe.one(f"sum{n}", s))

    def act_program(self, eng):
        k, u = self.k, self
        self.norm.act(eng)
        self.gate.act(eng)
        for s in S:
            eng.wait_ge(u.pe.sem, u.pe.at("gt", s))
            eng.copy(k.b("t4", s, slice(0, 8)), k.psum[s][3][0:8, :]).then_inc(u.act.sem, u.act.one("gt", s))

    def dve_program(self, eng):
        k, u = self.k, self
        self.norm.dve(eng)
        self.gate.dve(eng)
        for i in range(8):
            t, c = divmod(i, 2)
            for s in S:
                eng.wait_ge(u.pe.sem, u.pe.at(f"y{i}", s))
                if i == 0:
                    eng.wait_ge(u.dve.sem, u.dve.at("gate", s))
                if i >= 2:
                    eng.wait_ge(u.pe.sem, u.pe.at(f"sum{i - 2}", s))
                eng.tensor_tensor(k.b(f"t{5 + i % 2}", s).rearrange("p (e n) -> p e n", e=4),
                                  k.psum[s][c][:].rearrange("p (e n) -> p e n", e=4),
                                  self.gate.g(s, 8)[:, t * 8 + 4 * c:t * 8 + 4 * c + 4].unsqueeze(2).broadcast_to([128, 4, 128]),
                                  ALU.mult).then_inc(u.dve.sem, u.dve.one(f"z{i}", s))
        for s in S:
            eng.wait_ge(u.pe.sem, u.pe.at("sum7", s))
            eng.tensor_tensor(k.b("x", s), k.b("x", s), k.psum[s][2][:], ALU.add).then_inc(u.dve.sem, u.dve.one("x", s))


class L1Ffn(Sub):

    def __init__(self, core, prev):
        super().__init__(core, prev)
        self.pe = core.steps("l1f_pe", [*Norm.PE, "y"])
        self.act = core.steps("l1f_act", Norm.ACT)
        self.dve = core.steps("l1f_dve", [*Norm.DVE, "x"])
        self.norm = Norm(core, self)

    def pe_program(self, eng):
        k, u = self.k, self
        self.norm.pe(eng)
        for s in S:
            eng.wait_ge(u.dve.sem, u.dve.at("h", s))
            eng.matmul(k.psum[s][2][:], k.ternary[:], k.b("h", s), start=True, stop=True)\
               .then_inc(u.pe.sem, u.pe.one("y", s))

    def act_program(self, eng):
        self.norm.act(eng)

    def dve_program(self, eng):
        k, u = self.k, self
        self.norm.dve(eng)
        for s in S:
            eng.wait_ge(u.pe.sem, u.pe.at("y", s))
            eng.tensor_tensor(k.b("x", s), k.b("x", s), k.psum[s][2][:], ALU.add)\
               .then_inc(u.dve.sem, u.dve.one("x", s))


NTMP = 16


def small(k, ctx):
    t = lambda name, cols, dt=F32: ctx.enter_context(k.nc.sbuf_tensor(name, [128, cols], dt))
    k.eps5, k.l0a_bias, k.ternary, k.scratch = t("eps5", 1), t("l0a_bias", 1), t("ternary", 128), t("scratch", 8)
    k.vb = [t(f"vb{s}", 2 * 8 * 65) for s in S]
    k.vbd = [t(f"vbd{s}", 2 * 8 * 18) for s in S]
    k.fill0 = [t(f"fill0_{s}", 256) for s in S]
    k.rotated, k.rot_bias = t("rotated", 2 * D), t("rot_bias", 2)
    k.pope, k.angle = t("pope", 3 * T), t("angle", 8)
    k.turned = k.wide(0, 1, 1)
    k.minus_pi = t("minus_pi", 1)
    k.fill1 = [t(f"fill1_{s}", 256) for s in S]
    k.out_scale = t("out_scale", 1)
    k.gate = [t(f"gate{s}", 9 * 32) for s in S]
    k.vexp = t("vexp", 16 * 128)
    k.small = [t(f"small{s}", 64) for s in S]
    k.keymask = [t(f"keymask{s}", G) for s in S]


def setup_tensor(k, eng, pe, dve):
    eng.wait_ge(dve, 3)
    eng.matmul(k.psum[0][0][:, 0:1], k.const("mean"), k.scratch[:, 0:1], start=True, stop=True).then_inc(pe, 1)
    eng.matmul(k.psum[0][1][:, 0:D], k.wide(0, 0, 1)[:, 0:D], k.const("rot"), start=True, stop=True)
    eng.matmul(k.psum[0][1][:, D:2 * D], k.wide(0, 0, 1)[:, D:2 * D], k.const("rot"), start=True, stop=True)
    eng.matmul(k.psum[0][1][:, 2 * D:2 * D + 1], k.const("rot"), k.weight("l3a_bq"), start=True, stop=True)
    eng.matmul(k.psum[0][1][:, 2 * D + 1:2 * D + 2], k.const("rot"), k.weight("l3a_bk"), start=True, stop=True)\
       .then_inc(pe, 1)


def setup_scalar(k, eng, act, dve):
    eng.activation(k.angle[:, 0:1], k.weight("l2a_delta"), ACT.Sigmoid).then_inc(act, 1)
    eng.wait_ge(act, 1)
    eng.wait_ge(dve, 1)
    eng.activation(k.angle[:, 1:2], k.angle[:, 0:1], ACT.Sin, scale=float(2 * np.pi), bias=k.minus_pi[:, 0:1]).then_inc(act, 1)
    eng.activation(k.angle[:, 2:3], k.angle[:, 0:1], ACT.Sin, scale=float(np.pi)).then_inc(act, 1)


def setup_vector(k, eng, pe, dve, act):
    n = 0

    def link(ins):
        nonlocal n
        n += 1
        ins.then_inc(dve, 1)
        eng.wait_ge(dve, n)

    w = k.weight("l1f_w")
    link(eng.memset(k.minus_pi[:], -float(np.pi)))
    link(eng.memset(k.eps5[:], LN_EPS))
    link(eng.tensor_reduce(k.scratch[:, 0:1], w, AX.X, ALU.add, apply_absolute_value=True))
    eng.wait_ge(pe, 1)
    link(eng.tensor_scalar(k.scratch[:, 1:2], k.psum[0][0][:, 0:1], 1 / 128, LN_EPS, ALU.mult, ALU.max))
    link(eng.reciprocal(k.scratch[:, 2:3], k.scratch[:, 1:2]))
    link(eng.tensor_scalar(k.ternary[:], w, k.scratch[:, 2:3], 1.0, ALU.mult, ALU.min))
    link(eng.tensor_scalar(k.ternary[:], k.ternary[:], -1.0, float(3 << 22), ALU.max, ALU.add))
    link(eng.tensor_scalar(k.ternary[:], k.ternary[:], float(3 << 22), k.scratch[:, 1:2], ALU.subtract, ALU.mult))
    eng.wait_ge(act, 3)
    link(eng.tensor_tensor(k.angle[:, 3:4], k.angle[:, 2:3], k.angle[:, 2:3], ALU.mult))
    link(eng.tensor_scalar(k.angle[:, 4:5], k.angle[:, 3:4], -2.0, 1.0, ALU.mult, ALU.add))
    cos, sin = k.angle[:, 4:5], k.angle[:, 1:2]
    link(eng.tensor_scalar(k.turned[:, 0:T], k.const("psin"), sin, None, ALU.mult))
    link(eng.scalar_tensor_tensor(k.pope[:, T:2 * T], k.const("pcos"), cos, k.turned[:, 0:T], ALU.mult, ALU.subtract))
    link(eng.tensor_scalar(k.turned[:, T:2 * T], k.const("pcos"), sin, None, ALU.mult))
    link(eng.scalar_tensor_tensor(k.pope[:, 2 * T:3 * T], k.const("psin"), cos, k.turned[:, T:2 * T], ALU.mult, ALU.add))
    link(eng.tensor_scalar(k.pope[:, 2 * T:3 * T], k.pope[:, 2 * T:3 * T], k.const("psign"), None, ALU.mult))
    for g in range(4):
        rows, part = slice(32 * g, 32 * g + 32), 1 + g % 2
        link(eng.tensor_copy(k.pope[rows, 0:T], k.pope[rows, part * T:(part + 1) * T]))
    eng.wait_ge(pe, 2)
    link(eng.tensor_copy(k.rotated[:], k.psum[0][1][:, 0:2 * D]))
    link(eng.tensor_copy(k.rot_bias[:], k.psum[0][1][:, 2 * D:2 * D + 2]))
    for s in S:
        link(eng.memset(k.vbd[s][:], 0.0))
        for h2 in range(2):
            rows = slice(64 * h2, 64 * h2 + 64)
            link(eng.memset(k.vbd[s][rows, :].rearrange("p (q c) -> p q c", c=18)[:, :, 9 * h2 + 8:9 * h2 + 9], 1.0))
        link(eng.memset(k.vb[s].ap().rearrange("p (h c) -> p h c", c=65)[:, :, 64:65], 1.0))
    link(eng.tensor_scalar(k.out_scale[:], k.weight("l1x_out"), 1.0, None, ALU.add))
    for odd in range(2):
        for h in range(4):
            to = k.vexp[:].rearrange("p (v r) -> p v r", v=16)[:, :, odd * 64 + h * 16:odd * 64 + h * 16 + 16]
            cols = k.weight("l1a_v")[:, h * 32:(h + 1) * 32].rearrange("p (v o) -> p v o", o=2)[:, :, odd:odd + 1]
            link(eng.tensor_copy(to, cols.broadcast_to([128, 16, 16])))
    link(eng.memset(k.l0a_bias[:], float(20 * np.log(2.0) + 0.5 * np.log(128.0))))


LAYERS = [CtxNorm, L0Attn, L0Xattn, L0Ffn, L1Attn, L1Xattn, L1Ffn, L2Attn, L2Xattn, L2Ffn, L3Attn, L3Xattn, L3Ffn]


def pad(a, rows=128):
    out = np.zeros((rows, a.shape[1]), a.dtype)
    out[:a.shape[0]] = a
    return out


def col(v, times=1):
    return np.tile(np.reshape(v, (-1, 1)), (times, 1))


def weight_layouts(i):
    out = [("l0a_w", i["L0_attn_W_qkva"].T), ("l0a_gamma", col(i["L0_attn_gamma"]))]
    e8 = lambda a: a.transpose(1, 0, 2).reshape(a.shape[1], -1)
    out += [(n, col(i["L0_xattn_" + n[4:]])) for n in ("l0x_ln_l_w", "l0x_ln_l_b", "l0x_ln_c_w", "l0x_ln_c_b", "l0x_bo")]
    out += [("l0x_wq", i["L0_xattn_Wq"]), ("l0x_wkv", i["L0_xattn_Wkv"]),
            ("l0x_wo", i["L0_xattn_Wo"].reshape(8, 128, 128).transpose(1, 0, 2).reshape(128, -1))]
    out += [("l0f_wr", i["L0_ffn_Wr"]), ("l0f_w1", e8(i["L0_ffn_W1"])),
            ("l0f_b1", i["L0_ffn_b1"].reshape(8, 4, 128).transpose(2, 0, 1).reshape(128, 32)),
            ("l0f_w2", i["L0_ffn_W2"].reshape(8, 4, 128, 128).transpose(2, 0, 1, 3).reshape(128, -1)),
            ("l0f_b2", i["L0_ffn_b2"].T)]
    a = lambda n: i["L1_attn_" + n]
    two = lambda w: np.concatenate([w, w], axis=1)
    out += [("l1a_mu", col(a("x_proj_mu"))), ("l1a_w1", a("xl_w1").T), ("l1a_w2", pad(a("xl_w2").T)),
            ("l1a_b2", col(a("xl_b2")[:128])), ("l1a_b2e", pad(col(a("xl_b2")[128:]))),
            ("l1a_xo", a("x_out_w").T[:128]), ("l1a_xoe", pad(a("x_out_w").T[128:])), ("l1a_xb", a("x_bias").T),
            ("l1a_r", two(a("r_w").T)), ("l1a_k", two(a("k_w").T)), ("l1a_ww1", a("w_w1").T),
            ("l1a_ww2", pad(two(a("w_w2").T))), ("l1a_wb", col(a("w_b"), 2)), ("l1a_v", a("v_w").T),
            ("l1a_g", a("g_w").T), ("l1a_bonus", col(a("bonus"), 2)), ("l1a_gnw", col(a("gn_weight"))),
            ("l1a_gnb", col(a("gn_bias"))), ("l1a_o", a("o_w").T)]
    a = lambda n: i["L1_xattn_" + n]
    wide = lambda w: np.repeat(w.reshape(4, 3, 128).transpose(2, 1, 0), 32, axis=2).reshape(128, 384)
    out += [("l1x_ig", wide(a("igate_w"))), ("l1x_fg", wide(a("fgate_w"))),
            ("l1x_igb", col(np.repeat(a("igate_b"), 32))), ("l1x_fgb", col(np.repeat(a("fgate_b"), 32))),
            ("l1x_out", col(a("out_w"))), ("l1f_w", i["L1_ffn_weight"].T)]
    a = lambda n: i["L2_attn_" + n]
    swap = lambda w: w.reshape(w.shape[0], -1, 2, 16)[:, :, ::-1].reshape(w.shape)
    beside = lambda w: np.stack([w.reshape(64, 8, 32), swap(w).reshape(64, 8, 32)], axis=2).reshape(64, 512)
    four = lambda w: np.concatenate([w] * 4, axis=1)
    out += [("l2a_dkv", a("W_dkv")), ("l2a_uk", pad(a("W_uk"))), ("l2a_uv", pad(a("W_uv"))), ("l2a_dq", a("W_dq")),
            ("l2a_uq", pad(a("W_uq"))), ("l2a_qrq", pad(beside(a("W_qr")))),
            ("l2a_kr", four(a("W_kr"))), ("l2a_krs", four(swap(a("W_kr")))), ("l2a_delta", col(a("raw_delta"), 8)),
            ("l2a_out", a("W_out").reshape(4, 128, 128).transpose(1, 0, 2).reshape(128, -1))]
    a = lambda n: i["L2_xattn_" + n]
    out += [("l2x_wq", a("w_q")), ("l2x_wkv", a("w_kv")), ("l2x_wo", a("w_proj")), ("l2x_bo", col(a("b_proj"))),
            ("l2x_gx", col(a("g_x"))), ("l2x_bx", col(a("b_x"))), ("l2x_gkv", col(a("g_kv"))), ("l2x_bkv", col(a("b_kv")))]
    a = lambda n: i["L2_ffn_" + n]
    w2 = np.zeros((8, 384, 128), np.float32)
    w2[:, :352] = a("w2").transpose(0, 2, 1)
    out += [("l2f_gate", a("gate_w").T), ("l2f_w1", e8(a("w1").transpose(0, 2, 1))),
            ("l2f_w3", e8(a("w3").transpose(0, 2, 1))),
            ("l2f_w2", w2.reshape(8, 3, 128, 128).transpose(2, 0, 1, 3).reshape(128, -1))]
    a = lambda n: i["L3_attn_" + n]
    out += [("l3a_wq", a("Wq").T), ("l3a_wk", a("Wk").T), ("l3a_wv", a("Wv").T), ("l3a_wo", a("Wo").T),
            ("l3a_bq", col(a("bq"))), ("l3a_bk", col(a("bk"))), ("l3a_bv", col(a("bv"))), ("l3a_bo", col(a("bo")))]
    a = lambda n: i["L3_xattn_" + n]
    out += [("l3x_wq", a("Wq").T), ("l3x_wk", a("Wk").T), ("l3x_wv", a("Wv").T), ("l3x_bq", col(a("bq"))),
            ("l3x_bk", col(a("bk"))), ("l3x_bv", col(a("bv")))]
    a = lambda n: i["L3_ffn_" + n]
    out += [("l3f_w", e8(a("W_experts").transpose(0, 2, 1))), ("l3f_b", pad(a("b_experts"))),
            ("l3f_wr", a("W_router").T), ("l3f_br", np.repeat(a("b_router").reshape(1, 8), 128, axis=0))]
    return out


CHUNKS = [("l0a_w", "l1a_mu"), ("l1a_mu", None)]
MOE = ("l0f_", "l2f_")


def build(nc, weights_at, weights_n, moe_at, moe_n, x_d, ctx_d, ctok_d, m0_d, m1_d, w_d, moe_d, qk_d, c_d, out_d, layers, turns):
    with ExitStack() as ctx:
        k = Core(nc, ctx, weights_at, weights_n, moe_at, max(moe_n))
        sem = lambda n: ctx.enter_context(nc.semaphore(n))
        for name in ("x", "h", "c", "cn"):
            k.sbuf(name, G)
        k.sbuf("tmp", NTMP * G)
        k.sbuf("ctok", G)
        small(k, ctx)

        consts_in, weights_in = sem("consts_in"), [sem(f"weights_in{j}") for j in range(len(CHUNKS))]
        setup_pe, setup_dve, setup_act = sem("setup_pe"), sem("setup_dve"), sem("setup_act")
        x_in, c_in = [sem(f"x_in{s}") for s in S], [sem(f"c_in{s}") for s in S]
        ctok_in, mask_in = [sem(f"ctok_in{s}") for s in S], [sem(f"mask_in{s}") for s in S]
        x_out, moe_in = sem("x_out"), [sem(f"moe_in{j}") for j in range(2)]
        k.moe_in = moe_in
        k.c_in, k.ctok_in, k.mask_in = c_in, ctok_in, mask_in

        with nc.Block() as block:
            @block.sync
            def _(eng):
                eng.dma_start(k.c[:], c_d).then_inc(consts_in, 16)
                eng.dma_start(k.wide(0, 0, 1)[:, 0:2 * D], qk_d).then_inc(consts_in, 16)
                for j, (a, b) in enumerate(CHUNKS):
                    lo, hi = weights_at[a][0], weights_at[b][0] if b else weights_n
                    eng.dma_start(k.w[:, lo:hi], w_d[:, lo:hi]).then_inc(weights_in[j], 16)

            @block.tensor
            def _(eng):
                eng.wait_ge(consts_in, 32)
                for q in weights_in:
                    eng.wait_ge(q, 16)
                setup_tensor(k, eng, setup_pe, setup_dve)

            @block.scalar
            def _(eng):
                for q in weights_in:
                    eng.wait_ge(q, 16)
                setup_scalar(k, eng, setup_act, setup_dve)

            @block.vector
            def _(eng):
                eng.wait_ge(consts_in, 32)
                for q in weights_in:
                    eng.wait_ge(q, 16)
                setup_vector(k, eng, setup_pe, setup_dve, setup_act)

        prev, subs = Load(k, x_in), []
        for cls in layers:
            prev = cls(k, prev)
            subs.append(prev)

        with nc.Fori(0, turns) as turn:
            with nc.Block() as block:
                @block.sync
                def _(eng):
                    for s in S:
                        at = turn * (2 * G) + s * G
                        eng.dma_start(k.b("x", s), x_d[:, bass.ds(at, G)]).then_inc(x_in[s], 16)
                        eng.dma_start(k.b("c", s), ctx_d[:, bass.ds(at, G)]).then_inc(c_in[s], 16)
                        eng.dma_start(k.b("ctok", s), ctok_d[:, bass.ds(at, G)]).then_inc(ctok_in[s], 16)
                        for half in range(2):
                            rows = slice(64 * half, 64 * half + 64)
                            for to, m in ((k.fill0[s], m0_d), (k.fill1[s], m1_d)):
                                src = m[:, bass.ds(at, G)].rearrange("o (t b j) -> o t b j", b=2, j=T)[:, :, half, :]
                                eng.dma_start(to[rows, :].bitcast(I32).rearrange("p (t j) -> p t j", j=T),
                                              src.broadcast_to([64, NT, T])).then_inc(mask_in[s], 16)
                        eng.dma_start(k.keymask[s][:].bitcast(I32), m0_d[:, bass.ds(at, G)].broadcast_to([128, G]))\
                           .then_inc(mask_in[s], 16)
                        if s == 0:
                            eng.dma_start(k.moe[:, 0:moe_n[0]], moe_d[0]).then_inc(moe_in[0], 16)
                    first_moe = [u for u in subs if isinstance(u, L0Ffn)]
                    for u in first_moe:
                        for s in S:
                            u.output_ready(eng, s)
                    eng.wait_ge(moe_in[0], 16)
                    eng.dma_start(k.moe[:, 0:moe_n[1]], moe_d[1]).then_inc(moe_in[1], 16)
                    for s in S:
                        at = turn * (2 * G) + s * G
                        subs[-1].output_ready(eng, s)
                        eng.dma_start(out_d[:, bass.ds(at, G)], k.b("x", s)).then_inc(x_out, 16)
                    eng.wait_ge(moe_in[1], 16)
                    eng.wait_ge(x_out, 32)

                @block.tensor
                def _(eng):
                    for u in subs:
                        u.pe_program(eng)

                @block.scalar
                def _(eng):
                    for u in subs:
                        u.act_program(eng)

                @block.vector
                def _(eng):
                    for u in subs:
                        u.dve_program(eng)

                @block.gpsimd
                def _(eng):
                    for u in subs:
                        u.pool(eng)

            for q in k.sems + x_in + c_in + ctok_in + mask_in + moe_in + [x_out]:
                nc.sync.sem_clear(q)
            nc.all_engine_barrier()


def kernel(**inputs):
    import concourse.bacc as _bacc
    from concourse.bass_utils import run_bass_kernel_spmd as _run

    i = {n: np.asarray(a) for n, a in inputs.items()}
    tokens = lambda a: np.ascontiguousarray(a.reshape(B * T, D).T)
    entries = [(n, np.ascontiguousarray(a)) for n, a in weight_layouts(i)]
    packs = [[e for e in entries if not e[0].startswith(MOE)]] + [[e for e in entries if e[0].startswith(m)] for m in MOE]
    at, n = zip(*[columns([(name, a.shape[1]) for name, a in p]) for p in packs])
    pack = lambda p: np.concatenate([a for _, a in p], axis=1)
    arrays = {
        "x_t": tokens(i["x"]), "ctx_t": tokens(i["ctx_1024"]),
        "ctx_tok": np.ascontiguousarray(i["ctx_1024"].reshape(B * T // 128, 128, D).transpose(1, 0, 2).reshape(128, -1)),
        "mask0": i["mask_BxS2_ik0"].reshape(1, B * T), "mask1": i["mask_BxS2_ik1"].reshape(1, B * T),
        "weights_d": pack(packs[0]), "moe0_d": pack(packs[1]), "moe2_d": pack(packs[2]), "consts_d": constants(),
        "l3a_qk": np.concatenate([i["L3_attn_Wq"], i["L3_attn_Wk"]], axis=1),
    }
    nc = _bacc.Bacc("TRN2", target_bir_lowering=False, num_devices=1)
    d = {name: nc.dram_tensor(name, a.shape, mybir.dt.from_np(a.dtype), kind="ExternalInput").ap()
         for name, a in arrays.items()}
    out = nc.dram_tensor("out_t", (D, B * T), F32, kind="ExternalOutput").ap()
    build(nc, at[0], n[0], at[1:], n[1:], d["x_t"], d["ctx_t"], d["ctx_tok"], d["mask0"], d["mask1"], d["weights_d"],
          [d["moe0_d"], d["moe2_d"]], d["l3a_qk"], d["consts_d"],
          out, LAYERS, TURNS)
    r = _run(nc, [arrays], core_ids=[0])
    return np.ascontiguousarray(r.results[0]["out_t"].T).reshape(B, T, D)
```

```python
from contextlib import ExitStack

import numpy as np

import concourse.bass as bass
from concourse import mybir

F32 = mybir.dt.float32
I32 = mybir.dt.int32
ALU = mybir.AluOpType
ACT = mybir.ActivationFunctionType
AX = mybir.AxisListType

B, T, D = 64, 64, 128
G = 512
NB = G // T
NT = G // 128
TURNS = B * T // (2 * G)
S = (0, 1)
LN_EPS = 1e-5


class Steps:

    def __init__(self, sem, names):
        self.sem, self.names, self.done = sem, list(names), 0
        self.number = {n: k for k, n in enumerate(self.names)}
        assert len(self.number) == len(self.names)

    def at(self, name, s):
        return 2 * self.number[name] + s + 1

    def one(self, name, s):
        assert self.done == 2 * self.number[name] + s, (name, s, self.names[self.done // 2], self.done % 2)
        self.done += 1
        return 1


def many(*parts):
    out = []
    for p in parts:
        if isinstance(p, tuple):
            out += [f"{n}{j}" for j in range(p[-1]) for n in p[:-1]]
        else:
            out.append(p)
    return out


def columns(table):
    at, n = {}, 0
    for name, w in table:
        at[name] = (n, w)
        n += w
    return at, n


CONSTS = [("ident", 128), ("mean", 128), ("mean32", 128), ("earlier", 128), ("slot", 10), ("rev", 8),
          ("keep", 512), ("start", 512), ("row0", 1), ("row1", 1), ("tiny", 1), ("cap", 64), ("ones", 128),
          ("pcos", 64), ("psin", 64), ("psign", 1), ("rcos", 64), ("rsin", 64), ("head4", 4), ("rot", 128),
          ("ksum", 158), ("bonus_sum", 128)]
CONST_AT, CONST_N = columns(CONSTS)


def constants():
    c = {n: np.zeros((128, w), np.float32) for n, w in CONSTS}
    p = np.arange(128)
    c["ident"][p, p] = 1
    c["mean"][:] = 1 / 128
    c["mean32"][:] = np.where(p[:, None] // 32 == p[None] // 32, 1 / 32, 0)
    same = p[:, None] // T == p[None] // T
    c["earlier"][:] = same & (p[:, None] < p[None])
    c["slot"][:] = np.arange(10)
    c["rev"][:] = 8 - np.arange(8)
    c["keep"][:] = np.arange(G) % T != 0
    c["start"][:] = np.where(np.arange(G) % T == 0, -1e30, 0)
    c["row0"][:, 0], c["row1"][:, 0] = p % 32 == 0, p % 32 == 1
    c["tiny"][:] = 1e-8
    c["cap"][:] = np.where((p[:, None] % T) <= np.arange(T)[None], 0, -1e30)
    c["ones"][:] = 1
    pos = np.arange(T, dtype=np.float32)
    theta = (1.0 / np.float32(10000.0) ** (2.0 * np.arange(16, dtype=np.float32) / 32)).astype(np.float32)
    ang = (pos[None] * theta[p % 16][:, None]).astype(np.float32)
    c["pcos"][:], c["psin"][:] = np.cos(ang), np.sin(ang)
    c["psign"][:, 0] = np.where(p % 32 < 16, -1, 1)
    freq = (1.0 / np.float32(10000.0) ** (np.arange(0, 8, 2, dtype=np.float32) / 8)).astype(np.float32)
    ang = (pos[None] * freq[(p % 8) % 4][:, None]).astype(np.float32)
    c["rcos"][:], c["rsin"][:] = np.cos(ang), np.sin(ang)
    c["head4"][:] = (p[:, None] % 32) // 8 == np.arange(4)[None]
    even = p[p % 2 == 0]
    c["rot"][even + 1, even] = -1
    c["rot"][even, even + 1] = 1
    c["ksum"][p, ((p % 64) // 16) * 32 + p // 64 + 30] = 1
    q = p[:64]
    c["bonus_sum"][:64] = q[:, None] // 16 == p[None] // 32
    return np.concatenate([c[n] for n, _ in CONSTS], axis=1)


class Core:

    def __init__(self, nc, ctx, weights_at, weights_n, moe_at, moe_n):
        self.nc, self.ctx = nc, ctx
        self.moe_at = moe_at[0] | moe_at[1]
        self.moe = ctx.enter_context(nc.sbuf_tensor("moe_weights", [128, moe_n], F32))
        self.w_at = weights_at
        self.w = ctx.enter_context(nc.sbuf_tensor("weights", [128, weights_n], F32))
        self.c = ctx.enter_context(nc.sbuf_tensor("consts", [128, CONST_N], F32))
        self.psum = [[ctx.enter_context(nc.psum_tensor(f"psum{s}{k}", [128, G], F32)) for k in range(4)] for s in S]
        self.buf = {}
        self.sems = []

    def sbuf(self, name, cols, dt=F32):
        self.buf[name] = [self.ctx.enter_context(self.nc.sbuf_tensor(f"{name}{s}", [128, cols], dt)) for s in S]

    def const(self, name, rows=slice(0, 128)):
        o, w = CONST_AT[name]
        return self.c[rows, o:o + w]

    def weight(self, name, rows=slice(0, 128)):
        if name in self.moe_at:
            o, w = self.moe_at[name]
            return self.moe[rows, o:o + w]
        o, w = self.w_at[name]
        return self.w[rows, o:o + w]

    def steps(self, name, parts):
        sem = self.ctx.enter_context(self.nc.semaphore(name))
        self.sems.append(sem)
        return Steps(sem, many(*parts))

    def b(self, name, s, rows=slice(0, 128)):
        if name[0] == "t":
            return self.wide(s, int(name[1:]), 1, rows)
        return self.buf[name][s][rows, :]

    def wide(self, s, j, n, rows=slice(0, 128)):
        return self.buf["tmp"][s][rows, j * G:(j + n) * G]


def log_and_exp_table(eng):
    eng.preload_act_table_set("natural_log_exp_and_others")


def per_batch(ap):
    return ap.rearrange("p (b t) -> p b t", t=T)


class Norm:

    PE, DVE, ACT = ("mean", "var"), ("xc", "h"), ("sq", "ln", "rstd")

    def __init__(self, core, sub, src="x", out="h"):
        self.k, self.sub, self.src, self.out = core, sub, src, out

    def pe(self, eng):
        self.pe_mean(eng)
        self.pe_var(eng)

    def dve(self, eng):
        self.dve_centre(eng)
        self.dve_scale(eng)

    def pe_mean(self, eng):
        k, u = self.k, self.sub
        for s in S:
            u.input_ready(eng, s)
            eng.matmul(k.psum[s][0][:], k.const("mean"), k.b(self.src, s), start=True, stop=True)\
               .then_inc(u.pe.sem, u.pe.one("mean", s))

    def pe_var(self, eng):
        k, u = self.k, self.sub
        for s in S:
            eng.wait_ge(u.act.sem, u.act.at("sq", s))
            eng.matmul(k.psum[s][1][:], k.const("mean"), k.b("t1", s), start=True, stop=True)\
               .then_inc(u.pe.sem, u.pe.one("var", s))

    def dve_centre(self, eng):
        k, u = self.k, self.sub
        for s in S:
            eng.wait_ge(u.pe.sem, u.pe.at("mean", s))
            eng.tensor_tensor(k.b("t0", s), k.b(self.src, s), k.psum[s][0][:], ALU.subtract)\
               .then_inc(u.dve.sem, u.dve.one("xc", s))

    def dve_scale(self, eng):
        k, u = self.k, self.sub
        for s in S:
            eng.wait_ge(u.act.sem, u.act.at("rstd", s))
            eng.wait_ge(u.dve.sem, u.dve.at("xc", s))
            eng.tensor_tensor(k.b(self.out, s), k.b("t0", s), k.b("t1", s), ALU.mult)\
               .then_inc(u.dve.sem, u.dve.one("h", s))

    def act(self, eng):
        k, u = self.k, self.sub
        for s in S:
            eng.wait_ge(u.dve.sem, u.dve.at("xc", s))
            eng.activation(k.b("t1", s), k.b("t0", s), ACT.Square).then_inc(u.act.sem, u.act.one("sq", s))
        for s in S:
            eng.wait_ge(u.pe.sem, u.pe.at("var", s))
            eng.activation(k.b("t1", s), k.psum[s][1][:], ACT.Ln, bias=k.eps5[:, 0:1])\
               .then_inc(u.act.sem, u.act.one("ln", s))
        for s in S:
            eng.wait_ge(u.act.sem, u.act.at("ln", s))
            eng.activation(k.b("t1", s), k.b("t1", s), ACT.Exp, scale=-0.5)\
               .then_inc(u.act.sem, u.act.one("rstd", s))


class Sub:

    def __init__(self, core, prev):
        self.k, self.prev = core, prev

    def output_ready(self, eng, s):
        eng.wait_ge(self.dve.sem, self.dve.at("x", s))

    def input_ready(self, eng, s):
        self.prev.output_ready(eng, s)

    def pool_program(self, eng):
        pass


class Load:

    def __init__(self, core, x_in):
        self.x_in = x_in

    def output_ready(self, eng, s):
        eng.wait_ge(self.x_in[s], 16)


class L0Attn(Sub):

    SPLIT = 2.0 ** -56

    def __init__(self, core, prev):
        super().__init__(core, prev)
        self.pe = core.steps("l0a_pe", [*Norm.PE, "q", "kv", "a"])
        self.act = core.steps("l0a_act", ["sq", "ln", "rstd", "r2", "lnn", "lnlow", "rnorm", "sig"])
        self.dve = core.steps("l0a_dve", ["xc", "h", "n2", "n2low", "n2high", "lnsum", "xn", "gate0", "scan", "qy", "x"])
        self.norm = Norm(core, self)

    def pe_program(self, eng):
        k, u = self.k, self
        self.norm.pe(eng)
        for j, name in enumerate(("q", "kv", "a")):
            for s in S:
                if j == 0:
                    eng.wait_ge(u.dve.sem, u.dve.at("xn", s))
                bank = (0, 2, 3)[j]
                eng.matmul(k.psum[s][bank][:], k.weight("l0a_w")[:, j * D:(j + 1) * D], k.b("t3", s),
                           start=True, stop=True).then_inc(u.pe.sem, u.pe.one(name, s))

    def act_program(self, eng):
        k, u = self.k, self
        self.norm.act(eng)
        for s in S:
            eng.wait_ge(u.act.sem, u.act.at("rstd", s))
            eng.activation(k.b("t2", s), k.b("t1", s), ACT.Square).then_inc(u.act.sem, u.act.one("r2", s))
        for s in S:
            eng.wait_ge(u.dve.sem, u.dve.at("n2high", s))
            eng.activation(k.b("t2", s), k.b("t2", s), ACT.Ln).then_inc(u.act.sem, u.act.one("lnn", s))
        for s in S:
            eng.activation(k.b("t4", s), k.b("t4", s), ACT.Ln, scale=1 / self.SPLIT)\
               .then_inc(u.act.sem, u.act.one("lnlow", s))
        for s in S:
            eng.wait_ge(u.dve.sem, u.dve.at("lnsum", s))
            eng.activation(k.b("t2", s), k.b("t2", s), ACT.Exp, scale=-0.5)\
               .then_inc(u.act.sem, u.act.one("rnorm", s))
        for s in S:
            eng.wait_ge(u.pe.sem, u.pe.at("a", s))
            eng.activation(k.b("t4", s), k.psum[s][3][:], ACT.Sigmoid).then_inc(u.act.sem, u.act.one("sig", s))
        log_and_exp_table(eng)

    def dve_program(self, eng):
        k, u = self.k, self
        self.norm.dve(eng)
        for s in S:
            eng.wait_ge(u.act.sem, u.act.at("r2", s))
            eng.tensor_tensor(k.b("t2", s), k.psum[s][1][:], k.b("t2", s), ALU.mult)\
               .then_inc(u.dve.sem, u.dve.one("n2", s))
        for s in S:
            eng.wait_ge(u.dve.sem, u.dve.at("n2", s))
            eng.tensor_scalar(k.b("t4", s), k.b("t2", s), 1e-24 / D, self.SPLIT, ALU.max, ALU.min)\
               .then_inc(u.dve.sem, u.dve.one("n2low", s))
        for s in S:
            eng.wait_ge(u.dve.sem, u.dve.at("n2low", s))
            eng.tensor_scalar(k.b("t2", s), k.b("t2", s), self.SPLIT, None, ALU.max)\
               .then_inc(u.dve.sem, u.dve.one("n2high", s))
        for s in S:
            eng.wait_ge(u.act.sem, u.act.at("lnlow", s))
            eng.tensor_tensor(k.b("t2", s), k.b("t2", s), k.b("t4", s), ALU.add)\
               .then_inc(u.dve.sem, u.dve.one("lnsum", s))
        for s in S:
            eng.wait_ge(u.act.sem, u.act.at("rnorm", s))
            eng.wait_ge(u.dve.sem, u.dve.at("h", s))
            eng.scalar_tensor_tensor(k.b("t3", s), k.b("h", s), k.weight("l0a_gamma"), k.b("t2", s),
                                     ALU.mult, ALU.mult).then_inc(u.dve.sem, u.dve.one("xn", s))
        for s in S:
            eng.wait_ge(u.act.sem, u.act.at("sig", s))
            eng.memset(per_batch(k.b("t4", s))[:, :, 0:1], 0.0).then_inc(u.dve.sem, u.dve.one("gate0", s))
        for s in S:
            eng.wait_ge(u.dve.sem, u.dve.at("gate0", s))
            eng.wait_ge(u.pe.sem, u.pe.at("kv", s))
            eng.tensor_tensor_scan(k.b("t5", s), k.b("t4", s), k.psum[s][2][:], 0.0, ALU.mult, ALU.add)\
               .then_inc(u.dve.sem, u.dve.one("scan", s))
        for s in S:
            eng.wait_ge(u.dve.sem, u.dve.at("scan", s))
            eng.tensor_tensor(k.b("t5", s), k.b("t5", s), k.psum[s][0][:], ALU.mult)\
               .then_inc(u.dve.sem, u.dve.one("qy", s))
        for s in S:
            eng.wait_ge(u.dve.sem, u.dve.at("qy", s))
            eng.tensor_tensor(k.b("x", s), k.b("x", s), k.b("t5", s), ALU.add)\
               .then_inc(u.dve.sem, u.dve.one("x", s))


class CtxNorm(Sub):

    def __init__(self, core, prev):
        super().__init__(core, prev)
        self.pe = core.steps("ctx_pe", Norm.PE)
        self.act = core.steps("ctx_act", Norm.ACT)
        self.dve = core.steps("ctx_dve", Norm.DVE)
        self.norm = Norm(core, self, src="c", out="cn")

    def input_ready(self, eng, s):
        eng.wait_ge(self.k.c_in[s], 16)

    def output_ready(self, eng, s):
        eng.wait_ge(self.dve.sem, self.dve.at("h", s))
        self.prev.output_ready(eng, s)

    def pe_program(self, eng):
        self.norm.pe(eng)

    def act_program(self, eng):
        self.norm.act(eng)

    def dve_program(self, eng):
        self.norm.dve(eng)


class TwiceNorm(Norm):

    PE = Norm.PE
    ACT = (*Norm.ACT, "r2", "ln2", "rstd2")
    DVE = (*Norm.DVE, "var2", "lat", "latb")

    def __init__(self, core, sub, w, b):
        super().__init__(core, sub)
        self.w, self.bias = w, b

    def act(self, eng):
        super().act(eng)
        k, u = self.k, self.sub
        for s in S:
            eng.wait_ge(u.act.sem, u.act.at("rstd", s))
            eng.activation(k.b("t2", s), k.b("t1", s), ACT.Square).then_inc(u.act.sem, u.act.one("r2", s))
        for s in S:
            eng.wait_ge(u.dve.sem, u.dve.at("var2", s))
            eng.activation(k.b("t2", s), k.b("t2", s), ACT.Ln, bias=k.eps5[:, 0:1])\
               .then_inc(u.act.sem, u.act.one("ln2", s))
        for s in S:
            eng.wait_ge(u.act.sem, u.act.at("ln2", s))
            eng.activation(k.b("t2", s), k.b("t2", s), ACT.Exp, scale=-0.5)\
               .then_inc(u.act.sem, u.act.one("rstd2", s))

    def dve_scale(self, eng):
        super().dve_scale(eng)
        k, u = self.k, self.sub
        for s in S:
            eng.wait_ge(u.act.sem, u.act.at("r2", s))
            eng.tensor_tensor(k.b("t2", s), k.psum[s][1][:], k.b("t2", s), ALU.mult)\
               .then_inc(u.dve.sem, u.dve.one("var2", s))
        for s in S:
            eng.wait_ge(u.act.sem, u.act.at("rstd2", s))
            eng.wait_ge(u.dve.sem, u.dve.at("h", s))
            eng.scalar_tensor_tensor(k.b("t3", s), k.b("h", s), k.weight(self.w), k.b("t2", s), ALU.mult, ALU.mult)\
               .then_inc(u.dve.sem, u.dve.one("lat", s))
        for s in S:
            eng.wait_ge(u.dve.sem, u.dve.at("lat", s))
            eng.tensor_scalar(k.b("t3", s), k.b("t3", s), k.weight(self.bias), None, ALU.add)\
               .then_inc(u.dve.sem, u.dve.one("latb", s))


class L0Xattn(Sub):

    HEADS, DH = 8, 64

    def __init__(self, core, prev):
        super().__init__(core, prev)
        pe, act, dve = list(TwiceNorm.PE), list(TwiceNorm.ACT), [*TwiceNorm.DVE, "ctxa"]
        for hh in range(2):
            first = 4 * hh
            if hh == 0:
                pe += [n for p in range(4) for n in (f"q{p}", f"k{p}")]
                act += [f"qs{p}" for p in range(4)]
                dve += [f"ks{p}" for p in range(4)]
            pe += [f"v{first}", f"even{first}", f"odd{first}"]
            act += [f"vs{first}", f"exp{first}"]
            dve += [f"clip{first}"]
            for j in range(first, first + 4):
                more = j < first + 3
                if j > first:
                    act += [f"outs{j - 1}"]
                    dve += [f"recip{j - 1}", f"lo{j - 1}", f"hi{j - 1}"]
                pe += ([f"even{j + 1}", f"odd{j + 1}"] if more else []) + ([f"turn{j - 1}"] if j > first else [])
                pe += ([f"v{j + 1}"] if more else []) + [f"pv{j}"]
                if more:
                    act += [f"vs{j + 1}", f"exp{j + 1}"]
                    dve += [f"clip{j + 1}"]
            j = first + 3
            act += [f"outs{j}"]
            dve += [f"recip{j}", f"lo{j}", f"hi{j}"]
            if hh == 0:
                pe += ["k4", "k5", "turn3", "k6", "k7", "wo0", "q4", "q5", "q6", "q7"]
                act += ["qs4", "qs5", "qs6", "qs7"]
                dve += ["ks4", "ks5", "ks6", "ks7", "x_half"]
            else:
                pe += ["turn7", "wo1"]
                dve += ["x"]
        self.pe, self.act, self.dve = core.steps("l0x_pe", pe), core.steps("l0x_act", act), core.steps("l0x_dve", dve)
        self.norm = TwiceNorm(core, self, "l0x_ln_l_w", "l0x_ln_l_b")

    def q_bank(self, p):
        return (p + p // 4) % 2

    def pe_q(self, eng, p):
        k, u = self.k, self
        for s in S:
            if p == 0:
                eng.wait_ge(u.dve.sem, u.dve.at("latb", s))
            if p % 4 >= 2:
                eng.wait_ge(u.act.sem, u.act.at(f"qs{p - 2}", s))
            if p == 5:
                eng.wait_ge(u.dve.sem, u.dve.at("x_half", s))
            eng.matmul(k.psum[s][self.q_bank(p)][:], k.weight("l0x_wq")[:, p * 128:(p + 1) * 128], k.b("t3", s),
                       start=True, stop=True).then_inc(u.pe.sem, u.pe.one(f"q{p}", s))

    def pe_k(self, eng, p):
        k, u = self.k, self
        for s in S:
            if p == 0:
                eng.wait_ge(u.dve.sem, u.dve.at("ctxa", s))
            if p % 4 >= 2:
                eng.wait_ge(u.dve.sem, u.dve.at(f"ks{p - 2}", s))
            if p == 4:
                eng.wait_ge(u.dve.sem, u.dve.at("hi3", s))
            eng.matmul(k.psum[s][2 + p % 2][:], k.weight("l0x_wkv")[:, p * 128:(p + 1) * 128], k.b("t4", s),
                       start=True, stop=True).then_inc(u.pe.sem, u.pe.one(f"k{p}", s))

    def pe_values(self, eng, j):
        k, u = self.k, self
        t, hh = j % 4, j // 4
        for s in S:
            if t == 0:
                eng.wait_ge(u.act.sem, u.act.at(f"qs{4 * hh + 3}", s))
            else:
                eng.wait_ge(u.act.sem, u.act.at(f"outs{j - 2}" if t > 1 else f"vs{j - 1}", s))
            eng.matmul(k.psum[s][1][:], k.b("t4", s)[:, t * 128:(t + 1) * 128],
                       k.weight("l0x_wkv")[:, 1024 + hh * G:1024 + (hh + 1) * G],
                       start=True, stop=True).then_inc(u.pe.sem, u.pe.one(f"v{j}", s))

    def pe_scores(self, eng, j):
        k, u = self.k, self
        t = j % 4
        for odd, name in enumerate(("even", "odd")):
            half = slice(64 * odd, 64 * odd + 64)
            for s in S:
                if odd:
                    eng.wait_ge(u.pe.sem, u.pe.at(f"even{j}", s))
                elif t == 0:
                    eng.wait_ge(u.act.sem, u.act.at(f"qs{j + 3}", s))
                    eng.wait_ge(u.dve.sem, u.dve.at(f"ks{j + 3}", s))
                else:
                    eng.wait_ge(u.dve.sem, u.dve.at(f"clip{j - 1}", s))
                for h in range(odd, 8, 2):
                    for b in range(2):
                        at = t * 128 + b * T
                        mm = eng.matmul(k.psum[s][0][b * T:(b + 1) * T, h * T:(h + 1) * T],
                                        k.b(f"t{9 + h // 2}", s, half)[:, at:at + T],
                                        k.b(f"t{5 + h // 2}", s, half)[:, at:at + T], start=True, stop=True)
                mm.then_inc(u.pe.sem, u.pe.one(f"{name}{j}", s))

    def pe_turn(self, eng, j):
        k, u = self.k, self
        for s in S:
            eng.wait_ge(u.dve.sem, u.dve.at(f"hi{j}", s))
            eng.wait_ge(u.act.sem, u.act.at(f"vs{j + 1}" if j % 4 < 3 else f"outs{j - 1}", s))
            for p in range(4):
                mm = eng.transpose(k.psum[s][1][:, p * 128:(p + 1) * 128],
                                   k.b("t14", s)[:, p * 128:(p + 1) * 128], k.const("ident"))
            mm.then_inc(u.pe.sem, u.pe.one(f"turn{j}", s))

    def values(self, s, j):
        return self.k.vb[s][:, j % 2 * 520:(j % 2 + 1) * 520].rearrange("p (h c) -> p h c", c=65)

    def exps(self, s, j):
        return self.k.b("t15" if j % 2 else "t13", s)

    def pe_program(self, eng):
        k, u = self.k, self
        self.norm.pe(eng)
        for p in range(4):
            self.pe_q(eng, p)
            self.pe_k(eng, p)
        for hh in range(2):
            first = 4 * hh
            self.pe_values(eng, first)
            self.pe_scores(eng, first)
            for j in range(first, first + 4):
                more = j < first + 3
                if more:
                    self.pe_scores(eng, j + 1)
                if j > first:
                    self.pe_turn(eng, j - 1)
                if more:
                    self.pe_values(eng, j + 1)
                for s in S:
                    eng.wait_ge(u.act.sem, u.act.at(f"exp{j}", s))
                    if j > first:
                        eng.wait_ge(u.dve.sem, u.dve.at(f"hi{j - 1}", s))
                    for h in range(8):
                        for b in range(2):
                            rows = slice(b * T, (b + 1) * T)
                            mm = eng.matmul(k.psum[s][2 + h // 4][rows, (h % 4) * 65:(h % 4 + 1) * 65],
                                            self.exps(s, j)[rows, h * T:(h + 1) * T], self.values(s, j)[rows, h, :],
                                            start=True, stop=True)
                    mm.then_inc(u.pe.sem, u.pe.one(f"pv{j}", s))
            if hh == 0:
                self.pe_k(eng, 4)
                self.pe_k(eng, 5)
            self.pe_turn(eng, first + 3)
            if hh == 0:
                self.pe_k(eng, 6)
                self.pe_k(eng, 7)
            for s in S:
                eng.wait_ge(u.act.sem, u.act.at(f"outs{first + 3}", s))
                for p in range(4):
                    at = (first + p) * 128
                    mm = eng.matmul(k.psum[s][0][:], k.weight("l0x_wo")[:, at:at + 128], k.b(f"t{5 + p}", s),
                                    start=p == 0, stop=p == 3)
                mm.then_inc(u.pe.sem, u.pe.one(f"wo{hh}", s))
            if hh == 0:
                for p in range(4, 8):
                    self.pe_q(eng, p)

    def act_values_and_exp(self, eng, j):
        k, u = self.k, self
        for s in S:
            eng.wait_ge(u.pe.sem, u.pe.at(f"v{j}", s))
            eng.copy(self.values(s, j)[:, 0:8, 0:64], k.psum[s][1][:].rearrange("p (h c) -> p h c", c=64))\
               .then_inc(u.act.sem, u.act.one(f"vs{j}", s))
        for s in S:
            eng.wait_ge(u.dve.sem, u.dve.at(f"clip{j}", s))
            eng.activation(self.exps(s, j), self.exps(s, j), ACT.Exp, scale=0.125)\
               .then_inc(u.act.sem, u.act.one(f"exp{j}", s))

    def act_outs(self, eng, j):
        k, u = self.k, self
        t = j % 4
        for s in S:
            eng.wait_ge(u.pe.sem, u.pe.at(f"turn{j}", s))
            eng.copy(k.wide(s, 5, 4).rearrange("p (q n) -> p q n", n=G)[:, :, t * 128:(t + 1) * 128],
                     k.psum[s][1][:].rearrange("p (q n) -> p q n", n=128))\
               .then_inc(u.act.sem, u.act.one(f"outs{j}", s))

    def act_program(self, eng):
        k, u = self.k, self
        self.norm.act(eng)
        for hh in range(2):
            first = 4 * hh
            for p in range(first, first + 4):
                for s in S:
                    eng.wait_ge(u.pe.sem, u.pe.at(f"q{p}", s))
                    eng.copy(k.b(f"t{5 + p % 4}", s), k.psum[s][self.q_bank(p)][:]).then_inc(u.act.sem, u.act.one(f"qs{p}", s))
            self.act_values_and_exp(eng, first)
            for j in range(first, first + 4):
                if j > first:
                    self.act_outs(eng, j - 1)
                if j < first + 3:
                    self.act_values_and_exp(eng, j + 1)
            self.act_outs(eng, first + 3)

    def dve_clip(self, eng, j):
        k, u = self.k, self
        for s in S:
            eng.wait_ge(u.pe.sem, u.pe.at(f"odd{j}", s))
            eng.tensor_scalar(self.exps(s, j), k.psum[s][0][:], -88.0, 88.0, ALU.max, ALU.min)\
               .then_inc(u.dve.sem, u.dve.one(f"clip{j}", s))

    def dve_outputs(self, eng, j):
        k, u = self.k, self
        outs = lambda s, c: k.psum[s][2 + c][:, 0:260].rearrange("p (h c) -> p h c", c=65)
        for s in S:
            eng.wait_ge(u.pe.sem, u.pe.at(f"pv{j}", s))
            eng.reciprocal(k.small[s][:, 0:4], outs(s, 0)[:, :, 64])
            eng.reciprocal(k.small[s][:, 4:8], outs(s, 1)[:, :, 64])\
               .then_inc(u.dve.sem, u.dve.one(f"recip{j}", s))
        for c, name in enumerate(("lo", "hi")):
            for s in S:
                eng.wait_ge(u.dve.sem, u.dve.at(f"recip{j}", s))
                eng.tensor_tensor(k.b("t14", s)[:, c * 256:(c + 1) * 256].rearrange("p (h c) -> p h c", c=64),
                                  outs(s, c)[:, :, 0:64],
                                  k.small[s][:, 4 * c:4 * c + 4].unsqueeze(2).broadcast_to([128, 4, 64]),
                                  ALU.mult).then_inc(u.dve.sem, u.dve.one(f"{name}{j}", s))

    def dve_program(self, eng):
        k, u = self.k, self
        self.norm.dve(eng)
        for s in S:
            eng.tensor_scalar(k.b("t4", s), k.b("cn", s), k.weight("l0x_ln_c_w"), k.weight("l0x_ln_c_b"),
                              ALU.mult, ALU.add).then_inc(u.dve.sem, u.dve.one("ctxa", s))
        for hh in range(2):
            first = 4 * hh
            for p in range(first, first + 4):
                for s in S:
                    eng.wait_ge(u.pe.sem, u.pe.at(f"k{p}", s))
                    eng.tensor_copy(k.b(f"t{9 + p % 4}", s), k.psum[s][2 + p % 2][:])\
                       .then_inc(u.dve.sem, u.dve.one(f"ks{p}", s))
            if hh == 1:
                for s in S:
                    eng.wait_ge(u.pe.sem, u.pe.at("wo0", s))
                    eng.tensor_tensor(k.b("x", s), k.b("x", s), k.psum[s][0][:], ALU.add)\
                       .then_inc(u.dve.sem, u.dve.one("x_half", s))
            self.dve_clip(eng, first)
            for j in range(first, first + 4):
                if j > first:
                    self.dve_outputs(eng, j - 1)
                if j < first + 3:
                    self.dve_clip(eng, j + 1)
            self.dve_outputs(eng, first + 3)
        for s in S:
            eng.wait_ge(u.pe.sem, u.pe.at("wo1", s))
            eng.wait_ge(u.dve.sem, u.dve.at("x_half", s))
            eng.scalar_tensor_tensor(k.b("x", s), k.psum[s][0][:], k.weight("l0x_bo"), k.b("x", s),
                                     ALU.add, ALU.add).then_inc(u.dve.sem, u.dve.one("x", s))


class Gate:

    PE, ACT = ("logit",), ("gexp",)
    DVE = ("glogit", "gmax", "gsub", "gsum", "grecip", "gprob", "gm0", "ge0", "gkey0", "gmk0", "gsel0", "grest",
           "gm1", "ge1", "gkey1", "gmk1", "gsel1", "gboth", "gate")

    def __init__(self, core, sub, weight, bias=None):
        self.k, self.sub, self.weight, self.bias = core, sub, weight, bias

    def g(self, s, n):
        return self.k.gate[s][:, 32 * n:32 * n + 32]

    def pe(self, eng):
        k, u = self.k, self.sub
        for s in S:
            eng.wait_ge(u.dve.sem, u.dve.at("h", s))
            for t in range(NT):
                mm = eng.matmul(k.psum[s][2][:, t * 8:t * 8 + 8], k.b("h", s)[:, t * 128:(t + 1) * 128],
                                k.weight(self.weight), start=True, stop=True)
            mm.then_inc(u.pe.sem, u.pe.one("logit", s))

    def act(self, eng):
        k, u = self.k, self.sub
        for s in S:
            eng.wait_ge(u.dve.sem, u.dve.at("gsub", s))
            eng.activation(self.g(s, 0), self.g(s, 0), ACT.Exp).then_inc(u.act.sem, u.act.one("gexp", s))

    def dve(self, eng):
        k, u = self.k, self.sub
        g = self.g
        t8 = lambda ap: ap.rearrange("p (t e) -> p t e", e=8)
        sm = lambda s, j: k.small[s][:, 16 + 4 * j:20 + 4 * j]
        over = lambda ap: ap.unsqueeze(2).broadcast_to([128, NT, 8])
        rev = k.const("rev").unsqueeze(1).broadcast_to([128, NT, 8])
        for s in S:
            eng.wait_ge(u.pe.sem, u.pe.at("logit", s))
            if self.bias:
                ins = eng.tensor_tensor(t8(g(s, 0)), t8(k.psum[s][2][:, 0:32]),
                                        k.weight(self.bias).unsqueeze(1).broadcast_to([128, NT, 8]), ALU.add)
            else:
                ins = eng.tensor_copy(g(s, 0), k.psum[s][2][:, 0:32])
            ins.then_inc(u.dve.sem, u.dve.one("glogit", s))
        for s in S:
            eng.wait_ge(u.dve.sem, u.dve.at("glogit", s))
            eng.tensor_reduce(sm(s, 0), t8(g(s, 0)), AX.X, ALU.max).then_inc(u.dve.sem, u.dve.one("gmax", s))
        for s in S:
            eng.wait_ge(u.dve.sem, u.dve.at("gmax", s))
            eng.tensor_tensor(t8(g(s, 0)), t8(g(s, 0)), over(sm(s, 0)), ALU.subtract)\
               .then_inc(u.dve.sem, u.dve.one("gsub", s))
        for s in S:
            eng.wait_ge(u.act.sem, u.act.at("gexp", s))
            eng.tensor_reduce(sm(s, 1), t8(g(s, 0)), AX.X, ALU.add).then_inc(u.dve.sem, u.dve.one("gsum", s))
        for s in S:
            eng.wait_ge(u.dve.sem, u.dve.at("gsum", s))
            eng.reciprocal(sm(s, 2), sm(s, 1)).then_inc(u.dve.sem, u.dve.one("grecip", s))
        for s in S:
            eng.wait_ge(u.dve.sem, u.dve.at("grecip", s))
            eng.tensor_tensor(t8(g(s, 1)), t8(g(s, 0)), over(sm(s, 2)), ALU.mult).then_inc(u.dve.sem, u.dve.one("gprob", s))
        for n, src, cand, sel in ((0, 1, 2, 3), (1, 4, 5, 6)):
            for s in S:
                eng.wait_ge(u.dve.sem, u.dve.at("gprob" if n == 0 else "grest", s))
                eng.tensor_reduce(sm(s, 3 + n), t8(g(s, src)), AX.X, ALU.max).then_inc(u.dve.sem, u.dve.one(f"gm{n}", s))
            for s in S:
                eng.wait_ge(u.dve.sem, u.dve.at(f"gm{n}", s))
                eng.tensor_tensor(t8(g(s, cand)), t8(g(s, src)), over(sm(s, 3 + n)), ALU.is_equal)\
                   .then_inc(u.dve.sem, u.dve.one(f"ge{n}", s))
            for s in S:
                eng.wait_ge(u.dve.sem, u.dve.at(f"ge{n}", s))
                eng.tensor_tensor(t8(g(s, cand)), t8(g(s, cand)), rev, ALU.mult).then_inc(u.dve.sem, u.dve.one(f"gkey{n}", s))
            for s in S:
                eng.wait_ge(u.dve.sem, u.dve.at(f"gkey{n}", s))
                eng.tensor_reduce(sm(s, 5 + n), t8(g(s, cand)), AX.X, ALU.max).then_inc(u.dve.sem, u.dve.one(f"gmk{n}", s))
            for s in S:
                eng.wait_ge(u.dve.sem, u.dve.at(f"gmk{n}", s))
                eng.tensor_tensor(t8(g(s, sel)), t8(g(s, cand)), over(sm(s, 5 + n)), ALU.is_equal)\
                   .then_inc(u.dve.sem, u.dve.one(f"gsel{n}", s))
            if n == 0:
                for s in S:
                    eng.wait_ge(u.dve.sem, u.dve.at("gsel0", s))
                    eng.scalar_tensor_tensor(g(s, 4), g(s, 3), -2.0, g(s, 1), ALU.mult, ALU.add)\
                       .then_inc(u.dve.sem, u.dve.one("grest", s))
        for s in S:
            eng.wait_ge(u.dve.sem, u.dve.at("gsel1", s))
            eng.tensor_tensor(g(s, 7), g(s, 3), g(s, 6), ALU.add).then_inc(u.dve.sem, u.dve.one("gboth", s))
        for s in S:
            eng.wait_ge(u.dve.sem, u.dve.at("gboth", s))
            eng.tensor_tensor(g(s, 8), g(s, 1), g(s, 7), ALU.mult).then_inc(u.dve.sem, u.dve.one("gate", s))


class L0Ffn(Sub):

    E, CAP, HID = 8, 10, 4
    SLOTS = E * CAP

    def __init__(self, core, prev):
        super().__init__(core, prev)
        n = range(self.E // 2)
        self.pe = core.steps("l0f_pe", [*Norm.PE, *Gate.PE, "htok", "rank", "gt", "fill"]
                             + [f"{a}{j}" for j in n for a in ("up", "down")] + ["yt", "comb"])
        self.act = core.steps("l0f_act", [*Norm.ACT, *Gate.ACT, "htok", "gt", "fill"] + [f"relu{j}" for j in n] + ["yt"])
        self.dve = core.steps("l0f_dve", [*Norm.DVE, *Gate.DVE, "hot", "disp", "gated"] + [f"y{j}" for j in n] + ["x"])
        self.norm = Norm(core, self)
        self.gate = Gate(core, self, "l0f_wr")

    def places(self):
        return self.k.wide(0, 10, 3)[:, 0:1280]

    def results(self):
        return self.k.wide(1, 10, 3)[:, 0:1280]

    def hidden(self, odd):
        return self.k.wide(odd, 13, 2)[:, 0:640]

    def pe_program(self, eng):
        k, u = self.k, self
        self.norm.pe(eng)
        eng.wait_ge(k.moe_in[0], 16)
        self.gate.pe(eng)
        for s in S:
            for t in range(NT):
                mm = eng.transpose(k.psum[s][0][:, t * 128:(t + 1) * 128], k.b("h", s)[:, t * 128:(t + 1) * 128],
                                   k.const("ident"))
            mm.then_inc(u.pe.sem, u.pe.one("htok", s))
        for s in S:
            eng.wait_ge(u.dve.sem, u.dve.at("gboth", s))
            eng.matmul(k.psum[s][3][:, 0:32], k.const("earlier"), self.gate.g(s, 7), start=True, stop=True)\
               .then_inc(u.pe.sem, u.pe.one("rank", s))
        for s in S:
            eng.wait_ge(u.dve.sem, u.dve.at("gated", s))
            for t in range(NT):
                mm = eng.transpose(k.psum[s][1][0:80, t * 128:(t + 1) * 128], k.b("t5", s)[:, t * 80:(t + 1) * 80],
                                   k.const("ident"))
            mm.then_inc(u.pe.sem, u.pe.one("gt", s))
        for s in S:
            eng.wait_ge(u.act.sem, u.act.at("htok", s))
            for t in range(NT):
                for b in range(2):
                    rows = slice(b * T, (b + 1) * T)
                    mm = eng.matmul(k.psum[s][2 + b][:, t * 80:(t + 1) * 80], k.b("t6", s, rows)[:, t * 128:(t + 1) * 128],
                                    k.b("t4", s, rows)[:, t * 80:(t + 1) * 80], start=True, stop=True)
            mm.then_inc(u.pe.sem, u.pe.one("fill", s))
        for j in range(self.E // 2):
            for odd in range(2):
                e = 2 * j + odd
                if j == 0:
                    for s in S:
                        eng.wait_ge(u.act.sem, u.act.at("fill", s))
                        eng.wait_ge(u.act.sem, u.act.at("gt", s))
                else:
                    eng.wait_ge(u.act.sem, u.act.at(f"relu{j - 1}", odd))
                for c in range(self.HID):
                    mm = eng.matmul(k.psum[odd][c // 3][:, c % 3 * 160:(c % 3 + 1) * 160],
                                    k.weight("l0f_w1")[:, e * 512 + c * 128:e * 512 + (c + 1) * 128],
                                    self.places()[:, e * 160:(e + 1) * 160], start=True, stop=True)
                mm.then_inc(u.pe.sem, u.pe.one(f"up{j}", odd))
            for odd in range(2):
                e = 2 * j + odd
                eng.wait_ge(u.act.sem, u.act.at(f"relu{j}", odd))
                if j:
                    eng.wait_ge(u.dve.sem, u.dve.at(f"y{j - 1}", odd))
                for c in range(self.HID):
                    mm = eng.matmul(k.psum[odd][2][:, 0:160],
                                    k.weight("l0f_w2")[:, (e * 4 + c) * 128:(e * 4 + c + 1) * 128],
                                    self.hidden(odd)[:, c * 160:(c + 1) * 160], start=c == 0, stop=c == self.HID - 1)
                mm.then_inc(u.pe.sem, u.pe.one(f"down{j}", odd))
        for s in S:
            eng.wait_ge(u.dve.sem, u.dve.at("y3", 0))
            eng.wait_ge(u.dve.sem, u.dve.at("y3", 1))
            for b in range(NB):
                at = (s * NB + b) * 80
                mm = eng.transpose(k.psum[s][b // 4][0:80, b % 4 * 128:(b % 4 + 1) * 128], self.results()[:, at:at + 80],
                                   k.const("ident"))
            mm.then_inc(u.pe.sem, u.pe.one("yt", s))
        for s in S:
            eng.wait_ge(u.act.sem, u.act.at("yt", s))
            for b in range(NB):
                mm = eng.matmul(k.psum[s][2][:, b * T:(b + 1) * T],
                                k.wide(s, 8, 2, slice(0, 80))[:, b * 128:(b + 1) * 128],
                                k.b("t7", s, slice(0, 80))[:, b * T:(b + 1) * T], start=True, stop=True)
            mm.then_inc(u.pe.sem, u.pe.one("comb", s))

    def act_program(self, eng):
        k, u = self.k, self
        self.norm.act(eng)
        self.gate.act(eng)
        for s in S:
            eng.wait_ge(u.pe.sem, u.pe.at("htok", s))
            eng.copy(k.b("t6", s), k.psum[s][0][:]).then_inc(u.act.sem, u.act.one("htok", s))
        for s in S:
            eng.wait_ge(u.pe.sem, u.pe.at("gt", s))
            eng.copy(k.b("t7", s, slice(0, 80)), k.psum[s][1][0:80, :]).then_inc(u.act.sem, u.act.one("gt", s))
        for s in S:
            eng.wait_ge(u.pe.sem, u.pe.at("fill", s))
            for b in range(2):
                to = self.places().rearrange("p (e s t b c) -> p e s t b c", e=8, s=2, t=NT, b=2)[:, :, s, :, b, :]
                ins = eng.copy(to, k.psum[s][2 + b][:, 0:320].rearrange("p (t e c) -> p e t c", t=NT, e=8))
            ins.then_inc(u.act.sem, u.act.one("fill", s))
        for j in range(self.E // 2):
            for odd in range(2):
                e = 2 * j + odd
                eng.wait_ge(u.pe.sem, u.pe.at(f"up{j}", odd))
                for c in range(self.HID):
                    ins = eng.activation(self.hidden(odd)[:, c * 160:(c + 1) * 160],
                                         k.psum[odd][c // 3][:, c % 3 * 160:(c % 3 + 1) * 160], ACT.Relu,
                                         bias=k.weight("l0f_b1")[:, e * 4 + c:e * 4 + c + 1])
                ins.then_inc(u.act.sem, u.act.one(f"relu{j}", odd))
        for s in S:
            eng.wait_ge(u.pe.sem, u.pe.at("yt", s))
            for c in range(2):
                ins = eng.copy(k.wide(s, 8, 2, slice(0, 80))[:, c * G:(c + 1) * G], k.psum[s][c][0:80, :])
            ins.then_inc(u.act.sem, u.act.one("yt", s))

    def dve_program(self, eng):
        k, u = self.k, self
        self.norm.dve(eng)
        self.gate.dve(eng)
        hot = lambda name, s: k.b(name, s)[:, 0:320].rearrange("p (e c) -> p e c", c=self.CAP)
        over = lambda ap: ap.unsqueeze(2).broadcast_to([128, 32, self.CAP])
        for s in S:
            eng.wait_ge(u.pe.sem, u.pe.at("rank", s))
            eng.tensor_tensor(hot("t4", s), over(k.psum[s][3][:, 0:32]),
                              k.const("slot").unsqueeze(1).broadcast_to([128, 32, self.CAP]), ALU.is_equal)\
               .then_inc(u.dve.sem, u.dve.one("hot", s))
        for s in S:
            eng.wait_ge(u.dve.sem, u.dve.at("hot", s))
            eng.tensor_tensor(hot("t4", s), hot("t4", s), over(self.gate.g(s, 7)), ALU.mult)\
               .then_inc(u.dve.sem, u.dve.one("disp", s))
        for s in S:
            eng.wait_ge(u.dve.sem, u.dve.at("disp", s))
            eng.tensor_tensor(hot("t5", s), hot("t4", s), over(self.gate.g(s, 1)), ALU.mult)\
               .then_inc(u.dve.sem, u.dve.one("gated", s))
        for j in range(self.E // 2):
            for odd in range(2):
                e = 2 * j + odd
                eng.wait_ge(u.pe.sem, u.pe.at(f"down{j}", odd))
                eng.tensor_scalar(self.results().rearrange("p (b e c) -> p b e c", e=8, c=10)[:, :, e, :],
                                  k.psum[odd][2][:, 0:160].rearrange("p (b c) -> p b c", c=10),
                                  k.weight("l0f_b2")[:, e:e + 1], None, ALU.add).then_inc(u.dve.sem, u.dve.one(f"y{j}", odd))
        for s in S:
            eng.wait_ge(u.pe.sem, u.pe.at("comb", s))
            eng.tensor_tensor(k.b("x", s), k.b("x", s), k.psum[s][2][:], ALU.add).then_inc(u.dve.sem, u.dve.one("x", s))


class GroupNorm:

    PE, ACT, DVE = ("gmean", "gvar"), ("gsq", "gln", "grstd"), ("gxc", "gn")

    def __init__(self, core, sub, src, ready):
        self.k, self.sub, self.src, self.ready = core, sub, src, ready

    def pe(self, eng):
        k, u = self.k, self.sub
        for s in S:
            self.ready(eng, s)
            eng.matmul(k.psum[s][2][:], k.const("mean32"), k.b(self.src, s), start=True, stop=True)\
               .then_inc(u.pe.sem, u.pe.one("gmean", s))
        for s in S:
            eng.wait_ge(u.act.sem, u.act.at("gsq", s))
            eng.matmul(k.psum[s][3][:], k.const("mean32"), k.b("t13", s), start=True, stop=True)\
               .then_inc(u.pe.sem, u.pe.one("gvar", s))

    def act(self, eng):
        k, u = self.k, self.sub
        for s in S:
            eng.wait_ge(u.dve.sem, u.dve.at("gxc", s))
            eng.activation(k.b("t13", s), k.b("t12", s), ACT.Square).then_inc(u.act.sem, u.act.one("gsq", s))
        for s in S:
            eng.wait_ge(u.pe.sem, u.pe.at("gvar", s))
            eng.activation(k.b("t13", s), k.psum[s][3][:], ACT.Ln, bias=k.eps5[:, 0:1])\
               .then_inc(u.act.sem, u.act.one("gln", s))
        for s in S:
            eng.wait_ge(u.act.sem, u.act.at("gln", s))
            eng.activation(k.b("t13", s), k.b("t13", s), ACT.Exp, scale=-0.5).then_inc(u.act.sem, u.act.one("grstd", s))

    def dve(self, eng):
        k, u = self.k, self.sub
        for s in S:
            eng.wait_ge(u.pe.sem, u.pe.at("gmean", s))
            eng.tensor_tensor(k.b("t12", s), k.b(self.src, s), k.psum[s][2][:], ALU.subtract)\
               .then_inc(u.dve.sem, u.dve.one("gxc", s))
        for s in S:
            eng.wait_ge(u.act.sem, u.act.at("grstd", s))
            eng.wait_ge(u.dve.sem, u.dve.at("gxc", s))
            eng.tensor_tensor(k.b("t12", s), k.b("t12", s), k.b("t13", s), ALU.mult)\
               .then_inc(u.dve.sem, u.dve.one("gn", s))


class L1Xattn(Sub):

    def __init__(self, core, prev):
        super().__init__(core, prev)
        self.pe = core.steps("l1x_pe", ["mean", "fgc", "var", "igc", "fg", "ig", "qk01", "qk23", "logd", "num", *GroupNorm.PE])
        self.act = core.steps("l1x_act", [*Norm.ACT, "fabs", "fexp", "fln", "expnm", "dexp", "absd", "dln", "drec", *GroupNorm.ACT])
        self.dve = core.steps("l1x_dve", [*Norm.DVE, "f", "g", "lf", "cs", "gs", "m", "m1", "csm", "dmin", "c", "norm", "out", *GroupNorm.DVE, "x"])
        self.gps = core.steps("l1x_pool", ["g1"])
        self.norm = Norm(core, self)
        self.gn = GroupNorm(core, self, "t11", lambda eng, s: eng.wait_ge(self.dve.sem, self.dve.at("out", s)))

    def pe_program(self, eng):
        k, u = self.k, self
        place = [(h, t, b) for h in range(4) for t in range(NT) for b in range(2)]

        def gate(name, bank, part, src):
            for s in S:
                if part == 0:
                    eng.wait_ge(u.dve.sem, u.dve.at("h", s))
                else:
                    eng.wait_ge(k.c_in[s], 16)
                eng.matmul(k.psum[s][bank][:], k.weight("l1x_" + name[:2])[:, part * 128:(part + 1) * 128], k.b(src, s),
                           start=part == 1, stop=part == 0).then_inc(u.pe.sem, u.pe.one(name, s))

        def scores(name, heads):
            for s in S:
                if heads[0]:
                    eng.wait_ge(u.dve.sem, u.dve.at("g", s))
                for h, t, b in place:
                    if h in heads:
                        rows, at = slice(32 * h, 32 * h + 32), t * 128 + b * T
                        mm = eng.matmul(k.psum[s][h][b * T:(b + 1) * T, 256 + t * T:256 + (t + 1) * T],
                                        k.b("c", s, rows)[:, at:at + T], k.b("h", s, rows)[:, at:at + T], start=True,
                                        stop=True, tile_position=(32 * h, 64 * b))
                mm.then_inc(u.pe.sem, u.pe.one(name, s))

        self.norm.pe_mean(eng)
        gate("fgc", 3, 1, "c")
        self.norm.pe_var(eng)
        gate("igc", 2, 1, "c")
        gate("fg", 3, 0, "h")
        gate("ig", 2, 0, "h")
        scores("qk01", (0, 1))
        scores("qk23", (2, 3))
        for s in S:
            eng.wait_ge(u.gps.sem, u.gps.at("g1", s))
            eng.wait_ge(u.dve.sem, u.dve.at("m1", s))
            for h, t, b in place:
                rows, at = slice(32 * h, 32 * h + 32), t * 128 + b * T
                mm = eng.matmul(k.psum[s][h][b * T:(b + 1) * T, t * T:(t + 1) * T], k.b("t3", s, rows)[:, at:at + T],
                                k.b("t2", s, rows)[:, at:at + T], start=True, stop=True, tile_position=(32 * h, 64 * b))
            mm.then_inc(u.pe.sem, u.pe.one("logd", s))
        for s in S:
            eng.wait_ge(u.dve.sem, u.dve.at("c", s))
            eng.wait_ge(k.ctok_in[s], 16)
            for h, t, b in place:
                rows, cols = slice(64 * b, 64 * b + 64), slice((h * NT + t) * T, (h * NT + t + 1) * T)
                weights = k.wide(s, 8, 2, rows)[:, cols]
                heads = slice(32 * h, 32 * h + 32)
                eng.matmul(k.psum[s][b][heads, t * T:(t + 1) * T], k.b("ctok", s, rows)[:, t * 128 + 32 * h:t * 128 + 32 * h + 32],
                           weights, start=True, stop=True, tile_position=(64 * b, 32 * h))
                mm = eng.matmul(k.psum[s][b][heads, 256 + t * T:256 + (t + 1) * T], k.const("ones", rows)[:, 0:32],
                                weights, start=True, stop=True, tile_position=(64 * b, 32 * h))
            mm.then_inc(u.pe.sem, u.pe.one("num", s))
        self.gn.pe(eng)

    def act_program(self, eng):
        k, u = self.k, self
        self.norm.act(eng)
        for s in S:
            eng.wait_ge(u.dve.sem, u.dve.at("f", s))
            eng.activation(k.b("t3", s), k.b("t2", s), ACT.Abs).then_inc(u.act.sem, u.act.one("fabs", s))
        for s in S:
            eng.wait_ge(u.act.sem, u.act.at("fabs", s))
            eng.activation(k.b("t3", s), k.b("t3", s), ACT.Exp, scale=-1.0).then_inc(u.act.sem, u.act.one("fexp", s))
        for s in S:
            eng.wait_ge(u.act.sem, u.act.at("fexp", s))
            eng.activation(k.b("t3", s), k.b("t3", s), ACT.Ln, bias=1.0).then_inc(u.act.sem, u.act.one("fln", s))
        for s in S:
            eng.wait_ge(u.dve.sem, u.dve.at("csm", s))
            eng.activation(k.b("t7", s), k.b("t7", s), ACT.Exp, scale=-1.0).then_inc(u.act.sem, u.act.one("expnm", s))
        for s in S:
            eng.wait_ge(u.dve.sem, u.dve.at("dmin", s))
            eng.activation(k.wide(s, 8, 2), k.wide(s, 8, 2), ACT.Exp).then_inc(u.act.sem, u.act.one("dexp", s))
        for s in S:
            eng.wait_ge(u.pe.sem, u.pe.at("num", s))
            for b in range(2):
                ins = eng.activation(k.b("t10", s).rearrange("p (t b q) -> p t b q", b=2, q=T)[:, :, b, :],
                                     k.psum[s][b][:, 256:512].rearrange("p (t q) -> p t q", q=T), ACT.Abs)
            ins.then_inc(u.act.sem, u.act.one("absd", s))
        for s in S:
            eng.wait_ge(u.dve.sem, u.dve.at("norm", s))
            eng.activation(k.b("t10", s), k.b("t10", s), ACT.Ln, bias=k.const("tiny")).then_inc(u.act.sem, u.act.one("dln", s))
        for s in S:
            eng.wait_ge(u.act.sem, u.act.at("dln", s))
            eng.activation(k.b("t10", s), k.b("t10", s), ACT.Exp, scale=-1.0).then_inc(u.act.sem, u.act.one("drec", s))
        self.gn.act(eng)

    def dve_program(self, eng):
        k, u = self.k, self
        self.norm.dve(eng)
        for s in S:
            eng.wait_ge(u.pe.sem, u.pe.at("fg", s))
            eng.tensor_scalar(k.b("t2", s), k.psum[s][3][:], k.weight("l1x_fgb"), None, ALU.add)\
               .then_inc(u.dve.sem, u.dve.one("f", s))
        for s in S:
            eng.wait_ge(u.pe.sem, u.pe.at("ig", s))
            eng.tensor_scalar(k.b("t5", s), k.psum[s][2][:], k.weight("l1x_igb"), None, ALU.add)\
               .then_inc(u.dve.sem, u.dve.one("g", s))
        for s in S:
            eng.wait_ge(u.act.sem, u.act.at("fln", s))
            eng.scalar_tensor_tensor(k.b("t2", s), k.b("t2", s), 0.0, k.b("t3", s), ALU.min, ALU.subtract)\
               .then_inc(u.dve.sem, u.dve.one("lf", s))
        for s in S:
            eng.wait_ge(u.dve.sem, u.dve.at("lf", s))
            eng.tensor_tensor_scan(k.b("t4", s), k.const("keep"), k.b("t2", s), 0.0, ALU.mult, ALU.add)\
               .then_inc(u.dve.sem, u.dve.one("cs", s))
        for s in S:
            eng.wait_ge(u.dve.sem, u.dve.at("cs", s))
            late = per_batch(k.b("t5", s))[:, :, 1:T]
            eng.tensor_tensor(late, late, per_batch(k.b("t4", s))[:, :, 0:T - 1], ALU.subtract)\
               .then_inc(u.dve.sem, u.dve.one("gs", s))
        for s in S:
            eng.wait_ge(u.dve.sem, u.dve.at("gs", s))
            eng.tensor_tensor_scan(k.b("t6", s), k.const("start"), k.b("t5", s), 0.0, ALU.add, ALU.max)\
               .then_inc(u.dve.sem, u.dve.one("m", s))
        for s in S:
            eng.wait_ge(u.dve.sem, u.dve.at("m", s))
            eng.tensor_scalar(k.b("t2", s), k.b("t6", s), k.const("row1"), k.const("row0"), ALU.mult, ALU.add)\
               .then_inc(u.dve.sem, u.dve.one("m1", s))
        for s in S:
            eng.tensor_tensor(k.b("t7", s), k.b("t4", s), k.b("t6", s), ALU.add).then_inc(u.dve.sem, u.dve.one("csm", s))
        tiles = lambda ap: ap.rearrange("p (t q) -> p t q", q=T)
        for s in S:
            eng.wait_ge(u.pe.sem, u.pe.at("logd", s))
            for h in range(4):
                ins = eng.tensor_tensor(tiles(k.wide(s, 8, 2)[:, h * 256:(h + 1) * 256]), tiles(k.psum[s][h][:, 0:256]),
                                        k.const("cap").unsqueeze(1).broadcast_to([128, NT, T]), ALU.min)
            ins.then_inc(u.dve.sem, u.dve.one("dmin", s))
        for s in S:
            eng.wait_ge(u.act.sem, u.act.at("dexp", s))
            for h in range(4):
                w = k.wide(s, 8, 2)[:, h * 256:(h + 1) * 256]
                ins = eng.scalar_tensor_tensor(w, k.psum[s][h][:, 256:512], 32 ** -0.5, w, ALU.mult, ALU.mult)
            ins.then_inc(u.dve.sem, u.dve.one("c", s))
        for s in S:
            eng.wait_ge(u.act.sem, u.act.at("absd", s))
            eng.scalar_tensor_tensor(k.b("t10", s), k.b("t7", s), 1e18, k.b("t10", s), ALU.min, ALU.max)\
               .then_inc(u.dve.sem, u.dve.one("norm", s))
        for s in S:
            eng.wait_ge(u.act.sem, u.act.at("drec", s))
            tile = lambda name, b: k.b(name, s).rearrange("p (t b q) -> p t b q", b=2, q=T)[:, :, b, :]
            for b in range(2):
                ins = eng.tensor_tensor(tile("t11", b), tiles(k.psum[s][b][:, 0:256]), tile("t10", b), ALU.mult)
            ins.then_inc(u.dve.sem, u.dve.one("out", s))
        self.gn.dve(eng)
        for s in S:
            eng.wait_ge(u.dve.sem, u.dve.at("gn", s))
            eng.scalar_tensor_tensor(k.b("x", s), k.b("t12", s), k.out_scale[:, 0:1], k.b("x", s), ALU.mult, ALU.add)\
               .then_inc(u.dve.sem, u.dve.one("x", s))

    def pool_program(self, eng):
        k, u = self.k, self
        for s in S:
            eng.wait_ge(u.dve.sem, u.dve.at("gs", s))
            eng.tensor_scalar(k.b("t3", s), k.b("t5", s), k.const("row0"), k.const("row1"), ALU.mult, ALU.subtract)\
               .then_inc(u.gps.sem, u.gps.one("g1", s))


class L3Xattn(Sub):

    def __init__(self, core, prev):
        super().__init__(core, prev)
        self.pe = core.steps("l3x_pe", [*Norm.PE, "k", "v", "q", "score", "turn", "pv"])
        self.act = core.steps("l3x_act", [*Norm.ACT, "ks", "vs", "exp", "probs"])
        self.dve = core.steps("l3x_dve", ["fill", "fillneg", *Norm.DVE, "qs", "masked", "max", "sub", "sum", "recip", "scaled", "x"])
        self.norm = Norm(core, self)

    def pe_program(self, eng):
        k, u = self.k, self
        self.norm.pe(eng)
        for s in S:
            eng.wait_ge(k.c_in[s], 16)
            eng.matmul(k.psum[s][2][:], k.weight("l3x_wk"), k.b("c", s), start=True, stop=True)\
               .then_inc(u.pe.sem, u.pe.one("k", s))
        for s in S:
            for tp in range(2):
                for b in range(2):
                    for t2 in range(2):
                        at = (2 * tp + t2) * 128 + b * T
                        mm = eng.matmul(k.psum[s][3][64 * t2:64 * t2 + 64, (2 * tp + b) * 128:(2 * tp + b + 1) * 128],
                                        k.b("c", s)[:, at:at + T], k.weight("l3x_wv"), start=True, stop=True)
            mm.then_inc(u.pe.sem, u.pe.one("v", s))
        for s in S:
            eng.wait_ge(u.dve.sem, u.dve.at("h", s))
            eng.matmul(k.psum[s][0][:], k.weight("l3x_wq"), k.b("h", s), start=True, stop=True)\
               .then_inc(u.pe.sem, u.pe.one("q", s))
        for s in S:
            eng.wait_ge(u.act.sem, u.act.at("ks", s))
            eng.wait_ge(u.dve.sem, u.dve.at("qs", s))
            for t in range(NT):
                for b in range(2):
                    at = t * 128 + b * T
                    mm = eng.matmul(k.psum[s][2][b * T:(b + 1) * T, t * T:(t + 1) * T], k.b("t5", s)[:, at:at + T],
                                    k.b("t6", s)[:, at:at + T], start=True, stop=True)
            mm.then_inc(u.pe.sem, u.pe.one("score", s))
        for s in S:
            eng.wait_ge(u.dve.sem, u.dve.at("scaled", s))
            for tp in range(2):
                mm = eng.transpose(k.psum[s][0][:, tp * 128:(tp + 1) * 128], k.b("t11", s)[:, tp * 128:(tp + 1) * 128],
                                   k.const("ident"))
            mm.then_inc(u.pe.sem, u.pe.one("turn", s))
        for s in S:
            eng.wait_ge(u.act.sem, u.act.at("probs", s))
            eng.wait_ge(u.act.sem, u.act.at("vs", s))
            for tp in range(2):
                for b in range(2):
                    for t2 in range(2):
                        rows = slice(64 * t2, 64 * t2 + 64)
                        mm = eng.matmul(k.psum[s][1 + t2][:, (2 * tp + b) * T:(2 * tp + b + 1) * T],
                                        k.b("t7", s, rows)[:, (2 * tp + b) * 128:(2 * tp + b + 1) * 128],
                                        k.b("t12", s, rows)[:, tp * 128 + b * T:tp * 128 + (b + 1) * T], start=True, stop=True)
            mm.then_inc(u.pe.sem, u.pe.one("pv", s))

    def act_program(self, eng):
        k, u = self.k, self
        self.norm.act(eng)
        for s in S:
            eng.wait_ge(u.pe.sem, u.pe.at("k", s))
            eng.activation(k.b("t6", s), k.psum[s][2][:], ACT.Identity, bias=k.weight("l3x_bk"))\
               .then_inc(u.act.sem, u.act.one("ks", s))
        for s in S:
            eng.wait_ge(u.pe.sem, u.pe.at("v", s))
            eng.copy(k.b("t7", s), k.psum[s][3][:]).then_inc(u.act.sem, u.act.one("vs", s))
        for s in S:
            eng.wait_ge(u.dve.sem, u.dve.at("sub", s))
            eng.activation(k.b("t11", s)[:, 0:256], k.b("t11", s)[:, 0:256], ACT.Exp).then_inc(u.act.sem, u.act.one("exp", s))
        for s in S:
            eng.wait_ge(u.pe.sem, u.pe.at("turn", s))
            eng.copy(k.b("t12", s)[:, 0:256], k.psum[s][0][:, 0:256]).then_inc(u.act.sem, u.act.one("probs", s))

    def dve_program(self, eng):
        k, u = self.k, self
        for s in S:
            eng.wait_ge(k.mask_in[s], 80)
            eng.tensor_scalar(k.fill1[s][:], k.fill1[s][:].bitcast(I32), 0.0, 1.0, ALU.not_equal, ALU.subtract)\
               .then_inc(u.dve.sem, u.dve.one("fill", s))
        for s in S:
            eng.wait_ge(u.dve.sem, u.dve.at("fill", s))
            eng.tensor_scalar(k.fill1[s][:], k.fill1[s][:], 3e38, None, ALU.mult).then_inc(u.dve.sem, u.dve.one("fillneg", s))
        self.norm.dve(eng)
        for s in S:
            eng.wait_ge(u.pe.sem, u.pe.at("q", s))
            eng.tensor_scalar(k.b("t5", s), k.psum[s][0][:], k.weight("l3x_bq"), None, ALU.add)\
               .then_inc(u.dve.sem, u.dve.one("qs", s))
        w = lambda s: k.b("t11", s)[:, 0:256]
        tiles = lambda s: w(s).rearrange("p (t j) -> p t j", j=T)
        for s in S:
            eng.wait_ge(u.pe.sem, u.pe.at("score", s))
            eng.wait_ge(u.dve.sem, u.dve.at("fillneg", s))
            eng.scalar_tensor_tensor(w(s), k.psum[s][2][:, 0:256], 128 ** -0.5, k.fill1[s][:], ALU.mult, ALU.add)\
               .then_inc(u.dve.sem, u.dve.one("masked", s))
        for s in S:
            eng.wait_ge(u.dve.sem, u.dve.at("masked", s))
            eng.tensor_reduce(k.small[s][:, 0:4], tiles(s), AX.X, ALU.max).then_inc(u.dve.sem, u.dve.one("max", s))
        for s in S:
            eng.wait_ge(u.dve.sem, u.dve.at("max", s))
            eng.tensor_tensor(tiles(s), tiles(s), k.small[s][:, 0:4].unsqueeze(2).broadcast_to([128, 4, T]), ALU.subtract)\
               .then_inc(u.dve.sem, u.dve.one("sub", s))
        for s in S:
            eng.wait_ge(u.act.sem, u.act.at("exp", s))
            eng.tensor_reduce(k.small[s][:, 4:8], tiles(s), AX.X, ALU.add).then_inc(u.dve.sem, u.dve.one("sum", s))
        for s in S:
            eng.wait_ge(u.dve.sem, u.dve.at("sum", s))
            eng.reciprocal(k.small[s][:, 8:12], k.small[s][:, 4:8]).then_inc(u.dve.sem, u.dve.one("recip", s))
        for s in S:
            eng.wait_ge(u.dve.sem, u.dve.at("recip", s))
            eng.tensor_tensor(tiles(s), tiles(s), k.small[s][:, 8:12].unsqueeze(2).broadcast_to([128, 4, T]), ALU.mult)\
               .then_inc(u.dve.sem, u.dve.one("scaled", s))
        for s in S:
            eng.wait_ge(u.pe.sem, u.pe.at("pv", s))
            for t2 in range(2):
                to = k.b("x", s).rearrange("p (a t n) -> p a t n", t=2, n=128)[:, :, t2, :]
                ins = eng.scalar_tensor_tensor(to, k.psum[s][1 + t2][:, 0:256].rearrange("p (a n) -> p a n", n=128),
                                               k.weight("l3x_bv"), to, ALU.add, ALU.add)
            ins.then_inc(u.dve.sem, u.dve.one("x", s))
class Attention16:

    def __init__(self, core, sub, masked, scale, values, value_w, value_bias, out_w, out_bias,
                 values_ready, queries_ready):
        self.k, self.sub, self.masked, self.scale = core, sub, masked, scale
        self.values_ready, self.queries_ready = values_ready, queries_ready
        self.values, self.value_w, self.value_bias, self.out_w, self.out_bias = values, value_w, value_bias, out_w, out_bias

    PE = ["v0", "even0", "odd0"] + [
        n for j in range(8)
        for n in ([f"even{j + 1}", f"odd{j + 1}"] if j < 7 else []) + [f"turn{j}"]
        + ([f"back{j - 1}"] if j in (2, 4, 6) else []) + ([f"v{j + 1}"] if j in (1, 3, 5) else []) + [f"pv{j}"]] + ["back7", "wo"]
    ACT = ["vs0", "exp0"] + [
        n for j in range(8)
        for n in [f"probs{j}"] + ([f"outs{j - 1}"] if j in (2, 4, 6) else []) + ([f"exp{j + 1}"] if j < 7 else [])
        + ([f"vs{j + 1}"] if j in (1, 3, 5) else [])] + ["outs7"]

    POOL = ["spread0", "spread1", "spread2", "spread3"]

    @staticmethod
    def dve_steps(masked):
        soft = lambda j: ([f"fill{j}"] if masked else []) + [f"max{j}", f"sub{j}"]
        return soft(0) + [n for j in range(8) for n in ([f"recip{j - 1}", f"out{j - 1}"] if j else [])
                                       + (soft(j + 1) if j < 7 else [])] + ["recip7", "out7", "x"]

    def exps(self, s, j):
        return self.k.b("t15" if j % 2 else "t11", s)

    def pe_scores(self, eng, j):
        k, u = self.k, self.sub
        t, half = j // 2, j % 2
        for odd, name in enumerate(("even", "odd")):
            g = 2 * half + odd
            rows = slice(32 * g, 32 * g + 32)
            for s in S:
                if odd:
                    eng.wait_ge(u.pe.sem, u.pe.at(f"even{j}", s))
                else:
                    eng.wait_ge(u.gps.sem, u.gps.at(f"spread{t}", s))
                if j and not odd:
                    eng.wait_ge(u.dve.sem, u.dve.at(f"fill{j - 1}" if self.masked else f"sub{j - 1}", s))
                for b in range(2):
                    at = t * 128 + b * T
                    mm = eng.matmul(k.psum[s][0][b * T:(b + 1) * T, odd * 256:odd * 256 + 256], k.b("t5", s, rows)[:, at:at + T],
                                    k.wide(s, 7, 4, rows)[:, (2 * t + b) * 256:(2 * t + b + 1) * 256],
                                    start=True, stop=True, tile_position=(32 * g, 64 * b))
                mm.then_inc(u.pe.sem, u.pe.one(f"{name}{j}", s))

    def pe_values(self, eng, j):
        k, u = self.k, self.sub
        vw = k.weight(self.value_w[0])[:, self.value_w[1]:self.value_w[1] + D]
        for s in S:
            if j >= 4:
                eng.wait_ge(u.act.sem, u.act.at(f"outs{j - 3}", s))
            elif j:
                eng.wait_ge(u.act.sem, u.act.at("vs0", s))
            else:
                self.values_ready(eng, s)
            for b in range(2):
                at = (j // 2) * 128 + b * T
                for h2 in range(2):
                    mm = eng.matmul(k.psum[s][3][64 * h2:64 * h2 + 64, b * 128:(b + 1) * 128],
                                    k.b(self.values, s)[:, at:at + T], vw, start=True, stop=True)
            mm.then_inc(u.pe.sem, u.pe.one(f"v{j}", s))

    def pe_back(self, eng, j):
        k, u = self.k, self.sub
        for s in S:
            eng.wait_ge(u.dve.sem, u.dve.at(f"out{j}", s))
            eng.wait_ge(u.act.sem, u.act.at(f"vs{min(j + 1, 6)}", s))
            eng.transpose(k.psum[s][3][:, 0:128], k.b("t13", s)[:, 0:128], k.const("ident"))\
               .then_inc(u.pe.sem, u.pe.one(f"back{j}", s))

    def pe(self, eng):
        k, u = self.k, self.sub
        self.pe_values(eng, 0)
        for s in S:
            self.queries_ready(eng, s)
        self.pe_scores(eng, 0)
        for j in range(8):
            half = j % 2
            if j < 7:
                self.pe_scores(eng, j + 1)
            for s in S:
                eng.wait_ge(u.act.sem, u.act.at(f"exp{j}", s))
                for p in range(4):
                    mm = eng.transpose(k.psum[s][1][:, p * 128:(p + 1) * 128],
                                       self.exps(s, j)[:, p * 128:(p + 1) * 128], k.const("ident"))
                mm.then_inc(u.pe.sem, u.pe.one(f"turn{j}", s))
            if j in (2, 4, 6):
                self.pe_back(eng, j - 1)
            if j in (1, 3, 5):
                self.pe_values(eng, j + 1)
            for s in S:
                eng.wait_ge(u.act.sem, u.act.at(f"probs{j}", s))
                if j:
                    eng.wait_ge(u.dve.sem, u.dve.at(f"out{j - 1}", s))
                vbd = k.vbd[s].ap().rearrange("p (b q c) -> p b q c", b=2, c=18)
                for p in range(4):
                    for b in range(2):
                        mm = eng.matmul(k.psum[s][2][b * T:(b + 1) * T, half * 72 + p * 18:half * 72 + (p + 1) * 18],
                                        k.b("t12", s)[:, p * 128 + b * T:p * 128 + (b + 1) * T],
                                        vbd[:, b, 4 * half + p, :], start=True, stop=True)
                mm.then_inc(u.pe.sem, u.pe.one(f"pv{j}", s))
        self.pe_back(eng, 7)
        for s in S:
            eng.wait_ge(u.act.sem, u.act.at("outs7", s))
            eng.matmul(k.psum[s][1][:], k.weight(self.out_w), k.b("t14", s), start=True, stop=True)\
               .then_inc(u.pe.sem, u.pe.one("wo", s))

    def act_exp(self, eng, j):
        k, u = self.k, self.sub
        for s in S:
            eng.wait_ge(u.dve.sem, u.dve.at(f"sub{j}", s))
            eng.activation(self.exps(s, j), self.exps(s, j), ACT.Exp, scale=1.0 if self.masked else self.scale)\
               .then_inc(u.act.sem, u.act.one(f"exp{j}", s))

    def act_values(self, eng, j):
        k, u = self.k, self.sub
        for s in S:
            eng.wait_ge(u.pe.sem, u.pe.at(f"v{j}", s))
            if j:
                eng.wait_ge(u.pe.sem, u.pe.at(f"pv{j - 1}", s))
            for h2 in range(2):
                rows = slice(64 * h2, 64 * h2 + 64)
                ins = eng.copy(k.vbd[s][rows, :].rearrange("p (q c) -> p q c", c=18)[:, :, 9 * h2:9 * h2 + 8],
                               k.psum[s][3][rows, 0:256].rearrange("p (q c) -> p q c", c=16)[:, :, 8 * h2:8 * h2 + 8])
            ins.then_inc(u.act.sem, u.act.one(f"vs{j}", s))

    def act_outs(self, eng, j):
        k, u = self.k, self.sub
        for s in S:
            eng.wait_ge(u.pe.sem, u.pe.at(f"back{j}", s))
            to = k.b("t14", s)[:, (j // 2) * 128:(j // 2 + 1) * 128]
            if self.value_bias:
                ins = eng.activation(to, k.psum[s][3][:, 0:128], ACT.Identity, bias=k.weight(self.value_bias))
            else:
                ins = eng.copy(to, k.psum[s][3][:, 0:128])
            ins.then_inc(u.act.sem, u.act.one(f"outs{j}", s))

    def act(self, eng):
        k, u = self.k, self.sub
        self.act_values(eng, 0)
        self.act_exp(eng, 0)
        for j in range(8):
            for s in S:
                eng.wait_ge(u.pe.sem, u.pe.at(f"turn{j}", s))
                eng.copy(k.b("t12", s), k.psum[s][1][:]).then_inc(u.act.sem, u.act.one(f"probs{j}", s))
            if j in (2, 4, 6):
                self.act_outs(eng, j - 1)
            if j < 7:
                self.act_exp(eng, j + 1)
            if j in (1, 3, 5):
                self.act_values(eng, j + 1)
        self.act_outs(eng, 7)

    def dve_softmax(self, eng, j):
        k, u = self.k, self.sub
        heads = lambda ap: ap.rearrange("p (h j) -> p h j", j=T)
        if self.masked:
            for s in S:
                eng.wait_ge(u.pe.sem, u.pe.at(f"odd{j}", s))
                if j >= 2:
                    eng.wait_ge(u.pe.sem, u.pe.at(f"turn{j - 2}", s))
                eng.scalar_tensor_tensor(
                    heads(self.exps(s, j)), heads(k.psum[s][0][:]), self.scale,
                    k.fill0[s][:, (j // 2) * T:(j // 2 + 1) * T].unsqueeze(1).broadcast_to([128, 8, T]), ALU.mult, ALU.add)\
                   .then_inc(u.dve.sem, u.dve.one(f"fill{j}", s))
        scores = lambda s: self.exps(s, j) if self.masked else k.psum[s][0][:]
        for s in S:
            if self.masked:
                eng.wait_ge(u.dve.sem, u.dve.at(f"fill{j}", s))
            else:
                eng.wait_ge(u.pe.sem, u.pe.at(f"odd{j}", s))
                if j:
                    eng.wait_ge(u.dve.sem, u.dve.at(f"sub{j - 1}", s))
            eng.tensor_reduce(k.small[s][:, 0:8], heads(scores(s)), AX.X, ALU.max)\
               .then_inc(u.dve.sem, u.dve.one(f"max{j}", s))
        for s in S:
            eng.wait_ge(u.dve.sem, u.dve.at(f"max{j}", s))
            if j >= 2:
                eng.wait_ge(u.pe.sem, u.pe.at(f"turn{j - 2}", s))
            eng.tensor_tensor(heads(self.exps(s, j)), heads(scores(s)),
                              k.small[s][:, 0:8].unsqueeze(2).broadcast_to([128, 8, T]), ALU.subtract)\
               .then_inc(u.dve.sem, u.dve.one(f"sub{j}", s))

    def dve_outputs(self, eng, j):
        k, u = self.k, self.sub
        half = j % 2
        outs = lambda s: k.psum[s][2][:, half * 72:half * 72 + 72].rearrange("p (h c) -> p h c", c=9)
        for s in S:
            eng.wait_ge(u.pe.sem, u.pe.at(f"pv{j}", s))
            eng.reciprocal(k.small[s][:, 8:16], outs(s)[:, :, 8]).then_inc(u.dve.sem, u.dve.one(f"recip{j}", s))
        for s in S:
            eng.wait_ge(u.dve.sem, u.dve.at(f"recip{j}", s))
            eng.tensor_tensor(k.b("t13", s)[:, half * T:half * T + T].rearrange("p (h c) -> p h c", c=8),
                              outs(s)[:, :, 0:8], k.small[s][:, 8:16].unsqueeze(2).broadcast_to([128, 8, 8]), ALU.mult)\
               .then_inc(u.dve.sem, u.dve.one(f"out{j}", s))

    def pool(self, eng, keys_ready):
        k, u = self.k, self.sub
        for t in range(NT):
            for s in S:
                if t == 0:
                    keys_ready(eng, s)
                eng.tensor_tensor(k.b(f"t{7 + t}", s).rearrange("p (b h j) -> p b h j", h=4, j=T),
                                  per_batch(k.b("t6", s))[:, 2 * t:2 * t + 2].unsqueeze(2).broadcast_to([128, 2, 4, T]),
                                  k.const("head4").unsqueeze(1).unsqueeze(3).broadcast_to([128, 2, 4, T]), ALU.mult)\
                   .then_inc(u.gps.sem, u.gps.one(f"spread{t}", s))

    def dve(self, eng):
        k, u = self.k, self.sub
        self.dve_softmax(eng, 0)
        for j in range(8):
            if j:
                self.dve_outputs(eng, j - 1)
            if j < 7:
                self.dve_softmax(eng, j + 1)
        self.dve_outputs(eng, 7)
        for s in S:
            eng.wait_ge(u.pe.sem, u.pe.at("wo", s))
            eng.scalar_tensor_tensor(k.b("x", s), k.psum[s][1][:], k.weight(self.out_bias), k.b("x", s), ALU.add, ALU.add)\
               .then_inc(u.dve.sem, u.dve.one("x", s))


class L2Xattn(Sub):

    def __init__(self, core, prev):
        super().__init__(core, prev)
        self.pe = core.steps("l2x_pe", ["mean", "k", "var", "q", *Attention16.PE])
        self.act = core.steps("l2x_act", [*TwiceNorm.ACT, "qs", *Attention16.ACT])
        self.dve = core.steps("l2x_dve", ["xc", "ks", *TwiceNorm.DVE[1:], *Attention16.dve_steps(True)])
        self.gps = core.steps("l2x_pool", ["kvn", "masked", "keymask", "fill", *Attention16.POOL])
        self.norm = TwiceNorm(core, self, "l2x_gx", "l2x_bx")
        self.att = Attention16(core, self, True, 8 ** -0.5, "t4", ("l2x_wkv", D), None, "l2x_wo", "l2x_bo",
                               lambda eng, s: None, lambda eng, s: eng.wait_ge(self.act.sem, self.act.at("qs", s)))

    def pe_program(self, eng):
        k, u = self.k, self
        self.norm.pe_mean(eng)
        for s in S:
            eng.wait_ge(u.gps.sem, u.gps.at("kvn", s))
            eng.matmul(k.psum[s][2][:], k.weight("l2x_wkv")[:, 0:D], k.b("t4", s), start=True, stop=True)\
               .then_inc(u.pe.sem, u.pe.one("k", s))
        self.norm.pe_var(eng)
        for s in S:
            eng.wait_ge(u.dve.sem, u.dve.at("latb", s))
            eng.matmul(k.psum[s][0][:], k.weight("l2x_wq"), k.b("t3", s), start=True, stop=True)\
               .then_inc(u.pe.sem, u.pe.one("q", s))
        self.att.pe(eng)

    def act_program(self, eng):
        k, u = self.k, self
        self.norm.act(eng)
        for s in S:
            eng.wait_ge(u.pe.sem, u.pe.at("q", s))
            eng.copy(k.b("t5", s), k.psum[s][0][:]).then_inc(u.act.sem, u.act.one("qs", s))
        self.att.act(eng)

    def pool_program(self, eng):
        k, u = self.k, self
        for s in S:
            u.input_ready(eng, s)
            eng.tensor_scalar(k.b("t4", s), k.b("cn", s), k.weight("l2x_gkv"), k.weight("l2x_bkv"),
                              ALU.mult, ALU.add).then_inc(u.gps.sem, u.gps.one("kvn", s))
        for s in S:
            eng.wait_ge(k.mask_in[s], 80)
            eng.tensor_scalar(k.keymask[s][:], k.keymask[s][:].bitcast(I32), 0.0, -1.0, ALU.is_equal, ALU.mult)\
               .then_inc(u.gps.sem, u.gps.one("masked", s))
        for s in S:
            eng.wait_ge(u.gps.sem, u.gps.at("masked", s))
            eng.tensor_scalar(k.keymask[s][:], k.keymask[s][:], 1.0, None, ALU.add)\
               .then_inc(u.gps.sem, u.gps.one("keymask", s))
        for s in S:
            eng.tensor_scalar(k.fill0[s][:], k.fill0[s][:].bitcast(I32), 0.0, -1e9, ALU.is_equal, ALU.mult)\
               .then_inc(u.gps.sem, u.gps.one("fill", s))
        self.att.pool(eng, lambda eng, s: eng.wait_ge(u.dve.sem, u.dve.at("ks", s)))

    def dve_program(self, eng):
        k, u = self.k, self
        self.norm.dve_centre(eng)
        for s in S:
            eng.wait_ge(u.pe.sem, u.pe.at("k", s))
            eng.wait_ge(u.gps.sem, u.gps.at("keymask", s))
            eng.tensor_tensor(k.b("t6", s), k.psum[s][2][:], k.keymask[s][:], ALU.mult)\
               .then_inc(u.dve.sem, u.dve.one("ks", s))
        self.norm.dve_scale(eng)
        for s in S:
            eng.wait_ge(u.gps.sem, u.gps.at("fill", s))
        self.att.dve(eng)


class L3Attn(Sub):

    def __init__(self, core, prev):
        super().__init__(core, prev)
        self.pe = core.steps("l3a_pe", [*Norm.PE, "k", "kr", "q", "qr", *Attention16.PE])
        self.act = core.steps("l3a_act", [*Norm.ACT, *Attention16.ACT])
        self.dve = core.steps("l3a_dve", [*Norm.DVE, "kc", "ks", "krope", "qc", "qs", "qrope", *Attention16.dve_steps(False)])
        self.gps = core.steps("l3a_pool", Attention16.POOL)
        self.norm = Norm(core, self)
        self.att = Attention16(core, self, False, 8 ** -0.5, "h", ("l3a_wv", 0), "l3a_bv", "l3a_wo", "l3a_bo",
                               lambda eng, s: eng.wait_ge(self.dve.sem, self.dve.at("ks", s)),
                               lambda eng, s: eng.wait_ge(self.dve.sem, self.dve.at("qrope", s)))

    def pe_program(self, eng):
        k, u = self.k, self
        self.norm.pe(eng)
        for bank, name, w in ((2, "k", k.weight("l3a_wk")), (3, "kr", k.rotated[:, D:2 * D]), (0, "q", k.weight("l3a_wq")),
                              (1, "qr", k.rotated[:, 0:D])):
            for s in S:
                if name == "k":
                    eng.wait_ge(u.dve.sem, u.dve.at("h", s))
                eng.matmul(k.psum[s][bank][:], w, k.b("h", s), start=True, stop=True)\
                   .then_inc(u.pe.sem, u.pe.one(name, s))
        self.att.pe(eng)

    def act_program(self, eng):
        self.norm.act(eng)
        self.att.act(eng)

    def dve_program(self, eng):
        k, u = self.k, self
        self.norm.dve(eng)
        over = lambda table: k.const(table).unsqueeze(1).broadcast_to([128, NB, T])
        for bank, a, out, part, bias, rbias in ((2, "k", "t6", "t4", "l3a_bk", 1), (0, "q", "t5", "t3", "l3a_bq", 0)):
            for s in S:
                eng.wait_ge(u.pe.sem, u.pe.at(a, s))
                eng.scalar_tensor_tensor(per_batch(k.b(out, s)), per_batch(k.psum[s][bank][:]), k.weight(bias),
                                         over("rcos"), ALU.add, ALU.mult).then_inc(u.dve.sem, u.dve.one(a + "c", s))
            for s in S:
                eng.wait_ge(u.pe.sem, u.pe.at(a + "r", s))
                eng.scalar_tensor_tensor(per_batch(k.b(part, s)), per_batch(k.psum[s][bank + 1][:]),
                                         k.rot_bias[:, rbias:rbias + 1], over("rsin"), ALU.add, ALU.mult)\
                   .then_inc(u.dve.sem, u.dve.one(a + "s", s))
            for s in S:
                eng.wait_ge(u.dve.sem, u.dve.at(a + "s", s))
                eng.tensor_tensor(k.b(out, s), k.b(out, s), k.b(part, s), ALU.add)\
                   .then_inc(u.dve.sem, u.dve.one(a + "rope", s))
        self.att.dve(eng)

    def pool_program(self, eng):
        k, u = self.k, self
        self.att.pool(eng, lambda eng, s: eng.wait_ge(u.dve.sem, u.dve.at("krope", s)))


class L2Attn(Sub):

    ROPE = ["q0", "q1", "q2", "q3", "k", "ks"]
    BESIDE = ["k0", "k1", "k2", "k3", "q0", "q1"]

    def __init__(self, core, prev):
        super().__init__(core, prev)
        pe, act, dve = [*Norm.PE, "ckv", "cq"], [*Norm.ACT, "ckv", "cq"], [*Norm.DVE]
        for n, beside in zip(self.ROPE, self.BESIDE):
            pe += ["r_" + n, beside]
            act += [f"abs_{n}", f"exp_{n}", f"ln_{n}"] + ([beside] if beside[0] == "q" else [])
            dve += [f"mu_{n}", f"rot_{n}"] + ([beside] if beside[0] == "k" else [])
        pe += ["q2", "q3", "v0", "even0", "odd0"]
        act += ["q2", "q3", "vs0", "exp0"]
        dve += ["kr", "max0", "sub0"]
        for t in range(4):
            before, more = t > 0, t < 3
            pe += ([f"even{t + 1}", f"odd{t + 1}"] if more else []) + ([f"back{t - 1}"] if before else [])
            pe += [f"turn{t}"] + ([f"v{t + 1}"] if more else []) + [f"pv{t}"]
            act += ([f"outs{t - 1}"] if before else []) + [f"probs{t}"] + ([f"vs{t + 1}", f"exp{t + 1}"] if more else [])
            dve += ([f"recip{t - 1}", f"out{t - 1}"] if before else []) + ([f"max{t + 1}", f"sub{t + 1}"] if more else [])
        self.pe = core.steps("l2a_pe", pe + ["back3", "wo"])
        self.act = core.steps("l2a_act", act + ["outs3"])
        self.dve = core.steps("l2a_dve", dve + ["recip3", "out3", "x"])
        self.norm = Norm(core, self)

    QR = ("t0", "t1", "t13", "t14")
    PART = (*QR, "t15", "t8")

    def exps(self, s, t):
        return self.k.b("h" if t % 2 else "t15", s)

    def values(self, s, t):
        return self.k.vb[s][:, t % 2 * 520:(t % 2 + 1) * 520].rearrange("p (b q c) -> p b q c", b=2, c=65)

    def ckv(self, s):
        return self.k.b("t2", s, slice(0, 32))

    def cq(self, s):
        return self.k.b("t3", s, slice(0, 64))

    def pe_projection(self, eng, name):
        k, u = self.k, self
        p = int(name[1])
        for s in S:
            if name in ("k2", "k3"):
                eng.wait_ge(u.dve.sem, u.dve.at(f"k{p - 2}", s))
            elif name in ("q0", "q1"):
                eng.wait_ge(u.dve.sem, u.dve.at(f"k{p + 2}", s))
            elif name in ("q2", "q3"):
                eng.wait_ge(u.act.sem, u.act.at(f"q{p - 2}", s))
            if name[0] == "k":
                w, src = k.weight("l2a_uk", slice(0, 32)), self.ckv(s)
            else:
                w, src = k.weight("l2a_uq", slice(0, 64)), self.cq(s)
            eng.matmul(k.psum[s][2 + p % 2][:], w[:, p * 128:(p + 1) * 128], src, start=True, stop=True)\
               .then_inc(u.pe.sem, u.pe.one(name, s))

    def pe_values(self, eng, t):
        k, u = self.k, self
        w = k.weight("l2a_uv", slice(0, 32)).rearrange("p (q o c) -> p q o c", o=2, c=64)
        for s in S:
            if t:
                eng.wait_ge(u.act.sem, u.act.at(f"probs{t - 1}", s))
            else:
                eng.wait_ge(u.dve.sem, u.dve.at("mu_ks", s))
            for b in range(2):
                at = t * 128 + b * T
                for h2 in range(2):
                    mm = eng.matmul(k.psum[s][1][64 * h2:64 * h2 + 64, b * 256:(b + 1) * 256], self.ckv(s)[:, at:at + T],
                                    w[:, :, h2, :], start=True, stop=True)
            mm.then_inc(u.pe.sem, u.pe.one(f"v{t}", s))

    def pe_scores(self, eng, t):
        k, u = self.k, self
        for odd, name in enumerate(("even", "odd")):
            half = slice(64 * odd, 64 * odd + 64)
            for s in S:
                if odd:
                    eng.wait_ge(u.pe.sem, u.pe.at(f"even{t}", s))
                elif t:
                    eng.wait_ge(u.dve.sem, u.dve.at(f"sub{t - 1}", s))
                else:
                    eng.wait_ge(u.act.sem, u.act.at("q3", s))
                    eng.wait_ge(u.dve.sem, u.dve.at("kr", s))
                for h in range(odd, 8, 2):
                    for b in range(2):
                        at = t * 128 + b * T
                        out = k.psum[s][0][b * T:(b + 1) * T, h * T:(h + 1) * T]
                        eng.matmul(out, k.b(f"t{5 + h // 2}", s, half)[:, at:at + T],
                                   k.b(f"t{9 + h // 2}", s, half)[:, at:at + T], start=True, stop=False)
                        mm = eng.matmul(out, k.b(self.QR[h // 2], s, half)[:, at:at + T],
                                        k.b("t4", s, half)[:, at:at + T], start=False, stop=True)
                mm.then_inc(u.pe.sem, u.pe.one(f"{name}{t}", s))

    def pe_transposes(self, eng, name, t):
        k, u = self.k, self
        for s in S:
            if name == "turn":
                eng.wait_ge(u.act.sem, u.act.at(f"exp{t}", s))
                eng.wait_ge(u.act.sem, u.act.at(f"outs{t - 1}" if t else "vs0", s))
            else:
                eng.wait_ge(u.dve.sem, u.dve.at(f"out{t}", s))
                eng.wait_ge(u.act.sem, u.act.at(f"vs{t + 1}" if t < 3 else "probs3", s))
            for p in range(4):
                mm = eng.transpose(k.psum[s][1][:, p * 128:(p + 1) * 128],
                                   self.exps(s, t)[:, p * 128:(p + 1) * 128], k.const("ident"))
            mm.then_inc(u.pe.sem, u.pe.one(f"{name}{t}", s))

    def pe_program(self, eng):
        k, u = self.k, self
        self.norm.pe(eng)
        for s in S:
            eng.wait_ge(u.dve.sem, u.dve.at("h", s))
            eng.matmul(k.psum[s][2][0:32, :], k.weight("l2a_dkv"), k.b("h", s), start=True, stop=True)\
               .then_inc(u.pe.sem, u.pe.one("ckv", s))
        for s in S:
            eng.matmul(k.psum[s][3][0:64, :], k.weight("l2a_dq"), k.b("h", s), start=True, stop=True)\
               .then_inc(u.pe.sem, u.pe.one("cq", s))
        for j, n in enumerate(self.ROPE):
            for s in S:
                if j == 0:
                    eng.wait_ge(u.act.sem, u.act.at("cq", s))
                if j >= 2:
                    eng.wait_ge(u.dve.sem, u.dve.at("mu_" + self.ROPE[j - 2], s))
                if j < 4:
                    w = k.weight("l2a_qrq", slice(0, 64))[:, j * 128:(j + 1) * 128]
                    mm = eng.matmul(k.psum[s][j % 2][:], w, self.cq(s), start=True, stop=True)
                else:
                    mm = eng.matmul(k.psum[s][j % 2][:], k.weight(("l2a_kr", "l2a_krs")[j - 4]), k.b("h", s),
                                    start=True, stop=True)
                mm.then_inc(u.pe.sem, u.pe.one("r_" + n, s))
            self.pe_projection(eng, self.BESIDE[j])
        self.pe_projection(eng, "q2")
        self.pe_projection(eng, "q3")
        self.pe_values(eng, 0)
        self.pe_scores(eng, 0)
        for t in range(4):
            if t < 3:
                self.pe_scores(eng, t + 1)
            if t:
                self.pe_transposes(eng, "back", t - 1)
            self.pe_transposes(eng, "turn", t)
            if t < 3:
                self.pe_values(eng, t + 1)
            for s in S:
                eng.wait_ge(u.act.sem, u.act.at(f"probs{t}", s))
                if t:
                    eng.wait_ge(u.dve.sem, u.dve.at(f"out{t - 1}", s))
                for h in range(8):
                    half = slice(64 * (h % 2), 64 * (h % 2) + 64)
                    for b in range(2):
                        mm = eng.matmul(k.psum[s][2 + h % 2][b * T:(b + 1) * T, h // 2 * 65:(h // 2 + 1) * 65],
                                        k.b("t3", s, half)[:, h // 2 * 128 + b * T:h // 2 * 128 + (b + 1) * T],
                                        self.values(s, t)[half, b, h // 2, :], start=True, stop=True)
                mm.then_inc(u.pe.sem, u.pe.one(f"pv{t}", s))
        self.pe_transposes(eng, "back", 3)
        for s in S:
            eng.wait_ge(u.act.sem, u.act.at("outs3", s))
            for p in range(4):
                mm = eng.matmul(k.psum[s][0][:], k.weight("l2a_out")[:, p * 128:(p + 1) * 128], k.b(f"t{5 + p}", s),
                                start=p == 0, stop=p == 3)
            mm.then_inc(u.pe.sem, u.pe.one("wo", s))

    def act_query(self, eng, p):
        k, u = self.k, self
        for s in S:
            eng.wait_ge(u.pe.sem, u.pe.at(f"q{p}", s))
            if p == 3:
                eng.wait_ge(u.dve.sem, u.dve.at("kr", s))
            eng.copy(k.b(f"t{5 + p}", s), k.psum[s][2 + p % 2][:]).then_inc(u.act.sem, u.act.one(f"q{p}", s))

    def act_values(self, eng, t):
        k, u = self.k, self
        for s in S:
            eng.wait_ge(u.pe.sem, u.pe.at(f"v{t}", s))
            eng.copy(k.vb[s][:, t % 2 * 520:(t % 2 + 1) * 520].rearrange("p (h c) -> p h c", c=65)[:, :, 0:64],
                     k.psum[s][1][:].rearrange("p (h c) -> p h c", c=64)).then_inc(u.act.sem, u.act.one(f"vs{t}", s))

    def act_exp(self, eng, t):
        k, u = self.k, self
        for s in S:
            eng.wait_ge(u.dve.sem, u.dve.at(f"sub{t}", s))
            eng.activation(self.exps(s, t), self.exps(s, t), ACT.Exp, scale=96 ** -0.5)\
               .then_inc(u.act.sem, u.act.one(f"exp{t}", s))

    def act_outs(self, eng, t):
        k, u = self.k, self
        for s in S:
            eng.wait_ge(u.pe.sem, u.pe.at(f"back{t}", s))
            eng.copy(k.wide(s, 5, 4).rearrange("p (q n) -> p q n", n=G)[:, :, t * 128:(t + 1) * 128],
                     k.psum[s][1][:].rearrange("p (q n) -> p q n", n=128)).then_inc(u.act.sem, u.act.one(f"outs{t}", s))

    def act_program(self, eng):
        k, u = self.k, self
        self.norm.act(eng)
        for s in S:
            eng.wait_ge(u.pe.sem, u.pe.at("ckv", s))
            eng.copy(self.ckv(s), k.psum[s][2][0:32, :]).then_inc(u.act.sem, u.act.one("ckv", s))
        for s in S:
            eng.wait_ge(u.pe.sem, u.pe.at("cq", s))
            eng.copy(self.cq(s), k.psum[s][3][0:64, :]).then_inc(u.act.sem, u.act.one("cq", s))
        for j, n in enumerate(self.ROPE):
            part = self.PART[j]
            for s in S:
                eng.wait_ge(u.pe.sem, u.pe.at("r_" + n, s))
                eng.wait_ge(u.dve.sem, u.dve.at("h", s))
                eng.activation(k.b(part, s), k.psum[s][j % 2][:], ACT.Abs).then_inc(u.act.sem, u.act.one("abs_" + n, s))
            for s in S:
                eng.wait_ge(u.act.sem, u.act.at("abs_" + n, s))
                eng.activation(k.b(part, s), k.b(part, s), ACT.Exp, scale=-1.0).then_inc(u.act.sem, u.act.one("exp_" + n, s))
            for s in S:
                eng.wait_ge(u.act.sem, u.act.at("exp_" + n, s))
                eng.activation(k.b(part, s), k.b(part, s), ACT.Ln, bias=1.0).then_inc(u.act.sem, u.act.one("ln_" + n, s))
            if j >= 4:
                self.act_query(eng, j - 4)
        self.act_query(eng, 2)
        self.act_query(eng, 3)
        self.act_values(eng, 0)
        self.act_exp(eng, 0)
        for t in range(4):
            if t:
                self.act_outs(eng, t - 1)
            for s in S:
                eng.wait_ge(u.pe.sem, u.pe.at(f"turn{t}", s))
                eng.copy(k.b("t3", s), k.psum[s][1][:]).then_inc(u.act.sem, u.act.one(f"probs{t}", s))
            if t < 3:
                self.act_values(eng, t + 1)
                self.act_exp(eng, t + 1)
        self.act_outs(eng, 3)

    def dve_softmax(self, eng, t):
        k, u = self.k, self
        heads = lambda ap: ap.rearrange("p (h j) -> p h j", j=T)
        for s in S:
            eng.wait_ge(u.pe.sem, u.pe.at(f"odd{t}", s))
            if t:
                eng.wait_ge(u.dve.sem, u.dve.at(f"sub{t - 1}", s))
            eng.tensor_reduce(k.small[s][:, 0:8], heads(k.psum[s][0][:]), AX.X, ALU.max)\
               .then_inc(u.dve.sem, u.dve.one(f"max{t}", s))
        for s in S:
            eng.wait_ge(u.dve.sem, u.dve.at(f"max{t}", s))
            if t >= 2:
                eng.wait_ge(u.pe.sem, u.pe.at(f"back{t - 2}", s))
            eng.tensor_tensor(heads(self.exps(s, t)), heads(k.psum[s][0][:]),
                              k.small[s][:, 0:8].unsqueeze(2).broadcast_to([128, 8, T]), ALU.subtract)\
               .then_inc(u.dve.sem, u.dve.one(f"sub{t}", s))

    def dve_outputs(self, eng, t):
        k, u = self.k, self
        recips = lambda s, c: k.small[s][:, 8 + 4 * c:12 + 4 * c]
        outs = lambda s, c: k.psum[s][2 + c][:, 0:260].rearrange("p (q c) -> p q c", c=65)
        mine = lambda s, c: self.exps(s, t).rearrange("p (q o j) -> p q o j", o=2, j=T)[:, :, c, :]
        for s in S:
            eng.wait_ge(u.pe.sem, u.pe.at(f"pv{t}", s))
            for c in range(2):
                ins = eng.reciprocal(recips(s, c), outs(s, c)[:, :, 64])
            ins.then_inc(u.dve.sem, u.dve.one(f"recip{t}", s))
        for s in S:
            eng.wait_ge(u.dve.sem, u.dve.at(f"recip{t}", s))
            for c in range(2):
                ins = eng.tensor_tensor(mine(s, c), outs(s, c)[:, :, 0:64],
                                        recips(s, c).unsqueeze(2).broadcast_to([128, 4, T]), ALU.mult)
            ins.then_inc(u.dve.sem, u.dve.one(f"out{t}", s))

    def dve_program(self, eng):
        k, u = self.k, self
        self.norm.dve(eng)
        over = lambda table: table.unsqueeze(1).broadcast_to([128, NB, T])
        for j, n in enumerate(self.ROPE):
            part = self.PART[j]
            table = k.pope[:, 0:T] if j < 4 else k.pope[:, (j - 3) * T:(j - 2) * T]
            for s in S:
                eng.wait_ge(u.act.sem, u.act.at("ln_" + n, s))
                eng.scalar_tensor_tensor(k.b(part, s), k.psum[s][j % 2][:], 0.0, k.b(part, s), ALU.max, ALU.add)\
                   .then_inc(u.dve.sem, u.dve.one("mu_" + n, s))
            for s in S:
                eng.wait_ge(u.dve.sem, u.dve.at("mu_" + n, s))
                eng.tensor_tensor(per_batch(k.b(part, s)), per_batch(k.b(part, s)), over(table), ALU.mult)\
                   .then_inc(u.dve.sem, u.dve.one("rot_" + n, s))
            if j < 4:
                for s in S:
                    eng.wait_ge(u.pe.sem, u.pe.at(f"k{j}", s))
                    eng.tensor_copy(k.b(f"t{9 + j}", s), k.psum[s][2 + j % 2][:])\
                       .then_inc(u.dve.sem, u.dve.one(f"k{j}", s))
        for s in S:
            eng.wait_ge(u.dve.sem, u.dve.at("rot_ks", s))
            eng.tensor_tensor(k.b("t4", s), k.b("t15", s), k.b("t8", s), ALU.add).then_inc(u.dve.sem, u.dve.one("kr", s))
        self.dve_softmax(eng, 0)
        for t in range(4):
            if t:
                self.dve_outputs(eng, t - 1)
            if t < 3:
                self.dve_softmax(eng, t + 1)
        self.dve_outputs(eng, 3)
        for s in S:
            eng.wait_ge(u.pe.sem, u.pe.at("wo", s))
            eng.tensor_tensor(k.b("x", s), k.psum[s][0][:], k.b("x", s), ALU.add).then_inc(u.dve.sem, u.dve.one("x", s))


class L1Attn(Sub):

    PAIRS = 16

    def __init__(self, core, prev):
        super().__init__(core, prev)
        five = range(5)
        n = range(self.PAIRS)
        self.pe = core.steps("l1a_pe", [*Norm.PE, "w1", "x0", "x0e"] + [f"mu{j}" for j in five]
                             + ["r", "ww1", "k", "ww2", "v", "g", "bonus"]
                             + [a for j in range(17) for a in ([f"vb{j}"] if j < 16 else []) + ([f"os{j - 1}"] if j else [])]
                             + [*GroupNorm.PE, "y"])
        self.act = core.steps("l1a_act", [*Norm.ACT, "w1", "x1", "x1e", "r", "ww1", "ks", "ew", "wd", "vs", "silu", *GroupNorm.ACT])
        self.dve = core.steps("l1a_dve", [*Norm.DVE, "delta", "delta0", "lerp"] + [f"{a}{j}" for j in five for a in ("m", "in")]
                              + ["zeros", "ksh", "rbk", "xv", "bv"] + [f"{a}{j}" for j in n for a in ("kv", "scan", "rt")]
                              + ["o", *GroupNorm.DVE, "gnw", "gated", "x"])
        self.norm = Norm(core, self)
        self.gn = GroupNorm(core, self, "t6", lambda eng, s: eng.wait_ge(self.dve.sem, self.dve.at("o", s)))

    def pe_program(self, eng):
        k, u = self.k, self
        self.norm.pe(eng)
        low = slice(0, 32)
        for s in S:
            eng.wait_ge(u.dve.sem, u.dve.at("lerp", s))
            eng.matmul(k.psum[s][2][0:32, :], k.weight("l1a_w1"), k.b("t3", s), start=True, stop=True)\
               .then_inc(u.pe.sem, u.pe.one("w1", s))
        for s in S:
            eng.wait_ge(u.act.sem, u.act.at("w1", s))
            eng.matmul(k.psum[s][0][:], k.weight("l1a_w2", low)[:, 0:128], k.b("t4", s, low), start=True, stop=True)\
               .then_inc(u.pe.sem, u.pe.one("x0", s))
        for s in S:
            eng.matmul(k.psum[s][1][0:32, :], k.weight("l1a_w2", low)[:, 128:160], k.b("t4", s, low), start=True, stop=True)\
               .then_inc(u.pe.sem, u.pe.one("x0e", s))
        for j in range(5):
            for s in S:
                if j == 0:
                    eng.wait_ge(u.act.sem, u.act.at("x1e", s))
                if j >= 2:
                    eng.wait_ge(u.dve.sem, u.dve.at(f"m{j - 2}", s))
                rows = slice(32 * j, 32 * j + 32) if j < 4 else low
                w, x1 = (k.weight("l1a_xo", rows), k.b("t5", s, rows)) if j < 4 else (k.weight("l1a_xoe", low), k.b("t6", s, low))
                eng.matmul(k.psum[s][j % 2][:], w, x1, start=True, stop=True).then_inc(u.pe.sem, u.pe.one(f"mu{j}", s))
        for name, bank, w, x, ready in (("r", 2, "l1a_r", "t7", "in0"), ("ww1", 3, "l1a_ww1", "t8", "in1"),
                                        ("k", 1, "l1a_k", "t9", "in2"), ("ww2", 0, None, None, None),
                                        ("v", 2, "l1a_v", "t10", "in3"), ("g", 3, "l1a_g", "t11", "in4")):
            for s in S:
                if name == "ww2":
                    eng.wait_ge(u.act.sem, u.act.at("ww1", s))
                    eng.wait_ge(u.dve.sem, u.dve.at("in4", s))
                    mm = eng.matmul(k.psum[s][0][:], k.weight("l1a_ww2", slice(0, 64)), k.b("t4", s, slice(0, 64)),
                                    start=True, stop=True)
                else:
                    eng.wait_ge(u.dve.sem, u.dve.at(ready, s))
                    if name == "k":
                        eng.wait_ge(u.dve.sem, u.dve.at("m3", s))
                    if name in "vg":
                        eng.wait_ge(u.act.sem, u.act.at("ww1", s))
                    out = k.psum[s][bank][0:64, :] if name == "ww1" else k.psum[s][bank][:]
                    mm = eng.matmul(out, k.weight(w), k.b(x, s), start=True, stop=True)
                mm.then_inc(u.pe.sem, u.pe.one(name, s))
        for s in S:
            eng.wait_ge(u.dve.sem, u.dve.at("rbk", s))
            eng.wait_ge(u.act.sem, u.act.at("wd", s))
            eng.matmul(k.psum[s][0][:], k.const("bonus_sum", slice(0, 64)), k.b("t14", s, slice(0, 64)),
                       start=True, stop=True).then_inc(u.pe.sem, u.pe.one("bonus", s))
        for j in range(self.PAIRS + 1):
            if j < self.PAIRS:
                for s in S:
                    if j < 2:
                        eng.wait_ge(u.dve.sem, u.dve.at("bv", s))
                    else:
                        eng.wait_ge(u.dve.sem, u.dve.at(f"kv{j - 2}", s))
                    eng.matmul(k.psum[s][j % 2][:], k.vexp[:, j * 128:(j + 1) * 128], k.b("t15", s), start=True, stop=True)\
                       .then_inc(u.pe.sem, u.pe.one(f"vb{j}", s))
            if j:
                n = j - 1
                for s in S:
                    eng.wait_ge(u.dve.sem, u.dve.at(f"rt{n}", s))
                    eng.matmul(k.psum[s][2][:], k.const("ksum")[:, 30 - 2 * n:158 - 2 * n], k.b(f"t{4 + n % 2}", s),
                               start=n == 0, stop=n == self.PAIRS - 1).then_inc(u.pe.sem, u.pe.one(f"os{n}", s))
        self.gn.pe(eng)
        for s in S:
            eng.wait_ge(u.dve.sem, u.dve.at("gated", s))
            eng.matmul(k.psum[s][0][:], k.weight("l1a_o"), k.b("t12", s), start=True, stop=True)\
               .then_inc(u.pe.sem, u.pe.one("y", s))

    def act_program(self, eng):
        k, u = self.k, self
        self.norm.act(eng)
        late = lambda name, s: per_batch(k.b(name, s))[:, :, 1:T]
        early = lambda name, s: per_batch(k.b(name, s))[:, :, 0:T - 1]
        for s in S:
            eng.wait_ge(u.pe.sem, u.pe.at("w1", s))
            eng.activation(k.b("t4", s, slice(0, 32)), k.psum[s][2][0:32, :], ACT.Tanh).then_inc(u.act.sem, u.act.one("w1", s))
        for s in S:
            eng.wait_ge(u.pe.sem, u.pe.at("x0", s))
            eng.activation(k.b("t5", s), k.psum[s][0][:], ACT.Tanh, bias=k.weight("l1a_b2")).then_inc(u.act.sem, u.act.one("x1", s))
        for s in S:
            eng.wait_ge(u.pe.sem, u.pe.at("x0e", s))
            eng.activation(k.b("t6", s, slice(0, 32)), k.psum[s][1][0:32, :], ACT.Tanh,
                           bias=k.weight("l1a_b2e", slice(0, 32))).then_inc(u.act.sem, u.act.one("x1e", s))
        for s in S:
            eng.wait_ge(u.pe.sem, u.pe.at("r", s))
            eng.copy(k.b("t3", s), k.psum[s][2][:]).then_inc(u.act.sem, u.act.one("r", s))
        for s in S:
            eng.wait_ge(u.pe.sem, u.pe.at("ww1", s))
            eng.activation(k.b("t4", s, slice(0, 64)), k.psum[s][3][0:64, :], ACT.Tanh).then_inc(u.act.sem, u.act.one("ww1", s))
        for s in S:
            eng.wait_ge(u.pe.sem, u.pe.at("k", s))
            eng.copy(k.b("t9", s), k.psum[s][1][:]).then_inc(u.act.sem, u.act.one("ks", s))
        for s in S:
            eng.wait_ge(u.pe.sem, u.pe.at("ww2", s))
            eng.activation(k.b("t8", s), k.psum[s][0][:], ACT.Exp, bias=k.weight("l1a_wb")).then_inc(u.act.sem, u.act.one("ew", s))
        for s in S:
            eng.wait_ge(u.act.sem, u.act.at("ew", s))
            eng.wait_ge(u.dve.sem, u.dve.at("zeros", s))
            eng.activation(late("t12", s), early("t8", s), ACT.Exp, scale=-1.0).then_inc(u.act.sem, u.act.one("wd", s))
        for s in S:
            eng.wait_ge(u.pe.sem, u.pe.at("v", s))
            eng.wait_ge(u.act.sem, u.act.at("wd", s))
            eng.copy(k.b("t8", s), k.psum[s][2][:]).then_inc(u.act.sem, u.act.one("vs", s))
        for s in S:
            eng.wait_ge(u.pe.sem, u.pe.at("g", s))
            eng.activation(k.b("t11", s), k.psum[s][3][:], ACT.Silu).then_inc(u.act.sem, u.act.one("silu", s))
        log_and_exp_table(eng)
        self.gn.act(eng)

    def dve_program(self, eng):
        k, u = self.k, self
        self.norm.dve(eng)
        late = lambda name, s: per_batch(k.b(name, s))[:, :, 1:T]
        early = lambda name, s: per_batch(k.b(name, s))[:, :, 0:T - 1]
        first = lambda name, s: per_batch(k.b(name, s))[:, :, 0:1]
        for s in S:
            eng.wait_ge(u.dve.sem, u.dve.at("h", s))
            eng.tensor_tensor(late("t2", s), early("h", s), late("h", s), ALU.subtract).then_inc(u.dve.sem, u.dve.one("delta", s))
        for s in S:
            eng.tensor_scalar(first("t2", s), first("h", s), -1.0, None, ALU.mult).then_inc(u.dve.sem, u.dve.one("delta0", s))
        for s in S:
            eng.wait_ge(u.dve.sem, u.dve.at("delta0", s))
            eng.scalar_tensor_tensor(k.b("t3", s), k.b("t2", s), k.weight("l1a_mu"), k.b("h", s), ALU.mult, ALU.add)\
               .then_inc(u.dve.sem, u.dve.one("lerp", s))
        for j in range(5):
            for s in S:
                eng.wait_ge(u.pe.sem, u.pe.at(f"mu{j}", s))
                eng.scalar_tensor_tensor(k.b(f"t{7 + j}", s), k.psum[s][j % 2][:], k.weight("l1a_xb")[:, j:j + 1],
                                         k.b("t2", s), ALU.add, ALU.mult).then_inc(u.dve.sem, u.dve.one(f"m{j}", s))
            for s in S:
                eng.wait_ge(u.dve.sem, u.dve.at(f"m{j}", s))
                eng.tensor_tensor(k.b(f"t{7 + j}", s), k.b(f"t{7 + j}", s), k.b("h", s), ALU.add)\
                   .then_inc(u.dve.sem, u.dve.one(f"in{j}", s))
        for s in S:
            for name in ("t12", "t13", "t15"):
                ins = eng.memset(first(name, s), 0.0)
            ins.then_inc(u.dve.sem, u.dve.one("zeros", s))
        for s in S:
            eng.wait_ge(u.act.sem, u.act.at("ks", s))
            eng.tensor_copy(late("t13", s), early("t9", s)).then_inc(u.dve.sem, u.dve.one("ksh", s))
        for s in S:
            eng.scalar_tensor_tensor(k.b("t14", s), k.b("t3", s), k.weight("l1a_bonus"), k.b("t9", s), ALU.mult, ALU.mult)\
               .then_inc(u.dve.sem, u.dve.one("rbk", s))
        for s in S:
            eng.wait_ge(u.dve.sem, u.dve.at("in3", s))
            eng.tensor_copy(late("t15", s), early("t10", s)).then_inc(u.dve.sem, u.dve.one("xv", s))
        for s in S:
            eng.wait_ge(u.pe.sem, u.pe.at("bonus", s))
            eng.wait_ge(u.act.sem, u.act.at("vs", s))
            eng.tensor_tensor(k.b("t14", s), k.b("t8", s), k.psum[s][0][:], ALU.mult).then_inc(u.dve.sem, u.dve.one("bv", s))
        for j in range(self.PAIRS):
            w = f"t{4 + j % 2}"
            for s in S:
                eng.wait_ge(u.pe.sem, u.pe.at(f"vb{j}", s))
                if j >= 2:
                    eng.wait_ge(u.pe.sem, u.pe.at(f"os{j - 2}", s))
                eng.tensor_tensor(k.b(w, s), k.b("t13", s), k.psum[s][j % 2][:], ALU.mult).then_inc(u.dve.sem, u.dve.one(f"kv{j}", s))
            for s in S:
                eng.wait_ge(u.dve.sem, u.dve.at(f"kv{j}", s))
                eng.tensor_tensor_scan(k.b(w, s), k.b("t12", s), k.b(w, s), 0.0, ALU.mult, ALU.add)\
                   .then_inc(u.dve.sem, u.dve.one(f"scan{j}", s))
            for s in S:
                eng.wait_ge(u.dve.sem, u.dve.at(f"scan{j}", s))
                eng.tensor_tensor(k.b(w, s), k.b(w, s), k.b("t3", s), ALU.mult).then_inc(u.dve.sem, u.dve.one(f"rt{j}", s))
        for s in S:
            eng.wait_ge(u.pe.sem, u.pe.at("os15", s))
            eng.tensor_tensor(k.b("t6", s), k.b("t14", s), k.psum[s][2][:], ALU.add).then_inc(u.dve.sem, u.dve.one("o", s))
        self.gn.dve(eng)
        for s in S:
            eng.wait_ge(u.dve.sem, u.dve.at("gn", s))
            eng.tensor_scalar(k.b("t12", s), k.b("t12", s), k.weight("l1a_gnw"), k.weight("l1a_gnb"), ALU.mult, ALU.add)\
               .then_inc(u.dve.sem, u.dve.one("gnw", s))
        for s in S:
            eng.wait_ge(u.dve.sem, u.dve.at("gnw", s))
            eng.tensor_tensor(k.b("t12", s), k.b("t12", s), k.b("t11", s), ALU.mult).then_inc(u.dve.sem, u.dve.one("gated", s))
        for s in S:
            eng.wait_ge(u.pe.sem, u.pe.at("y", s))
            eng.tensor_tensor(k.b("x", s), k.b("x", s), k.psum[s][0][:], ALU.add).then_inc(u.dve.sem, u.dve.one("x", s))


class L2Ffn(Sub):

    TILES = (128, 128, 96)

    def __init__(self, core, prev):
        super().__init__(core, prev)
        n = range(24)
        self.pe = core.steps("l2f_pe", [*Norm.PE, *Gate.PE, "gt"]
                             + [a for i in range(25) for a in ([f"gb{i // 3}"] if i % 3 == 0 and i < 24 else [])
                                + ([f"u{i}", f"v{i}"] if i < 24 else []) + ([f"d{i - 1}"] if i else [])])
        self.act = core.steps("l2f_act", [*Norm.ACT, *Gate.ACT, "gt"] + [f"silu{i}" for i in n])
        self.dve = core.steps("l2f_dve", [*Norm.DVE, *Gate.DVE, "wsum", "wrecip", "weights"]
                              + [a for i in n for a in ([f"xg{i // 3}"] if i % 3 == 0 else []) + [f"hid{i}"]] + ["x"])
        self.norm = Norm(core, self)
        self.gate = Gate(core, self, "l2f_gate")

    def pe_program(self, eng):
        k, u = self.k, self
        self.norm.pe(eng)
        eng.wait_ge(k.moe_in[1], 16)
        self.gate.pe(eng)
        for s in S:
            eng.wait_ge(u.dve.sem, u.dve.at("weights", s))
            for t in range(NT):
                mm = eng.transpose(k.psum[s][3][0:8, t * 128:(t + 1) * 128], self.gate.g(s, 8)[:, t * 8:t * 8 + 8],
                                   k.const("ident"))
            mm.then_inc(u.pe.sem, u.pe.one("gt", s))
        for i in range(25):
            e, c = divmod(i, 3)
            if c == 0 and i < 24:
                for s in S:
                    if e == 0:
                        eng.wait_ge(u.act.sem, u.act.at("gt", s))
                    else:
                        eng.wait_ge(u.dve.sem, u.dve.at(f"xg{e - 1}", s))
                    one = k.const("ident", slice(0, 8))[:, e:e + 1].broadcast_to([8, 128])
                    eng.matmul(k.psum[s][3][:], one, k.b("t4", s, slice(0, 8)), start=True, stop=True)\
                       .then_inc(u.pe.sem, u.pe.one(f"gb{e}", s))
            if i < 24:
                m = self.TILES[c]
                for s in S:
                    if i:
                        eng.wait_ge(u.act.sem, u.act.at(f"silu{i - 1}", s))
                    w = k.weight("l2f_w1")[:, e * 352 + c * 128:e * 352 + c * 128 + m]
                    eng.matmul(k.psum[s][0][0:m, :], w, k.b("h", s), start=True, stop=True)\
                       .then_inc(u.pe.sem, u.pe.one(f"u{i}", s))
                for s in S:
                    if i:
                        eng.wait_ge(u.dve.sem, u.dve.at(f"hid{i - 1}", s))
                    if c == 0:
                        eng.wait_ge(u.dve.sem, u.dve.at(f"xg{e}", s))
                    w = k.weight("l2f_w3")[:, e * 352 + c * 128:e * 352 + c * 128 + m]
                    eng.matmul(k.psum[s][1][0:m, :], w, k.b(f"t{5 + e % 2}", s), start=True, stop=True)\
                       .then_inc(u.pe.sem, u.pe.one(f"v{i}", s))
            if i:
                n = i - 1
                m = self.TILES[n % 3]
                for s in S:
                    eng.wait_ge(u.dve.sem, u.dve.at(f"hid{n}", s))
                    eng.matmul(k.psum[s][2][:], k.weight("l2f_w2", slice(0, m))[:, n * 128:(n + 1) * 128],
                               k.b(f"t{9 + n % 2}", s, slice(0, m)), start=n == 0, stop=n == 23)\
                       .then_inc(u.pe.sem, u.pe.one(f"d{n}", s))

    def act_program(self, eng):
        k, u = self.k, self
        self.norm.act(eng)
        self.gate.act(eng)
        for s in S:
            eng.wait_ge(u.pe.sem, u.pe.at("gt", s))
            eng.copy(k.b("t4", s, slice(0, 8)), k.psum[s][3][0:8, :]).then_inc(u.act.sem, u.act.one("gt", s))
        for i in range(24):
            rows = slice(0, self.TILES[i % 3])
            for s in S:
                eng.wait_ge(u.pe.sem, u.pe.at(f"u{i}", s))
                if i >= 2:
                    eng.wait_ge(u.dve.sem, u.dve.at(f"hid{i - 2}", s))
                eng.activation(k.b(f"t{7 + i % 2}", s, rows), k.psum[s][0][rows, :], ACT.Silu)\
                   .then_inc(u.act.sem, u.act.one(f"silu{i}", s))
        log_and_exp_table(eng)

    def dve_program(self, eng):
        k, u = self.k, self
        self.norm.dve(eng)
        self.gate.dve(eng)
        g8 = lambda s: self.gate.g(s, 8).rearrange("p (t e) -> p t e", e=8)
        for s in S:
            eng.wait_ge(u.dve.sem, u.dve.at("gate", s))
            eng.tensor_reduce(k.small[s][:, 44:48], g8(s), AX.X, ALU.add).then_inc(u.dve.sem, u.dve.one("wsum", s))
        for s in S:
            eng.wait_ge(u.dve.sem, u.dve.at("wsum", s))
            eng.reciprocal(k.small[s][:, 48:52], k.small[s][:, 44:48]).then_inc(u.dve.sem, u.dve.one("wrecip", s))
        for s in S:
            eng.wait_ge(u.dve.sem, u.dve.at("wrecip", s))
            eng.tensor_tensor(g8(s), g8(s), k.small[s][:, 48:52].unsqueeze(2).broadcast_to([128, NT, 8]), ALU.mult)\
               .then_inc(u.dve.sem, u.dve.one("weights", s))
        for i in range(24):
            e, rows = i // 3, slice(0, self.TILES[i % 3])
            if i % 3 == 0:
                for s in S:
                    eng.wait_ge(u.pe.sem, u.pe.at(f"gb{e}", s))
                    eng.tensor_tensor(k.b(f"t{5 + e % 2}", s), k.b("h", s), k.psum[s][3][:], ALU.mult)\
                       .then_inc(u.dve.sem, u.dve.one(f"xg{e}", s))
            for s in S:
                eng.wait_ge(u.pe.sem, u.pe.at(f"v{i}", s))
                eng.wait_ge(u.act.sem, u.act.at(f"silu{i}", s))
                eng.tensor_tensor(k.b(f"t{9 + i % 2}", s, rows), k.b(f"t{7 + i % 2}", s, rows), k.psum[s][1][rows, :],
                                  ALU.mult).then_inc(u.dve.sem, u.dve.one(f"hid{i}", s))
        for s in S:
            eng.wait_ge(u.pe.sem, u.pe.at("d23", s))
            eng.tensor_tensor(k.b("x", s), k.b("x", s), k.psum[s][2][:], ALU.add).then_inc(u.dve.sem, u.dve.one("x", s))


class L3Ffn(Sub):

    def __init__(self, core, prev):
        super().__init__(core, prev)
        self.pe = core.steps("l3f_pe", [*Norm.PE, *Gate.PE, "gt"]
                             + [a for i in range(9) for a in ([f"y{i}"] if i < 8 else []) + ([f"sum{i - 1}"] if i else [])])
        self.act = core.steps("l3f_act", [*Norm.ACT, *Gate.ACT, "gt"])
        self.dve = core.steps("l3f_dve", [*Norm.DVE, *Gate.DVE] + [f"z{i}" for i in range(8)] + ["x"])
        self.norm = Norm(core, self)
        self.gate = Gate(core, self, "l3f_wr", "l3f_br")

    def pe_program(self, eng):
        k, u = self.k, self
        self.norm.pe(eng)
        self.gate.pe(eng)
        for s in S:
            eng.wait_ge(u.dve.sem, u.dve.at("gate", s))
            for t in range(NT):
                mm = eng.transpose(k.psum[s][3][0:8, t * 128:(t + 1) * 128], self.gate.g(s, 8)[:, t * 8:t * 8 + 8],
                                   k.const("ident"))
            mm.then_inc(u.pe.sem, u.pe.one("gt", s))
        for i in range(9):
            if i < 8:
                t, c = divmod(i, 2)
                for s in S:
                    if i >= 2:
                        eng.wait_ge(u.dve.sem, u.dve.at(f"z{i - 2}", s))
                    eng.matmul(k.psum[s][c][:], k.b("h", s)[:, t * 128:(t + 1) * 128], k.weight("l3f_w")[:, c * G:(c + 1) * G],
                               start=True, stop=True).then_inc(u.pe.sem, u.pe.one(f"y{i}", s))
            if i:
                n = i - 1
                t, c = divmod(n, 2)
                for s in S:
                    out = k.psum[s][2][:, t * 128:(t + 1) * 128]
                    if n == 0:
                        eng.wait_ge(u.act.sem, u.act.at("gt", s))
                    if c == 0:
                        eng.matmul(out, k.weight("l3f_b", slice(0, 8)), k.b("t4", s, slice(0, 8))[:, t * 128:(t + 1) * 128],
                                   start=True, stop=False)
                    eng.wait_ge(u.dve.sem, u.dve.at(f"z{n}", s))
                    for e in range(4):
                        mm = eng.matmul(out, k.b(f"t{5 + n % 2}", s)[:, e * 128:(e + 1) * 128], k.const("ident"),
                                        start=False, stop=c == 1 and e == 3)
                    mm.then_inc(u.pe.sem, u.pe.one(f"sum{n}", s))

    def act_program(self, eng):
        k, u = self.k, self
        self.norm.act(eng)
        self.gate.act(eng)
        for s in S:
            eng.wait_ge(u.pe.sem, u.pe.at("gt", s))
            eng.copy(k.b("t4", s, slice(0, 8)), k.psum[s][3][0:8, :]).then_inc(u.act.sem, u.act.one("gt", s))

    def dve_program(self, eng):
        k, u = self.k, self
        self.norm.dve(eng)
        self.gate.dve(eng)
        for i in range(8):
            t, c = divmod(i, 2)
            for s in S:
                eng.wait_ge(u.pe.sem, u.pe.at(f"y{i}", s))
                if i == 0:
                    eng.wait_ge(u.dve.sem, u.dve.at("gate", s))
                if i >= 2:
                    eng.wait_ge(u.pe.sem, u.pe.at(f"sum{i - 2}", s))
                eng.tensor_tensor(k.b(f"t{5 + i % 2}", s).rearrange("p (e n) -> p e n", e=4),
                                  k.psum[s][c][:].rearrange("p (e n) -> p e n", e=4),
                                  self.gate.g(s, 8)[:, t * 8 + 4 * c:t * 8 + 4 * c + 4].unsqueeze(2).broadcast_to([128, 4, 128]),
                                  ALU.mult).then_inc(u.dve.sem, u.dve.one(f"z{i}", s))
        for s in S:
            eng.wait_ge(u.pe.sem, u.pe.at("sum7", s))
            eng.tensor_tensor(k.b("x", s), k.b("x", s), k.psum[s][2][:], ALU.add).then_inc(u.dve.sem, u.dve.one("x", s))


class L1Ffn(Sub):

    def __init__(self, core, prev):
        super().__init__(core, prev)
        self.pe = core.steps("l1f_pe", [*Norm.PE, "y"])
        self.act = core.steps("l1f_act", Norm.ACT)
        self.dve = core.steps("l1f_dve", [*Norm.DVE, "x"])
        self.norm = Norm(core, self)

    def pe_program(self, eng):
        k, u = self.k, self
        self.norm.pe(eng)
        for s in S:
            eng.wait_ge(u.dve.sem, u.dve.at("h", s))
            eng.matmul(k.psum[s][2][:], k.ternary[:], k.b("h", s), start=True, stop=True)\
               .then_inc(u.pe.sem, u.pe.one("y", s))

    def act_program(self, eng):
        self.norm.act(eng)

    def dve_program(self, eng):
        k, u = self.k, self
        self.norm.dve(eng)
        for s in S:
            eng.wait_ge(u.pe.sem, u.pe.at("y", s))
            eng.tensor_tensor(k.b("x", s), k.b("x", s), k.psum[s][2][:], ALU.add)\
               .then_inc(u.dve.sem, u.dve.one("x", s))


NTMP = 16


def small(k, ctx):
    t = lambda name, cols, dt=F32: ctx.enter_context(k.nc.sbuf_tensor(name, [128, cols], dt))
    k.eps5, k.ternary, k.scratch = t("eps5", 1), t("ternary", 128), t("scratch", 8)
    k.vb = [t(f"vb{s}", 2 * 8 * 65) for s in S]
    k.vbd = [t(f"vbd{s}", 2 * 8 * 18) for s in S]
    k.fill0 = [t(f"fill0_{s}", 256) for s in S]
    k.rotated, k.rot_bias = t("rotated", 2 * D), t("rot_bias", 2)
    k.pope, k.angle = t("pope", 3 * T), t("angle", 8)
    k.turned = k.wide(0, 1, 1)
    k.minus_pi = t("minus_pi", 1)
    k.fill1 = [t(f"fill1_{s}", 256) for s in S]
    k.out_scale = t("out_scale", 1)
    k.gate = [t(f"gate{s}", 9 * 32) for s in S]
    k.vexp = t("vexp", 16 * 128)
    k.small = [t(f"small{s}", 64) for s in S]
    k.keymask = [t(f"keymask{s}", G) for s in S]


def setup_tensor(k, eng, pe, dve):
    eng.wait_ge(dve, 3)
    eng.matmul(k.psum[0][0][:, 0:1], k.const("mean"), k.scratch[:, 0:1], start=True, stop=True).then_inc(pe, 1)
    eng.matmul(k.psum[0][1][:, 0:D], k.wide(0, 0, 1)[:, 0:D], k.const("rot"), start=True, stop=True)
    eng.matmul(k.psum[0][1][:, D:2 * D], k.wide(0, 0, 1)[:, D:2 * D], k.const("rot"), start=True, stop=True)
    eng.matmul(k.psum[0][1][:, 2 * D:2 * D + 1], k.const("rot"), k.weight("l3a_bq"), start=True, stop=True)
    eng.matmul(k.psum[0][1][:, 2 * D + 1:2 * D + 2], k.const("rot"), k.weight("l3a_bk"), start=True, stop=True)\
       .then_inc(pe, 1)


def setup_scalar(k, eng, act, dve):
    eng.activation(k.angle[:, 0:1], k.weight("l2a_delta"), ACT.Sigmoid).then_inc(act, 1)
    eng.wait_ge(act, 1)
    eng.wait_ge(dve, 1)
    eng.activation(k.angle[:, 1:2], k.angle[:, 0:1], ACT.Sin, scale=float(2 * np.pi), bias=k.minus_pi[:, 0:1]).then_inc(act, 1)
    eng.activation(k.angle[:, 2:3], k.angle[:, 0:1], ACT.Sin, scale=float(np.pi)).then_inc(act, 1)


def setup_vector(k, eng, pe, dve, act):
    n = 0

    def link(ins):
        nonlocal n
        n += 1
        ins.then_inc(dve, 1)
        eng.wait_ge(dve, n)

    w = k.weight("l1f_w")
    link(eng.memset(k.minus_pi[:], -float(np.pi)))
    link(eng.memset(k.eps5[:], LN_EPS))
    link(eng.tensor_reduce(k.scratch[:, 0:1], w, AX.X, ALU.add, apply_absolute_value=True))
    eng.wait_ge(pe, 1)
    link(eng.tensor_scalar(k.scratch[:, 1:2], k.psum[0][0][:, 0:1], 1 / 128, LN_EPS, ALU.mult, ALU.max))
    link(eng.reciprocal(k.scratch[:, 2:3], k.scratch[:, 1:2]))
    link(eng.tensor_scalar(k.ternary[:], w, k.scratch[:, 2:3], 1.0, ALU.mult, ALU.min))
    link(eng.tensor_scalar(k.ternary[:], k.ternary[:], -1.0, float(3 << 22), ALU.max, ALU.add))
    link(eng.tensor_scalar(k.ternary[:], k.ternary[:], float(3 << 22), k.scratch[:, 1:2], ALU.subtract, ALU.mult))
    eng.wait_ge(act, 3)
    link(eng.tensor_tensor(k.angle[:, 3:4], k.angle[:, 2:3], k.angle[:, 2:3], ALU.mult))
    link(eng.tensor_scalar(k.angle[:, 4:5], k.angle[:, 3:4], -2.0, 1.0, ALU.mult, ALU.add))
    cos, sin = k.angle[:, 4:5], k.angle[:, 1:2]
    link(eng.tensor_scalar(k.turned[:, 0:T], k.const("psin"), sin, None, ALU.mult))
    link(eng.scalar_tensor_tensor(k.pope[:, T:2 * T], k.const("pcos"), cos, k.turned[:, 0:T], ALU.mult, ALU.subtract))
    link(eng.tensor_scalar(k.turned[:, T:2 * T], k.const("pcos"), sin, None, ALU.mult))
    link(eng.scalar_tensor_tensor(k.pope[:, 2 * T:3 * T], k.const("psin"), cos, k.turned[:, T:2 * T], ALU.mult, ALU.add))
    link(eng.tensor_scalar(k.pope[:, 2 * T:3 * T], k.pope[:, 2 * T:3 * T], k.const("psign"), None, ALU.mult))
    for g in range(4):
        rows, part = slice(32 * g, 32 * g + 32), 1 + g % 2
        link(eng.tensor_copy(k.pope[rows, 0:T], k.pope[rows, part * T:(part + 1) * T]))
    eng.wait_ge(pe, 2)
    link(eng.tensor_copy(k.rotated[:], k.psum[0][1][:, 0:2 * D]))
    link(eng.tensor_copy(k.rot_bias[:], k.psum[0][1][:, 2 * D:2 * D + 2]))
    for s in S:
        link(eng.memset(k.vbd[s][:], 0.0))
        for h2 in range(2):
            rows = slice(64 * h2, 64 * h2 + 64)
            link(eng.memset(k.vbd[s][rows, :].rearrange("p (q c) -> p q c", c=18)[:, :, 9 * h2 + 8:9 * h2 + 9], 1.0))
        link(eng.memset(k.vb[s].ap().rearrange("p (h c) -> p h c", c=65)[:, :, 64:65], 1.0))
    for name in ("l1x_ig", "l1x_fg"):
        w = k.weight(name)
        link(eng.tensor_tensor(w[:, 128:256], w[:, 128:256], w[:, 256:384], ALU.add))
    link(eng.tensor_scalar(k.out_scale[:], k.weight("l1x_out"), 1.0, None, ALU.add))
    for odd in range(2):
        for h in range(4):
            to = k.vexp[:].rearrange("p (v r) -> p v r", v=16)[:, :, odd * 64 + h * 16:odd * 64 + h * 16 + 16]
            cols = k.weight("l1a_v")[:, h * 32:(h + 1) * 32].rearrange("p (v o) -> p v o", o=2)[:, :, odd:odd + 1]
            link(eng.tensor_copy(to, cols.broadcast_to([128, 16, 16])))


LAYERS = [CtxNorm, L0Attn, L0Xattn, L0Ffn, L1Attn, L1Xattn, L1Ffn, L2Attn, L2Xattn, L2Ffn, L3Attn, L3Xattn, L3Ffn]


def pad(a, rows=128):
    out = np.zeros((rows, a.shape[1]), a.dtype)
    out[:a.shape[0]] = a
    return out


def col(v, times=1):
    return np.tile(np.reshape(v, (-1, 1)), (times, 1))


def weight_layouts(i):
    out = [("l0a_w", i["L0_attn_W_qkva"].T), ("l0a_gamma", col(i["L0_attn_gamma"]))]
    e8 = lambda a: a.transpose(1, 0, 2).reshape(a.shape[1], -1)
    out += [(n, col(i["L0_xattn_" + n[4:]])) for n in ("l0x_ln_l_w", "l0x_ln_l_b", "l0x_ln_c_w", "l0x_ln_c_b", "l0x_bo")]
    out += [("l0x_wq", i["L0_xattn_Wq"]), ("l0x_wkv", i["L0_xattn_Wkv"]),
            ("l0x_wo", i["L0_xattn_Wo"].reshape(8, 128, 128).transpose(1, 0, 2).reshape(128, -1))]
    out += [("l0f_wr", i["L0_ffn_Wr"]), ("l0f_w1", e8(i["L0_ffn_W1"])),
            ("l0f_b1", i["L0_ffn_b1"].reshape(8, 4, 128).transpose(2, 0, 1).reshape(128, 32)),
            ("l0f_w2", i["L0_ffn_W2"].reshape(8, 4, 128, 128).transpose(2, 0, 1, 3).reshape(128, -1)),
            ("l0f_b2", i["L0_ffn_b2"].T)]
    a = lambda n: i["L1_attn_" + n]
    two = lambda w: np.concatenate([w, w], axis=1)
    out += [("l1a_mu", col(a("x_proj_mu"))), ("l1a_w1", a("xl_w1").T), ("l1a_w2", pad(a("xl_w2").T)),
            ("l1a_b2", col(a("xl_b2")[:128])), ("l1a_b2e", pad(col(a("xl_b2")[128:]))),
            ("l1a_xo", a("x_out_w").T[:128]), ("l1a_xoe", pad(a("x_out_w").T[128:])), ("l1a_xb", a("x_bias").T),
            ("l1a_r", two(a("r_w").T)), ("l1a_k", two(a("k_w").T)), ("l1a_ww1", a("w_w1").T),
            ("l1a_ww2", pad(two(a("w_w2").T))), ("l1a_wb", col(a("w_b"), 2)), ("l1a_v", a("v_w").T),
            ("l1a_g", a("g_w").T), ("l1a_bonus", col(a("bonus"), 2)), ("l1a_gnw", col(a("gn_weight"))),
            ("l1a_gnb", col(a("gn_bias"))), ("l1a_o", a("o_w").T)]
    a = lambda n: i["L1_xattn_" + n]
    wide = lambda w: np.repeat(w.reshape(4, 3, 128).transpose(2, 1, 0), 32, axis=2).reshape(128, 384)
    out += [("l1x_ig", wide(a("igate_w"))), ("l1x_fg", wide(a("fgate_w"))),
            ("l1x_igb", col(np.repeat(a("igate_b"), 32))), ("l1x_fgb", col(np.repeat(a("fgate_b"), 32))),
            ("l1x_out", col(a("out_w"))), ("l1f_w", i["L1_ffn_weight"].T)]
    a = lambda n: i["L2_attn_" + n]
    swap = lambda w: w.reshape(w.shape[0], -1, 2, 16)[:, :, ::-1].reshape(w.shape)
    beside = lambda w: np.stack([w.reshape(64, 8, 32), swap(w).reshape(64, 8, 32)], axis=2).reshape(64, 512)
    four = lambda w: np.concatenate([w] * 4, axis=1)
    out += [("l2a_dkv", a("W_dkv")), ("l2a_uk", pad(a("W_uk"))), ("l2a_uv", pad(a("W_uv"))), ("l2a_dq", a("W_dq")),
            ("l2a_uq", pad(a("W_uq"))), ("l2a_qrq", pad(beside(a("W_qr")))),
            ("l2a_kr", four(a("W_kr"))), ("l2a_krs", four(swap(a("W_kr")))), ("l2a_delta", col(a("raw_delta"), 8)),
            ("l2a_out", a("W_out").reshape(4, 128, 128).transpose(1, 0, 2).reshape(128, -1))]
    a = lambda n: i["L2_xattn_" + n]
    out += [("l2x_wq", a("w_q")), ("l2x_wkv", a("w_kv")), ("l2x_wo", a("w_proj")), ("l2x_bo", col(a("b_proj"))),
            ("l2x_gx", col(a("g_x"))), ("l2x_bx", col(a("b_x"))), ("l2x_gkv", col(a("g_kv"))), ("l2x_bkv", col(a("b_kv")))]
    a = lambda n: i["L2_ffn_" + n]
    w2 = np.zeros((8, 384, 128), np.float32)
    w2[:, :352] = a("w2").transpose(0, 2, 1)
    out += [("l2f_gate", a("gate_w").T), ("l2f_w1", e8(a("w1").transpose(0, 2, 1))),
            ("l2f_w3", e8(a("w3").transpose(0, 2, 1))),
            ("l2f_w2", w2.reshape(8, 3, 128, 128).transpose(2, 0, 1, 3).reshape(128, -1))]
    a = lambda n: i["L3_attn_" + n]
    out += [("l3a_wq", a("Wq").T), ("l3a_wk", a("Wk").T), ("l3a_wv", a("Wv").T), ("l3a_wo", a("Wo").T),
            ("l3a_bq", col(a("bq"))), ("l3a_bk", col(a("bk"))), ("l3a_bv", col(a("bv"))), ("l3a_bo", col(a("bo")))]
    a = lambda n: i["L3_xattn_" + n]
    out += [("l3x_wq", a("Wq").T), ("l3x_wk", a("Wk").T), ("l3x_wv", a("Wv").T), ("l3x_bq", col(a("bq"))),
            ("l3x_bk", col(a("bk"))), ("l3x_bv", col(a("bv")))]
    a = lambda n: i["L3_ffn_" + n]
    out += [("l3f_w", e8(a("W_experts").transpose(0, 2, 1))), ("l3f_b", pad(a("b_experts"))),
            ("l3f_wr", a("W_router").T), ("l3f_br", np.repeat(a("b_router").reshape(1, 8), 128, axis=0))]
    return out


CHUNKS = [("l0a_w", "l1a_mu"), ("l1a_mu", None)]
MOE = ("l0f_", "l2f_")


def build(nc, weights_at, weights_n, moe_at, moe_n, x_d, ctx_d, ctok_d, m0_d, m1_d, w_d, moe_d, qk_d, c_d, out_d, layers, turns):
    with ExitStack() as ctx:
        k = Core(nc, ctx, weights_at, weights_n, moe_at, max(moe_n))
        sem = lambda n: ctx.enter_context(nc.semaphore(n))
        for name in ("x", "h", "c", "cn"):
            k.sbuf(name, G)
        k.sbuf("tmp", NTMP * G)
        k.sbuf("ctok", G)
        small(k, ctx)

        consts_in, weights_in = sem("consts_in"), [sem(f"weights_in{j}") for j in range(len(CHUNKS))]
        setup_pe, setup_dve, setup_act = sem("setup_pe"), sem("setup_dve"), sem("setup_act")
        x_in, c_in = [sem(f"x_in{s}") for s in S], [sem(f"c_in{s}") for s in S]
        ctok_in, mask_in = [sem(f"ctok_in{s}") for s in S], [sem(f"mask_in{s}") for s in S]
        x_out, moe_in = sem("x_out"), [sem(f"moe_in{j}") for j in range(2)]
        k.moe_in = moe_in
        k.c_in, k.ctok_in, k.mask_in = c_in, ctok_in, mask_in

        with nc.Block() as block:
            @block.sync
            def _(eng):
                eng.dma_start(k.c[:], c_d).then_inc(consts_in, 16)
                eng.dma_start(k.wide(0, 0, 1)[:, 0:2 * D], qk_d).then_inc(consts_in, 16)
                for j, (a, b) in enumerate(CHUNKS):
                    lo, hi = weights_at[a][0], weights_at[b][0] if b else weights_n
                    eng.dma_start(k.w[:, lo:hi], w_d[:, lo:hi]).then_inc(weights_in[j], 16)

            @block.tensor
            def _(eng):
                eng.wait_ge(consts_in, 32)
                for q in weights_in:
                    eng.wait_ge(q, 16)
                setup_tensor(k, eng, setup_pe, setup_dve)

            @block.scalar
            def _(eng):
                for q in weights_in:
                    eng.wait_ge(q, 16)
                setup_scalar(k, eng, setup_act, setup_dve)

            @block.vector
            def _(eng):
                eng.wait_ge(consts_in, 32)
                for q in weights_in:
                    eng.wait_ge(q, 16)
                setup_vector(k, eng, setup_pe, setup_dve, setup_act)

        prev, subs = Load(k, x_in), []
        for cls in layers:
            prev = cls(k, prev)
            subs.append(prev)

        with nc.Fori(0, turns) as turn:
            with nc.Block() as block:
                @block.sync
                def _(eng):
                    for s in S:
                        at = turn * (2 * G) + s * G
                        eng.dma_start(k.b("x", s), x_d[:, bass.ds(at, G)]).then_inc(x_in[s], 16)
                        eng.dma_start(k.b("c", s), ctx_d[:, bass.ds(at, G)]).then_inc(c_in[s], 16)
                    eng.dma_start(k.moe[:, 0:moe_n[0]], moe_d[0]).then_inc(moe_in[0], 16)
                    for s in S:
                        at = turn * (2 * G) + s * G
                        eng.dma_start(k.b("ctok", s), ctok_d[:, bass.ds(at, G)]).then_inc(ctok_in[s], 16)
                        for half in range(2):
                            rows = slice(64 * half, 64 * half + 64)
                            for to, m in ((k.fill0[s], m0_d), (k.fill1[s], m1_d)):
                                src = m[:, bass.ds(at, G)].rearrange("o (t b j) -> o t b j", b=2, j=T)[:, :, half, :]
                                eng.dma_start(to[rows, :].bitcast(I32).rearrange("p (t j) -> p t j", j=T),
                                              src.broadcast_to([64, NT, T])).then_inc(mask_in[s], 16)
                        eng.dma_start(k.keymask[s][:].bitcast(I32), m0_d[:, bass.ds(at, G)].broadcast_to([128, G]))\
                           .then_inc(mask_in[s], 16)
                    first_moe = [u for u in subs if isinstance(u, L0Ffn)]
                    for u in first_moe:
                        for s in S:
                            u.output_ready(eng, s)
                    eng.wait_ge(moe_in[0], 16)
                    eng.dma_start(k.moe[:, 0:moe_n[1]], moe_d[1]).then_inc(moe_in[1], 16)
                    for s in S:
                        at = turn * (2 * G) + s * G
                        subs[-1].output_ready(eng, s)
                        eng.dma_start(out_d[:, bass.ds(at, G)], k.b("x", s)).then_inc(x_out, 16)
                    eng.wait_ge(moe_in[1], 16)
                    eng.wait_ge(x_out, 32)

                @block.tensor
                def _(eng):
                    for u in subs:
                        u.pe_program(eng)

                @block.scalar
                def _(eng):
                    log_and_exp_table(eng)
                    for u in subs:
                        u.act_program(eng)

                @block.vector
                def _(eng):
                    for u in subs:
                        u.dve_program(eng)

                @block.gpsimd
                def _(eng):
                    for u in subs:
                        u.pool_program(eng)

            for q in k.sems + x_in + c_in + ctok_in + mask_in + moe_in + [x_out]:
                nc.sync.sem_clear(q)
            nc.all_engine_barrier()


def kernel(**inputs):
    import concourse.bacc as _bacc
    from concourse.bass_utils import run_bass_kernel_spmd as _run

    i = {n: np.asarray(a) for n, a in inputs.items()}
    tokens = lambda a: np.ascontiguousarray(a.reshape(B * T, D).T)
    entries = [(n, np.ascontiguousarray(a)) for n, a in weight_layouts(i)]
    packs = [[e for e in entries if not e[0].startswith(MOE)]] + [[e for e in entries if e[0].startswith(m)] for m in MOE]
    at, n = zip(*[columns([(name, a.shape[1]) for name, a in p]) for p in packs])
    pack = lambda p: np.concatenate([a for _, a in p], axis=1)
    arrays = {
        "x_t": tokens(i["x"]), "ctx_t": tokens(i["ctx_1024"]),
        "ctx_tok": np.ascontiguousarray(i["ctx_1024"].reshape(B * T // 128, 128, D).transpose(1, 0, 2).reshape(128, -1)),
        "mask0": i["mask_BxS2_ik0"].reshape(1, B * T), "mask1": i["mask_BxS2_ik1"].reshape(1, B * T),
        "weights_d": pack(packs[0]), "moe0_d": pack(packs[1]), "moe2_d": pack(packs[2]), "consts_d": constants(),
        "l3a_qk": np.concatenate([i["L3_attn_Wq"], i["L3_attn_Wk"]], axis=1),
    }
    nc = _bacc.Bacc("TRN2", target_bir_lowering=False, num_devices=1)
    d = {name: nc.dram_tensor(name, a.shape, mybir.dt.from_np(a.dtype), kind="ExternalInput").ap()
         for name, a in arrays.items()}
    out = nc.dram_tensor("out_t", (D, B * T), F32, kind="ExternalOutput").ap()
    build(nc, at[0], n[0], at[1:], n[1:], d["x_t"], d["ctx_t"], d["ctx_tok"], d["mask0"], d["mask1"], d["weights_d"],
          [d["moe0_d"], d["moe2_d"]], d["l3a_qk"], d["consts_d"],
          out, LAYERS, TURNS)
    r = _run(nc, [arrays], core_ids=[0])
    return np.ascontiguousarray(r.results[0]["out_t"].T).reshape(B, T, D)
```

```python
from contextlib import ExitStack

import numpy as np

import concourse.bass as bass
from concourse import mybir

F32 = mybir.dt.float32
I32 = mybir.dt.int32
ALU = mybir.AluOpType
ACT = mybir.ActivationFunctionType
AX = mybir.AxisListType

B, T, D = 64, 64, 128
G = 512
NB = G // T
NT = G // 128
TURNS = B * T // (2 * G)
S = (0, 1)
INPUT = "t13"
LN_EPS = 1e-5


class Steps:

    def __init__(self, sem, names):
        self.sem, self.done = sem, 0
        self.order = [(n, s) for joined in names for s in S for n in joined.split("+")]
        self.number = {step: k for k, step in enumerate(self.order)}
        assert len(self.number) == len(self.order)

    def at(self, name, s):
        return self.number[name, s] + 1

    def one(self, name, s):
        assert self.order[self.done] == (name, s), (name, s, self.order[self.done])
        self.done += 1
        return 1


def columns(table):
    at, n = {}, 0
    for name, w in table:
        at[name] = (n, w)
        n += w
    return at, n


CONSTS = [("ident", 128), ("mean", 128), ("mean32", 128), ("centre", 128), ("centre32", 128), ("earlier", 128), ("slot", 10), ("rev", 8),
          ("keep", 512), ("start", 512), ("row0", 1), ("row1", 1), ("tiny", 1), ("eps2", 1), ("cap", 64), ("ones", 128),
          ("pcos", 64), ("psin", 64), ("psign", 1), ("rcos", 64), ("rsin", 64), ("head4", 4), ("rot", 128),
          ("ksum", 158), ("bonus_sum", 128)]
CONST_AT, CONST_N = columns(CONSTS)


def constants():
    c = {n: np.zeros((128, w), np.float32) for n, w in CONSTS}
    p = np.arange(128)
    c["ident"][p, p] = 1
    c["mean"][:] = 1 / 128
    c["mean32"][:] = np.where(p[:, None] // 32 == p[None] // 32, 1 / 32, 0)
    c["centre"][:], c["centre32"][:] = np.eye(128) - c["mean"], np.eye(128) - c["mean32"]
    same = p[:, None] // T == p[None] // T
    c["earlier"][:] = same & (p[:, None] < p[None])
    c["slot"][:] = np.arange(10)
    c["rev"][:] = 8 - np.arange(8)
    c["keep"][:] = np.arange(G) % T != 0
    c["start"][:] = np.where(np.arange(G) % T == 0, -1e30, 0)
    c["row0"][:, 0], c["row1"][:, 0] = p % 32 == 0, p % 32 == 1
    c["tiny"][:], c["eps2"][:] = 1e-8, LN_EPS ** 2
    c["cap"][:] = np.where((p[:, None] % T) <= np.arange(T)[None], 0, -1e30)
    c["ones"][:] = 1
    pos = np.arange(T, dtype=np.float32)
    theta = (1.0 / np.float32(10000.0) ** (2.0 * np.arange(16, dtype=np.float32) / 32)).astype(np.float32)
    ang = (pos[None] * theta[p % 16][:, None]).astype(np.float32)
    c["pcos"][:], c["psin"][:] = np.cos(ang), np.sin(ang)
    c["psign"][:, 0] = np.where(p % 32 < 16, -1, 1)
    freq = (1.0 / np.float32(10000.0) ** (np.arange(0, 8, 2, dtype=np.float32) / 8)).astype(np.float32)
    ang = (pos[None] * freq[(p % 8) % 4][:, None]).astype(np.float32)
    c["rcos"][:], c["rsin"][:] = np.cos(ang), np.sin(ang)
    c["head4"][:] = (p[:, None] % 32) // 8 == np.arange(4)[None]
    even = p[p % 2 == 0]
    c["rot"][even + 1, even] = -1
    c["rot"][even, even + 1] = 1
    c["ksum"][p, ((p % 64) // 16) * 32 + p // 64 + 30] = 1
    q = p[:64]
    c["bonus_sum"][:64] = q[:, None] // 16 == p[None] // 32
    return np.concatenate([c[n] for n, _ in CONSTS], axis=1)


class Core:

    def __init__(self, nc, ctx, weights_at, weights_n, moe_at, moe_n):
        self.nc, self.ctx = nc, ctx
        self.moe_at = moe_at[0] | moe_at[1]
        self.moe = ctx.enter_context(nc.sbuf_tensor("moe_weights", [128, moe_n], F32))
        self.w_at = weights_at
        self.w = ctx.enter_context(nc.sbuf_tensor("weights", [128, weights_n], F32))
        self.c = ctx.enter_context(nc.sbuf_tensor("consts", [128, CONST_N], F32))
        self.psum = [[ctx.enter_context(nc.psum_tensor(f"psum{s}{k}", [128, G], F32)) for k in range(4)] for s in S]
        self.buf = {}
        self.sems = []

    def sbuf(self, name, cols, dt=F32):
        self.buf[name] = [self.ctx.enter_context(self.nc.sbuf_tensor(f"{name}{s}", [128, cols], dt)) for s in S]

    def const(self, name, rows=slice(0, 128)):
        o, w = CONST_AT[name]
        return self.c[rows, o:o + w]

    def weight(self, name, rows=slice(0, 128)):
        if name in self.moe_at:
            o, w = self.moe_at[name]
            return self.moe[rows, o:o + w]
        o, w = self.w_at[name]
        return self.w[rows, o:o + w]

    def steps(self, name, parts):
        sem = self.ctx.enter_context(self.nc.semaphore(name))
        self.sems.append(sem)
        return Steps(sem, parts)

    def b(self, name, s, rows=slice(0, 128)):
        if name[0] == "t":
            return self.wide(s, int(name[1:]), 1, rows)
        return self.buf[name][s][rows, :]

    def wide(self, s, j, n, rows=slice(0, 128)):
        return self.buf["tmp"][s][rows, j * G:(j + n) * G]


def log_and_exp_table(eng):
    eng.preload_act_table_set("natural_log_exp_and_others")


def per_batch(ap):
    return ap.rearrange("p (b t) -> p b t", t=T)


class Norm:

    PE, DVE, ACT = ("centre", "var"), ("h",), ("sq", "ln+rstd")

    def __init__(self, core, sub, src="x", out="h", banks=(0, 1), work="t1"):
        self.k, self.sub, self.src, self.out, self.banks = core, sub, src, out, banks
        self.rstd = work
        self.ln = dict(bias=core.eps5[:, 0:1])

    def centred(self, s):
        return self.k.psum[s][self.banks[0]][:]

    def pe(self, eng):
        self.pe_centre(eng)
        self.pe_var(eng)

    def pe_centre(self, eng):
        k, u = self.k, self.sub
        for s in S:
            u.input_ready(eng, s)
            eng.matmul(self.centred(s), k.const("centre"), k.b(self.src, s), start=True, stop=True)\
               .then_inc(u.pe.sem, u.pe.one("centre", s))

    def pe_var(self, eng):
        k, u = self.k, self.sub
        for s in S:
            eng.wait_ge(u.act.sem, u.act.at("sq", s))
            eng.matmul(k.psum[s][self.banks[1]][:], k.const("mean"), k.b(self.rstd, s), start=True, stop=True)\
               .then_inc(u.pe.sem, u.pe.one("var", s))

    def dve(self, eng):
        k, u = self.k, self.sub
        for s in S:
            eng.wait_ge(u.act.sem, u.act.at("rstd", s))
            eng.tensor_tensor(k.b(self.out, s), self.centred(s), k.b(self.rstd, s), ALU.mult)\
               .then_inc(u.dve.sem, u.dve.one("h", s))

    def act(self, eng):
        self.act_squares(eng)
        self.act_rstd(eng)

    def act_squares(self, eng):
        k, u = self.k, self.sub
        for s in S:
            eng.wait_ge(u.pe.sem, u.pe.at("centre", s))
            eng.activation(k.b(self.rstd, s), self.centred(s), ACT.Square).then_inc(u.act.sem, u.act.one("sq", s))

    def act_rstd(self, eng):
        k, u = self.k, self.sub
        for s in S:
            eng.wait_ge(u.pe.sem, u.pe.at("var", s))
            eng.activation(k.b(self.rstd, s), k.psum[s][self.banks[1]][:], ACT.Ln, **self.ln)\
               .then_inc(u.act.sem, u.act.one("ln", s))
            eng.wait_ge(u.act.sem, u.act.at("ln", s))
            eng.activation(k.b(self.rstd, s), k.b(self.rstd, s), ACT.Exp, scale=-0.5)\
               .then_inc(u.act.sem, u.act.one("rstd", s))


class Sub:

    def __init__(self, core, prev):
        self.k, self.prev = core, prev

    def output_ready(self, eng, s):
        eng.wait_ge(self.dve.sem, self.dve.at("x", s))

    def input_ready(self, eng, s):
        self.prev.output_ready(eng, s)

    def pool_program(self, eng):
        pass


class Load:

    def output_ready(self, eng, s):
        pass


class L0Attn(Sub):

    SPLIT = 2.0 ** -56

    def __init__(self, core, prev):
        super().__init__(core, prev)
        self.pe = core.steps("l0a_pe", ["centre", "var", "q", "kv", "a"])
        self.act = core.steps("l0a_act", ["sq", "lnhigh", "lnlow", "rnorm", "sig"])
        self.dve = core.steps("l0a_dve", ["high", "low", "lnsum", "xn", "gate0", "scan", "qy", "x"])
        self.norm = Norm(core, self, src=INPUT)

    def pe_program(self, eng):
        k, u = self.k, self
        self.norm.pe_centre(eng)
        self.prev.norm.pe_centre(eng)
        self.norm.pe_var(eng)
        self.prev.norm.pe_var(eng)
        for j, name in enumerate(("q", "kv", "a")):
            for s in S:
                if j == 0:
                    eng.wait_ge(u.dve.sem, u.dve.at("xn", s))
                bank = (0, 2, 3)[j]
                if j == 1:
                    eng.wait_ge(u.prev.dve.sem, u.prev.dve.at("h", s))
                eng.matmul(k.psum[s][bank][:], k.weight("l0a_w")[:, j * D:(j + 1) * D], k.b("t3", s),
                           start=True, stop=True).then_inc(u.pe.sem, u.pe.one(name, s))

    def act_program(self, eng):
        k, u = self.k, self
        self.norm.act_squares(eng)
        self.prev.norm.act_squares(eng)
        for s in S:
            eng.wait_ge(u.dve.sem, u.dve.at("high", s))
            eng.activation(k.b("t2", s), k.b("t2", s), ACT.Ln).then_inc(u.act.sem, u.act.one("lnhigh", s))
        for s in S:
            eng.wait_ge(u.dve.sem, u.dve.at("low", s))
            eng.activation(k.b("t4", s), k.b("t4", s), ACT.Ln, scale=1 / self.SPLIT)\
               .then_inc(u.act.sem, u.act.one("lnlow", s))
        for s in S:
            eng.wait_ge(u.dve.sem, u.dve.at("lnsum", s))
            eng.activation(k.b("t2", s), k.b("t2", s), ACT.Exp, scale=-0.5)\
               .then_inc(u.act.sem, u.act.one("rnorm", s))
        self.prev.norm.act_rstd(eng)
        for s in S:
            eng.wait_ge(u.pe.sem, u.pe.at("a", s))
            eng.activation(k.b("t4", s), k.psum[s][3][:], ACT.Sigmoid).then_inc(u.act.sem, u.act.one("sig", s))
        log_and_exp_table(eng)

    def dve_program(self, eng):
        k, u = self.k, self
        for s in S:
            eng.wait_ge(u.pe.sem, u.pe.at("var", s))
            eng.tensor_scalar(k.b("t2", s), k.psum[s][1][:], self.SPLIT, None, ALU.max)\
               .then_inc(u.dve.sem, u.dve.one("high", s))
        for s in S:
            eng.tensor_scalar(k.b("t4", s), k.psum[s][1][:], 1e-24 * LN_EPS / D, self.SPLIT, ALU.max, ALU.min)\
               .then_inc(u.dve.sem, u.dve.one("low", s))
        for s in S:
            eng.wait_ge(u.act.sem, u.act.at("lnlow", s))
            eng.tensor_tensor(k.b("t2", s), k.b("t2", s), k.b("t4", s), ALU.add)\
               .then_inc(u.dve.sem, u.dve.one("lnsum", s))
        for s in S:
            eng.wait_ge(u.act.sem, u.act.at("rnorm", s))
            eng.scalar_tensor_tensor(k.b("t3", s), self.norm.centred(s), k.weight("l0a_gamma"), k.b("t2", s),
                                     ALU.mult, ALU.mult).then_inc(u.dve.sem, u.dve.one("xn", s))
        self.prev.norm.dve(eng)
        for s in S:
            eng.wait_ge(u.act.sem, u.act.at("sig", s))
            eng.memset(per_batch(k.b("t4", s))[:, :, 0:1], 0.0).then_inc(u.dve.sem, u.dve.one("gate0", s))
        for s in S:
            eng.wait_ge(u.dve.sem, u.dve.at("gate0", s))
            eng.wait_ge(u.pe.sem, u.pe.at("kv", s))
            eng.tensor_tensor_scan(k.b("t5", s), k.b("t4", s), k.psum[s][2][:], 0.0, ALU.mult, ALU.add)\
               .then_inc(u.dve.sem, u.dve.one("scan", s))
        for s in S:
            eng.wait_ge(u.dve.sem, u.dve.at("scan", s))
            eng.tensor_tensor(k.b("t5", s), k.b("t5", s), k.psum[s][0][:], ALU.mult)\
               .then_inc(u.dve.sem, u.dve.one("qy", s))
        for s in S:
            if s == 0:
                eng.wait_ge(k.x_free, 32)
            eng.wait_ge(u.dve.sem, u.dve.at("qy", s))
            eng.tensor_tensor(k.b("x", s), k.b(INPUT, s), k.b("t5", s), ALU.add)\
               .then_inc(u.dve.sem, u.dve.one("x", s))


class CtxNorm(Sub):

    def __init__(self, core, prev):
        super().__init__(core, prev)
        self.pe = core.steps("ctx_pe", Norm.PE)
        self.act = core.steps("ctx_act", Norm.ACT)
        self.dve = core.steps("ctx_dve", Norm.DVE)
        self.norm = Norm(core, self, src="c", out="cn", banks=(2, 3), work="t9")

    def output_ready(self, eng, s):
        self.prev.output_ready(eng, s)

    def pe_program(self, eng):
        pass

    act_program = dve_program = pe_program


class TwiceNorm(Norm):

    DVE = ("lat+latb",)

    def __init__(self, core, sub, w, b):
        super().__init__(core, sub)
        self.w, self.bias = w, b
        self.ln = dict(scale=1 + LN_EPS, bias=core.const("eps2"))

    def dve(self, eng):
        k, u = self.k, self.sub
        for s in S:
            eng.wait_ge(u.act.sem, u.act.at("rstd", s))
            eng.scalar_tensor_tensor(k.b("t3", s), self.centred(s), k.weight(self.w), k.b("t1", s), ALU.mult, ALU.mult)\
               .then_inc(u.dve.sem, u.dve.one("lat", s))
            eng.wait_ge(u.dve.sem, u.dve.at("lat", s))
            eng.tensor_scalar(k.b("t3", s), k.b("t3", s), k.weight(self.bias), None, ALU.add)\
               .then_inc(u.dve.sem, u.dve.one("latb", s))


class L0Xattn(Sub):

    HEADS, DH = 8, 64

    def __init__(self, core, prev):
        super().__init__(core, prev)
        pe, act = ["centre", "k0", "k1", "var", "k2", "k3"], list(TwiceNorm.ACT)
        dve = ["ks0", "ks1", *TwiceNorm.DVE, "ks2", "ks3"]
        for hh in range(2):
            first = 4 * hh
            if hh == 0:
                pe += [f"q{p}" for p in range(4)]
                act += [f"qs{p}" for p in range(4)]
            pe += [f"v{first}", f"even{first}", f"odd{first}"]
            act += [f"vs{first}", f"exp{first}"]
            dve += [f"clip{first}"]
            for j in range(first, first + 4):
                more = j < first + 3
                if j > first:
                    act += [f"outs{j - 1}"]
                    dve += [f"recip{j - 1}", f"lo{j - 1}", f"hi{j - 1}"]
                pe += ([f"even{j + 1}", f"odd{j + 1}"] if more else []) + ([f"turn{j - 1}"] if j > first else [])
                pe += ([f"v{j + 1}"] if more else []) + [f"pv{j}"]
                if more:
                    act += [f"vs{j + 1}", f"exp{j + 1}"]
                    dve += [f"clip{j + 1}"]
            j = first + 3
            act += [f"outs{j}"]
            dve += [f"recip{j}", f"lo{j}", f"hi{j}"]
            if hh == 0:
                pe += ["k4", "k5", "turn3", "k6", "k7", "wo0", "q4", "q5", "q6", "q7"]
                act += ["qs4", "qs5", "qs6", "qs7"]
                dve += ["ks4", "ks5", "ks6", "ks7", "x_half"]
            else:
                pe += ["turn7", "wo1"]
                dve += ["x"]
        self.pe, self.act, self.dve = core.steps("l0x_pe", pe), core.steps("l0x_act", act), core.steps("l0x_dve", dve)
        self.gps = core.steps("l0x_pool", ["ctxa"])
        self.norm = TwiceNorm(core, self, "l0x_ln_l_w", "l0x_ln_l_b")

    def q_bank(self, p):
        return (p + p // 4) % 2

    def pe_q(self, eng, p):
        k, u = self.k, self
        for s in S:
            if p == 0:
                eng.wait_ge(u.dve.sem, u.dve.at("latb", s))
            if p % 4 >= 2:
                eng.wait_ge(u.act.sem, u.act.at(f"qs{p - 2}", s))
            if p == 5:
                eng.wait_ge(u.dve.sem, u.dve.at("x_half", s))
            eng.matmul(k.psum[s][self.q_bank(p)][:], k.weight("l0x_wq")[:, p * 128:(p + 1) * 128], k.b("t3", s),
                       start=True, stop=True).then_inc(u.pe.sem, u.pe.one(f"q{p}", s))

    def pe_k(self, eng, p):
        k, u = self.k, self
        for s in S:
            if p == 0:
                eng.wait_ge(u.gps.sem, u.gps.at("ctxa", s))
            if p % 4 >= 2:
                eng.wait_ge(u.dve.sem, u.dve.at(f"ks{p - 2}", s))
            if p == 4:
                eng.wait_ge(u.dve.sem, u.dve.at("hi3", s))
            eng.matmul(k.psum[s][2 + p % 2][:], k.weight("l0x_wkv")[:, p * 128:(p + 1) * 128], k.b("t4", s),
                       start=True, stop=True).then_inc(u.pe.sem, u.pe.one(f"k{p}", s))

    def pe_values(self, eng, j):
        k, u = self.k, self
        t, hh = j % 4, j // 4
        for s in S:
            if t == 0:
                eng.wait_ge(u.act.sem, u.act.at(f"qs{4 * hh + 3}", s))
            else:
                eng.wait_ge(u.act.sem, u.act.at(f"outs{j - 2}" if t > 1 else f"vs{j - 1}", s))
            eng.matmul(k.psum[s][1][:], k.b("t4", s)[:, t * 128:(t + 1) * 128],
                       k.weight("l0x_wkv")[:, 1024 + hh * G:1024 + (hh + 1) * G],
                       start=True, stop=True).then_inc(u.pe.sem, u.pe.one(f"v{j}", s))

    def pe_scores(self, eng, j):
        k, u = self.k, self
        t = j % 4
        for odd, name in enumerate(("even", "odd")):
            half = slice(64 * odd, 64 * odd + 64)
            for s in S:
                if odd:
                    eng.wait_ge(u.pe.sem, u.pe.at(f"even{j}", s))
                elif t == 0:
                    eng.wait_ge(u.act.sem, u.act.at(f"qs{j + 3}", s))
                    eng.wait_ge(u.dve.sem, u.dve.at(f"ks{j + 3}", s))
                else:
                    eng.wait_ge(u.dve.sem, u.dve.at(f"clip{j - 1}", s))
                for h in range(odd, 8, 2):
                    for b in range(2):
                        at = t * 128 + b * T
                        mm = eng.matmul(k.psum[s][0][b * T:(b + 1) * T, h * T:(h + 1) * T],
                                        k.b(f"t{9 + h // 2}", s, half)[:, at:at + T],
                                        k.b(f"t{5 + h // 2}", s, half)[:, at:at + T], start=True, stop=True)
                mm.then_inc(u.pe.sem, u.pe.one(f"{name}{j}", s))

    def pe_turn(self, eng, j):
        k, u = self.k, self
        for s in S:
            eng.wait_ge(u.dve.sem, u.dve.at(f"hi{j}", s))
            eng.wait_ge(u.act.sem, u.act.at(f"vs{j + 1}" if j % 4 < 3 else f"outs{j - 1}", s))
            for p in range(4):
                mm = eng.transpose(k.psum[s][1][:, p * 128:(p + 1) * 128],
                                   k.b("t14", s)[:, p * 128:(p + 1) * 128], k.const("ident"))
            mm.then_inc(u.pe.sem, u.pe.one(f"turn{j}", s))

    def values(self, s, j):
        return self.k.vb[s][:, j % 2 * 520:(j % 2 + 1) * 520].rearrange("p (h c) -> p h c", c=65)

    def exps(self, s, j):
        return self.k.b("t15" if j % 2 else "t13", s)

    def pe_program(self, eng):
        k, u = self.k, self
        self.norm.pe_centre(eng)
        self.pe_k(eng, 0)
        self.pe_k(eng, 1)
        self.norm.pe_var(eng)
        self.pe_k(eng, 2)
        self.pe_k(eng, 3)
        for p in range(4):
            self.pe_q(eng, p)
        for hh in range(2):
            first = 4 * hh
            self.pe_values(eng, first)
            self.pe_scores(eng, first)
            for j in range(first, first + 4):
                more = j < first + 3
                if more:
                    self.pe_scores(eng, j + 1)
                if j > first:
                    self.pe_turn(eng, j - 1)
                if more:
                    self.pe_values(eng, j + 1)
                for s in S:
                    eng.wait_ge(u.act.sem, u.act.at(f"exp{j}", s))
                    if j > first:
                        eng.wait_ge(u.dve.sem, u.dve.at(f"hi{j - 1}", s))
                    for h in range(8):
                        for b in range(2):
                            rows = slice(b * T, (b + 1) * T)
                            mm = eng.matmul(k.psum[s][2 + h // 4][rows, (h % 4) * 65:(h % 4 + 1) * 65],
                                            self.exps(s, j)[rows, h * T:(h + 1) * T], self.values(s, j)[rows, h, :],
                                            start=True, stop=True)
                    mm.then_inc(u.pe.sem, u.pe.one(f"pv{j}", s))
            if hh == 0:
                self.pe_k(eng, 4)
                self.pe_k(eng, 5)
            self.pe_turn(eng, first + 3)
            if hh == 0:
                self.pe_k(eng, 6)
                self.pe_k(eng, 7)
            for s in S:
                eng.wait_ge(u.act.sem, u.act.at(f"outs{first + 3}", s))
                for p in range(4):
                    at = (first + p) * 128
                    mm = eng.matmul(k.psum[s][0][:], k.weight("l0x_wo")[:, at:at + 128], k.b(f"t{5 + p}", s),
                                    start=p == 0, stop=p == 3)
                mm.then_inc(u.pe.sem, u.pe.one(f"wo{hh}", s))
            if hh == 0:
                for p in range(4, 8):
                    self.pe_q(eng, p)

    def act_values_and_exp(self, eng, j):
        k, u = self.k, self
        for s in S:
            eng.wait_ge(u.pe.sem, u.pe.at(f"v{j}", s))
            eng.copy(self.values(s, j)[:, 0:8, 0:64], k.psum[s][1][:].rearrange("p (h c) -> p h c", c=64))\
               .then_inc(u.act.sem, u.act.one(f"vs{j}", s))
        for s in S:
            eng.wait_ge(u.dve.sem, u.dve.at(f"clip{j}", s))
            eng.activation(self.exps(s, j), self.exps(s, j), ACT.Exp, scale=0.125)\
               .then_inc(u.act.sem, u.act.one(f"exp{j}", s))

    def act_outs(self, eng, j):
        k, u = self.k, self
        t = j % 4
        for s in S:
            eng.wait_ge(u.pe.sem, u.pe.at(f"turn{j}", s))
            eng.copy(k.wide(s, 5, 4).rearrange("p (q n) -> p q n", n=G)[:, :, t * 128:(t + 1) * 128],
                     k.psum[s][1][:].rearrange("p (q n) -> p q n", n=128))\
               .then_inc(u.act.sem, u.act.one(f"outs{j}", s))

    def act_program(self, eng):
        k, u = self.k, self
        self.norm.act(eng)
        for hh in range(2):
            first = 4 * hh
            for p in range(first, first + 4):
                for s in S:
                    eng.wait_ge(u.pe.sem, u.pe.at(f"q{p}", s))
                    eng.copy(k.b(f"t{5 + p % 4}", s), k.psum[s][self.q_bank(p)][:]).then_inc(u.act.sem, u.act.one(f"qs{p}", s))
            self.act_values_and_exp(eng, first)
            for j in range(first, first + 4):
                if j > first:
                    self.act_outs(eng, j - 1)
                if j < first + 3:
                    self.act_values_and_exp(eng, j + 1)
            self.act_outs(eng, first + 3)

    def dve_clip(self, eng, j):
        k, u = self.k, self
        for s in S:
            eng.wait_ge(u.pe.sem, u.pe.at(f"odd{j}", s))
            eng.tensor_scalar(self.exps(s, j), k.psum[s][0][:], -88.0, 88.0, ALU.max, ALU.min)\
               .then_inc(u.dve.sem, u.dve.one(f"clip{j}", s))

    def dve_outputs(self, eng, j):
        k, u = self.k, self
        outs = lambda s, c: k.psum[s][2 + c][:, 0:260].rearrange("p (h c) -> p h c", c=65)
        for s in S:
            eng.wait_ge(u.pe.sem, u.pe.at(f"pv{j}", s))
            eng.reciprocal(k.small[s][:, 0:4], outs(s, 0)[:, :, 64])
            eng.reciprocal(k.small[s][:, 4:8], outs(s, 1)[:, :, 64])\
               .then_inc(u.dve.sem, u.dve.one(f"recip{j}", s))
        for c, name in enumerate(("lo", "hi")):
            for s in S:
                eng.wait_ge(u.dve.sem, u.dve.at(f"recip{j}", s))
                eng.tensor_tensor(k.b("t14", s)[:, c * 256:(c + 1) * 256].rearrange("p (h c) -> p h c", c=64),
                                  outs(s, c)[:, :, 0:64],
                                  k.small[s][:, 4 * c:4 * c + 4].unsqueeze(2).broadcast_to([128, 4, 64]),
                                  ALU.mult).then_inc(u.dve.sem, u.dve.one(f"{name}{j}", s))

    def dve_keys(self, eng, p):
        k, u = self.k, self
        for s in S:
            eng.wait_ge(u.pe.sem, u.pe.at(f"k{p}", s))
            eng.tensor_copy(k.b(f"t{9 + p % 4}", s), k.psum[s][2 + p % 2][:]).then_inc(u.dve.sem, u.dve.one(f"ks{p}", s))

    def dve_program(self, eng):
        k, u = self.k, self
        self.dve_keys(eng, 0)
        self.dve_keys(eng, 1)
        self.norm.dve(eng)
        self.dve_keys(eng, 2)
        self.dve_keys(eng, 3)
        for hh in range(2):
            first = 4 * hh
            if hh == 1:
                for p in range(4, 8):
                    self.dve_keys(eng, p)
            if hh == 1:
                for s in S:
                    eng.wait_ge(u.pe.sem, u.pe.at("wo0", s))
                    eng.tensor_tensor(k.b("x", s), k.b("x", s), k.psum[s][0][:], ALU.add)\
                       .then_inc(u.dve.sem, u.dve.one("x_half", s))
            self.dve_clip(eng, first)
            for j in range(first, first + 4):
                if j > first:
                    self.dve_outputs(eng, j - 1)
                if j < first + 3:
                    self.dve_clip(eng, j + 1)
            self.dve_outputs(eng, first + 3)
        for s in S:
            eng.wait_ge(u.pe.sem, u.pe.at("wo1", s))
            eng.wait_ge(u.dve.sem, u.dve.at("x_half", s))
            eng.scalar_tensor_tensor(k.b("x", s), k.psum[s][0][:], k.weight("l0x_bo"), k.b("x", s),
                                     ALU.add, ALU.add).then_inc(u.dve.sem, u.dve.one("x", s))

    def pool_program(self, eng):
        k, u = self.k, self
        for s in S:
            u.input_ready(eng, s)
            eng.tensor_scalar(k.b("t4", s), k.b("cn", s), k.weight("l0x_ln_c_w"), k.weight("l0x_ln_c_b"),
                              ALU.mult, ALU.add).then_inc(u.gps.sem, u.gps.one("ctxa", s))


class Gate:

    PE, ACT = ("logit",), ("gexp",)
    DVE = ("glogit", "gmax", "gsub", "gsum", "grecip", "gprob", "gm0", "ge0", "gkey0", "gmk0", "gsel0", "grest",
           "gm1", "ge1", "gkey1", "gmk1", "gsel1", "gboth", "gate")

    def __init__(self, core, sub, weight, bias=None):
        self.k, self.sub, self.weight, self.bias = core, sub, weight, bias

    def g(self, s, n):
        return self.k.gate[s][:, 32 * n:32 * n + 32]

    def pe(self, eng):
        k, u = self.k, self.sub
        for s in S:
            eng.wait_ge(u.dve.sem, u.dve.at("h", s))
            for t in range(NT):
                mm = eng.matmul(k.psum[s][2][:, t * 8:t * 8 + 8], k.b("h", s)[:, t * 128:(t + 1) * 128],
                                k.weight(self.weight), start=True, stop=True)
            mm.then_inc(u.pe.sem, u.pe.one("logit", s))

    def act(self, eng):
        k, u = self.k, self.sub
        for s in S:
            eng.wait_ge(u.dve.sem, u.dve.at("gsub", s))
            eng.activation(self.g(s, 0), self.g(s, 0), ACT.Exp).then_inc(u.act.sem, u.act.one("gexp", s))

    def dve(self, eng):
        k, u = self.k, self.sub
        g = self.g
        t8 = lambda ap: ap.rearrange("p (t e) -> p t e", e=8)
        sm = lambda s, j: k.small[s][:, 16 + 4 * j:20 + 4 * j]
        over = lambda ap: ap.unsqueeze(2).broadcast_to([128, NT, 8])
        rev = k.const("rev").unsqueeze(1).broadcast_to([128, NT, 8])
        for s in S:
            eng.wait_ge(u.pe.sem, u.pe.at("logit", s))
            if self.bias:
                ins = eng.tensor_tensor(t8(g(s, 0)), t8(k.psum[s][2][:, 0:32]),
                                        k.weight(self.bias).unsqueeze(1).broadcast_to([128, NT, 8]), ALU.add)
            else:
                ins = eng.tensor_copy(g(s, 0), k.psum[s][2][:, 0:32])
            ins.then_inc(u.dve.sem, u.dve.one("glogit", s))
        for s in S:
            eng.wait_ge(u.dve.sem, u.dve.at("glogit", s))
            eng.tensor_reduce(sm(s, 0), t8(g(s, 0)), AX.X, ALU.max).then_inc(u.dve.sem, u.dve.one("gmax", s))
        for s in S:
            eng.wait_ge(u.dve.sem, u.dve.at("gmax", s))
            eng.tensor_tensor(t8(g(s, 0)), t8(g(s, 0)), over(sm(s, 0)), ALU.subtract)\
               .then_inc(u.dve.sem, u.dve.one("gsub", s))
        for s in S:
            eng.wait_ge(u.act.sem, u.act.at("gexp", s))
            eng.tensor_reduce(sm(s, 1), t8(g(s, 0)), AX.X, ALU.add).then_inc(u.dve.sem, u.dve.one("gsum", s))
        for s in S:
            eng.wait_ge(u.dve.sem, u.dve.at("gsum", s))
            eng.reciprocal(sm(s, 2), sm(s, 1)).then_inc(u.dve.sem, u.dve.one("grecip", s))
        for s in S:
            eng.wait_ge(u.dve.sem, u.dve.at("grecip", s))
            eng.tensor_tensor(t8(g(s, 1)), t8(g(s, 0)), over(sm(s, 2)), ALU.mult).then_inc(u.dve.sem, u.dve.one("gprob", s))
        for n, src, cand, sel in ((0, 1, 2, 3), (1, 4, 5, 6)):
            for s in S:
                eng.wait_ge(u.dve.sem, u.dve.at("gprob" if n == 0 else "grest", s))
                eng.tensor_reduce(sm(s, 3 + n), t8(g(s, src)), AX.X, ALU.max).then_inc(u.dve.sem, u.dve.one(f"gm{n}", s))
            for s in S:
                eng.wait_ge(u.dve.sem, u.dve.at(f"gm{n}", s))
                eng.tensor_tensor(t8(g(s, cand)), t8(g(s, src)), over(sm(s, 3 + n)), ALU.is_equal)\
                   .then_inc(u.dve.sem, u.dve.one(f"ge{n}", s))
            for s in S:
                eng.wait_ge(u.dve.sem, u.dve.at(f"ge{n}", s))
                eng.tensor_tensor(t8(g(s, cand)), t8(g(s, cand)), rev, ALU.mult).then_inc(u.dve.sem, u.dve.one(f"gkey{n}", s))
            for s in S:
                eng.wait_ge(u.dve.sem, u.dve.at(f"gkey{n}", s))
                eng.tensor_reduce(sm(s, 5 + n), t8(g(s, cand)), AX.X, ALU.max).then_inc(u.dve.sem, u.dve.one(f"gmk{n}", s))
            for s in S:
                eng.wait_ge(u.dve.sem, u.dve.at(f"gmk{n}", s))
                eng.tensor_tensor(t8(g(s, sel)), t8(g(s, cand)), over(sm(s, 5 + n)), ALU.is_equal)\
                   .then_inc(u.dve.sem, u.dve.one(f"gsel{n}", s))
            if n == 0:
                for s in S:
                    eng.wait_ge(u.dve.sem, u.dve.at("gsel0", s))
                    eng.scalar_tensor_tensor(g(s, 4), g(s, 3), -2.0, g(s, 1), ALU.mult, ALU.add)\
                       .then_inc(u.dve.sem, u.dve.one("grest", s))
        for s in S:
            eng.wait_ge(u.dve.sem, u.dve.at("gsel1", s))
            eng.tensor_tensor(g(s, 7), g(s, 3), g(s, 6), ALU.add).then_inc(u.dve.sem, u.dve.one("gboth", s))
        for s in S:
            eng.wait_ge(u.dve.sem, u.dve.at("gboth", s))
            eng.tensor_tensor(g(s, 8), g(s, 1), g(s, 7), ALU.mult).then_inc(u.dve.sem, u.dve.one("gate", s))


class L0Ffn(Sub):

    E, CAP, HID = 8, 10, 4
    SLOTS = E * CAP

    def __init__(self, core, prev):
        super().__init__(core, prev)
        n = range(self.E // 2)
        self.pe = core.steps("l0f_pe", [*Norm.PE, *Gate.PE, "htok", "rank", "gt", "fill"]
                             + [f"{a}{j}" for j in n for a in ("up", "down")] + ["yt", "comb"])
        self.act = core.steps("l0f_act", [*Norm.ACT, *Gate.ACT, "htok", "gt", "fill"] + [f"relu{j}" for j in n] + ["yt"])
        self.dve = core.steps("l0f_dve", [*Norm.DVE, *Gate.DVE, "hot", "disp", "gated"] + [f"y{j}" for j in n] + ["x"])
        self.norm = Norm(core, self)
        self.gate = Gate(core, self, "l0f_wr")

    def places(self):
        return self.k.wide(0, 10, 3)[:, 0:1280]

    def results(self):
        return self.k.wide(1, 10, 3)[:, 0:1280]

    def hidden(self, odd):
        return self.k.wide(odd, 13, 2)[:, 0:640]

    def pe_program(self, eng):
        k, u = self.k, self
        self.norm.pe(eng)
        eng.wait_ge(k.moe_in[0], 16)
        self.gate.pe(eng)
        for s in S:
            for t in range(NT):
                mm = eng.transpose(k.psum[s][0][:, t * 128:(t + 1) * 128], k.b("h", s)[:, t * 128:(t + 1) * 128],
                                   k.const("ident"))
            mm.then_inc(u.pe.sem, u.pe.one("htok", s))
        for s in S:
            eng.wait_ge(u.dve.sem, u.dve.at("gboth", s))
            eng.matmul(k.psum[s][3][:, 0:32], k.const("earlier"), self.gate.g(s, 7), start=True, stop=True)\
               .then_inc(u.pe.sem, u.pe.one("rank", s))
        for s in S:
            eng.wait_ge(u.dve.sem, u.dve.at("gated", s))
            for t in range(NT):
                mm = eng.transpose(k.psum[s][1][0:80, t * 128:(t + 1) * 128], k.b("t5", s)[:, t * 80:(t + 1) * 80],
                                   k.const("ident"))
            mm.then_inc(u.pe.sem, u.pe.one("gt", s))
        for s in S:
            eng.wait_ge(u.act.sem, u.act.at("htok", s))
            for t in range(NT):
                for b in range(2):
                    rows = slice(b * T, (b + 1) * T)
                    mm = eng.matmul(k.psum[s][2 + b][:, t * 80:(t + 1) * 80], k.b("t6", s, rows)[:, t * 128:(t + 1) * 128],
                                    k.b("t4", s, rows)[:, t * 80:(t + 1) * 80], start=True, stop=True)
            mm.then_inc(u.pe.sem, u.pe.one("fill", s))
        for j in range(self.E // 2):
            for odd in range(2):
                e = 2 * j + odd
                if j == 0:
                    for s in S:
                        eng.wait_ge(u.act.sem, u.act.at("fill", s))
                        eng.wait_ge(u.act.sem, u.act.at("gt", s))
                else:
                    eng.wait_ge(u.act.sem, u.act.at(f"relu{j - 1}", odd))
                for c in range(self.HID):
                    mm = eng.matmul(k.psum[odd][c // 3][:, c % 3 * 160:(c % 3 + 1) * 160],
                                    k.weight("l0f_w1")[:, e * 512 + c * 128:e * 512 + (c + 1) * 128],
                                    self.places()[:, e * 160:(e + 1) * 160], start=True, stop=True)
                mm.then_inc(u.pe.sem, u.pe.one(f"up{j}", odd))
            for odd in range(2):
                e = 2 * j + odd
                eng.wait_ge(u.act.sem, u.act.at(f"relu{j}", odd))
                if j:
                    eng.wait_ge(u.dve.sem, u.dve.at(f"y{j - 1}", odd))
                for c in range(self.HID):
                    mm = eng.matmul(k.psum[odd][2][:, 0:160],
                                    k.weight("l0f_w2")[:, (e * 4 + c) * 128:(e * 4 + c + 1) * 128],
                                    self.hidden(odd)[:, c * 160:(c + 1) * 160], start=c == 0, stop=c == self.HID - 1)
                mm.then_inc(u.pe.sem, u.pe.one(f"down{j}", odd))
        for s in S:
            eng.wait_ge(u.dve.sem, u.dve.at("y3", 0))
            eng.wait_ge(u.dve.sem, u.dve.at("y3", 1))
            for b in range(NB):
                at = (s * NB + b) * 80
                mm = eng.transpose(k.psum[s][b // 4][0:80, b % 4 * 128:(b % 4 + 1) * 128], self.results()[:, at:at + 80],
                                   k.const("ident"))
            mm.then_inc(u.pe.sem, u.pe.one("yt", s))
        for s in S:
            eng.wait_ge(u.act.sem, u.act.at("yt", s))
            for b in range(NB):
                mm = eng.matmul(k.psum[s][2][:, b * T:(b + 1) * T],
                                k.wide(s, 8, 2, slice(0, 80))[:, b * 128:(b + 1) * 128],
                                k.b("t7", s, slice(0, 80))[:, b * T:(b + 1) * T], start=True, stop=True)
            mm.then_inc(u.pe.sem, u.pe.one("comb", s))

    def act_program(self, eng):
        k, u = self.k, self
        self.norm.act(eng)
        self.gate.act(eng)
        for s in S:
            eng.wait_ge(u.pe.sem, u.pe.at("htok", s))
            eng.copy(k.b("t6", s), k.psum[s][0][:]).then_inc(u.act.sem, u.act.one("htok", s))
        for s in S:
            eng.wait_ge(u.pe.sem, u.pe.at("gt", s))
            eng.copy(k.b("t7", s, slice(0, 80)), k.psum[s][1][0:80, :]).then_inc(u.act.sem, u.act.one("gt", s))
        for s in S:
            eng.wait_ge(u.pe.sem, u.pe.at("fill", s))
            for b in range(2):
                to = self.places().rearrange("p (e s t b c) -> p e s t b c", e=8, s=2, t=NT, b=2)[:, :, s, :, b, :]
                ins = eng.copy(to, k.psum[s][2 + b][:, 0:320].rearrange("p (t e c) -> p e t c", t=NT, e=8))
            ins.then_inc(u.act.sem, u.act.one("fill", s))
        for j in range(self.E // 2):
            for odd in range(2):
                e = 2 * j + odd
                eng.wait_ge(u.pe.sem, u.pe.at(f"up{j}", odd))
                for c in range(self.HID):
                    ins = eng.activation(self.hidden(odd)[:, c * 160:(c + 1) * 160],
                                         k.psum[odd][c // 3][:, c % 3 * 160:(c % 3 + 1) * 160], ACT.Relu,
                                         bias=k.weight("l0f_b1")[:, e * 4 + c:e * 4 + c + 1])
                ins.then_inc(u.act.sem, u.act.one(f"relu{j}", odd))
        for s in S:
            eng.wait_ge(u.pe.sem, u.pe.at("yt", s))
            for c in range(2):
                ins = eng.copy(k.wide(s, 8, 2, slice(0, 80))[:, c * G:(c + 1) * G], k.psum[s][c][0:80, :])
            ins.then_inc(u.act.sem, u.act.one("yt", s))

    def dve_program(self, eng):
        k, u = self.k, self
        self.norm.dve(eng)
        self.gate.dve(eng)
        hot = lambda name, s: k.b(name, s)[:, 0:320].rearrange("p (e c) -> p e c", c=self.CAP)
        over = lambda ap: ap.unsqueeze(2).broadcast_to([128, 32, self.CAP])
        for s in S:
            eng.wait_ge(u.pe.sem, u.pe.at("rank", s))
            eng.tensor_tensor(hot("t4", s), over(k.psum[s][3][:, 0:32]),
                              k.const("slot").unsqueeze(1).broadcast_to([128, 32, self.CAP]), ALU.is_equal)\
               .then_inc(u.dve.sem, u.dve.one("hot", s))
        for s in S:
            eng.wait_ge(u.dve.sem, u.dve.at("hot", s))
            eng.tensor_tensor(hot("t4", s), hot("t4", s), over(self.gate.g(s, 7)), ALU.mult)\
               .then_inc(u.dve.sem, u.dve.one("disp", s))
        for s in S:
            eng.wait_ge(u.dve.sem, u.dve.at("disp", s))
            eng.tensor_tensor(hot("t5", s), hot("t4", s), over(self.gate.g(s, 1)), ALU.mult)\
               .then_inc(u.dve.sem, u.dve.one("gated", s))
        for j in range(self.E // 2):
            for odd in range(2):
                e = 2 * j + odd
                eng.wait_ge(u.pe.sem, u.pe.at(f"down{j}", odd))
                eng.tensor_scalar(self.results().rearrange("p (b e c) -> p b e c", e=8, c=10)[:, :, e, :],
                                  k.psum[odd][2][:, 0:160].rearrange("p (b c) -> p b c", c=10),
                                  k.weight("l0f_b2")[:, e:e + 1], None, ALU.add).then_inc(u.dve.sem, u.dve.one(f"y{j}", odd))
        for s in S:
            eng.wait_ge(u.pe.sem, u.pe.at("comb", s))
            eng.tensor_tensor(k.b("x", s), k.b("x", s), k.psum[s][2][:], ALU.add).then_inc(u.dve.sem, u.dve.one("x", s))


class GroupNorm:

    PE, ACT, DVE = ("gcentre", "gvar"), ("gsq", "gln+grstd"), ("gn",)

    def __init__(self, core, sub, src, ready):
        self.k, self.sub, self.src, self.ready = core, sub, src, ready

    def pe(self, eng):
        k, u = self.k, self.sub
        for s in S:
            self.ready(eng, s)
            eng.matmul(k.psum[s][2][:], k.const("centre32"), k.b(self.src, s), start=True, stop=True)\
               .then_inc(u.pe.sem, u.pe.one("gcentre", s))
        for s in S:
            eng.wait_ge(u.act.sem, u.act.at("gsq", s))
            eng.matmul(k.psum[s][3][:], k.const("mean32"), k.b("t13", s), start=True, stop=True)\
               .then_inc(u.pe.sem, u.pe.one("gvar", s))

    def act(self, eng):
        k, u = self.k, self.sub
        for s in S:
            eng.wait_ge(u.pe.sem, u.pe.at("gcentre", s))
            eng.activation(k.b("t13", s), k.psum[s][2][:], ACT.Square).then_inc(u.act.sem, u.act.one("gsq", s))
        for s in S:
            eng.wait_ge(u.pe.sem, u.pe.at("gvar", s))
            eng.activation(k.b("t13", s), k.psum[s][3][:], ACT.Ln, bias=k.eps5[:, 0:1])\
               .then_inc(u.act.sem, u.act.one("gln", s))
            eng.wait_ge(u.act.sem, u.act.at("gln", s))
            eng.activation(k.b("t13", s), k.b("t13", s), ACT.Exp, scale=-0.5).then_inc(u.act.sem, u.act.one("grstd", s))

    def dve(self, eng):
        for s in S:
            self.dve_one(eng, s)

    def dve_one(self, eng, s):
        k, u = self.k, self.sub
        eng.wait_ge(u.act.sem, u.act.at("grstd", s))
        eng.tensor_tensor(k.b("t12", s), k.psum[s][2][:], k.b("t13", s), ALU.mult).then_inc(u.dve.sem, u.dve.one("gn", s))


class L1Xattn(Sub):

    def __init__(self, core, prev):
        super().__init__(core, prev)
        self.pe = core.steps("l1x_pe", ["centre", "fgc", "var", "igc", "fg", "ig", "qk01", "qk23", "logd", "num", *GroupNorm.PE])
        self.act = core.steps("l1x_act", [*Norm.ACT, "fabs", "fexp", "fln", "expnm", "dexp", "absd+dln+drec", *GroupNorm.ACT])
        self.dve = core.steps("l1x_dve", [*Norm.DVE, "f", "g", "lf", "cs", "gs", "m", "m1", "csm", "dmin+c", "norm+out", *GroupNorm.DVE, "x"])
        self.gps = core.steps("l1x_pool", ["g1"])
        self.norm = Norm(core, self)
        self.gn = GroupNorm(core, self, "t11", lambda eng, s: eng.wait_ge(self.dve.sem, self.dve.at("out", s)))

    def pe_program(self, eng):
        k, u = self.k, self
        place = [(h, t, b) for h in range(4) for t in range(NT) for b in range(2)]

        def gate(name, bank, part, src):
            for s in S:
                if part == 0:
                    eng.wait_ge(u.dve.sem, u.dve.at("h", s))
                eng.matmul(k.psum[s][bank][:], k.weight("l1x_" + name[:2])[:, part * 128:(part + 1) * 128], k.b(src, s),
                           start=part == 1, stop=part == 0).then_inc(u.pe.sem, u.pe.one(name, s))

        def scores(name, heads):
            for s in S:
                if heads[0]:
                    eng.wait_ge(u.dve.sem, u.dve.at("g", s))
                for h, t, b in place:
                    if h in heads:
                        rows, at = slice(32 * h, 32 * h + 32), t * 128 + b * T
                        mm = eng.matmul(k.psum[s][h][b * T:(b + 1) * T, 256 + t * T:256 + (t + 1) * T],
                                        k.b("c", s, rows)[:, at:at + T], k.b("h", s, rows)[:, at:at + T], start=True,
                                        stop=True, tile_position=(32 * h, 64 * b))
                mm.then_inc(u.pe.sem, u.pe.one(name, s))

        self.norm.pe_centre(eng)
        gate("fgc", 3, 1, "c")
        self.norm.pe_var(eng)
        gate("igc", 2, 1, "c")
        gate("fg", 3, 0, "h")
        gate("ig", 2, 0, "h")
        scores("qk01", (0, 1))
        scores("qk23", (2, 3))
        for s in S:
            eng.wait_ge(u.gps.sem, u.gps.at("g1", s))
            eng.wait_ge(u.dve.sem, u.dve.at("m1", s))
            for h, t, b in place:
                rows, at = slice(32 * h, 32 * h + 32), t * 128 + b * T
                mm = eng.matmul(k.psum[s][h][b * T:(b + 1) * T, t * T:(t + 1) * T], k.b("t3", s, rows)[:, at:at + T],
                                k.b("t2", s, rows)[:, at:at + T], start=True, stop=True, tile_position=(32 * h, 64 * b))
            mm.then_inc(u.pe.sem, u.pe.one("logd", s))
        for s in S:
            eng.wait_ge(u.dve.sem, u.dve.at("c", s))
            eng.wait_ge(k.ctok_in[s], 16)
            for h, t, b in place:
                rows, cols = slice(64 * b, 64 * b + 64), slice((h * NT + t) * T, (h * NT + t + 1) * T)
                weights = k.wide(s, 8, 2, rows)[:, cols]
                heads = slice(32 * h, 32 * h + 32)
                eng.matmul(k.psum[s][b][heads, t * T:(t + 1) * T], k.b("ctok", s, rows)[:, t * 128 + 32 * h:t * 128 + 32 * h + 32],
                           weights, start=True, stop=True, tile_position=(64 * b, 32 * h))
                mm = eng.matmul(k.psum[s][b][heads, 256 + t * T:256 + (t + 1) * T], k.const("ones", rows)[:, 0:32],
                                weights, start=True, stop=True, tile_position=(64 * b, 32 * h))
            mm.then_inc(u.pe.sem, u.pe.one("num", s))
        self.gn.pe(eng)

    def act_program(self, eng):
        k, u = self.k, self
        self.norm.act(eng)
        for s in S:
            eng.wait_ge(u.dve.sem, u.dve.at("f", s))
            eng.activation(k.b("t3", s), k.b("t2", s), ACT.Abs).then_inc(u.act.sem, u.act.one("fabs", s))
        for s in S:
            eng.wait_ge(u.act.sem, u.act.at("fabs", s))
            eng.activation(k.b("t3", s), k.b("t3", s), ACT.Exp, scale=-1.0).then_inc(u.act.sem, u.act.one("fexp", s))
        for s in S:
            eng.wait_ge(u.act.sem, u.act.at("fexp", s))
            eng.activation(k.b("t3", s), k.b("t3", s), ACT.Ln, bias=1.0).then_inc(u.act.sem, u.act.one("fln", s))
        for s in S:
            eng.wait_ge(u.dve.sem, u.dve.at("csm", s))
            eng.activation(k.b("t7", s), k.b("t7", s), ACT.Exp, scale=-1.0).then_inc(u.act.sem, u.act.one("expnm", s))
        for s in S:
            eng.wait_ge(u.dve.sem, u.dve.at("dmin", s))
            eng.activation(k.wide(s, 8, 2), k.wide(s, 8, 2), ACT.Exp).then_inc(u.act.sem, u.act.one("dexp", s))
        for s in S:
            eng.wait_ge(u.pe.sem, u.pe.at("num", s))
            for b in range(2):
                ins = eng.activation(k.b("t10", s).rearrange("p (t b q) -> p t b q", b=2, q=T)[:, :, b, :],
                                     k.psum[s][b][:, 256:512].rearrange("p (t q) -> p t q", q=T), ACT.Abs)
            ins.then_inc(u.act.sem, u.act.one("absd", s))
            eng.wait_ge(u.dve.sem, u.dve.at("norm", s))
            eng.activation(k.b("t10", s), k.b("t10", s), ACT.Ln, bias=k.const("tiny")).then_inc(u.act.sem, u.act.one("dln", s))
            eng.wait_ge(u.act.sem, u.act.at("dln", s))
            eng.activation(k.b("t10", s), k.b("t10", s), ACT.Exp, scale=-1.0).then_inc(u.act.sem, u.act.one("drec", s))
        self.gn.act(eng)

    def dve_program(self, eng):
        k, u = self.k, self
        self.norm.dve(eng)
        for s in S:
            eng.wait_ge(u.pe.sem, u.pe.at("fg", s))
            eng.tensor_scalar(k.b("t2", s), k.psum[s][3][:], k.weight("l1x_fgb"), None, ALU.add)\
               .then_inc(u.dve.sem, u.dve.one("f", s))
        for s in S:
            eng.wait_ge(u.pe.sem, u.pe.at("ig", s))
            eng.tensor_scalar(k.b("t5", s), k.psum[s][2][:], k.weight("l1x_igb"), None, ALU.add)\
               .then_inc(u.dve.sem, u.dve.one("g", s))
        for s in S:
            eng.wait_ge(u.act.sem, u.act.at("fln", s))
            eng.scalar_tensor_tensor(k.b("t2", s), k.b("t2", s), 0.0, k.b("t3", s), ALU.min, ALU.subtract)\
               .then_inc(u.dve.sem, u.dve.one("lf", s))
        for s in S:
            eng.wait_ge(u.dve.sem, u.dve.at("lf", s))
            eng.tensor_tensor_scan(k.b("t4", s), k.const("keep"), k.b("t2", s), 0.0, ALU.mult, ALU.add)\
               .then_inc(u.dve.sem, u.dve.one("cs", s))
        for s in S:
            eng.wait_ge(u.dve.sem, u.dve.at("cs", s))
            late = per_batch(k.b("t5", s))[:, :, 1:T]
            eng.tensor_tensor(late, late, per_batch(k.b("t4", s))[:, :, 0:T - 1], ALU.subtract)\
               .then_inc(u.dve.sem, u.dve.one("gs", s))
        for s in S:
            eng.wait_ge(u.dve.sem, u.dve.at("gs", s))
            eng.tensor_tensor_scan(k.b("t6", s), k.const("start"), k.b("t5", s), 0.0, ALU.add, ALU.max)\
               .then_inc(u.dve.sem, u.dve.one("m", s))
        for s in S:
            eng.wait_ge(u.dve.sem, u.dve.at("m", s))
            eng.tensor_scalar(k.b("t2", s), k.b("t6", s), k.const("row1"), k.const("row0"), ALU.mult, ALU.add)\
               .then_inc(u.dve.sem, u.dve.one("m1", s))
        for s in S:
            eng.tensor_tensor(k.b("t7", s), k.b("t4", s), k.b("t6", s), ALU.add).then_inc(u.dve.sem, u.dve.one("csm", s))
        tiles = lambda ap: ap.rearrange("p (t q) -> p t q", q=T)
        for s in S:
            eng.wait_ge(u.pe.sem, u.pe.at("logd", s))
            for h in range(4):
                ins = eng.tensor_tensor(tiles(k.wide(s, 8, 2)[:, h * 256:(h + 1) * 256]), tiles(k.psum[s][h][:, 0:256]),
                                        k.const("cap").unsqueeze(1).broadcast_to([128, NT, T]), ALU.min)
            ins.then_inc(u.dve.sem, u.dve.one("dmin", s))
            eng.wait_ge(u.act.sem, u.act.at("dexp", s))
            for h in range(4):
                w = k.wide(s, 8, 2)[:, h * 256:(h + 1) * 256]
                ins = eng.scalar_tensor_tensor(w, k.psum[s][h][:, 256:512], 32 ** -0.5, w, ALU.mult, ALU.mult)
            ins.then_inc(u.dve.sem, u.dve.one("c", s))
        for s in S:
            eng.wait_ge(u.act.sem, u.act.at("absd", s))
            eng.scalar_tensor_tensor(k.b("t10", s), k.b("t7", s), 1e18, k.b("t10", s), ALU.min, ALU.max)\
               .then_inc(u.dve.sem, u.dve.one("norm", s))
            eng.wait_ge(u.act.sem, u.act.at("drec", s))
            tile = lambda name, b: k.b(name, s).rearrange("p (t b q) -> p t b q", b=2, q=T)[:, :, b, :]
            for b in range(2):
                ins = eng.tensor_tensor(tile("t11", b), tiles(k.psum[s][b][:, 0:256]), tile("t10", b), ALU.mult)
            ins.then_inc(u.dve.sem, u.dve.one("out", s))
        self.gn.dve(eng)
        for s in S:
            eng.wait_ge(u.dve.sem, u.dve.at("gn", s))
            eng.scalar_tensor_tensor(k.b("x", s), k.b("t12", s), k.out_scale[:, 0:1], k.b("x", s), ALU.mult, ALU.add)\
               .then_inc(u.dve.sem, u.dve.one("x", s))

    def pool_program(self, eng):
        k, u = self.k, self
        for s in S:
            eng.wait_ge(u.dve.sem, u.dve.at("gs", s))
            eng.tensor_scalar(k.b("t3", s), k.b("t5", s), k.const("row0"), k.const("row1"), ALU.mult, ALU.subtract)\
               .then_inc(u.gps.sem, u.gps.one("g1", s))


class L3Xattn(Sub):

    def __init__(self, core, prev):
        super().__init__(core, prev)
        self.pe = core.steps("l3x_pe", [*Norm.PE, "k", "v", "q", "score", "turn", "pv"])
        self.act = core.steps("l3x_act", [*Norm.ACT, "ks", "vs", "exp", "probs"])
        self.dve = core.steps("l3x_dve", ["fill", "fillneg", *Norm.DVE, "qs", "masked+max+sub", "sum+recip+scaled", "x"])
        self.norm = Norm(core, self)

    def pe_program(self, eng):
        k, u = self.k, self
        self.norm.pe(eng)
        for s in S:
            eng.matmul(k.psum[s][2][:], k.weight("l3x_wk"), k.b("c", s), start=True, stop=True)\
               .then_inc(u.pe.sem, u.pe.one("k", s))
        for s in S:
            for tp in range(2):
                for b in range(2):
                    for t2 in range(2):
                        at = (2 * tp + t2) * 128 + b * T
                        mm = eng.matmul(k.psum[s][3][64 * t2:64 * t2 + 64, (2 * tp + b) * 128:(2 * tp + b + 1) * 128],
                                        k.b("c", s)[:, at:at + T], k.weight("l3x_wv"), start=True, stop=True)
            mm.then_inc(u.pe.sem, u.pe.one("v", s))
        for s in S:
            eng.wait_ge(u.dve.sem, u.dve.at("h", s))
            eng.matmul(k.psum[s][0][:], k.weight("l3x_wq"), k.b("h", s), start=True, stop=True)\
               .then_inc(u.pe.sem, u.pe.one("q", s))
        for s in S:
            eng.wait_ge(u.act.sem, u.act.at("ks", s))
            eng.wait_ge(u.dve.sem, u.dve.at("qs", s))
            for t in range(NT):
                for b in range(2):
                    at = t * 128 + b * T
                    mm = eng.matmul(k.psum[s][2][b * T:(b + 1) * T, t * T:(t + 1) * T], k.b("t5", s)[:, at:at + T],
                                    k.b("t6", s)[:, at:at + T], start=True, stop=True)
            mm.then_inc(u.pe.sem, u.pe.one("score", s))
        for s in S:
            eng.wait_ge(u.dve.sem, u.dve.at("scaled", s))
            for tp in range(2):
                mm = eng.transpose(k.psum[s][0][:, tp * 128:(tp + 1) * 128], k.b("t11", s)[:, tp * 128:(tp + 1) * 128],
                                   k.const("ident"))
            mm.then_inc(u.pe.sem, u.pe.one("turn", s))
        for s in S:
            eng.wait_ge(u.act.sem, u.act.at("probs", s))
            eng.wait_ge(u.act.sem, u.act.at("vs", s))
            for tp in range(2):
                for b in range(2):
                    for t2 in range(2):
                        rows = slice(64 * t2, 64 * t2 + 64)
                        mm = eng.matmul(k.psum[s][1 + t2][:, (2 * tp + b) * T:(2 * tp + b + 1) * T],
                                        k.b("t7", s, rows)[:, (2 * tp + b) * 128:(2 * tp + b + 1) * 128],
                                        k.b("t12", s, rows)[:, tp * 128 + b * T:tp * 128 + (b + 1) * T], start=True, stop=True)
            mm.then_inc(u.pe.sem, u.pe.one("pv", s))

    def act_program(self, eng):
        k, u = self.k, self
        self.norm.act(eng)
        for s in S:
            eng.wait_ge(u.pe.sem, u.pe.at("k", s))
            eng.activation(k.b("t6", s), k.psum[s][2][:], ACT.Identity, bias=k.weight("l3x_bk"))\
               .then_inc(u.act.sem, u.act.one("ks", s))
        for s in S:
            eng.wait_ge(u.pe.sem, u.pe.at("v", s))
            eng.copy(k.b("t7", s), k.psum[s][3][:]).then_inc(u.act.sem, u.act.one("vs", s))
        for s in S:
            eng.wait_ge(u.dve.sem, u.dve.at("sub", s))
            eng.activation(k.b("t11", s)[:, 0:256], k.b("t11", s)[:, 0:256], ACT.Exp).then_inc(u.act.sem, u.act.one("exp", s))
        for s in S:
            eng.wait_ge(u.pe.sem, u.pe.at("turn", s))
            eng.copy(k.b("t12", s)[:, 0:256], k.psum[s][0][:, 0:256]).then_inc(u.act.sem, u.act.one("probs", s))

    def dve_program(self, eng):
        k, u = self.k, self
        for s in S:
            eng.wait_ge(k.mask_in[s], 80)
            eng.tensor_scalar(k.fill1[s][:], k.fill1[s][:].bitcast(I32), 0.0, 1.0, ALU.not_equal, ALU.subtract)\
               .then_inc(u.dve.sem, u.dve.one("fill", s))
        for s in S:
            eng.wait_ge(u.dve.sem, u.dve.at("fill", s))
            eng.tensor_scalar(k.fill1[s][:], k.fill1[s][:], 3e38, None, ALU.mult).then_inc(u.dve.sem, u.dve.one("fillneg", s))
        self.norm.dve(eng)
        for s in S:
            eng.wait_ge(u.pe.sem, u.pe.at("q", s))
            eng.tensor_scalar(k.b("t5", s), k.psum[s][0][:], k.weight("l3x_bq"), None, ALU.add)\
               .then_inc(u.dve.sem, u.dve.one("qs", s))
        w = lambda s: k.b("t11", s)[:, 0:256]
        tiles = lambda s: w(s).rearrange("p (t j) -> p t j", j=T)
        for s in S:
            eng.wait_ge(u.pe.sem, u.pe.at("score", s))
            eng.wait_ge(u.dve.sem, u.dve.at("fillneg", s))
            eng.scalar_tensor_tensor(w(s), k.psum[s][2][:, 0:256], 128 ** -0.5, k.fill1[s][:], ALU.mult, ALU.add)\
               .then_inc(u.dve.sem, u.dve.one("masked", s))
            eng.wait_ge(u.dve.sem, u.dve.at("masked", s))
            eng.tensor_reduce(k.small[s][:, 0:4], tiles(s), AX.X, ALU.max).then_inc(u.dve.sem, u.dve.one("max", s))
            eng.wait_ge(u.dve.sem, u.dve.at("max", s))
            eng.tensor_tensor(tiles(s), tiles(s), k.small[s][:, 0:4].unsqueeze(2).broadcast_to([128, 4, T]), ALU.subtract)\
               .then_inc(u.dve.sem, u.dve.one("sub", s))
        for s in S:
            eng.wait_ge(u.act.sem, u.act.at("exp", s))
            eng.tensor_reduce(k.small[s][:, 4:8], tiles(s), AX.X, ALU.add).then_inc(u.dve.sem, u.dve.one("sum", s))
            eng.wait_ge(u.dve.sem, u.dve.at("sum", s))
            eng.reciprocal(k.small[s][:, 8:12], k.small[s][:, 4:8]).then_inc(u.dve.sem, u.dve.one("recip", s))
            eng.wait_ge(u.dve.sem, u.dve.at("recip", s))
            eng.tensor_tensor(tiles(s), tiles(s), k.small[s][:, 8:12].unsqueeze(2).broadcast_to([128, 4, T]), ALU.mult)\
               .then_inc(u.dve.sem, u.dve.one("scaled", s))
        for s in S:
            eng.wait_ge(u.pe.sem, u.pe.at("pv", s))
            for t2 in range(2):
                to = k.b("x", s).rearrange("p (a t n) -> p a t n", t=2, n=128)[:, :, t2, :]
                ins = eng.scalar_tensor_tensor(to, k.psum[s][1 + t2][:, 0:256].rearrange("p (a n) -> p a n", n=128),
                                               k.weight("l3x_bv"), to, ALU.add, ALU.add)
            ins.then_inc(u.dve.sem, u.dve.one("x", s))
class Attention16:

    def __init__(self, core, sub, masked, scale, values, value_w, value_bias, out_w, out_bias,
                 values_ready, queries_ready):
        self.k, self.sub, self.masked, self.scale = core, sub, masked, scale
        self.values_ready, self.queries_ready = values_ready, queries_ready
        self.values, self.value_w, self.value_bias, self.out_w, self.out_bias = values, value_w, value_bias, out_w, out_bias

    PE = ["v0", "even0", "odd0"] + [
        n for j in range(8)
        for n in ([f"even{j + 1}", f"odd{j + 1}"] if j < 7 else []) + [f"turn{j}"]
        + ([f"back{j - 1}"] if j in (2, 4, 6) else []) + ([f"v{j + 1}"] if j in (1, 3, 5) else []) + [f"pv{j}"]] + ["back7", "wo"]
    ACT = ["vs0", "exp0"] + [
        n for j in range(8)
        for n in [f"probs{j}"] + ([f"outs{j - 1}"] if j in (2, 4, 6) else []) + ([f"exp{j + 1}"] if j < 7 else [])
        + ([f"vs{j + 1}"] if j in (1, 3, 5) else [])] + ["outs7"]

    POOL = ["spread0", "spread1", "spread2", "spread3"]

    @staticmethod
    def dve_steps(masked):
        soft = lambda j: ([f"fill{j}"] if masked else []) + [f"max{j}", f"sub{j}"]
        return soft(0) + [n for j in range(8) for n in ([f"recip{j - 1}", f"out{j - 1}"] if j else [])
                                       + (soft(j + 1) if j < 7 else [])] + ["recip7", "out7", "x"]

    def exps(self, s, j):
        return self.k.b("t15" if j % 2 else "t11", s)

    def pe_scores(self, eng, j):
        k, u = self.k, self.sub
        t, half = j // 2, j % 2
        for odd, name in enumerate(("even", "odd")):
            g = 2 * half + odd
            rows = slice(32 * g, 32 * g + 32)
            for s in S:
                if odd:
                    eng.wait_ge(u.pe.sem, u.pe.at(f"even{j}", s))
                else:
                    eng.wait_ge(u.gps.sem, u.gps.at(f"spread{t}", s))
                if j and not odd:
                    eng.wait_ge(u.dve.sem, u.dve.at(f"fill{j - 1}" if self.masked else f"sub{j - 1}", s))
                for b in range(2):
                    at = t * 128 + b * T
                    mm = eng.matmul(k.psum[s][0][b * T:(b + 1) * T, odd * 256:odd * 256 + 256], k.b("t5", s, rows)[:, at:at + T],
                                    k.wide(s, 7, 4, rows)[:, (2 * t + b) * 256:(2 * t + b + 1) * 256],
                                    start=True, stop=True, tile_position=(32 * g, 64 * b))
                mm.then_inc(u.pe.sem, u.pe.one(f"{name}{j}", s))

    def pe_values(self, eng, j):
        k, u = self.k, self.sub
        vw = k.weight(self.value_w[0])[:, self.value_w[1]:self.value_w[1] + D].rearrange("p (q o c) -> p q o c", o=2, c=8)
        for s in S:
            if j >= 4:
                eng.wait_ge(u.act.sem, u.act.at(f"outs{j - 3}", s))
            elif j:
                eng.wait_ge(u.act.sem, u.act.at("vs0", s))
            else:
                self.values_ready(eng, s)
            for b in range(2):
                at = (j // 2) * 128 + b * T
                for h2 in range(2):
                    mm = eng.matmul(k.psum[s][3][64 * h2:64 * h2 + 64, b * T:(b + 1) * T],
                                    k.b(self.values, s)[:, at:at + T], vw[:, :, h2, :], start=True, stop=True)
            mm.then_inc(u.pe.sem, u.pe.one(f"v{j}", s))

    def pe_back(self, eng, j):
        k, u = self.k, self.sub
        for s in S:
            eng.wait_ge(u.dve.sem, u.dve.at(f"out{j}", s))
            eng.wait_ge(u.act.sem, u.act.at(f"vs{min(j + 1, 6)}", s))
            eng.transpose(k.psum[s][3][:, 0:128], k.b("t13", s)[:, 0:128], k.const("ident"))\
               .then_inc(u.pe.sem, u.pe.one(f"back{j}", s))

    def pe(self, eng):
        k, u = self.k, self.sub
        self.pe_values(eng, 0)
        for s in S:
            self.queries_ready(eng, s)
        self.pe_scores(eng, 0)
        for j in range(8):
            half = j % 2
            if j < 7:
                self.pe_scores(eng, j + 1)
            for s in S:
                eng.wait_ge(u.act.sem, u.act.at(f"exp{j}", s))
                for p in range(4):
                    mm = eng.transpose(k.psum[s][1][:, p * 128:(p + 1) * 128],
                                       self.exps(s, j)[:, p * 128:(p + 1) * 128], k.const("ident"))
                mm.then_inc(u.pe.sem, u.pe.one(f"turn{j}", s))
            if j in (2, 4, 6):
                self.pe_back(eng, j - 1)
            if j in (1, 3, 5):
                self.pe_values(eng, j + 1)
            for s in S:
                eng.wait_ge(u.act.sem, u.act.at(f"probs{j}", s))
                if j:
                    eng.wait_ge(u.dve.sem, u.dve.at(f"out{j - 1}", s))
                vbd = k.vbd[s].ap().rearrange("p (b q c) -> p b q c", b=2, c=18)
                for p in range(4):
                    for b in range(2):
                        mm = eng.matmul(k.psum[s][2][b * T:(b + 1) * T, half * 72 + p * 18:half * 72 + (p + 1) * 18],
                                        k.b("t12", s)[:, p * 128 + b * T:p * 128 + (b + 1) * T],
                                        vbd[:, b, 4 * half + p, :], start=True, stop=True)
                mm.then_inc(u.pe.sem, u.pe.one(f"pv{j}", s))
        self.pe_back(eng, 7)
        for s in S:
            eng.wait_ge(u.act.sem, u.act.at("outs7", s))
            eng.matmul(k.psum[s][1][:], k.weight(self.out_w), k.b("t14", s), start=True, stop=True)\
               .then_inc(u.pe.sem, u.pe.one("wo", s))

    def act_exp(self, eng, j):
        k, u = self.k, self.sub
        for s in S:
            eng.wait_ge(u.dve.sem, u.dve.at(f"sub{j}", s))
            eng.activation(self.exps(s, j), self.exps(s, j), ACT.Exp, scale=1.0 if self.masked else self.scale)\
               .then_inc(u.act.sem, u.act.one(f"exp{j}", s))

    def act_values(self, eng, j):
        k, u = self.k, self.sub
        for s in S:
            eng.wait_ge(u.pe.sem, u.pe.at(f"v{j}", s))
            if j:
                eng.wait_ge(u.pe.sem, u.pe.at(f"pv{j - 1}", s))
            for h2 in range(2):
                rows = slice(64 * h2, 64 * h2 + 64)
                ins = eng.copy(k.vbd[s][rows, :].rearrange("p (q c) -> p q c", c=18)[:, :, 9 * h2:9 * h2 + 8],
                               k.psum[s][3][rows, 0:128].rearrange("p (q c) -> p q c", c=8))
            ins.then_inc(u.act.sem, u.act.one(f"vs{j}", s))

    def act_outs(self, eng, j):
        k, u = self.k, self.sub
        for s in S:
            eng.wait_ge(u.pe.sem, u.pe.at(f"back{j}", s))
            to = k.b("t14", s)[:, (j // 2) * 128:(j // 2 + 1) * 128]
            if self.value_bias:
                ins = eng.activation(to, k.psum[s][3][:, 0:128], ACT.Identity, bias=k.weight(self.value_bias))
            else:
                ins = eng.copy(to, k.psum[s][3][:, 0:128])
            ins.then_inc(u.act.sem, u.act.one(f"outs{j}", s))

    def act(self, eng):
        k, u = self.k, self.sub
        self.act_values(eng, 0)
        self.act_exp(eng, 0)
        for j in range(8):
            for s in S:
                eng.wait_ge(u.pe.sem, u.pe.at(f"turn{j}", s))
                eng.copy(k.b("t12", s), k.psum[s][1][:]).then_inc(u.act.sem, u.act.one(f"probs{j}", s))
            if j in (2, 4, 6):
                self.act_outs(eng, j - 1)
            if j < 7:
                self.act_exp(eng, j + 1)
            if j in (1, 3, 5):
                self.act_values(eng, j + 1)
        self.act_outs(eng, 7)

    def dve_softmax(self, eng, j):
        k, u = self.k, self.sub
        heads = lambda ap: ap.rearrange("p (h j) -> p h j", j=T)
        if self.masked:
            for s in S:
                eng.wait_ge(u.pe.sem, u.pe.at(f"odd{j}", s))
                if j >= 2:
                    eng.wait_ge(u.pe.sem, u.pe.at(f"turn{j - 2}", s))
                eng.scalar_tensor_tensor(
                    heads(self.exps(s, j)), heads(k.psum[s][0][:]), self.scale,
                    k.fill0[s][:, (j // 2) * T:(j // 2 + 1) * T].unsqueeze(1).broadcast_to([128, 8, T]), ALU.mult, ALU.add)\
                   .then_inc(u.dve.sem, u.dve.one(f"fill{j}", s))
        scores = lambda s: self.exps(s, j) if self.masked else k.psum[s][0][:]
        for s in S:
            if self.masked:
                eng.wait_ge(u.dve.sem, u.dve.at(f"fill{j}", s))
            else:
                eng.wait_ge(u.pe.sem, u.pe.at(f"odd{j}", s))
                if j:
                    eng.wait_ge(u.dve.sem, u.dve.at(f"sub{j - 1}", s))
            eng.tensor_reduce(k.small[s][:, 0:8], heads(scores(s)), AX.X, ALU.max)\
               .then_inc(u.dve.sem, u.dve.one(f"max{j}", s))
        for s in S:
            eng.wait_ge(u.dve.sem, u.dve.at(f"max{j}", s))
            if j >= 2:
                eng.wait_ge(u.pe.sem, u.pe.at(f"turn{j - 2}", s))
            eng.tensor_tensor(heads(self.exps(s, j)), heads(scores(s)),
                              k.small[s][:, 0:8].unsqueeze(2).broadcast_to([128, 8, T]), ALU.subtract)\
               .then_inc(u.dve.sem, u.dve.one(f"sub{j}", s))

    def dve_outputs(self, eng, j):
        k, u = self.k, self.sub
        half = j % 2
        outs = lambda s: k.psum[s][2][:, half * 72:half * 72 + 72].rearrange("p (h c) -> p h c", c=9)
        for s in S:
            eng.wait_ge(u.pe.sem, u.pe.at(f"pv{j}", s))
            eng.reciprocal(k.small[s][:, 8:16], outs(s)[:, :, 8]).then_inc(u.dve.sem, u.dve.one(f"recip{j}", s))
        for s in S:
            eng.wait_ge(u.dve.sem, u.dve.at(f"recip{j}", s))
            eng.tensor_tensor(k.b("t13", s)[:, half * T:half * T + T].rearrange("p (h c) -> p h c", c=8),
                              outs(s)[:, :, 0:8], k.small[s][:, 8:16].unsqueeze(2).broadcast_to([128, 8, 8]), ALU.mult)\
               .then_inc(u.dve.sem, u.dve.one(f"out{j}", s))

    def pool(self, eng, keys_ready):
        k, u = self.k, self.sub
        for t in range(NT):
            for s in S:
                if t == 0:
                    keys_ready(eng, s)
                eng.tensor_tensor(k.b(f"t{7 + t}", s).rearrange("p (b h j) -> p b h j", h=4, j=T),
                                  per_batch(k.b("t6", s))[:, 2 * t:2 * t + 2].unsqueeze(2).broadcast_to([128, 2, 4, T]),
                                  k.const("head4").unsqueeze(1).unsqueeze(3).broadcast_to([128, 2, 4, T]), ALU.mult)\
                   .then_inc(u.gps.sem, u.gps.one(f"spread{t}", s))

    def dve(self, eng):
        k, u = self.k, self.sub
        self.dve_softmax(eng, 0)
        for j in range(8):
            if j:
                self.dve_outputs(eng, j - 1)
            if j < 7:
                self.dve_softmax(eng, j + 1)
        self.dve_outputs(eng, 7)
        for s in S:
            eng.wait_ge(u.pe.sem, u.pe.at("wo", s))
            eng.scalar_tensor_tensor(k.b("x", s), k.psum[s][1][:], k.weight(self.out_bias), k.b("x", s), ALU.add, ALU.add)\
               .then_inc(u.dve.sem, u.dve.one("x", s))


class L2Xattn(Sub):

    def __init__(self, core, prev):
        super().__init__(core, prev)
        self.pe = core.steps("l2x_pe", ["centre", "k", "var", "q", *Attention16.PE])
        self.act = core.steps("l2x_act", [*TwiceNorm.ACT, "qs", *Attention16.ACT])
        self.dve = core.steps("l2x_dve", ["ks", *TwiceNorm.DVE, *Attention16.dve_steps(True)])
        self.gps = core.steps("l2x_pool", ["masked", "keymask", "fill", "kvn", *Attention16.POOL])
        self.norm = TwiceNorm(core, self, "l2x_gx", "l2x_bx")
        self.att = Attention16(core, self, True, 8 ** -0.5, "t4", ("l2x_wkv", D), None, "l2x_wo", "l2x_bo",
                               lambda eng, s: None, lambda eng, s: eng.wait_ge(self.act.sem, self.act.at("qs", s)))

    def pe_program(self, eng):
        k, u = self.k, self
        self.norm.pe_centre(eng)
        for s in S:
            eng.wait_ge(u.gps.sem, u.gps.at("kvn", s))
            eng.matmul(k.psum[s][2][:], k.weight("l2x_wkv")[:, 0:D], k.b("t4", s), start=True, stop=True)\
               .then_inc(u.pe.sem, u.pe.one("k", s))
        self.norm.pe_var(eng)
        for s in S:
            eng.wait_ge(u.dve.sem, u.dve.at("latb", s))
            eng.matmul(k.psum[s][0][:], k.weight("l2x_wq"), k.b("t3", s), start=True, stop=True)\
               .then_inc(u.pe.sem, u.pe.one("q", s))
        self.att.pe(eng)

    def act_program(self, eng):
        k, u = self.k, self
        self.norm.act(eng)
        for s in S:
            eng.wait_ge(u.pe.sem, u.pe.at("q", s))
            eng.copy(k.b("t5", s), k.psum[s][0][:]).then_inc(u.act.sem, u.act.one("qs", s))
        self.att.act(eng)

    def pool_program(self, eng):
        k, u = self.k, self
        for s in S:
            eng.wait_ge(k.mask_in[s], 80)
            eng.tensor_scalar(k.keymask[s][:], k.keymask[s][:].bitcast(I32), 0.0, -1.0, ALU.is_equal, ALU.mult)\
               .then_inc(u.gps.sem, u.gps.one("masked", s))
        for s in S:
            eng.wait_ge(u.gps.sem, u.gps.at("masked", s))
            eng.tensor_scalar(k.keymask[s][:], k.keymask[s][:], 1.0, None, ALU.add)\
               .then_inc(u.gps.sem, u.gps.one("keymask", s))
        for s in S:
            eng.tensor_scalar(k.fill0[s][:], k.fill0[s][:].bitcast(I32), 0.0, -1e9, ALU.is_equal, ALU.mult)\
               .then_inc(u.gps.sem, u.gps.one("fill", s))
        for s in S:
            u.input_ready(eng, s)
            eng.tensor_scalar(k.b("t4", s), k.b("cn", s), k.weight("l2x_gkv"), k.weight("l2x_bkv"),
                              ALU.mult, ALU.add).then_inc(u.gps.sem, u.gps.one("kvn", s))
        self.att.pool(eng, lambda eng, s: eng.wait_ge(u.dve.sem, u.dve.at("ks", s)))

    def dve_program(self, eng):
        k, u = self.k, self
        for s in S:
            eng.wait_ge(u.pe.sem, u.pe.at("k", s))
            eng.wait_ge(u.gps.sem, u.gps.at("keymask", s))
            eng.tensor_tensor(k.b("t6", s), k.psum[s][2][:], k.keymask[s][:], ALU.mult)\
               .then_inc(u.dve.sem, u.dve.one("ks", s))
        self.norm.dve(eng)
        for s in S:
            eng.wait_ge(u.gps.sem, u.gps.at("fill", s))
        self.att.dve(eng)


class L3Attn(Sub):

    def __init__(self, core, prev):
        super().__init__(core, prev)
        self.pe = core.steps("l3a_pe", [*Norm.PE, "k", "kr", "q", "qr", *Attention16.PE])
        self.act = core.steps("l3a_act", [*Norm.ACT, *Attention16.ACT])
        self.dve = core.steps("l3a_dve", [*Norm.DVE, "kc", "ks", "krope", "qc", "qs", "qrope", *Attention16.dve_steps(False)])
        self.gps = core.steps("l3a_pool", Attention16.POOL)
        self.norm = Norm(core, self)
        self.att = Attention16(core, self, False, 8 ** -0.5, "h", ("l3a_wv", 0), "l3a_bv", "l3a_wo", "l3a_bo",
                               lambda eng, s: eng.wait_ge(self.dve.sem, self.dve.at("ks", s)),
                               lambda eng, s: eng.wait_ge(self.dve.sem, self.dve.at("qrope", s)))

    def pe_program(self, eng):
        k, u = self.k, self
        self.norm.pe(eng)
        for bank, name, w in ((2, "k", k.weight("l3a_wk")), (3, "kr", k.rotated[:, D:2 * D]), (0, "q", k.weight("l3a_wq")),
                              (1, "qr", k.rotated[:, 0:D])):
            for s in S:
                if name == "k":
                    eng.wait_ge(u.dve.sem, u.dve.at("h", s))
                eng.matmul(k.psum[s][bank][:], w, k.b("h", s), start=True, stop=True)\
                   .then_inc(u.pe.sem, u.pe.one(name, s))
        self.att.pe(eng)

    def act_program(self, eng):
        self.norm.act(eng)
        self.att.act(eng)

    def dve_program(self, eng):
        k, u = self.k, self
        self.norm.dve(eng)
        over = lambda table: k.const(table).unsqueeze(1).broadcast_to([128, NB, T])
        for bank, a, out, part, bias, rbias in ((2, "k", "t6", "t4", "l3a_bk", 1), (0, "q", "t5", "t3", "l3a_bq", 0)):
            for s in S:
                eng.wait_ge(u.pe.sem, u.pe.at(a, s))
                eng.scalar_tensor_tensor(per_batch(k.b(out, s)), per_batch(k.psum[s][bank][:]), k.weight(bias),
                                         over("rcos"), ALU.add, ALU.mult).then_inc(u.dve.sem, u.dve.one(a + "c", s))
            for s in S:
                eng.wait_ge(u.pe.sem, u.pe.at(a + "r", s))
                eng.scalar_tensor_tensor(per_batch(k.b(part, s)), per_batch(k.psum[s][bank + 1][:]),
                                         k.rot_bias[:, rbias:rbias + 1], over("rsin"), ALU.add, ALU.mult)\
                   .then_inc(u.dve.sem, u.dve.one(a + "s", s))
            for s in S:
                eng.wait_ge(u.dve.sem, u.dve.at(a + "s", s))
                eng.tensor_tensor(k.b(out, s), k.b(out, s), k.b(part, s), ALU.add)\
                   .then_inc(u.dve.sem, u.dve.one(a + "rope", s))
        self.att.dve(eng)

    def pool_program(self, eng):
        k, u = self.k, self
        self.att.pool(eng, lambda eng, s: eng.wait_ge(u.dve.sem, u.dve.at("krope", s)))


class L2Attn(Sub):

    ROPE = ["q0", "q1", "q2", "q3", "k", "ks"]
    BESIDE = ["k0", "k1", "k2", "k3", "q0", "q1"]

    def __init__(self, core, prev):
        super().__init__(core, prev)
        pe, act, dve = [*Norm.PE, "ckv", "cq"], [*Norm.ACT, "ckv", "cq"], [*Norm.DVE]
        for n, beside in zip(self.ROPE, self.BESIDE):
            pe += ["r_" + n, beside]
            act += [f"abs_{n}", f"exp_{n}", f"ln_{n}"] + ([beside] if beside[0] == "q" else [])
            dve += [f"mu_{n}", f"rot_{n}"] + ([beside] if beside[0] == "k" else [])
        pe += ["q2", "q3", "v0", "even0", "odd0"]
        act += ["q2", "q3", "vs0", "exp0"]
        dve += ["kr", "max0", "sub0"]
        for t in range(4):
            before, more = t > 0, t < 3
            pe += ([f"even{t + 1}", f"odd{t + 1}"] if more else []) + ([f"back{t - 1}"] if before else [])
            pe += [f"turn{t}"] + ([f"v{t + 1}"] if more else []) + [f"pv{t}"]
            act += ([f"outs{t - 1}"] if before else []) + [f"probs{t}"] + ([f"vs{t + 1}", f"exp{t + 1}"] if more else [])
            dve += ([f"recip{t - 1}", f"out{t - 1}"] if before else []) + ([f"max{t + 1}", f"sub{t + 1}"] if more else [])
        self.pe = core.steps("l2a_pe", pe + ["back3", "wo"])
        self.act = core.steps("l2a_act", act + ["outs3"])
        self.dve = core.steps("l2a_dve", dve + ["recip3", "out3", "x"])
        self.norm = Norm(core, self)

    QR = ("t0", "t1", "t13", "t14")
    PART = (*QR, "t15", "t8")

    def exps(self, s, t):
        return self.k.b("h" if t % 2 else "t15", s)

    def values(self, s, t):
        return self.k.vb[s][:, t % 2 * 520:(t % 2 + 1) * 520].rearrange("p (b q c) -> p b q c", b=2, c=65)

    def ckv(self, s):
        return self.k.b("t2", s, slice(0, 32))

    def cq(self, s):
        return self.k.b("t3", s, slice(0, 64))

    def pe_projection(self, eng, name):
        k, u = self.k, self
        p = int(name[1])
        for s in S:
            if name in ("k2", "k3"):
                eng.wait_ge(u.dve.sem, u.dve.at(f"k{p - 2}", s))
            elif name in ("q0", "q1"):
                eng.wait_ge(u.dve.sem, u.dve.at(f"k{p + 2}", s))
            elif name in ("q2", "q3"):
                eng.wait_ge(u.act.sem, u.act.at(f"q{p - 2}", s))
            if name[0] == "k":
                w, src = k.weight("l2a_uk", slice(0, 32)), self.ckv(s)
            else:
                w, src = k.weight("l2a_uq", slice(0, 64)), self.cq(s)
            eng.matmul(k.psum[s][2 + p % 2][:], w[:, p * 128:(p + 1) * 128], src, start=True, stop=True)\
               .then_inc(u.pe.sem, u.pe.one(name, s))

    def pe_values(self, eng, t):
        k, u = self.k, self
        w = k.weight("l2a_uv", slice(0, 32)).rearrange("p (q o c) -> p q o c", o=2, c=64)
        for s in S:
            if t:
                eng.wait_ge(u.act.sem, u.act.at(f"probs{t - 1}", s))
            else:
                eng.wait_ge(u.dve.sem, u.dve.at("mu_ks", s))
            for b in range(2):
                at = t * 128 + b * T
                for h2 in range(2):
                    mm = eng.matmul(k.psum[s][1][64 * h2:64 * h2 + 64, b * 256:(b + 1) * 256], self.ckv(s)[:, at:at + T],
                                    w[:, :, h2, :], start=True, stop=True)
            mm.then_inc(u.pe.sem, u.pe.one(f"v{t}", s))

    def pe_scores(self, eng, t):
        k, u = self.k, self
        for odd, name in enumerate(("even", "odd")):
            half = slice(64 * odd, 64 * odd + 64)
            for s in S:
                if odd:
                    eng.wait_ge(u.pe.sem, u.pe.at(f"even{t}", s))
                elif t:
                    eng.wait_ge(u.dve.sem, u.dve.at(f"sub{t - 1}", s))
                else:
                    eng.wait_ge(u.act.sem, u.act.at("q3", s))
                    eng.wait_ge(u.dve.sem, u.dve.at("kr", s))
                for h in range(odd, 8, 2):
                    for b in range(2):
                        at = t * 128 + b * T
                        out = k.psum[s][0][b * T:(b + 1) * T, h * T:(h + 1) * T]
                        eng.matmul(out, k.b(f"t{5 + h // 2}", s, half)[:, at:at + T],
                                   k.b(f"t{9 + h // 2}", s, half)[:, at:at + T], start=True, stop=False)
                        mm = eng.matmul(out, k.b(self.QR[h // 2], s, half)[:, at:at + T],
                                        k.b("t4", s, half)[:, at:at + T], start=False, stop=True)
                mm.then_inc(u.pe.sem, u.pe.one(f"{name}{t}", s))

    def pe_transposes(self, eng, name, t):
        k, u = self.k, self
        for s in S:
            if name == "turn":
                eng.wait_ge(u.act.sem, u.act.at(f"exp{t}", s))
                eng.wait_ge(u.act.sem, u.act.at(f"outs{t - 1}" if t else "vs0", s))
            else:
                eng.wait_ge(u.dve.sem, u.dve.at(f"out{t}", s))
                eng.wait_ge(u.act.sem, u.act.at(f"vs{t + 1}" if t < 3 else "probs3", s))
            for p in range(4):
                mm = eng.transpose(k.psum[s][1][:, p * 128:(p + 1) * 128],
                                   self.exps(s, t)[:, p * 128:(p + 1) * 128], k.const("ident"))
            mm.then_inc(u.pe.sem, u.pe.one(f"{name}{t}", s))

    def pe_program(self, eng):
        k, u = self.k, self
        self.norm.pe(eng)
        for s in S:
            eng.wait_ge(u.dve.sem, u.dve.at("h", s))
            eng.matmul(k.psum[s][2][0:32, :], k.weight("l2a_dkv"), k.b("h", s), start=True, stop=True)\
               .then_inc(u.pe.sem, u.pe.one("ckv", s))
        for s in S:
            eng.matmul(k.psum[s][3][0:64, :], k.weight("l2a_dq"), k.b("h", s), start=True, stop=True)\
               .then_inc(u.pe.sem, u.pe.one("cq", s))
        for j, n in enumerate(self.ROPE):
            for s in S:
                if j == 0:
                    eng.wait_ge(u.act.sem, u.act.at("cq", s))
                if j >= 2:
                    eng.wait_ge(u.dve.sem, u.dve.at("mu_" + self.ROPE[j - 2], s))
                if j < 4:
                    w = k.weight("l2a_qrq", slice(0, 64))[:, j * 128:(j + 1) * 128]
                    mm = eng.matmul(k.psum[s][j % 2][:], w, self.cq(s), start=True, stop=True)
                else:
                    mm = eng.matmul(k.psum[s][j % 2][:], k.weight(("l2a_kr", "l2a_krs")[j - 4]), k.b("h", s),
                                    start=True, stop=True)
                mm.then_inc(u.pe.sem, u.pe.one("r_" + n, s))
            self.pe_projection(eng, self.BESIDE[j])
        self.pe_projection(eng, "q2")
        self.pe_projection(eng, "q3")
        self.pe_values(eng, 0)
        self.pe_scores(eng, 0)
        for t in range(4):
            if t < 3:
                self.pe_scores(eng, t + 1)
            if t:
                self.pe_transposes(eng, "back", t - 1)
            self.pe_transposes(eng, "turn", t)
            if t < 3:
                self.pe_values(eng, t + 1)
            for s in S:
                eng.wait_ge(u.act.sem, u.act.at(f"probs{t}", s))
                if t:
                    eng.wait_ge(u.dve.sem, u.dve.at(f"out{t - 1}", s))
                for h in range(8):
                    half = slice(64 * (h % 2), 64 * (h % 2) + 64)
                    for b in range(2):
                        mm = eng.matmul(k.psum[s][2 + h % 2][b * T:(b + 1) * T, h // 2 * 65:(h // 2 + 1) * 65],
                                        k.b("t3", s, half)[:, h // 2 * 128 + b * T:h // 2 * 128 + (b + 1) * T],
                                        self.values(s, t)[half, b, h // 2, :], start=True, stop=True)
                mm.then_inc(u.pe.sem, u.pe.one(f"pv{t}", s))
        self.pe_transposes(eng, "back", 3)
        for s in S:
            eng.wait_ge(u.act.sem, u.act.at("outs3", s))
            for p in range(4):
                mm = eng.matmul(k.psum[s][0][:], k.weight("l2a_out")[:, p * 128:(p + 1) * 128], k.b(f"t{5 + p}", s),
                                start=p == 0, stop=p == 3)
            mm.then_inc(u.pe.sem, u.pe.one("wo", s))

    def act_query(self, eng, p):
        k, u = self.k, self
        for s in S:
            eng.wait_ge(u.pe.sem, u.pe.at(f"q{p}", s))
            if p == 3:
                eng.wait_ge(u.dve.sem, u.dve.at("kr", s))
            eng.copy(k.b(f"t{5 + p}", s), k.psum[s][2 + p % 2][:]).then_inc(u.act.sem, u.act.one(f"q{p}", s))

    def act_values(self, eng, t):
        k, u = self.k, self
        for s in S:
            eng.wait_ge(u.pe.sem, u.pe.at(f"v{t}", s))
            eng.copy(k.vb[s][:, t % 2 * 520:(t % 2 + 1) * 520].rearrange("p (h c) -> p h c", c=65)[:, :, 0:64],
                     k.psum[s][1][:].rearrange("p (h c) -> p h c", c=64)).then_inc(u.act.sem, u.act.one(f"vs{t}", s))

    def act_exp(self, eng, t):
        k, u = self.k, self
        for s in S:
            eng.wait_ge(u.dve.sem, u.dve.at(f"sub{t}", s))
            eng.activation(self.exps(s, t), self.exps(s, t), ACT.Exp, scale=96 ** -0.5)\
               .then_inc(u.act.sem, u.act.one(f"exp{t}", s))

    def act_outs(self, eng, t):
        k, u = self.k, self
        for s in S:
            eng.wait_ge(u.pe.sem, u.pe.at(f"back{t}", s))
            eng.copy(k.wide(s, 5, 4).rearrange("p (q n) -> p q n", n=G)[:, :, t * 128:(t + 1) * 128],
                     k.psum[s][1][:].rearrange("p (q n) -> p q n", n=128)).then_inc(u.act.sem, u.act.one(f"outs{t}", s))

    def act_program(self, eng):
        k, u = self.k, self
        self.norm.act(eng)
        for s in S:
            eng.wait_ge(u.pe.sem, u.pe.at("ckv", s))
            eng.copy(self.ckv(s), k.psum[s][2][0:32, :]).then_inc(u.act.sem, u.act.one("ckv", s))
        for s in S:
            eng.wait_ge(u.pe.sem, u.pe.at("cq", s))
            eng.copy(self.cq(s), k.psum[s][3][0:64, :]).then_inc(u.act.sem, u.act.one("cq", s))
        for j, n in enumerate(self.ROPE):
            part = self.PART[j]
            for s in S:
                eng.wait_ge(u.pe.sem, u.pe.at("r_" + n, s))
                eng.wait_ge(u.dve.sem, u.dve.at("h", s))
                eng.activation(k.b(part, s), k.psum[s][j % 2][:], ACT.Abs).then_inc(u.act.sem, u.act.one("abs_" + n, s))
            for s in S:
                eng.wait_ge(u.act.sem, u.act.at("abs_" + n, s))
                eng.activation(k.b(part, s), k.b(part, s), ACT.Exp, scale=-1.0).then_inc(u.act.sem, u.act.one("exp_" + n, s))
            for s in S:
                eng.wait_ge(u.act.sem, u.act.at("exp_" + n, s))
                eng.activation(k.b(part, s), k.b(part, s), ACT.Ln, bias=1.0).then_inc(u.act.sem, u.act.one("ln_" + n, s))
            if j >= 4:
                self.act_query(eng, j - 4)
        self.act_query(eng, 2)
        self.act_query(eng, 3)
        self.act_values(eng, 0)
        self.act_exp(eng, 0)
        for t in range(4):
            if t:
                self.act_outs(eng, t - 1)
            for s in S:
                eng.wait_ge(u.pe.sem, u.pe.at(f"turn{t}", s))
                eng.copy(k.b("t3", s), k.psum[s][1][:]).then_inc(u.act.sem, u.act.one(f"probs{t}", s))
            if t < 3:
                self.act_values(eng, t + 1)
                self.act_exp(eng, t + 1)
        self.act_outs(eng, 3)

    def dve_softmax(self, eng, t):
        k, u = self.k, self
        heads = lambda ap: ap.rearrange("p (h j) -> p h j", j=T)
        for s in S:
            eng.wait_ge(u.pe.sem, u.pe.at(f"odd{t}", s))
            if t:
                eng.wait_ge(u.dve.sem, u.dve.at(f"sub{t - 1}", s))
            eng.tensor_reduce(k.small[s][:, 0:8], heads(k.psum[s][0][:]), AX.X, ALU.max)\
               .then_inc(u.dve.sem, u.dve.one(f"max{t}", s))
        for s in S:
            eng.wait_ge(u.dve.sem, u.dve.at(f"max{t}", s))
            if t >= 2:
                eng.wait_ge(u.pe.sem, u.pe.at(f"back{t - 2}", s))
            eng.tensor_tensor(heads(self.exps(s, t)), heads(k.psum[s][0][:]),
                              k.small[s][:, 0:8].unsqueeze(2).broadcast_to([128, 8, T]), ALU.subtract)\
               .then_inc(u.dve.sem, u.dve.one(f"sub{t}", s))

    def dve_outputs(self, eng, t):
        k, u = self.k, self
        recips = lambda s, c: k.small[s][:, 8 + 4 * c:12 + 4 * c]
        outs = lambda s, c: k.psum[s][2 + c][:, 0:260].rearrange("p (q c) -> p q c", c=65)
        mine = lambda s, c: self.exps(s, t).rearrange("p (q o j) -> p q o j", o=2, j=T)[:, :, c, :]
        for s in S:
            eng.wait_ge(u.pe.sem, u.pe.at(f"pv{t}", s))
            for c in range(2):
                ins = eng.reciprocal(recips(s, c), outs(s, c)[:, :, 64])
            ins.then_inc(u.dve.sem, u.dve.one(f"recip{t}", s))
        for s in S:
            eng.wait_ge(u.dve.sem, u.dve.at(f"recip{t}", s))
            for c in range(2):
                ins = eng.tensor_tensor(mine(s, c), outs(s, c)[:, :, 0:64],
                                        recips(s, c).unsqueeze(2).broadcast_to([128, 4, T]), ALU.mult)
            ins.then_inc(u.dve.sem, u.dve.one(f"out{t}", s))

    def dve_program(self, eng):
        k, u = self.k, self
        self.norm.dve(eng)
        over = lambda table: table.unsqueeze(1).broadcast_to([128, NB, T])
        for j, n in enumerate(self.ROPE):
            part = self.PART[j]
            table = k.pope[:, 0:T] if j < 4 else k.pope[:, (j - 3) * T:(j - 2) * T]
            for s in S:
                eng.wait_ge(u.act.sem, u.act.at("ln_" + n, s))
                eng.scalar_tensor_tensor(k.b(part, s), k.psum[s][j % 2][:], 0.0, k.b(part, s), ALU.max, ALU.add)\
                   .then_inc(u.dve.sem, u.dve.one("mu_" + n, s))
            for s in S:
                eng.wait_ge(u.dve.sem, u.dve.at("mu_" + n, s))
                eng.tensor_tensor(per_batch(k.b(part, s)), per_batch(k.b(part, s)), over(table), ALU.mult)\
                   .then_inc(u.dve.sem, u.dve.one("rot_" + n, s))
            if j < 4:
                for s in S:
                    eng.wait_ge(u.pe.sem, u.pe.at(f"k{j}", s))
                    eng.tensor_copy(k.b(f"t{9 + j}", s), k.psum[s][2 + j % 2][:])\
                       .then_inc(u.dve.sem, u.dve.one(f"k{j}", s))
        for s in S:
            eng.wait_ge(u.dve.sem, u.dve.at("rot_ks", s))
            eng.tensor_tensor(k.b("t4", s), k.b("t15", s), k.b("t8", s), ALU.add).then_inc(u.dve.sem, u.dve.one("kr", s))
        self.dve_softmax(eng, 0)
        for t in range(4):
            if t:
                self.dve_outputs(eng, t - 1)
            if t < 3:
                self.dve_softmax(eng, t + 1)
        self.dve_outputs(eng, 3)
        for s in S:
            eng.wait_ge(u.pe.sem, u.pe.at("wo", s))
            eng.tensor_tensor(k.b("x", s), k.psum[s][0][:], k.b("x", s), ALU.add).then_inc(u.dve.sem, u.dve.one("x", s))


class L1Attn(Sub):

    PAIRS = 16

    def __init__(self, core, prev):
        super().__init__(core, prev)
        five = range(5)
        n = range(self.PAIRS)
        self.pe = core.steps("l1a_pe", [*Norm.PE, "w1", "x0", "x0e"] + [f"mu{j}" for j in five]
                             + ["r", "ww1", "k", "ww2", "v", "g", "bonus"]
                             + [a for j in range(17) for a in ([f"vb{j}"] if j < 16 else []) + ([f"os{j - 1}"] if j else [])]
                             + [*GroupNorm.PE, "y"])
        self.act = core.steps("l1a_act", [*Norm.ACT, "w1", "x1", "x1e", "r", "ww1", "ks", "ew", "wd", "vs", "silu", *GroupNorm.ACT])
        self.dve = core.steps("l1a_dve", [*Norm.DVE, "delta", "delta0", "lerp"] + [f"{a}{j}" for j in five for a in ("m", "in")]
                              + ["zeros", "ksh", "rbk", "xv", "bv"] + [f"{a}{j}" for j in n for a in ("kv", "scan", "rt")]
                              + ["o", "gn+gnw+gated", "x"])
        self.norm = Norm(core, self)
        self.gn = GroupNorm(core, self, "t6", lambda eng, s: eng.wait_ge(self.dve.sem, self.dve.at("o", s)))

    def pe_program(self, eng):
        k, u = self.k, self
        self.norm.pe(eng)
        low = slice(0, 32)
        for s in S:
            eng.wait_ge(u.dve.sem, u.dve.at("lerp", s))
            eng.matmul(k.psum[s][2][0:32, :], k.weight("l1a_w1"), k.b("t3", s), start=True, stop=True)\
               .then_inc(u.pe.sem, u.pe.one("w1", s))
        for s in S:
            eng.wait_ge(u.act.sem, u.act.at("w1", s))
            eng.matmul(k.psum[s][0][:], k.weight("l1a_w2", low)[:, 0:128], k.b("t4", s, low), start=True, stop=True)\
               .then_inc(u.pe.sem, u.pe.one("x0", s))
        for s in S:
            eng.matmul(k.psum[s][1][0:32, :], k.weight("l1a_w2", low)[:, 128:160], k.b("t4", s, low), start=True, stop=True)\
               .then_inc(u.pe.sem, u.pe.one("x0e", s))
        for j in range(5):
            for s in S:
                if j == 0:
                    eng.wait_ge(u.act.sem, u.act.at("x1e", s))
                if j >= 2:
                    eng.wait_ge(u.dve.sem, u.dve.at(f"m{j - 2}", s))
                rows = slice(32 * j, 32 * j + 32) if j < 4 else low
                w, x1 = (k.weight("l1a_xo", rows), k.b("t5", s, rows)) if j < 4 else (k.weight("l1a_xoe", low), k.b("t6", s, low))
                eng.matmul(k.psum[s][j % 2][:], w, x1, start=True, stop=True).then_inc(u.pe.sem, u.pe.one(f"mu{j}", s))
        for name, bank, w, x, ready in (("r", 2, "l1a_r", "t7", "in0"), ("ww1", 3, "l1a_ww1", "t8", "in1"),
                                        ("k", 1, "l1a_k", "t9", "in2"), ("ww2", 0, None, None, None),
                                        ("v", 2, "l1a_v", "t10", "in3"), ("g", 3, "l1a_g", "t11", "in4")):
            for s in S:
                if name == "ww2":
                    eng.wait_ge(u.act.sem, u.act.at("ww1", s))
                    eng.wait_ge(u.dve.sem, u.dve.at("in4", s))
                    mm = eng.matmul(k.psum[s][0][:], k.weight("l1a_ww2", slice(0, 64)), k.b("t4", s, slice(0, 64)),
                                    start=True, stop=True)
                else:
                    eng.wait_ge(u.dve.sem, u.dve.at(ready, s))
                    if name == "k":
                        eng.wait_ge(u.dve.sem, u.dve.at("m3", s))
                    if name in "vg":
                        eng.wait_ge(u.act.sem, u.act.at("ww1", s))
                    out = k.psum[s][bank][0:64, :] if name == "ww1" else k.psum[s][bank][:]
                    mm = eng.matmul(out, k.weight(w), k.b(x, s), start=True, stop=True)
                mm.then_inc(u.pe.sem, u.pe.one(name, s))
        for s in S:
            eng.wait_ge(u.dve.sem, u.dve.at("rbk", s))
            eng.wait_ge(u.act.sem, u.act.at("wd", s))
            eng.matmul(k.psum[s][0][:], k.const("bonus_sum", slice(0, 64)), k.b("t14", s, slice(0, 64)),
                       start=True, stop=True).then_inc(u.pe.sem, u.pe.one("bonus", s))
        for j in range(self.PAIRS + 1):
            if j < self.PAIRS:
                for s in S:
                    if j < 2:
                        eng.wait_ge(u.dve.sem, u.dve.at("bv", s))
                    else:
                        eng.wait_ge(u.dve.sem, u.dve.at(f"kv{j - 2}", s))
                    eng.matmul(k.psum[s][j % 2][:], k.vexp[:, j * 128:(j + 1) * 128], k.b("t15", s), start=True, stop=True)\
                       .then_inc(u.pe.sem, u.pe.one(f"vb{j}", s))
            if j:
                n = j - 1
                for s in S:
                    eng.wait_ge(u.dve.sem, u.dve.at(f"rt{n}", s))
                    eng.matmul(k.psum[s][2][:], k.const("ksum")[:, 30 - 2 * n:158 - 2 * n], k.b(f"t{4 + n % 2}", s),
                               start=n == 0, stop=n == self.PAIRS - 1).then_inc(u.pe.sem, u.pe.one(f"os{n}", s))
        self.gn.pe(eng)
        for s in S:
            eng.wait_ge(u.dve.sem, u.dve.at("gated", s))
            eng.matmul(k.psum[s][0][:], k.weight("l1a_o"), k.b("t12", s), start=True, stop=True)\
               .then_inc(u.pe.sem, u.pe.one("y", s))

    def act_program(self, eng):
        k, u = self.k, self
        self.norm.act(eng)
        late = lambda name, s: per_batch(k.b(name, s))[:, :, 1:T]
        early = lambda name, s: per_batch(k.b(name, s))[:, :, 0:T - 1]
        for s in S:
            eng.wait_ge(u.pe.sem, u.pe.at("w1", s))
            eng.activation(k.b("t4", s, slice(0, 32)), k.psum[s][2][0:32, :], ACT.Tanh).then_inc(u.act.sem, u.act.one("w1", s))
        for s in S:
            eng.wait_ge(u.pe.sem, u.pe.at("x0", s))
            eng.activation(k.b("t5", s), k.psum[s][0][:], ACT.Tanh, bias=k.weight("l1a_b2")).then_inc(u.act.sem, u.act.one("x1", s))
        for s in S:
            eng.wait_ge(u.pe.sem, u.pe.at("x0e", s))
            eng.activation(k.b("t6", s, slice(0, 32)), k.psum[s][1][0:32, :], ACT.Tanh,
                           bias=k.weight("l1a_b2e", slice(0, 32))).then_inc(u.act.sem, u.act.one("x1e", s))
        for s in S:
            eng.wait_ge(u.pe.sem, u.pe.at("r", s))
            eng.copy(k.b("t3", s), k.psum[s][2][:]).then_inc(u.act.sem, u.act.one("r", s))
        for s in S:
            eng.wait_ge(u.pe.sem, u.pe.at("ww1", s))
            eng.activation(k.b("t4", s, slice(0, 64)), k.psum[s][3][0:64, :], ACT.Tanh).then_inc(u.act.sem, u.act.one("ww1", s))
        for s in S:
            eng.wait_ge(u.pe.sem, u.pe.at("k", s))
            eng.copy(k.b("t9", s), k.psum[s][1][:]).then_inc(u.act.sem, u.act.one("ks", s))
        for s in S:
            eng.wait_ge(u.pe.sem, u.pe.at("ww2", s))
            eng.activation(k.b("t8", s), k.psum[s][0][:], ACT.Exp, bias=k.weight("l1a_wb")).then_inc(u.act.sem, u.act.one("ew", s))
        for s in S:
            eng.wait_ge(u.act.sem, u.act.at("ew", s))
            eng.wait_ge(u.dve.sem, u.dve.at("zeros", s))
            eng.activation(late("t12", s), early("t8", s), ACT.Exp, scale=-1.0).then_inc(u.act.sem, u.act.one("wd", s))
        for s in S:
            eng.wait_ge(u.pe.sem, u.pe.at("v", s))
            eng.wait_ge(u.act.sem, u.act.at("wd", s))
            eng.copy(k.b("t8", s), k.psum[s][2][:]).then_inc(u.act.sem, u.act.one("vs", s))
        for s in S:
            eng.wait_ge(u.pe.sem, u.pe.at("g", s))
            eng.activation(k.b("t11", s), k.psum[s][3][:], ACT.Silu).then_inc(u.act.sem, u.act.one("silu", s))
        log_and_exp_table(eng)
        self.gn.act(eng)

    def dve_program(self, eng):
        k, u = self.k, self
        self.norm.dve(eng)
        late = lambda name, s: per_batch(k.b(name, s))[:, :, 1:T]
        early = lambda name, s: per_batch(k.b(name, s))[:, :, 0:T - 1]
        first = lambda name, s: per_batch(k.b(name, s))[:, :, 0:1]
        for s in S:
            eng.wait_ge(u.dve.sem, u.dve.at("h", s))
            eng.tensor_tensor(late("t2", s), early("h", s), late("h", s), ALU.subtract).then_inc(u.dve.sem, u.dve.one("delta", s))
        for s in S:
            eng.tensor_scalar(first("t2", s), first("h", s), -1.0, None, ALU.mult).then_inc(u.dve.sem, u.dve.one("delta0", s))
        for s in S:
            eng.wait_ge(u.dve.sem, u.dve.at("delta0", s))
            eng.scalar_tensor_tensor(k.b("t3", s), k.b("t2", s), k.weight("l1a_mu"), k.b("h", s), ALU.mult, ALU.add)\
               .then_inc(u.dve.sem, u.dve.one("lerp", s))
        for j in range(5):
            for s in S:
                eng.wait_ge(u.pe.sem, u.pe.at(f"mu{j}", s))
                eng.scalar_tensor_tensor(k.b(f"t{7 + j}", s), k.psum[s][j % 2][:], k.weight("l1a_xb")[:, j:j + 1],
                                         k.b("t2", s), ALU.add, ALU.mult).then_inc(u.dve.sem, u.dve.one(f"m{j}", s))
            for s in S:
                eng.wait_ge(u.dve.sem, u.dve.at(f"m{j}", s))
                eng.tensor_tensor(k.b(f"t{7 + j}", s), k.b(f"t{7 + j}", s), k.b("h", s), ALU.add)\
                   .then_inc(u.dve.sem, u.dve.one(f"in{j}", s))
        for s in S:
            for name in ("t12", "t13", "t15"):
                ins = eng.memset(first(name, s), 0.0)
            ins.then_inc(u.dve.sem, u.dve.one("zeros", s))
        for s in S:
            eng.wait_ge(u.act.sem, u.act.at("ks", s))
            eng.tensor_copy(late("t13", s), early("t9", s)).then_inc(u.dve.sem, u.dve.one("ksh", s))
        for s in S:
            eng.scalar_tensor_tensor(k.b("t14", s), k.b("t3", s), k.weight("l1a_bonus"), k.b("t9", s), ALU.mult, ALU.mult)\
               .then_inc(u.dve.sem, u.dve.one("rbk", s))
        for s in S:
            eng.wait_ge(u.dve.sem, u.dve.at("in3", s))
            eng.tensor_copy(late("t15", s), early("t10", s)).then_inc(u.dve.sem, u.dve.one("xv", s))
        for s in S:
            eng.wait_ge(u.pe.sem, u.pe.at("bonus", s))
            eng.wait_ge(u.act.sem, u.act.at("vs", s))
            eng.tensor_tensor(k.b("t14", s), k.b("t8", s), k.psum[s][0][:], ALU.mult).then_inc(u.dve.sem, u.dve.one("bv", s))
        for j in range(self.PAIRS):
            w = f"t{4 + j % 2}"
            for s in S:
                eng.wait_ge(u.pe.sem, u.pe.at(f"vb{j}", s))
                if j >= 2:
                    eng.wait_ge(u.pe.sem, u.pe.at(f"os{j - 2}", s))
                eng.tensor_tensor(k.b(w, s), k.b("t13", s), k.psum[s][j % 2][:], ALU.mult).then_inc(u.dve.sem, u.dve.one(f"kv{j}", s))
            for s in S:
                eng.wait_ge(u.dve.sem, u.dve.at(f"kv{j}", s))
                eng.tensor_tensor_scan(k.b(w, s), k.b("t12", s), k.b(w, s), 0.0, ALU.mult, ALU.add)\
                   .then_inc(u.dve.sem, u.dve.one(f"scan{j}", s))
            for s in S:
                eng.wait_ge(u.dve.sem, u.dve.at(f"scan{j}", s))
                eng.tensor_tensor(k.b(w, s), k.b(w, s), k.b("t3", s), ALU.mult).then_inc(u.dve.sem, u.dve.one(f"rt{j}", s))
        for s in S:
            eng.wait_ge(u.pe.sem, u.pe.at("os15", s))
            eng.tensor_tensor(k.b("t6", s), k.b("t14", s), k.psum[s][2][:], ALU.add).then_inc(u.dve.sem, u.dve.one("o", s))
        for s in S:
            self.gn.dve_one(eng, s)
            eng.wait_ge(u.dve.sem, u.dve.at("gn", s))
            eng.tensor_scalar(k.b("t12", s), k.b("t12", s), k.weight("l1a_gnw"), k.weight("l1a_gnb"), ALU.mult, ALU.add)\
               .then_inc(u.dve.sem, u.dve.one("gnw", s))
            eng.wait_ge(u.dve.sem, u.dve.at("gnw", s))
            eng.tensor_tensor(k.b("t12", s), k.b("t12", s), k.b("t11", s), ALU.mult).then_inc(u.dve.sem, u.dve.one("gated", s))
        for s in S:
            eng.wait_ge(u.pe.sem, u.pe.at("y", s))
            eng.tensor_tensor(k.b("x", s), k.b("x", s), k.psum[s][0][:], ALU.add).then_inc(u.dve.sem, u.dve.one("x", s))


def add_expert(k, u, gate, eng, e, product, bank):
    for s in S:
        eng.wait_ge(u.pe.sem, u.pe.at(product, s))
        if e:
            eng.wait_ge(u.dve.sem, u.dve.at(f"acc{e - 1}", s))
        for t in range(NT):
            to, weight = k.b("t5", s)[:, t * 128:(t + 1) * 128], gate.g(s, 8)[:, t * 8 + e:t * 8 + e + 1]
            out = k.psum[s][bank][:, t * 128:(t + 1) * 128]
            if e:
                ins = eng.scalar_tensor_tensor(to, out, weight, to, ALU.mult, ALU.add)
            else:
                ins = eng.tensor_scalar(to, out, weight, None, ALU.mult)
        ins.then_inc(u.dve.sem, u.dve.one(f"acc{e}", s))


class L2Ffn(Sub):

    TILES = (128, 128, 96)

    def __init__(self, core, prev):
        super().__init__(core, prev)
        n = range(24)
        self.pe = core.steps("l2f_pe", [*Norm.PE, *Gate.PE]
                             + [a for i in n for a in [f"u{i}", f"v{i}"] + ([f"d{i // 3 - 1}"] if i % 3 == 0 and i else [])]
                             + ["d7", "back"])
        self.act = core.steps("l2f_act", [*Norm.ACT, *Gate.ACT] + [f"silu{i}" for i in n])
        self.dve = core.steps("l2f_dve", [*Norm.DVE, *Gate.DVE, "wsum", "wrecip", "weights"]
                              + [a for i in n for a in [f"hid{i}"] + ([f"acc{i // 3 - 1}"] if i % 3 == 1 and i > 1 else [])]
                              + ["acc7", "x"])
        self.norm = Norm(core, self)
        self.gate = Gate(core, self, "l2f_gate")

    def hidden(self, s, i, rows):
        return self.k.b(f"t{9 + i % 6}", s, rows)

    def pe_down(self, eng, e):
        k, u = self.k, self
        for s in S:
            eng.wait_ge(u.dve.sem, u.dve.at(f"hid{3 * e + 2}", s))
            if e >= 2:
                eng.wait_ge(u.dve.sem, u.dve.at(f"acc{e - 2}", s))
            for t in range(NT):
                for c, m in enumerate(self.TILES):
                    rows, at = slice(0, m), (3 * e + c) * 128
                    mm = eng.matmul(k.psum[s][2 + e % 2][:, t * 128:(t + 1) * 128],
                                    self.hidden(s, 3 * e + c, rows)[:, t * 128:(t + 1) * 128],
                                    k.weight("l2f_w2", rows)[:, at:at + 128], start=c == 0, stop=c == 2)
            mm.then_inc(u.pe.sem, u.pe.one(f"d{e}", s))

    def pe_program(self, eng):
        k, u = self.k, self
        self.norm.pe(eng)
        eng.wait_ge(k.moe_in[1], 16)
        self.gate.pe(eng)
        for i in range(24):
            e, c = divmod(i, 3)
            m = self.TILES[c]
            for bank, name, w in ((0, "u", "l2f_w1"), (1, "v", "l2f_w3")):
                for s in S:
                    if i:
                        q, step = (u.dve, f"hid{i - 1}") if bank else (u.act, f"silu{i - 1}")
                        eng.wait_ge(q.sem, q.at(step, s))
                    eng.matmul(k.psum[s][bank][0:m, :], k.weight(w)[:, e * 352 + c * 128:e * 352 + c * 128 + m],
                               k.b("h", s), start=True, stop=True).then_inc(u.pe.sem, u.pe.one(f"{name}{i}", s))
            if c == 0 and e:
                self.pe_down(eng, e - 1)
        self.pe_down(eng, 7)
        for s in S:
            eng.wait_ge(u.dve.sem, u.dve.at("acc7", s))
            for t in range(NT):
                mm = eng.transpose(k.psum[s][0][:, t * 128:(t + 1) * 128], k.b("t5", s)[:, t * 128:(t + 1) * 128],
                                   k.const("ident"))
            mm.then_inc(u.pe.sem, u.pe.one("back", s))

    def act_program(self, eng):
        k, u = self.k, self
        self.norm.act(eng)
        self.gate.act(eng)
        for i in range(24):
            rows = slice(0, self.TILES[i % 3])
            for s in S:
                eng.wait_ge(u.pe.sem, u.pe.at(f"u{i}", s))
                if i >= 2:
                    eng.wait_ge(u.dve.sem, u.dve.at(f"hid{i - 2}", s))
                eng.activation(k.b(f"t{7 + i % 2}", s, rows), k.psum[s][0][rows, :], ACT.Silu)\
                   .then_inc(u.act.sem, u.act.one(f"silu{i}", s))
        log_and_exp_table(eng)

    def dve_program(self, eng):
        k, u = self.k, self
        self.norm.dve(eng)
        self.gate.dve(eng)
        g8 = lambda s: self.gate.g(s, 8).rearrange("p (t e) -> p t e", e=8)
        for s in S:
            eng.wait_ge(u.dve.sem, u.dve.at("gate", s))
            eng.tensor_reduce(k.small[s][:, 44:48], g8(s), AX.X, ALU.add).then_inc(u.dve.sem, u.dve.one("wsum", s))
        for s in S:
            eng.wait_ge(u.dve.sem, u.dve.at("wsum", s))
            eng.reciprocal(k.small[s][:, 48:52], k.small[s][:, 44:48]).then_inc(u.dve.sem, u.dve.one("wrecip", s))
        for s in S:
            eng.wait_ge(u.dve.sem, u.dve.at("wrecip", s))
            eng.tensor_tensor(g8(s), g8(s), k.small[s][:, 48:52].unsqueeze(2).broadcast_to([128, NT, 8]), ALU.mult)\
               .then_inc(u.dve.sem, u.dve.one("weights", s))
        for i in range(24):
            rows = slice(0, self.TILES[i % 3])
            for s in S:
                eng.wait_ge(u.pe.sem, u.pe.at(f"v{i}", s))
                eng.wait_ge(u.act.sem, u.act.at(f"silu{i}", s))
                eng.tensor_tensor(self.hidden(s, i, rows), k.b(f"t{7 + i % 2}", s, rows), k.psum[s][1][rows, :],
                                  ALU.mult).then_inc(u.dve.sem, u.dve.one(f"hid{i}", s))
            if i % 3 == 1 and i > 1:
                if i == 4:
                    for s in S:
                        eng.wait_ge(u.dve.sem, u.dve.at("weights", s))
                add_expert(k, u, self.gate, eng, i // 3 - 1, f"d{i // 3 - 1}", 2 + (i // 3 - 1) % 2)
        add_expert(k, u, self.gate, eng, 7, "d7", 3)
        for s in S:
            eng.wait_ge(u.pe.sem, u.pe.at("back", s))
            eng.tensor_tensor(k.b("x", s), k.b("x", s), k.psum[s][0][:], ALU.add).then_inc(u.dve.sem, u.dve.one("x", s))


class L3Ffn(Sub):

    def __init__(self, core, prev):
        super().__init__(core, prev)
        n = range(8)
        self.pe = core.steps("l3f_pe", [*Norm.PE, *Gate.PE, "y0", "y1", "gt"] + [f"y{e}" for e in n[2:]] + ["back"])
        self.act = core.steps("l3f_act", [*Norm.ACT, *Gate.ACT, "gt"])
        self.dve = core.steps("l3f_dve", [*Norm.DVE, *Gate.DVE] + [f"acc{e}" for e in n] + ["x"])
        self.norm = Norm(core, self)
        self.gate = Gate(core, self, "l3f_wr", "l3f_br")

    def pe_program(self, eng):
        k, u = self.k, self
        self.norm.pe(eng)
        self.gate.pe(eng)
        for e in range(8):
            for s in S:
                if e >= 2:
                    eng.wait_ge(u.dve.sem, u.dve.at(f"acc{e - 2}", s))
                for t in range(NT):
                    mm = eng.matmul(k.psum[s][e % 2][:, t * 128:(t + 1) * 128], k.b("h", s)[:, t * 128:(t + 1) * 128],
                                    k.weight("l3f_w")[:, e * 128:(e + 1) * 128], start=True, stop=True)
                mm.then_inc(u.pe.sem, u.pe.one(f"y{e}", s))
            if e == 1:
                for s in S:
                    eng.wait_ge(u.dve.sem, u.dve.at("gate", s))
                    for t in range(NT):
                        mm = eng.transpose(k.psum[s][3][0:8, t * 128:(t + 1) * 128],
                                           self.gate.g(s, 8)[:, t * 8:t * 8 + 8], k.const("ident"))
                    mm.then_inc(u.pe.sem, u.pe.one("gt", s))
        for s in S:
            eng.wait_ge(u.act.sem, u.act.at("gt", s))
            eng.wait_ge(u.dve.sem, u.dve.at("acc7", s))
            for t in range(NT):
                out = k.psum[s][2][:, t * 128:(t + 1) * 128]
                eng.matmul(out, k.weight("l3f_b", slice(0, 8)), k.b("t4", s, slice(0, 8))[:, t * 128:(t + 1) * 128],
                           start=True, stop=False)
                mm = eng.matmul(out, k.b("t5", s)[:, t * 128:(t + 1) * 128], k.const("ident"), start=False, stop=True)
            mm.then_inc(u.pe.sem, u.pe.one("back", s))

    def act_program(self, eng):
        k, u = self.k, self
        self.norm.act(eng)
        self.gate.act(eng)
        for s in S:
            eng.wait_ge(u.pe.sem, u.pe.at("gt", s))
            eng.copy(k.b("t4", s, slice(0, 8)), k.psum[s][3][0:8, :]).then_inc(u.act.sem, u.act.one("gt", s))

    def dve_program(self, eng):
        k, u = self.k, self
        self.norm.dve(eng)
        self.gate.dve(eng)
        for e in range(8):
            if e == 0:
                for s in S:
                    eng.wait_ge(u.dve.sem, u.dve.at("gate", s))
            add_expert(k, u, self.gate, eng, e, f"y{e}", e % 2)
        for s in S:
            eng.wait_ge(u.pe.sem, u.pe.at("back", s))
            eng.tensor_tensor(k.b("x", s), k.b("x", s), k.psum[s][2][:], ALU.add).then_inc(u.dve.sem, u.dve.one("x", s))


class L1Ffn(Sub):

    def __init__(self, core, prev):
        super().__init__(core, prev)
        self.pe = core.steps("l1f_pe", [*Norm.PE, "y"])
        self.act = core.steps("l1f_act", Norm.ACT)
        self.dve = core.steps("l1f_dve", [*Norm.DVE, "x"])
        self.norm = Norm(core, self)

    def pe_program(self, eng):
        k, u = self.k, self
        self.norm.pe(eng)
        for s in S:
            eng.wait_ge(u.dve.sem, u.dve.at("h", s))
            eng.matmul(k.psum[s][2][:], k.ternary[:], k.b("h", s), start=True, stop=True)\
               .then_inc(u.pe.sem, u.pe.one("y", s))

    def act_program(self, eng):
        self.norm.act(eng)

    def dve_program(self, eng):
        k, u = self.k, self
        self.norm.dve(eng)
        for s in S:
            eng.wait_ge(u.pe.sem, u.pe.at("y", s))
            eng.tensor_tensor(k.b("x", s), k.b("x", s), k.psum[s][2][:], ALU.add)\
               .then_inc(u.dve.sem, u.dve.one("x", s))


NTMP = 16


def small(k, ctx):
    t = lambda name, cols, dt=F32: ctx.enter_context(k.nc.sbuf_tensor(name, [128, cols], dt))
    k.eps5, k.ternary, k.scratch = t("eps5", 1), t("ternary", 128), t("scratch", 8)
    k.vb = [t(f"vb{s}", 2 * 8 * 65) for s in S]
    k.vbd = [t(f"vbd{s}", 2 * 8 * 18) for s in S]
    k.fill0 = [t(f"fill0_{s}", 256) for s in S]
    k.rotated, k.rot_bias = t("rotated", 2 * D), t("rot_bias", 2)
    k.pope, k.angle = t("pope", 3 * T), t("angle", 8)
    k.turned = k.wide(0, 1, 1)
    k.minus_pi = t("minus_pi", 1)
    k.fill1 = [t(f"fill1_{s}", 256) for s in S]
    k.out_scale = t("out_scale", 1)
    k.gate = [t(f"gate{s}", 9 * 32) for s in S]
    k.vexp = t("vexp", 16 * 128)
    k.small = [t(f"small{s}", 64) for s in S]
    k.keymask = [t(f"keymask{s}", G) for s in S]


def setup_tensor(k, eng, pe, dve):
    eng.wait_ge(dve, 3)
    eng.matmul(k.psum[0][0][:, 0:1], k.const("mean"), k.scratch[:, 0:1], start=True, stop=True).then_inc(pe, 1)
    eng.matmul(k.psum[0][1][:, 0:D], k.wide(0, 0, 1)[:, 0:D], k.const("rot"), start=True, stop=True)
    eng.matmul(k.psum[0][1][:, D:2 * D], k.wide(0, 0, 1)[:, D:2 * D], k.const("rot"), start=True, stop=True)
    eng.matmul(k.psum[0][1][:, 2 * D:2 * D + 1], k.const("rot"), k.weight("l3a_bq"), start=True, stop=True)
    eng.matmul(k.psum[0][1][:, 2 * D + 1:2 * D + 2], k.const("rot"), k.weight("l3a_bk"), start=True, stop=True)\
       .then_inc(pe, 1)


def setup_scalar(k, eng, act, dve):
    eng.activation(k.angle[:, 0:1], k.weight("l2a_delta"), ACT.Sigmoid).then_inc(act, 1)
    eng.wait_ge(act, 1)
    eng.wait_ge(dve, 1)
    eng.activation(k.angle[:, 1:2], k.angle[:, 0:1], ACT.Sin, scale=float(2 * np.pi), bias=k.minus_pi[:, 0:1]).then_inc(act, 1)
    eng.activation(k.angle[:, 2:3], k.angle[:, 0:1], ACT.Sin, scale=float(np.pi)).then_inc(act, 1)


def setup_vector(k, eng, pe, dve, act):
    n = 0

    def link(ins):
        nonlocal n
        n += 1
        ins.then_inc(dve, 1)
        eng.wait_ge(dve, n)

    w = k.weight("l1f_w")
    link(eng.memset(k.minus_pi[:], -float(np.pi)))
    link(eng.memset(k.eps5[:], LN_EPS))
    link(eng.tensor_reduce(k.scratch[:, 0:1], w, AX.X, ALU.add, apply_absolute_value=True))
    eng.wait_ge(pe, 1)
    link(eng.tensor_scalar(k.scratch[:, 1:2], k.psum[0][0][:, 0:1], 1 / 128, LN_EPS, ALU.mult, ALU.max))
    link(eng.reciprocal(k.scratch[:, 2:3], k.scratch[:, 1:2]))
    link(eng.tensor_scalar(k.ternary[:], w, k.scratch[:, 2:3], 1.0, ALU.mult, ALU.min))
    link(eng.tensor_scalar(k.ternary[:], k.ternary[:], -1.0, float(3 << 22), ALU.max, ALU.add))
    link(eng.tensor_scalar(k.ternary[:], k.ternary[:], float(3 << 22), k.scratch[:, 1:2], ALU.subtract, ALU.mult))
    eng.wait_ge(act, 3)
    link(eng.tensor_tensor(k.angle[:, 3:4], k.angle[:, 2:3], k.angle[:, 2:3], ALU.mult))
    link(eng.tensor_scalar(k.angle[:, 4:5], k.angle[:, 3:4], -2.0, 1.0, ALU.mult, ALU.add))
    cos, sin = k.angle[:, 4:5], k.angle[:, 1:2]
    link(eng.tensor_scalar(k.turned[:, 0:T], k.const("psin"), sin, None, ALU.mult))
    link(eng.scalar_tensor_tensor(k.pope[:, T:2 * T], k.const("pcos"), cos, k.turned[:, 0:T], ALU.mult, ALU.subtract))
    link(eng.tensor_scalar(k.turned[:, T:2 * T], k.const("pcos"), sin, None, ALU.mult))
    link(eng.scalar_tensor_tensor(k.pope[:, 2 * T:3 * T], k.const("psin"), cos, k.turned[:, T:2 * T], ALU.mult, ALU.add))
    link(eng.tensor_scalar(k.pope[:, 2 * T:3 * T], k.pope[:, 2 * T:3 * T], k.const("psign"), None, ALU.mult))
    for g in range(4):
        rows, part = slice(32 * g, 32 * g + 32), 1 + g % 2
        link(eng.tensor_copy(k.pope[rows, 0:T], k.pope[rows, part * T:(part + 1) * T]))
    eng.wait_ge(pe, 2)
    link(eng.tensor_copy(k.rotated[:], k.psum[0][1][:, 0:2 * D]))
    link(eng.tensor_copy(k.rot_bias[:], k.psum[0][1][:, 2 * D:2 * D + 2]))
    for s in S:
        link(eng.memset(k.vbd[s][:], 0.0))
        for h2 in range(2):
            rows = slice(64 * h2, 64 * h2 + 64)
            link(eng.memset(k.vbd[s][rows, :].rearrange("p (q c) -> p q c", c=18)[:, :, 9 * h2 + 8:9 * h2 + 9], 1.0))
        link(eng.memset(k.vb[s].ap().rearrange("p (h c) -> p h c", c=65)[:, :, 64:65], 1.0))
    for name in ("l1x_ig", "l1x_fg"):
        w = k.weight(name)
        link(eng.tensor_tensor(w[:, 128:256], w[:, 128:256], w[:, 256:384], ALU.add))
    link(eng.tensor_scalar(k.out_scale[:], k.weight("l1x_out"), 1.0, None, ALU.add))
    for odd in range(2):
        for h in range(4):
            to = k.vexp[:].rearrange("p (v r) -> p v r", v=16)[:, :, odd * 64 + h * 16:odd * 64 + h * 16 + 16]
            cols = k.weight("l1a_v")[:, h * 32:(h + 1) * 32].rearrange("p (v o) -> p v o", o=2)[:, :, odd:odd + 1]
            link(eng.tensor_copy(to, cols.broadcast_to([128, 16, 16])))


LAYERS = [CtxNorm, L0Attn, L0Xattn, L0Ffn, L1Attn, L1Xattn, L1Ffn, L2Attn, L2Xattn, L2Ffn, L3Attn, L3Xattn, L3Ffn]


def pad(a, rows=128):
    out = np.zeros((rows, a.shape[1]), a.dtype)
    out[:a.shape[0]] = a
    return out


def col(v, times=1):
    return np.tile(np.reshape(v, (-1, 1)), (times, 1))


def weight_layouts(i):
    out = [("l0a_w", i["L0_attn_W_qkva"].T), ("l0a_gamma", col(i["L0_attn_gamma"]))]
    e8 = lambda a: a.transpose(1, 0, 2).reshape(a.shape[1], -1)
    out += [(n, col(i["L0_xattn_" + n[4:]])) for n in ("l0x_ln_l_w", "l0x_ln_l_b", "l0x_ln_c_w", "l0x_ln_c_b", "l0x_bo")]
    out += [("l0x_wq", i["L0_xattn_Wq"]), ("l0x_wkv", i["L0_xattn_Wkv"]),
            ("l0x_wo", i["L0_xattn_Wo"].reshape(8, 128, 128).transpose(1, 0, 2).reshape(128, -1))]
    out += [("l0f_wr", i["L0_ffn_Wr"]), ("l0f_w1", e8(i["L0_ffn_W1"])),
            ("l0f_b1", i["L0_ffn_b1"].reshape(8, 4, 128).transpose(2, 0, 1).reshape(128, 32)),
            ("l0f_w2", i["L0_ffn_W2"].reshape(8, 4, 128, 128).transpose(2, 0, 1, 3).reshape(128, -1)),
            ("l0f_b2", i["L0_ffn_b2"].T)]
    a = lambda n: i["L1_attn_" + n]
    two = lambda w: np.concatenate([w, w], axis=1)
    out += [("l1a_mu", col(a("x_proj_mu"))), ("l1a_w1", a("xl_w1").T), ("l1a_w2", pad(a("xl_w2").T)),
            ("l1a_b2", col(a("xl_b2")[:128])), ("l1a_b2e", pad(col(a("xl_b2")[128:]))),
            ("l1a_xo", a("x_out_w").T[:128]), ("l1a_xoe", pad(a("x_out_w").T[128:])), ("l1a_xb", a("x_bias").T),
            ("l1a_r", two(a("r_w").T)), ("l1a_k", two(a("k_w").T)), ("l1a_ww1", a("w_w1").T),
            ("l1a_ww2", pad(two(a("w_w2").T))), ("l1a_wb", col(a("w_b"), 2)), ("l1a_v", a("v_w").T),
            ("l1a_g", a("g_w").T), ("l1a_bonus", col(a("bonus"), 2)), ("l1a_gnw", col(a("gn_weight"))),
            ("l1a_gnb", col(a("gn_bias"))), ("l1a_o", a("o_w").T)]
    a = lambda n: i["L1_xattn_" + n]
    wide = lambda w: np.repeat(w.reshape(4, 3, 128).transpose(2, 1, 0), 32, axis=2).reshape(128, 384)
    out += [("l1x_ig", wide(a("igate_w"))), ("l1x_fg", wide(a("fgate_w"))),
            ("l1x_igb", col(np.repeat(a("igate_b"), 32))), ("l1x_fgb", col(np.repeat(a("fgate_b"), 32))),
            ("l1x_out", col(a("out_w"))), ("l1f_w", i["L1_ffn_weight"].T)]
    a = lambda n: i["L2_attn_" + n]
    swap = lambda w: w.reshape(w.shape[0], -1, 2, 16)[:, :, ::-1].reshape(w.shape)
    beside = lambda w: np.stack([w.reshape(64, 8, 32), swap(w).reshape(64, 8, 32)], axis=2).reshape(64, 512)
    four = lambda w: np.concatenate([w] * 4, axis=1)
    out += [("l2a_dkv", a("W_dkv")), ("l2a_uk", pad(a("W_uk"))), ("l2a_uv", pad(a("W_uv"))), ("l2a_dq", a("W_dq")),
            ("l2a_uq", pad(a("W_uq"))), ("l2a_qrq", pad(beside(a("W_qr")))),
            ("l2a_kr", four(a("W_kr"))), ("l2a_krs", four(swap(a("W_kr")))), ("l2a_delta", col(a("raw_delta"), 8)),
            ("l2a_out", a("W_out").reshape(4, 128, 128).transpose(1, 0, 2).reshape(128, -1))]
    a = lambda n: i["L2_xattn_" + n]
    out += [("l2x_wq", a("w_q")), ("l2x_wkv", a("w_kv")), ("l2x_wo", a("w_proj")), ("l2x_bo", col(a("b_proj"))),
            ("l2x_gx", col(a("g_x"))), ("l2x_bx", col(a("b_x"))), ("l2x_gkv", col(a("g_kv"))), ("l2x_bkv", col(a("b_kv")))]
    a = lambda n: i["L2_ffn_" + n]
    w2 = np.zeros((8, 384, 128), np.float32)
    w2[:, :352] = a("w2").transpose(0, 2, 1)
    out += [("l2f_gate", a("gate_w").T), ("l2f_w1", e8(a("w1").transpose(0, 2, 1))),
            ("l2f_w3", e8(a("w3").transpose(0, 2, 1))),
            ("l2f_w2", w2.reshape(8, 3, 128, 128).transpose(2, 0, 1, 3).reshape(128, -1))]
    a = lambda n: i["L3_attn_" + n]
    out += [("l3a_wq", a("Wq").T), ("l3a_wk", a("Wk").T), ("l3a_wv", a("Wv").T), ("l3a_wo", a("Wo").T),
            ("l3a_bq", col(a("bq"))), ("l3a_bk", col(a("bk"))), ("l3a_bv", col(a("bv"))), ("l3a_bo", col(a("bo")))]
    a = lambda n: i["L3_xattn_" + n]
    out += [("l3x_wq", a("Wq").T), ("l3x_wk", a("Wk").T), ("l3x_wv", a("Wv").T), ("l3x_bq", col(a("bq"))),
            ("l3x_bk", col(a("bk"))), ("l3x_bv", col(a("bv")))]
    a = lambda n: i["L3_ffn_" + n]
    out += [("l3f_w", e8(a("W_experts").transpose(0, 2, 1))), ("l3f_b", pad(a("b_experts"))),
            ("l3f_wr", a("W_router").T), ("l3f_br", np.repeat(a("b_router").reshape(1, 8), 128, axis=0))]
    return out


SETUP = ("l1f_w", "l2a_delta", "l3a_bq", "l3a_bk", "l1x_out", "l1a_v", "l1x_ig", "l1x_fg")
FIRST = ("l0a_", "l0x_")


def chunk(name):
    return 0 if name in SETUP else 1 if name.startswith(FIRST) else 2


MOE = ("l0f_", "l2f_")


def build(nc, weights_at, weights_n, moe_at, moe_n, x_d, ctx_d, ctok_d, m0_d, m1_d, w_d, moe_d, qk_d, c_d, out_d, layers, turns):
    with ExitStack() as ctx:
        k = Core(nc, ctx, weights_at, weights_n, moe_at, max(moe_n))
        sem = lambda n: ctx.enter_context(nc.semaphore(n))
        for name in ("x", "h", "c", "cn"):
            k.sbuf(name, G)
        k.sbuf("tmp", NTMP * G)
        k.sbuf("ctok", G)
        small(k, ctx)

        consts_in, weights_in = sem("consts_in"), [sem(f"weights_in{j}") for j in range(3)]
        setup_pe, setup_dve, setup_act = sem("setup_pe"), sem("setup_dve"), sem("setup_act")
        first_in, next_in = sem("first_in"), sem("next_in")
        ctok_in, mask_in = [sem(f"ctok_in{s}") for s in S], [sem(f"mask_in{s}") for s in S]
        x_free, moe_in = sem("x_free"), [sem(f"moe_in{j}") for j in range(2)]
        k.moe_in, k.x_free = moe_in, x_free
        k.ctok_in, k.mask_in = ctok_in, mask_in

        def load_chunk(eng, j):
            cols = [weights_at[n] for n in weights_at if chunk(n) == j]
            lo, hi = min(o for o, _ in cols), max(o + w for o, w in cols)
            eng.dma_start(k.w[:, lo:hi], w_d[:, lo:hi]).then_inc(weights_in[j], 16)

        def each_sublayer(eng):
            eng.wait_ge(weights_in[1], 16)
            later = [u for u in subs if not isinstance(u, (CtxNorm, L0Attn, L0Xattn, L0Ffn))]
            for u in subs:
                if u in later[:1]:
                    eng.wait_ge(weights_in[2], 16)
                yield u

        with nc.Block() as block:
            @block.sync
            def _(eng):
                eng.dma_start(k.c[:], c_d).then_inc(consts_in, 16)
                eng.dma_start(k.wide(0, 0, 1)[:, 0:2 * D], qk_d).then_inc(consts_in, 16)
                load_chunk(eng, 0)
                for s in S:
                    eng.dma_start(k.b(INPUT, s), x_d[:, s * G:(s + 1) * G]).then_inc(first_in, 16)
                    eng.dma_start(k.b("c", s), ctx_d[:, s * G:(s + 1) * G]).then_inc(first_in, 16)
                load_chunk(eng, 1)
                eng.wait_ge(first_in, 64)

            @block.tensor
            def _(eng):
                eng.wait_ge(consts_in, 32)
                eng.wait_ge(weights_in[0], 16)
                setup_tensor(k, eng, setup_pe, setup_dve)

            @block.scalar
            def _(eng):
                load_chunk(eng, 2)
                eng.wait_ge(weights_in[0], 16)
                setup_scalar(k, eng, setup_act, setup_dve)

            @block.vector
            def _(eng):
                eng.wait_ge(consts_in, 32)
                eng.memset(k.scratch[:, 7:8], 0.0).then_inc(x_free, 32)
                eng.wait_ge(weights_in[0], 16)
                setup_vector(k, eng, setup_pe, setup_dve, setup_act)

        prev, subs = Load(), []
        for cls in layers:
            prev = cls(k, prev)
            subs.append(prev)

        with nc.Fori(0, turns) as turn:
            with nc.Block() as block:
                @block.sync
                def _(eng):
                    eng.dma_start(k.moe[:, 0:moe_n[0]], moe_d[0]).then_inc(moe_in[0], 16)
                    for s in S:
                        at = turn * (2 * G) + s * G
                        eng.dma_start(k.b("ctok", s), ctok_d[:, bass.ds(at, G)]).then_inc(ctok_in[s], 16)
                        for half in range(2):
                            rows = slice(64 * half, 64 * half + 64)
                            for to, m in ((k.fill0[s], m0_d), (k.fill1[s], m1_d)):
                                src = m[:, bass.ds(at, G)].rearrange("o (t b j) -> o t b j", b=2, j=T)[:, :, half, :]
                                eng.dma_start(to[rows, :].bitcast(I32).rearrange("p (t j) -> p t j", j=T),
                                              src.broadcast_to([64, NT, T])).then_inc(mask_in[s], 16)
                        eng.dma_start(k.keymask[s][:].bitcast(I32), m0_d[:, bass.ds(at, G)].broadcast_to([128, G]))\
                           .then_inc(mask_in[s], 16)
                    first_moe = [u for u in subs if isinstance(u, L0Ffn)]
                    for u in first_moe:
                        for s in S:
                            u.output_ready(eng, s)
                    if first_moe:
                        eng.sem_clear(x_free)
                    eng.wait_ge(moe_in[0], 16)
                    eng.dma_start(k.moe[:, 0:moe_n[1]], moe_d[1]).then_inc(moe_in[1], 16)
                    for cls, to, src in ((L3Attn, INPUT, x_d), (L3Xattn, "c", ctx_d)):
                        for u in subs:
                            if isinstance(u, cls):
                                for s in S:
                                    at = turn * (2 * G) + (2 + s) * G
                                    u.output_ready(eng, s)
                                    eng.dma_start(k.b(to, s), src[:, bass.ds(at, G)]).then_inc(next_in, 16)
                    for s in S:
                        at = turn * (2 * G) + s * G
                        subs[-1].output_ready(eng, s)
                        eng.dma_start(out_d[:, bass.ds(at, G)], k.b("x", s)).then_inc(x_free, 16)
                    eng.wait_ge(moe_in[1], 16)
                    eng.wait_ge(next_in, 64)

                @block.tensor
                def _(eng):
                    for u in each_sublayer(eng):
                        u.pe_program(eng)

                @block.scalar
                def _(eng):
                    log_and_exp_table(eng)
                    for u in each_sublayer(eng):
                        u.act_program(eng)

                @block.vector
                def _(eng):
                    for u in each_sublayer(eng):
                        u.dve_program(eng)

                @block.gpsimd
                def _(eng):
                    for u in each_sublayer(eng):
                        u.pool_program(eng)

            for q in k.sems + [next_in] + ctok_in + mask_in + moe_in:
                nc.sync.sem_clear(q)
            nc.all_engine_barrier()
        nc.sync.wait_ge(x_free, 32)


def kernel(**inputs):
    import concourse.bacc as _bacc
    from concourse.bass_utils import run_bass_kernel_spmd as _run

    i = {n: np.asarray(a) for n, a in inputs.items()}
    tokens = lambda a: np.ascontiguousarray(a.reshape(B * T, D).T)
    ahead = lambda a: np.concatenate([a, a[:, :2 * G]], axis=1)
    entries = [(n, np.ascontiguousarray(a)) for n, a in weight_layouts(i)]
    entries.sort(key=lambda e: chunk(e[0]))
    packs = [[e for e in entries if not e[0].startswith(MOE)]] + [[e for e in entries if e[0].startswith(m)] for m in MOE]
    at, n = zip(*[columns([(name, a.shape[1]) for name, a in p]) for p in packs])
    pack = lambda p: np.concatenate([a for _, a in p], axis=1)
    arrays = {
        "x_t": ahead(tokens(i["x"])), "ctx_t": ahead(tokens(i["ctx_1024"])),
        "ctx_tok": np.ascontiguousarray(i["ctx_1024"].reshape(B * T // 128, 128, D).transpose(1, 0, 2).reshape(128, -1)),
        "mask0": i["mask_BxS2_ik0"].reshape(1, B * T), "mask1": i["mask_BxS2_ik1"].reshape(1, B * T),
        "weights_d": pack(packs[0]), "moe0_d": pack(packs[1]), "moe2_d": pack(packs[2]), "consts_d": constants(),
        "l3a_qk": np.concatenate([i["L3_attn_Wq"], i["L3_attn_Wk"]], axis=1),
    }
    nc = _bacc.Bacc("TRN2", target_bir_lowering=False, num_devices=1)
    d = {name: nc.dram_tensor(name, a.shape, mybir.dt.from_np(a.dtype), kind="ExternalInput").ap()
         for name, a in arrays.items()}
    out = nc.dram_tensor("out_t", (D, B * T), F32, kind="ExternalOutput").ap()
    build(nc, at[0], n[0], at[1:], n[1:], d["x_t"], d["ctx_t"], d["ctx_tok"], d["mask0"], d["mask1"], d["weights_d"],
          [d["moe0_d"], d["moe2_d"]], d["l3a_qk"], d["consts_d"],
          out, LAYERS, TURNS)
    r = _run(nc, [arrays], core_ids=[0])
    return np.ascontiguousarray(r.results[0]["out_t"].T).reshape(B, T, D)
```
